# Optimizing a Trainium2 kernel written in Bass

```python
import numpy as np
import jax
import jax.numpy as jnp

def _softmax(x, axis=-1):
    return jax.nn.softmax(x, axis=axis)

def _gelu(x):
    return jax.nn.gelu(x, approximate=True)

def _silu(x):
    return jax.nn.silu(x)

def _sigmoid(x):
    return jax.nn.sigmoid(x)

def _layernorm(x, axis=-1, eps=1e-05):
    m = jnp.mean(x, axis=axis, keepdims=True)
    v = jnp.var(x, axis=axis, keepdims=True)
    return (x - m) / jnp.sqrt(v + eps)

def _scatter_add(tgt, idx, src, axis=0):
    return tgt.at[idx].add(src)

def _segment_sum(src, seg, n):
    return jax.ops.segment_sum(src, seg, n)
kernel_name = 'mk_gps_d4_gnn_r32_ca62fe'

def setup_inputs(seed: int=0):
    np.random.seed(seed)
    _w = jnp.asarray

    def _rec_inputs():
        import jax
        import jax.numpy as jnp
        _gk = jax.random.key(seed)
        x = -0.0002117 + 1 * jax.random.normal(jax.random.fold_in(_gk, 1), (3125, 256), jnp.float32)
        src = jax.random.randint(jax.random.fold_in(_gk, 2), (50000,), 0, 3125, jnp.int32)
        dst = jax.random.randint(jax.random.fold_in(_gk, 3), (50000,), 0, 3125, jnp.int32)
        _o = jnp.argsort(dst, stable=True)
        src = src[_o]
        dst = dst[_o]
        edge_attr_64 = 0.000279952 + 1.00013 * jax.random.normal(jax.random.fold_in(_gk, 12), (50000, 64), jnp.float32)
        edge_weight = jax.random.uniform(jax.random.fold_in(_gk, 14), (50000,), jnp.float32, 0.0, 1)
        return (x, src, dst, edge_attr_64, edge_weight)
    x, src, dst, edge_attr_64, edge_weight = _rec_inputs()

    def _L0_gnn_setup():
        import jax, jax.numpy as jnp
        import numpy as np
        N = 3125
        E = 100000
        F_IN = 256
        F_OUT = 256
        key = jax.random.key(seed)
        k1, k2, k3, k4, k5 = jax.random.split(key, 5)
        x = jax.random.normal(k1, (N, F_IN), dtype=jnp.float32)
        edge_row = jax.random.randint(k2, (E,), 0, N, dtype=jnp.int32)
        edge_col = jax.random.randint(k3, (E,), 0, N, dtype=jnp.int32)
        edge_val = jax.random.uniform(k4, (E,), dtype=jnp.float32)
        W = jax.random.normal(k5, (2 * F_IN, F_OUT), dtype=jnp.float32) * (1.0 / np.sqrt(2 * F_IN))
        b = jnp.zeros((F_OUT,), dtype=jnp.float32)
        return {'x': x, 'edge_row': edge_row, 'edge_col': edge_col, 'edge_val': edge_val, 'W': W, 'b': b}
    _L0_gnn_all = _L0_gnn_setup()
    _L0_gnn_in = {k: v for k, v in _L0_gnn_all.items() if k in ('W', 'b')}
    del _L0_gnn_all

    def _L0_mix_setup():
        import jax, jax.numpy as jnp
        import numpy as np
        import math
        EMBED = 256
        HEADS = 4
        HEAD_DIM = EMBED // HEADS
        OUT_DIM = 256
        LN_EPS = 1e-05

        def _qkv_init(key):
            spread = math.sqrt(3.0 / EMBED)
            gain, delta = (0.01, 0.01)
            w = jax.random.uniform(key, (EMBED, EMBED), minval=-spread, maxval=spread) * gain
            return w + delta * jnp.eye(EMBED, dtype=w.dtype)

        def _layer_norm(x, g, b):
            mu = jnp.mean(x, axis=-1, keepdims=True)
            var = jnp.mean(jnp.square(x - mu), axis=-1, keepdims=True)
            return (x - mu) * jax.lax.rsqrt(var + LN_EPS) * g + b

        def _split_heads(x, B, S):
            return x.reshape(B, S, HEADS, HEAD_DIM).transpose(0, 2, 1, 3)
        key = jax.random.key(seed)
        ks = jax.random.split(key, 6)
        seq = jax.random.normal(ks[0], (4, 256, EMBED), dtype=jnp.float32)
        wq = _qkv_init(ks[1])
        wk = _qkv_init(ks[2])
        wv = _qkv_init(ks[3])
        bound = 1.0 / math.sqrt(EMBED)
        wo = jax.random.uniform(ks[4], (OUT_DIM, EMBED), minval=-bound, maxval=bound)
        bo = jax.random.uniform(ks[5], (OUT_DIM,), minval=-bound, maxval=bound)
        ln_k_g = jnp.ones((HEAD_DIM,), jnp.float32)
        ln_k_b = jnp.zeros((HEAD_DIM,), jnp.float32)
        ln_v_g = jnp.ones((HEAD_DIM,), jnp.float32)
        ln_v_b = jnp.zeros((HEAD_DIM,), jnp.float32)
        return {'seq': seq, 'wq': wq, 'wk': wk, 'wv': wv, 'wo': wo, 'bo': bo, 'ln_k_g': ln_k_g, 'ln_k_b': ln_k_b, 'ln_v_g': ln_v_g, 'ln_v_b': ln_v_b}
    _L0_mix_all = _L0_mix_setup()
    _L0_mix_in = {k: v for k, v in _L0_mix_all.items() if k in ('wq', 'wk', 'wv', 'wo', 'bo', 'ln_k_g', 'ln_k_b', 'ln_v_g', 'ln_v_b')}
    del _L0_mix_all

    def _L0_ffn_setup():
        import jax, jax.numpy as jnp
        import numpy as np
        B, K, D = (512, 16, 256)
        E = 32
        H = int(D * 0.25)
        key = jax.random.key(seed)
        ks = jax.random.split(key, 7)
        d_rs = D ** (-0.5)
        h_rs = H ** (-0.5)
        x = jax.random.normal(ks[0], (B, K, D), dtype=jnp.float32)
        router_w = jax.random.uniform(ks[1], (E, D), jnp.float32, -d_rs, d_rs)
        router_b = jax.random.uniform(ks[2], (E,), jnp.float32, -d_rs, d_rs)
        W1 = jax.random.uniform(ks[3], (E, D, H), jnp.float32, -h_rs, h_rs)
        b1 = jax.random.uniform(ks[4], (E, H), jnp.float32, -h_rs, h_rs)
        W2 = jax.random.uniform(ks[5], (E, H, D), jnp.float32, -d_rs, d_rs)
        b2 = jax.random.uniform(ks[6], (E, D), jnp.float32, -d_rs, d_rs)
        return {'x': x, 'router_w': router_w, 'router_b': router_b, 'W1': W1, 'b1': b1, 'W2': W2, 'b2': b2}
    _L0_ffn_all = _L0_ffn_setup()
    _L0_ffn_in = {k: v for k, v in _L0_ffn_all.items() if k in ('router_w', 'router_b', 'W1', 'b1', 'W2', 'b2')}
    del _L0_ffn_all

    def _L1_gnn_setup():
        import jax, jax.numpy as jnp
        import numpy as np
        N_NODES = 3125
        N_EDGES = 10000
        D_IN = 256
        D_H = 256
        D_OUT = 256

        def gcn_layer(x, W, b, src, dst, num_nodes):
            ones = jnp.ones(src.shape[0], dtype=x.dtype)
            deg = jax.ops.segment_sum(ones, dst, num_segments=num_nodes)
            dinv = jnp.where(deg > 0, jax.lax.rsqrt(deg), 0.0)
            norm = dinv[src] * dinv[dst]
            h = x @ W
            msg = h[src] * norm[:, None]
            out = jax.ops.segment_sum(msg, dst, num_segments=num_nodes)
            return out + b
        key = jax.random.key(seed)
        ks = jax.random.split(key, 8)
        x = jax.random.normal(ks[0], (N_NODES, D_IN), dtype=jnp.float32)
        edge_index = jax.random.randint(ks[1], (2, N_EDGES), 0, N_NODES, dtype=jnp.int64)

        def glorot(k, fan_in, fan_out):
            s = jnp.sqrt(6.0 / (fan_in + fan_out)).astype(jnp.float32)
            return jax.random.uniform(k, (fan_in, fan_out), jnp.float32, -s, s)
        return {'x': x, 'edge_index': edge_index, 'W1': glorot(ks[2], D_IN, D_H), 'b1': jnp.zeros((D_H,), jnp.float32), 'W2': glorot(ks[3], D_H, D_H), 'b2': jnp.zeros((D_H,), jnp.float32), 'W3': glorot(ks[4], D_H, D_OUT), 'b3': jnp.zeros((D_OUT,), jnp.float32)}
    _L1_gnn_all = _L1_gnn_setup()
    _L1_gnn_in = {k: v for k, v in _L1_gnn_all.items() if k in ('W1', 'b1', 'W2', 'b2', 'W3', 'b3')}
    del _L1_gnn_all

    def _L1_mix_setup():
        import jax, jax.numpy as jnp
        import numpy as np
        DIM = 256
        HEADS = 4
        DIM_HEAD = 32
        NUM_MEM = 4
        HIDDEN = HEADS * DIM_HEAD
        SCALE = DIM_HEAD ** (-0.5)

        def rmsnorm(x, g):
            n = jnp.linalg.norm(x, axis=-1, keepdims=True)
            return x / jnp.maximum(n, 1e-12) * g * x.shape[-1] ** 0.5
        key = jax.random.key(seed)
        ks = jax.random.split(key, 8)
        B, N = (4, 512)
        return {'x': jax.random.normal(ks[0], (B, N, DIM), jnp.float32), 't': jax.random.normal(ks[1], (B,), jnp.float32), 'w_qkv': jax.random.normal(ks[2], (DIM, 3 * HIDDEN), jnp.float32) * 0.02, 'mem_kv': jax.random.normal(ks[3], (2, HEADS, DIM_HEAD, NUM_MEM), jnp.float32), 'w_out': jax.random.normal(ks[4], (HIDDEN, DIM), jnp.float32) * 0.02, 'b_out': jnp.zeros((DIM,), jnp.float32), 'g_out': jnp.ones((DIM,), jnp.float32), 'g_pre': jnp.ones((DIM,), jnp.float32)}
    _L1_mix_all = _L1_mix_setup()
    _L1_mix_in = {k: v for k, v in _L1_mix_all.items() if k in ('t', 'w_qkv', 'mem_kv', 'w_out', 'b_out', 'g_out', 'g_pre')}
    del _L1_mix_all

    def _L1_ffn_setup():
        import jax, jax.numpy as jnp
        import numpy as np
        B, S, D = (8, 128, 256)
        H = 4 * D
        CAPACITY = 0.5
        key = jax.random.key(seed)
        ks = jax.random.split(key, 6)
        x = jax.random.normal(ks[0], (B, S, D), dtype=jnp.float32)
        attention_mask = jnp.zeros((B, 1, 1, S), dtype=jnp.float32)
        wr = jax.random.normal(ks[1], (D, 1), dtype=jnp.float32) * 0.02
        br = jnp.zeros((1,), dtype=jnp.float32)
        w1 = jax.random.normal(ks[2], (D, H), dtype=jnp.float32) * 0.02
        b1 = jnp.zeros((H,), dtype=jnp.float32)
        w2 = jax.random.normal(ks[3], (H, D), dtype=jnp.float32) * 0.02
        b2 = jnp.zeros((D,), dtype=jnp.float32)
        return {'x': x, 'attention_mask': attention_mask, 'wr': wr, 'br': br, 'w1': w1, 'b1': b1, 'w2': w2, 'b2': b2}
    _L1_ffn_all = _L1_ffn_setup()
    _L1_ffn_in = {k: v for k, v in _L1_ffn_all.items() if k in ('attention_mask', 'wr', 'br', 'w1', 'b1', 'w2', 'b2')}
    del _L1_ffn_all

    def _L2_gnn_setup():
        import jax, jax.numpy as jnp
        import numpy as np
        N = 3125
        E = 10000
        CIN = 256
        EDIM = 64
        EEMB = 256
        H = 1024
        LN_EPS = 1e-05

        def _ln(x, g, b):
            m = jnp.mean(x, axis=-1, keepdims=True)
            v = jnp.var(x, axis=-1, keepdims=True)
            return (x - m) * jax.lax.rsqrt(v + LN_EPS) * g + b
        key = jax.random.key(seed)
        ks = jax.random.split(key, 16)

        def w(k, i, o):
            return (jax.random.normal(k, (i, o), jnp.float32) / np.sqrt(i)).astype(jnp.float32)
        return {'x': jax.random.normal(ks[0], (N, CIN), jnp.float32), 'edge_index': jax.random.randint(ks[1], (2, E), 0, N, dtype=jnp.int64), 'edge_attr': jax.random.normal(ks[2], (E, EDIM), jnp.float32), 'eps': jnp.float32(0.0), 'ee_w1': w(ks[3], EDIM, EEMB), 'ee_b1': jnp.zeros((EEMB,), jnp.float32), 'ee_w2': w(ks[4], EEMB, CIN), 'ee_b2': jnp.zeros((CIN,), jnp.float32), 'w1': w(ks[5], CIN, H), 'b1': jnp.zeros((H,), jnp.float32), 'g1': jnp.ones((H,), jnp.float32), 'be1': jnp.zeros((H,), jnp.float32), 'w2': w(ks[6], H, H), 'b2': jnp.zeros((H,), jnp.float32), 'g2': jnp.ones((H,), jnp.float32), 'be2': jnp.zeros((H,), jnp.float32), 'w3': w(ks[7], H, CIN), 'b3': jnp.zeros((CIN,), jnp.float32), 'bn_g': jnp.ones((CIN,), jnp.float32), 'bn_b': jnp.zeros((CIN,), jnp.float32)}
    _L2_gnn_all = _L2_gnn_setup()
    _L2_gnn_in = {k: v for k, v in _L2_gnn_all.items() if k in ('eps', 'ee_w1', 'ee_b1', 'ee_w2', 'ee_b2', 'w1', 'b1', 'g1', 'be1', 'w2', 'b2', 'g2', 'be2', 'w3', 'b3', 'bn_g', 'bn_b')}
    del _L2_gnn_all

    def _L2_mix_setup():
        import jax, jax.numpy as jnp
        import numpy as np
        D_MODEL = 256
        NUM_HEADS = 8
        DEPTH = D_MODEL // NUM_HEADS
        B, L = (32, 128)

        def _feature_map(x):
            return jax.nn.elu(x) + 1.0
        key = jax.random.key(seed)
        ks = jax.random.split(key, 9)
        sc = 1.0 / np.sqrt(D_MODEL)
        return {'x': jax.random.normal(ks[0], (B, L, D_MODEL), dtype=jnp.float32), 'wq': jax.random.normal(ks[1], (D_MODEL, D_MODEL), dtype=jnp.float32) * sc, 'bq': jnp.zeros((D_MODEL,), dtype=jnp.float32), 'wk': jax.random.normal(ks[2], (D_MODEL, D_MODEL), dtype=jnp.float32) * sc, 'bk': jnp.zeros((D_MODEL,), dtype=jnp.float32), 'wv': jax.random.normal(ks[3], (D_MODEL, D_MODEL), dtype=jnp.float32) * sc, 'bv': jnp.zeros((D_MODEL,), dtype=jnp.float32), 'wo': jax.random.normal(ks[4], (D_MODEL, D_MODEL), dtype=jnp.float32) * sc, 'bo': jnp.zeros((D_MODEL,), dtype=jnp.float32)}
    _L2_mix_all = _L2_mix_setup()
    _L2_mix_in = {k: v for k, v in _L2_mix_all.items() if k in ('wq', 'bq', 'wk', 'bk', 'wv', 'bv', 'wo', 'bo')}
    del _L2_mix_all

    def _L2_ffn_setup():
        import jax, jax.numpy as jnp
        import numpy as np
        B, A = (128, 8)
        IN, OUT = (256, 256)
        SH1, SH2 = (256, 128)
        EH1, EH2 = (128, 64)
        E, TOPK = (4, 2)

        def _shared_mlp(x, W1, b1, W2, b2, W3, b3):
            h = jax.nn.relu(x @ W1 + b1)
            h = jax.nn.relu(h @ W2 + b2)
            return h @ W3 + b3

        def _experts_mlp(x, eW1, eb1, eW2, eb2, eW3, eb3):
            h = jax.nn.relu(jnp.einsum('baf,efh->ebah', x, eW1) + eb1[:, None, None, :])
            h = jax.nn.relu(jnp.einsum('ebah,ehg->ebag', h, eW2) + eb2[:, None, None, :])
            o = jnp.einsum('ebag,ego->ebao', h, eW3) + eb3[:, None, None, :]
            return jnp.moveaxis(o, 0, -1)
        key = jax.random.key(seed)
        ks = jax.random.split(key, 16)
        s = 0.05
        return {'x': jax.random.normal(ks[0], (B, A, IN), jnp.float32), 'sW1': jax.random.normal(ks[1], (IN, SH1), jnp.float32) * s, 'sb1': jnp.zeros((SH1,), jnp.float32), 'sW2': jax.random.normal(ks[2], (SH1, SH2), jnp.float32) * s, 'sb2': jnp.zeros((SH2,), jnp.float32), 'sW3': jax.random.normal(ks[3], (SH2, OUT), jnp.float32) * s, 'sb3': jnp.zeros((OUT,), jnp.float32), 'eW1': jax.random.normal(ks[4], (E, IN, EH1), jnp.float32) * s, 'eb1': jnp.zeros((E, EH1), jnp.float32), 'eW2': jax.random.normal(ks[5], (E, EH1, EH2), jnp.float32) * s, 'eb2': jnp.zeros((E, EH2), jnp.float32), 'eW3': jax.random.normal(ks[6], (E, EH2, OUT), jnp.float32) * s, 'eb3': jnp.zeros((E, OUT), jnp.float32), 'gW': jax.random.normal(ks[7], (IN, E), jnp.float32) * s, 'gb': jnp.zeros((E,), jnp.float32)}
    _L2_ffn_all = _L2_ffn_setup()
    _L2_ffn_in = {k: v for k, v in _L2_ffn_all.items() if k in ('sW1', 'sb1', 'sW2', 'sb2', 'sW3', 'sb3', 'eW1', 'eb1', 'eW2', 'eb2', 'eW3', 'eb3', 'gW', 'gb')}
    del _L2_ffn_all

    def _L3_gnn_setup():
        import jax, jax.numpy as jnp
        import numpy as np
        N_NODES = 50000
        N_EDGES = 10000
        HIDDEN = 256
        LN_EPS = 1e-05
        NORM_EPS = 1e-12
        key = jax.random.key(seed)
        ks = jax.random.split(key, 4)
        scale = 1.0 / np.sqrt(HIDDEN)
        return {'x': jax.random.normal(ks[0], (N_NODES, HIDDEN), dtype=jnp.float32), 'edge_index': jax.random.randint(ks[1], (2, N_EDGES), 0, N_NODES, dtype=jnp.int64), 'W_l': jax.random.normal(ks[2], (HIDDEN, HIDDEN), dtype=jnp.float32) * scale, 'b_l': jnp.zeros((HIDDEN,), dtype=jnp.float32), 'W_r': jax.random.normal(ks[3], (HIDDEN, HIDDEN), dtype=jnp.float32) * scale, 'gamma': jnp.ones((HIDDEN,), dtype=jnp.float32), 'beta': jnp.zeros((HIDDEN,), dtype=jnp.float32)}
    _L3_gnn_all = _L3_gnn_setup()
    _L3_gnn_in = {k: v for k, v in _L3_gnn_all.items() if k in ('W_l', 'b_l', 'W_r', 'gamma', 'beta')}
    del _L3_gnn_all

    def _L3_mix_setup():
        import jax, jax.numpy as jnp
        import numpy as np
        NUM_HEADS = 8
        key = jax.random.key(seed)
        ks = jax.random.split(key, 5)
        B, N, C = (8, 512, 256)
        x = jax.random.normal(ks[0], (B, N, C), dtype=jnp.float32)
        Wq = jax.random.normal(ks[1], (C, C), dtype=jnp.float32) * 0.02
        Wkv = jax.random.normal(ks[2], (2 * C, C), dtype=jnp.float32) * 0.02
        Wproj = jax.random.normal(ks[3], (C, C), dtype=jnp.float32) * 0.02
        bproj = jnp.zeros((C,), dtype=jnp.float32)
        return {'x': x, 'Wq': Wq, 'Wkv': Wkv, 'Wproj': Wproj, 'bproj': bproj}
    _L3_mix_all = _L3_mix_setup()
    _L3_mix_in = {k: v for k, v in _L3_mix_all.items() if k in ('Wq', 'Wkv', 'Wproj', 'bproj')}
    del _L3_mix_all

    def _L3_ffn_setup():
        import jax, jax.numpy as jnp
        import numpy as np
        B, S, H, F, E, K = (8, 128, 256, 512, 16, 2)
        EPS = 1e-05
        key = jax.random.key(seed)
        ks = jax.random.split(key, 9)
        sc = 0.02
        return {'x': jax.random.normal(ks[0], (B, S, H), dtype=jnp.float32), 'gate_w': jax.random.normal(ks[1], (H, E), dtype=jnp.float32) * sc, 'gate_b': jnp.zeros((E,), dtype=jnp.float32), 'w1': jax.random.normal(ks[2], (E, H, F), dtype=jnp.float32) * sc, 'b1': jnp.zeros((E, F), dtype=jnp.float32), 'w2': jax.random.normal(ks[3], (E, F, H), dtype=jnp.float32) * sc, 'b2': jnp.zeros((E, H), dtype=jnp.float32), 'gamma': jnp.ones((H,), dtype=jnp.float32), 'beta': jnp.zeros((H,), dtype=jnp.float32)}
    _L3_ffn_all = _L3_ffn_setup()
    _L3_ffn_in = {k: v for k, v in _L3_ffn_all.items() if k in ('gate_w', 'gate_b', 'w1', 'b1', 'w2', 'b2', 'gamma', 'beta')}
    del _L3_ffn_all
    return {'x': x, 'src': src, 'dst': dst, 'edge_attr_64': edge_attr_64, 'edge_weight': edge_weight, 'L0_gnn_W': _L0_gnn_in['W'], 'L0_gnn_b': _L0_gnn_in['b'], 'L0_mix_wq': _L0_mix_in['wq'], 'L0_mix_wk': _L0_mix_in['wk'], 'L0_mix_wv': _L0_mix_in['wv'], 'L0_mix_wo': _L0_mix_in['wo'], 'L0_mix_bo': _L0_mix_in['bo'], 'L0_mix_ln_k_g': _L0_mix_in['ln_k_g'], 'L0_mix_ln_k_b': _L0_mix_in['ln_k_b'], 'L0_mix_ln_v_g': _L0_mix_in['ln_v_g'], 'L0_mix_ln_v_b': _L0_mix_in['ln_v_b'], 'L0_ffn_router_w': _L0_ffn_in['router_w'], 'L0_ffn_router_b': _L0_ffn_in['router_b'], 'L0_ffn_W1': _L0_ffn_in['W1'], 'L0_ffn_b1': _L0_ffn_in['b1'], 'L0_ffn_W2': _L0_ffn_in['W2'], 'L0_ffn_b2': _L0_ffn_in['b2'], 'L1_gnn_W1': _L1_gnn_in['W1'], 'L1_gnn_b1': _L1_gnn_in['b1'], 'L1_gnn_W2': _L1_gnn_in['W2'], 'L1_gnn_b2': _L1_gnn_in['b2'], 'L1_gnn_W3': _L1_gnn_in['W3'], 'L1_gnn_b3': _L1_gnn_in['b3'], 'L1_mix_t': _L1_mix_in['t'], 'L1_mix_w_qkv': _L1_mix_in['w_qkv'], 'L1_mix_mem_kv': _L1_mix_in['mem_kv'], 'L1_mix_w_out': _L1_mix_in['w_out'], 'L1_mix_b_out': _L1_mix_in['b_out'], 'L1_mix_g_out': _L1_mix_in['g_out'], 'L1_mix_g_pre': _L1_mix_in['g_pre'], 'L1_ffn_attention_mask': _L1_ffn_in['attention_mask'], 'L1_ffn_wr': _L1_ffn_in['wr'], 'L1_ffn_br': _L1_ffn_in['br'], 'L1_ffn_w1': _L1_ffn_in['w1'], 'L1_ffn_b1': _L1_ffn_in['b1'], 'L1_ffn_w2': _L1_ffn_in['w2'], 'L1_ffn_b2': _L1_ffn_in['b2'], 'L2_gnn_eps': _L2_gnn_in['eps'], 'L2_gnn_ee_w1': _L2_gnn_in['ee_w1'], 'L2_gnn_ee_b1': _L2_gnn_in['ee_b1'], 'L2_gnn_ee_w2': _L2_gnn_in['ee_w2'], 'L2_gnn_ee_b2': _L2_gnn_in['ee_b2'], 'L2_gnn_w1': _L2_gnn_in['w1'], 'L2_gnn_b1': _L2_gnn_in['b1'], 'L2_gnn_g1': _L2_gnn_in['g1'], 'L2_gnn_be1': _L2_gnn_in['be1'], 'L2_gnn_w2': _L2_gnn_in['w2'], 'L2_gnn_b2': _L2_gnn_in['b2'], 'L2_gnn_g2': _L2_gnn_in['g2'], 'L2_gnn_be2': _L2_gnn_in['be2'], 'L2_gnn_w3': _L2_gnn_in['w3'], 'L2_gnn_b3': _L2_gnn_in['b3'], 'L2_gnn_bn_g': _L2_gnn_in['bn_g'], 'L2_gnn_bn_b': _L2_gnn_in['bn_b'], 'L2_mix_wq': _L2_mix_in['wq'], 'L2_mix_bq': _L2_mix_in['bq'], 'L2_mix_wk': _L2_mix_in['wk'], 'L2_mix_bk': _L2_mix_in['bk'], 'L2_mix_wv': _L2_mix_in['wv'], 'L2_mix_bv': _L2_mix_in['bv'], 'L2_mix_wo': _L2_mix_in['wo'], 'L2_mix_bo': _L2_mix_in['bo'], 'L2_ffn_sW1': _L2_ffn_in['sW1'], 'L2_ffn_sb1': _L2_ffn_in['sb1'], 'L2_ffn_sW2': _L2_ffn_in['sW2'], 'L2_ffn_sb2': _L2_ffn_in['sb2'], 'L2_ffn_sW3': _L2_ffn_in['sW3'], 'L2_ffn_sb3': _L2_ffn_in['sb3'], 'L2_ffn_eW1': _L2_ffn_in['eW1'], 'L2_ffn_eb1': _L2_ffn_in['eb1'], 'L2_ffn_eW2': _L2_ffn_in['eW2'], 'L2_ffn_eb2': _L2_ffn_in['eb2'], 'L2_ffn_eW3': _L2_ffn_in['eW3'], 'L2_ffn_eb3': _L2_ffn_in['eb3'], 'L2_ffn_gW': _L2_ffn_in['gW'], 'L2_ffn_gb': _L2_ffn_in['gb'], 'L3_gnn_W_l': _L3_gnn_in['W_l'], 'L3_gnn_b_l': _L3_gnn_in['b_l'], 'L3_gnn_W_r': _L3_gnn_in['W_r'], 'L3_gnn_gamma': _L3_gnn_in['gamma'], 'L3_gnn_beta': _L3_gnn_in['beta'], 'L3_mix_Wq': _L3_mix_in['Wq'], 'L3_mix_Wkv': _L3_mix_in['Wkv'], 'L3_mix_Wproj': _L3_mix_in['Wproj'], 'L3_mix_bproj': _L3_mix_in['bproj'], 'L3_ffn_gate_w': _L3_ffn_in['gate_w'], 'L3_ffn_gate_b': _L3_ffn_in['gate_b'], 'L3_ffn_w1': _L3_ffn_in['w1'], 'L3_ffn_b1': _L3_ffn_in['b1'], 'L3_ffn_w2': _L3_ffn_in['w2'], 'L3_ffn_b2': _L3_ffn_in['b2'], 'L3_ffn_gamma': _L3_ffn_in['gamma'], 'L3_ffn_beta': _L3_ffn_in['beta']}

def reference(x, src, dst, edge_attr_64, edge_weight, L0_gnn_W, L0_gnn_b, L0_mix_wq, L0_mix_wk, L0_mix_wv, L0_mix_wo, L0_mix_bo, L0_mix_ln_k_g, L0_mix_ln_k_b, L0_mix_ln_v_g, L0_mix_ln_v_b, L0_ffn_router_w, L0_ffn_router_b, L0_ffn_W1, L0_ffn_b1, L0_ffn_W2, L0_ffn_b2, L1_gnn_W1, L1_gnn_b1, L1_gnn_W2, L1_gnn_b2, L1_gnn_W3, L1_gnn_b3, L1_mix_t, L1_mix_w_qkv, L1_mix_mem_kv, L1_mix_w_out, L1_mix_b_out, L1_mix_g_out, L1_mix_g_pre, L1_ffn_attention_mask, L1_ffn_wr, L1_ffn_br, L1_ffn_w1, L1_ffn_b1, L1_ffn_w2, L1_ffn_b2, L2_gnn_eps, L2_gnn_ee_w1, L2_gnn_ee_b1, L2_gnn_ee_w2, L2_gnn_ee_b2, L2_gnn_w1, L2_gnn_b1, L2_gnn_g1, L2_gnn_be1, L2_gnn_w2, L2_gnn_b2, L2_gnn_g2, L2_gnn_be2, L2_gnn_w3, L2_gnn_b3, L2_gnn_bn_g, L2_gnn_bn_b, L2_mix_wq, L2_mix_bq, L2_mix_wk, L2_mix_bk, L2_mix_wv, L2_mix_bv, L2_mix_wo, L2_mix_bo, L2_ffn_sW1, L2_ffn_sb1, L2_ffn_sW2, L2_ffn_sb2, L2_ffn_sW3, L2_ffn_sb3, L2_ffn_eW1, L2_ffn_eb1, L2_ffn_eW2, L2_ffn_eb2, L2_ffn_eW3, L2_ffn_eb3, L2_ffn_gW, L2_ffn_gb, L3_gnn_W_l, L3_gnn_b_l, L3_gnn_W_r, L3_gnn_gamma, L3_gnn_beta, L3_mix_Wq, L3_mix_Wkv, L3_mix_Wproj, L3_mix_bproj, L3_ffn_gate_w, L3_ffn_gate_b, L3_ffn_w1, L3_ffn_b1, L3_ffn_w2, L3_ffn_b2, L3_ffn_gamma, L3_ffn_beta):
    import jax
    import jax.numpy as jnp

    def _L0_gnn_ref(x, edge_row, edge_col, edge_val, W, b):
        import jax, jax.numpy as jnp
        import numpy as np
        N = 3125
        E = 100000
        F_IN = 256
        F_OUT = 256
        gathered = edge_val[:, None] * x[edge_col]
        support = jax.ops.segment_sum(gathered, edge_row, num_segments=N)
        h = jnp.concatenate([x, support], axis=1)
        out = h @ W + b
        return jax.nn.relu(out)

    def _L0_mix_ref(seq, wq, wk, wv, wo, bo, ln_k_g, ln_k_b, ln_v_g, ln_v_b):
        import jax, jax.numpy as jnp
        import numpy as np
        import math
        EMBED = 256
        HEADS = 4
        HEAD_DIM = EMBED // HEADS
        OUT_DIM = 256
        LN_EPS = 1e-05

        def _qkv_init(key):
            spread = math.sqrt(3.0 / EMBED)
            gain, delta = (0.01, 0.01)
            w = jax.random.uniform(key, (EMBED, EMBED), minval=-spread, maxval=spread) * gain
            return w + delta * jnp.eye(EMBED, dtype=w.dtype)

        def _layer_norm(x, g, b):
            mu = jnp.mean(x, axis=-1, keepdims=True)
            var = jnp.mean(jnp.square(x - mu), axis=-1, keepdims=True)
            return (x - mu) * jax.lax.rsqrt(var + LN_EPS) * g + b

        def _split_heads(x, B, S):
            return x.reshape(B, S, HEADS, HEAD_DIM).transpose(0, 2, 1, 3)
        B, S, _ = seq.shape
        q = _split_heads(seq @ wq.T, B, S)
        k = _split_heads(seq @ wk.T, B, S)
        v = _split_heads(seq @ wv.T, B, S)
        k = _layer_norm(k, ln_k_g, ln_k_b)
        v = _layer_norm(v, ln_v_g, ln_v_b)
        kv = jnp.einsum('bhsd,bhse->bhde', k, v) / S
        ga = jnp.einsum('bhsd,bhde->bhse', q, kv)
        ga = ga.transpose(0, 2, 1, 3).reshape(B, S, EMBED)
        return ga @ wo.T + bo

    def _L0_ffn_ref(x, router_w, router_b, W1, b1, W2, b2):
        import jax, jax.numpy as jnp
        import numpy as np
        B, K, D = (512, 16, 256)
        E = 32
        H = int(D * 0.25)
        xf = x.reshape(-1, D)
        logits = xf @ router_w.T + router_b
        idx = jnp.argmax(logits, axis=-1)
        w1t = jnp.take(W1, idx, axis=0)
        h = jnp.einsum('nd,ndh->nh', xf, w1t) + jnp.take(b1, idx, axis=0)
        h = jax.nn.relu(h)
        w2t = jnp.take(W2, idx, axis=0)
        out = jnp.einsum('nh,nhd->nd', h, w2t) + jnp.take(b2, idx, axis=0)
        out = jax.nn.relu(out)
        return out.reshape(x.shape)

    def _L1_gnn_ref(x, edge_index, W1, b1, W2, b2, W3, b3):
        import jax, jax.numpy as jnp
        import numpy as np
        N_NODES = 3125
        N_EDGES = 10000
        D_IN = 256
        D_H = 256
        D_OUT = 256

        def gcn_layer(x, W, b, src, dst, num_nodes):
            ones = jnp.ones(src.shape[0], dtype=x.dtype)
            deg = jax.ops.segment_sum(ones, dst, num_segments=num_nodes)
            dinv = jnp.where(deg > 0, jax.lax.rsqrt(deg), 0.0)
            norm = dinv[src] * dinv[dst]
            h = x @ W
            msg = h[src] * norm[:, None]
            out = jax.ops.segment_sum(msg, dst, num_segments=num_nodes)
            return out + b
        num_nodes = x.shape[0]
        loop = jnp.arange(num_nodes, dtype=edge_index.dtype)
        src = jnp.concatenate([edge_index[0], loop])
        dst = jnp.concatenate([edge_index[1], loop])
        h = gcn_layer(x, W1, b1, src, dst, num_nodes)
        h = gcn_layer(h, W2, b2, src, dst, num_nodes)
        h = gcn_layer(h, W3, b3, src, dst, num_nodes)
        return h

    def _L1_mix_ref(x, t, w_qkv, mem_kv, w_out, b_out, g_out, g_pre):
        import jax, jax.numpy as jnp
        import numpy as np
        DIM = 256
        HEADS = 4
        DIM_HEAD = 32
        NUM_MEM = 4
        HIDDEN = HEADS * DIM_HEAD
        SCALE = DIM_HEAD ** (-0.5)

        def rmsnorm(x, g):
            n = jnp.linalg.norm(x, axis=-1, keepdims=True)
            return x / jnp.maximum(n, 1e-12) * g * x.shape[-1] ** 0.5
        b, n, c = x.shape
        xn = rmsnorm(x, g_pre)
        qkv = xn @ w_qkv
        q, k, v = jnp.split(qkv, 3, axis=-1)

        def to_heads(z):
            return z.reshape(b, n, HEADS, DIM_HEAD).transpose(0, 2, 3, 1)
        q, k, v = map(to_heads, (q, k, v))
        mk = jnp.broadcast_to(mem_kv[0], (b, HEADS, DIM_HEAD, NUM_MEM))
        mv = jnp.broadcast_to(mem_kv[1], (b, HEADS, DIM_HEAD, NUM_MEM))
        k = jnp.concatenate([mk, k], axis=-1)
        v = jnp.concatenate([mv, v], axis=-1)
        q = jax.nn.softmax(q, axis=-2) * SCALE
        k = jax.nn.softmax(k, axis=-1)
        context = jnp.einsum('bhdn,bhen->bhde', k, v)
        out = jnp.einsum('bhde,bhdn->bhen', context, q)
        out = out.transpose(0, 3, 1, 2).reshape(b, n, HIDDEN)
        out = rmsnorm(out @ w_out + b_out, g_out)
        return out + x

    def _L1_ffn_ref(x, attention_mask, wr, br, w1, b1, w2, b2):
        import jax, jax.numpy as jnp
        import numpy as np
        B, S, D = (8, 128, 256)
        H = 4 * D
        CAPACITY = 0.5
        b, s, d = x.shape
        weights = (jnp.einsum('bsd,do->bso', x, wr) + br)[..., 0]
        k = max(1, int(CAPACITY * s))
        kk = k - 1 if k > 1 else 1
        _, idx = jax.lax.top_k(weights, k)
        sel_idx = idx[:, :kk]
        sel = jnp.take_along_axis(x, sel_idx[:, :, None], axis=1)
        h = jax.nn.gelu(jnp.einsum('bkd,dh->bkh', sel, w1) + b1)
        y = jnp.einsum('bkh,hd->bkd', h, w2) + b2
        w_sel = jnp.take_along_axis(weights, sel_idx, axis=1)
        y = y * w_sel[..., None]
        batch_idx = jnp.arange(b)[:, None]
        processed = jnp.zeros_like(x).at[batch_idx, sel_idx].set(y)
        return processed + x

    def _L2_gnn_ref(x, edge_index, edge_attr, eps, ee_w1, ee_b1, ee_w2, ee_b2, w1, b1, g1, be1, w2, b2, g2, be2, w3, b3, bn_g, bn_b):
        import jax, jax.numpy as jnp
        import numpy as np
        N = 3125
        E = 10000
        CIN = 256
        EDIM = 64
        EEMB = 256
        H = 1024
        LN_EPS = 1e-05

        def _ln(x, g, b):
            m = jnp.mean(x, axis=-1, keepdims=True)
            v = jnp.var(x, axis=-1, keepdims=True)
            return (x - m) * jax.lax.rsqrt(v + LN_EPS) * g + b
        n = x.shape[0]
        sl = jnp.arange(n, dtype=edge_index.dtype)
        ei = jnp.concatenate([edge_index, jnp.stack([sl, sl], axis=0)], axis=1)
        ea = jnp.concatenate([edge_attr, jnp.zeros((n, edge_attr.shape[1]), edge_attr.dtype)], axis=0)
        src, dst = (ei[0], ei[1])
        e = jax.nn.relu(ea @ ee_w1 + ee_b1) @ ee_w2 + ee_b2
        msg = x[src] + e
        agg = jax.ops.segment_sum(msg, dst, num_segments=n)
        h = (1.0 + eps) * x + agg
        h = jax.nn.relu(_ln(h @ w1 + b1, g1, be1))
        h = jax.nn.relu(_ln(h @ w2 + b2, g2, be2))
        y = h @ w3 + b3
        out = x + y
        out = _ln(out, bn_g, bn_b)
        return jax.nn.relu(out)

    def _L2_mix_ref(x, wq, bq, wk, bk, wv, bv, wo, bo):
        import jax, jax.numpy as jnp
        import numpy as np
        D_MODEL = 256
        NUM_HEADS = 8
        DEPTH = D_MODEL // NUM_HEADS
        B, L = (32, 128)

        def _feature_map(x):
            return jax.nn.elu(x) + 1.0
        b, l, _ = x.shape
        q = (x @ wq + bq).reshape(b, l, NUM_HEADS, DEPTH)
        k = (x @ wk + bk).reshape(b, l, NUM_HEADS, DEPTH)
        v = (x @ wv + bv).reshape(b, l, NUM_HEADS, DEPTH)
        q = _feature_map(q)
        k = _feature_map(k)
        kv = jnp.einsum('blhd,blhe->bhde', k, v)
        k_sum = jnp.sum(k, axis=1)
        qkv = jnp.einsum('blhd,bhde->blhe', q, kv)
        normalizer = jnp.einsum('blhd,bhd->blh', q, k_sum) + 1e-06
        out = qkv / normalizer[..., None]
        out = out.reshape(b, l, D_MODEL)
        return out @ wo + bo

    def _L2_ffn_ref(x, sW1, sb1, sW2, sb2, sW3, sb3, eW1, eb1, eW2, eb2, eW3, eb3, gW, gb):
        import jax, jax.numpy as jnp
        import numpy as np
        B, A = (128, 8)
        IN, OUT = (256, 256)
        SH1, SH2 = (256, 128)
        EH1, EH2 = (128, 64)
        E, TOPK = (4, 2)

        def _shared_mlp(x, W1, b1, W2, b2, W3, b3):
            h = jax.nn.relu(x @ W1 + b1)
            h = jax.nn.relu(h @ W2 + b2)
            return h @ W3 + b3

        def _experts_mlp(x, eW1, eb1, eW2, eb2, eW3, eb3):
            h = jax.nn.relu(jnp.einsum('baf,efh->ebah', x, eW1) + eb1[:, None, None, :])
            h = jax.nn.relu(jnp.einsum('ebah,ehg->ebag', h, eW2) + eb2[:, None, None, :])
            o = jnp.einsum('ebag,ego->ebao', h, eW3) + eb3[:, None, None, :]
            return jnp.moveaxis(o, 0, -1)
        all_out = _experts_mlp(x, eW1, eb1, eW2, eb2, eW3, eb3)
        shared = _shared_mlp(x, sW1, sb1, sW2, sb2, sW3, sb3)
        gates = jax.nn.softmax(x @ gW + gb, axis=-1)
        topv, topi = jax.lax.top_k(gates, TOPK)
        topw = jax.nn.softmax(topv, axis=-1)
        sel = jnp.take_along_axis(all_out, topi[:, :, None, :], axis=-1)
        gated = jnp.sum(sel * topw[:, :, None, :], axis=-1)
        return shared + gated

    def _L3_gnn_ref(x, edge_index, W_l, b_l, W_r, gamma, beta):
        import jax, jax.numpy as jnp
        import numpy as np
        N_NODES = 50000
        N_EDGES = 10000
        HIDDEN = 256
        LN_EPS = 1e-05
        NORM_EPS = 1e-12
        src, dst = (edge_index[0], edge_index[1])
        n = x.shape[0]
        summed = jax.ops.segment_sum(x[src], dst, num_segments=n)
        count = jax.ops.segment_sum(jnp.ones_like(src, dtype=x.dtype), dst, num_segments=n)
        mean_aggr = summed / jnp.maximum(count, 1.0)[:, None]
        h = mean_aggr @ W_l.T + b_l + x @ W_r.T
        norm = jnp.linalg.norm(h, axis=-1, keepdims=True)
        h = h / jnp.maximum(norm, NORM_EPS)
        h = jax.nn.relu(h) + x
        mu = jnp.mean(h, axis=-1, keepdims=True)
        var = jnp.var(h, axis=-1, keepdims=True)
        out = (h - mu) * jax.lax.rsqrt(var + LN_EPS) * gamma + beta
        return out

    def _L3_mix_ref(x, Wq, Wkv, Wproj, bproj):
        import jax, jax.numpy as jnp
        import numpy as np
        NUM_HEADS = 8
        B, N, C = x.shape
        h = NUM_HEADS
        d = C // h
        q = jnp.einsum('bnc,oc->bno', x, Wq).reshape(B, N, h, d).transpose(0, 2, 1, 3)
        kv = jnp.einsum('bnc,oc->bno', x, Wkv).reshape(B, N, 2, h, d)
        k = kv[:, :, 0].transpose(0, 2, 1, 3)
        v = kv[:, :, 1].transpose(0, 2, 1, 3)
        q = jax.nn.elu(q) + 1.0
        k = jax.nn.elu(k) + 1.0
        k_sum = k.sum(axis=2)
        D_inv = 1.0 / jnp.maximum(jnp.einsum('bhnd,bhd->bhn', q, k_sum), 1e-06)
        context = jnp.einsum('bhnd,bhne->bhde', k, v)
        attn = jnp.einsum('bhnd,bhde->bhne', q, context) * D_inv[..., None]
        out = attn.transpose(0, 2, 1, 3).reshape(B, N, C)
        out = jnp.einsum('bnc,oc->bno', out, Wproj) + bproj
        return out

    def _L3_ffn_ref(x, gate_w, gate_b, w1, b1, w2, b2, gamma, beta):
        import jax, jax.numpy as jnp
        import numpy as np
        B, S, H, F, E, K = (8, 128, 256, 512, 16, 2)
        EPS = 1e-05
        gate_logits = x @ gate_w + gate_b
        topk_vals, topk_idx = jax.lax.top_k(gate_logits, K)
        topk_w = jax.nn.softmax(topk_vals, axis=-1)
        h = jax.nn.relu(jnp.einsum('bsh,ehf->bsef', x, w1) + b1)
        expert_out = jnp.einsum('bsef,efh->bseh', h, w2) + b2
        sel = jnp.take_along_axis(expert_out, topk_idx[:, :, :, None], axis=2)
        moe = jnp.sum(topk_w[..., None] * sel, axis=2)
        y = x + moe
        mu = jnp.mean(y, axis=-1, keepdims=True)
        var = jnp.var(y, axis=-1, keepdims=True)
        return (y - mu) / jnp.sqrt(var + EPS) * gamma + beta
    edge_index = jnp.stack([src, dst])
    xn = _layernorm(x, axis=-1)
    x = x + _L0_gnn_ref(xn, src, dst, edge_weight, L0_gnn_W, L0_gnn_b) + _L0_mix_ref(xn[None], L0_mix_wq, L0_mix_wk, L0_mix_wv, L0_mix_wo, L0_mix_bo, L0_mix_ln_k_g, L0_mix_ln_k_b, L0_mix_ln_v_g, L0_mix_ln_v_b)[0]
    x = x + _L0_ffn_ref(_layernorm(x, axis=-1)[None], L0_ffn_router_w, L0_ffn_router_b, L0_ffn_W1, L0_ffn_b1, L0_ffn_W2, L0_ffn_b2)[0]
    xn = _layernorm(x, axis=-1)
    x = x + _L1_gnn_ref(xn, edge_index, L1_gnn_W1, L1_gnn_b1, L1_gnn_W2, L1_gnn_b2, L1_gnn_W3, L1_gnn_b3) + _L1_mix_ref(xn[None], L1_mix_t, L1_mix_w_qkv, L1_mix_mem_kv, L1_mix_w_out, L1_mix_b_out, L1_mix_g_out, L1_mix_g_pre)[0]
    x = x + _L1_ffn_ref(_layernorm(x, axis=-1)[None], L1_ffn_attention_mask, L1_ffn_wr, L1_ffn_br, L1_ffn_w1, L1_ffn_b1, L1_ffn_w2, L1_ffn_b2)[0]
    xn = _layernorm(x, axis=-1)
    x = x + _L2_gnn_ref(xn, edge_index, edge_attr_64, L2_gnn_eps, L2_gnn_ee_w1, L2_gnn_ee_b1, L2_gnn_ee_w2, L2_gnn_ee_b2, L2_gnn_w1, L2_gnn_b1, L2_gnn_g1, L2_gnn_be1, L2_gnn_w2, L2_gnn_b2, L2_gnn_g2, L2_gnn_be2, L2_gnn_w3, L2_gnn_b3, L2_gnn_bn_g, L2_gnn_bn_b) + _L2_mix_ref(xn[None], L2_mix_wq, L2_mix_bq, L2_mix_wk, L2_mix_bk, L2_mix_wv, L2_mix_bv, L2_mix_wo, L2_mix_bo)[0]
    x = x + _L2_ffn_ref(_layernorm(x, axis=-1)[None], L2_ffn_sW1, L2_ffn_sb1, L2_ffn_sW2, L2_ffn_sb2, L2_ffn_sW3, L2_ffn_sb3, L2_ffn_eW1, L2_ffn_eb1, L2_ffn_eW2, L2_ffn_eb2, L2_ffn_eW3, L2_ffn_eb3, L2_ffn_gW, L2_ffn_gb)[0]
    xn = _layernorm(x, axis=-1)
    x = x + _L3_gnn_ref(xn, edge_index, L3_gnn_W_l, L3_gnn_b_l, L3_gnn_W_r, L3_gnn_gamma, L3_gnn_beta) + _L3_mix_ref(xn[None], L3_mix_Wq, L3_mix_Wkv, L3_mix_Wproj, L3_mix_bproj)[0]
    x = x + _L3_ffn_ref(_layernorm(x, axis=-1)[None], L3_ffn_gate_w, L3_ffn_gate_b, L3_ffn_w1, L3_ffn_b1, L3_ffn_w2, L3_ffn_b2, L3_ffn_gamma, L3_ffn_beta)[0]
    return x

_drawn_inputs = setup_inputs


def setup_inputs(seed=0):
    import zlib

    import numpy as np

    out = dict(_drawn_inputs(seed))
    spreads = {'L0_gnn_b': (0.0, 0.1),
     'L0_mix_ln_k_g': (1.0, 0.6),
     'L0_mix_ln_k_b': (0.0, 0.8),
     'L0_mix_ln_v_g': (1.0, 0.6),
     'L0_mix_ln_v_b': (0.0, 0.8),
     'L1_gnn_b1': (0.0, 0.1),
     'L1_gnn_b2': (0.0, 0.1),
     'L1_gnn_b3': (0.0, 0.1),
     'L1_mix_b_out': (0.0, 0.1),
     'L1_mix_g_out': (1.0, 0.2),
     'L1_mix_g_pre': (1.0, 0.6),
     'L1_ffn_b1': (0.0, 0.8),
     'L1_ffn_b2': (0.0, 0.8),
     'L2_gnn_ee_b1': (0.0, 2.0),
     'L2_gnn_ee_b2': (0.0, 1.616),
     'L2_gnn_b1': (0.0, 2.0),
     'L2_gnn_g1': (1.0, 0.6),
     'L2_gnn_be1': (0.0, 0.8),
     'L2_gnn_b2': (0.0, 0.688),
     'L2_gnn_g2': (1.0, 0.6),
     'L2_gnn_be2': (0.0, 0.8),
     'L2_gnn_b3': (0.0, 0.563),
     'L2_gnn_bn_g': (1.0, 0.2),
     'L2_gnn_bn_b': (0.0, 0.488),
     'L2_mix_bq': (0.0, 2.0),
     'L2_mix_bk': (0.0, 2.0),
     'L2_mix_bv': (0.0, 0.32),
     'L2_mix_bo': (0.0, 0.343),
     'L2_ffn_sb1': (0.0, 2.0),
     'L2_ffn_sb2': (0.0, 2.0),
     'L2_ffn_sb3': (0.0, 0.973),
     'L2_ffn_eb1': (0.0, 0.8),
     'L2_ffn_eb2': (0.0, 0.8),
     'L2_ffn_eb3': (0.0, 1.573),
     'L2_ffn_gb': (0.0, 0.8),
     'L3_gnn_b_l': (0.0, 2.0),
     'L3_gnn_gamma': (1.0, 0.6),
     'L3_gnn_beta': (0.0, 1.303),
     'L3_mix_bproj': (0.0, 1.215),
     'L3_ffn_gate_b': (0.0, 0.69),
     'L3_ffn_b1': (0.0, 2.0),
     'L3_ffn_b2': (0.0, 2.0),
     'L3_ffn_gamma': (1.0, 0.6),
     'L3_ffn_beta': (0.0, 1.448)}
    factors = {'edge_attr_64': 3.121,
     'L0_mix_wq': 8.0,
     'L0_mix_wk': 7.261,
     'L0_mix_wv': 7.75,
     'L0_mix_wo': 6.643,
     'L0_ffn_b1': 8.0,
     'L0_ffn_b2': 3.585,
     'L1_mix_w_qkv': 8.0,
     'L1_mix_mem_kv': 8.0,
     'L1_mix_w_out': 8.0,
     'L1_ffn_wr': 7.626,
     'L1_ffn_w1': 8.0,
     'L1_ffn_w2': 7.416,
     'L2_gnn_ee_w1': 3.01,
     'L2_mix_wq': 25.137,
     'L2_mix_wk': 23.358,
     'L2_ffn_eW1': 5.509,
     'L2_ffn_eW2': 4.594,
     'L2_ffn_eW3': 3.837,
     'L2_ffn_gW': 3.587,
     'L3_gnn_W_l': 64.0,
     'L3_gnn_W_r': 63.184,
     'L3_mix_Wq': 46.307,
     'L3_mix_Wkv': 6.998,
     'L3_mix_Wproj': 6.64,
     'L3_ffn_gate_w': 3.443,
     'L3_ffn_w1': 5.556,
     'L3_ffn_w2': 4.393,
     'L2_ffn_sW1': 4.804,
     'L2_ffn_sW2': 3.354}
    for name, (base, spread) in spreads.items():
        noise = np.random.default_rng([zlib.crc32(name.encode()), seed]).standard_normal(out[name].shape)
        drawn = base * np.exp(spread * noise) if base else spread * noise
        out[name] = jnp.asarray(drawn.astype(out[name].dtype))
    for name, factor in factors.items():
        out[name] = (out[name] * factor).astype(out[name].dtype)
    return out
```

```python
from contextlib import ExitStack

import numpy as np

import concourse.bass as bass
from concourse import mybir

F32, BF16, I32, I16 = mybir.dt.float32, mybir.dt.bfloat16, mybir.dt.int32, mybir.dt.int16
ALU = mybir.AluOpType
ACT = mybir.ActivationFunctionType
AX = mybir.AxisListType.X

NODES, D = 3125, 256
T, R = 25, 125
EDGES, CH = 50000, 128
PAIRS = -(-EDGES // (2 * CH))
NCH = 2 * PAIRS
EDIM = 64
LN_EPS = 1e-5
BIG = 4096.0
CTB = 7
CENTRED = [(g * 500, min(500, NODES - g * 500)) for g in range(CTB)]


class Stage:

    def __init__(self, nc, name):
        self.nc, self.name, self.stack, self.sems = nc, name, ExitStack(), []

    def __enter__(self):
        self.stack.__enter__()
        return self

    def __exit__(self, *e):
        self.stack.__exit__(*e)
        if self.sems and e[0] is None:
            self.nc.clear_and_free_semaphores(self.sems)
            self.nc.all_engine_barrier(sem_only=True)

    def sb(self, name, shape, dt=F32):
        return self.stack.enter_context(self.nc.sbuf_tensor(f"{self.name}_{name}", shape, dt))

    def ps(self, name, shape, dt=F32):
        return self.stack.enter_context(self.nc.psum_tensor(f"{self.name}_{name}", shape, dt))

    def sem(self, name):
        self.sems.append(self.nc.alloc_semaphore(f"{self.name}_{name}"))
        return self.sems[-1]

    def block(self):
        return self.stack.enter_context(self.nc.Block())


def tiles(eng, body):
    with eng.Fori(0, T // 2) as i:
        body(2 * i, 0)
        body(2 * i + 1, 1)
    body(T - 1, 0)


def groups(eng, body):
    with eng.Fori(0, 5) as i:
        body(5 * i, 3, 2 * i, 0)
        body(5 * i + 3, 2, 2 * i + 1, 1)


def settle(eng, started):
    eng.sem_inc(started, 1)


def rows(t, n=1):
    return bass.ds(t * R, n * R)



def plan_edges(nc, d, k):
    with Stage(nc, "plan") as s:
        dst_i, src_i = s.sb("dst_i", [CH, NCH], I32), s.sb("src_i", [CH, NCH], I32)
        pair_up, pair_down = s.sb("pair_up", [CH, NCH]), s.sb("pair_down", [CH, NCH])
        rel, over, inside = (s.sb(n, [CH, NCH]) for n in ("rel", "over", "inside"))
        ends = s.sb("ends", [CH, 2 * T])
        most, spare = s.sb("most", [2 * T, 1]), s.sb("spare", [2 * T, 1])
        line = s.sb("line", [1, 2, T])
        plan = s.sb("plan", [1, 3, T])
        ones = s.sb("ones", [1, T])
        cum = s.sb("cum", [1, T])
        plan_i = s.sb("plan_i", [1, 3, T], I32)
        ends_t = s.ps("ends_t", [CH, CH])
        loaded, ends_ready, turned, most_ready, stored, back = map(
            s.sem, ("loaded", "ends_ready", "turned", "most_ready", "stored", "back"))
        planned = s.sem("planned")
        block = s.block()

        @block.sync
        def _(sp):
            sp.dma_start(dst_i[:], d["dst"]).then_inc(loaded, 16)
            sp.dma_start(src_i[:], d["src"]).then_inc(loaded, 16)
            sp.dma_start(pair_up[:], d["pair_up"]).then_inc(loaded, 16)
            sp.dma_start(pair_down[:], d["pair_down"]).then_inc(loaded, 16)
            sp.dma_start(k["weight"][:], d["weight"]).then_inc(loaded, 16)
            sp.dma_start(k["ident"][:], d["ident"]).then_inc(loaded, 16)
            sp.wait_ge(most_ready, 1)
            sp.dma_start(k["ends_dram"], most[:]).then_inc(stored, 16)
            sp.wait_ge(stored, 16)
            sp.dma_start(line[:], k["ends_dram"].rearrange("(a b t) o -> a b (t o)", a=1, b=2)).then_inc(back, 16)
            sp.wait_ge(planned, 1)
            sp.dma_start(k["plan_dram"], plan_i[:]).then_inc(stored, 16)
            sp.wait_ge(stored, 32)

        @block.vector
        def _(dve):
            dve.wait_ge(loaded, 96)
            dve.tensor_copy(k["dst"][:], dst_i[:])
            dve.tensor_copy(over[:], src_i[:])
            dve.memset(ones[:], 1.0)
            dve.drain()
            dve.tensor_scalar(k["src_base"][:], over[:], float(R), float(R), ALU.is_ge, ALU.mult)
            dve.drain()
            for t in range(2, T):
                dve.tensor_scalar(inside[:], over[:], float(t * R), float(R), ALU.is_ge, ALU.mult)
                dve.drain()
                dve.tensor_tensor(k["src_base"][:], k["src_base"][:], inside[:], ALU.add)
                dve.drain()
            dve.tensor_tensor(k["src_place"][:], over[:], k["src_base"][:], ALU.subtract)
            dve.drain()
            for t in range(T):
                dve.tensor_scalar(over[:], k["dst"][:], float(t * R), None, ALU.is_ge)
                dve.tensor_scalar(rel[:], k["dst"][:], float((t + 1) * R), None, ALU.is_lt)
                dve.drain()
                dve.tensor_tensor(inside[:], over[:], rel[:], ALU.mult)
                dve.drain()
                dve.tensor_tensor(over[:], inside[:], pair_up[:], ALU.mult)
                dve.tensor_tensor(rel[:], inside[:], pair_down[:], ALU.mult)
                dve.drain()
                dve.tensor_reduce(ends[:, t:t + 1], over[:], AX, ALU.max)
                dve.tensor_reduce(ends[:, T + t:T + t + 1], rel[:], AX, ALU.max)
                dve.drain()
            dve.drain().then_inc(ends_ready, 1)
            dve.wait_ge(turned, 1)
            dve.tensor_reduce(most[:], ends_t[0:2 * T, :], AX, ALU.max).then_inc(most_ready, 1)
            dve.wait_ge(back, 16)
            dve.tensor_scalar(plan[:, 0, :], line[:, 1, :], -1.0, float(PAIRS), ALU.mult, ALU.add)
            dve.drain()
            dve.tensor_tensor(plan[:, 1, :], line[:, 0, :], plan[:, 0, :], ALU.subtract)
            dve.tensor_scalar(plan[:, 0, :], plan[:, 0, :], float(PAIRS - 1), None, ALU.min)
            dve.drain()
            dve.tensor_scalar(plan[:, 1, :], plan[:, 1, :], 1.0, None, ALU.max)
            dve.drain()
            dve.tensor_tensor_scan(cum[:], ones[:], plan[:, 1, :], 0.0, ALU.mult, ALU.add)
            dve.drain()
            dve.tensor_tensor(plan[:, 2, :], cum[:], plan[:, 1, :], ALU.subtract)
            dve.drain()
            dve.tensor_copy(plan_i[:], plan[:]).then_inc(planned, 1)

        @block.tensor
        def _(pe):
            pe.wait_ge(ends_ready, 1)
            pe.transpose(ends_t[0:2 * T, :], ends[:], k["ident"][:]).then_inc(turned, 1)


def walk(eng, k, plan, body_tile_start, body_pair, body_tile_end):
    with eng.Fori(0, T) as t:
        first = eng.value_load(plan[0:1, 0, bass.ds(t, 1)], min_val=0, max_val=PAIRS - 1)
        count = eng.value_load(plan[0:1, 1, bass.ds(t, 1)], min_val=1, max_val=PAIRS)
        before = eng.value_load(plan[0:1, 2, bass.ds(t, 1)], min_val=0, max_val=T * PAIRS)
        body_tile_start(t)
        with eng.Fori(0, count) as j:
            pair = k["nc"].s_assert_within(first + j, 0, PAIRS - 1, skip_runtime_bounds_check_because="the plan keeps first + count at most PAIRS")
            body_pair(t, pair, before + j)
        body_tile_end(t)


def first_places(nc, d, k):
    with Stage(nc, "first") as s:
        row = [s.sb(f"row{b}", [CH, 2 * CH], I32) for b in range(2)]
        rowf = [s.sb(f"rowf{b}", [CH, 2 * CH]) for b in range(2)]
        src_i = s.sb("src_i", [CH, NCH], I32)
        src, moved = s.sb("src", [CH, NCH]), s.sb("moved", [CH, NCH])
        own, before = s.sb("own", [CH, 1]), s.sb("before", [CH, CH])
        same = [s.sb(f"same{b}", [CH, CH]) for b in range(2)]
        count = s.sb("count", [CH, NCH])
        loaded, row0, row1, row_free = map(s.sem, ("loaded", "row0", "row1", "row_free"))
        block = s.block()

        @block.sync
        def _(sp):
            sp.dma_start(src_i[:], d["src"]).then_inc(loaded, 16)
            sp.dma_start(own[:], d["own_row"]).then_inc(loaded, 16)
            sp.dma_start(before[:], d["before"]).then_inc(loaded, 16)
            with sp.Fori(0, PAIRS // 2) as i:
                for b in range(2):
                    sp.wait_ge(row_free, 2 * i + (b + 1))
                    sp.dma_start(row[b][:], d["src_row"][:, bass.ds((2 * i + b) * 2 * CH, 2 * CH)].broadcast_to((CH, 2 * CH))
                                 ).then_inc(row0 if b == 0 else row1, 16)
            sp.wait_ge(loaded, 48)

        @block.vector
        def _(dve):
            dve.sem_inc(row_free, 2)
            dve.wait_ge(loaded, 48)
            dve.tensor_copy(src[:], src_i[:])
            dve.drain()
            with dve.Fori(0, PAIRS // 2) as i:
                for b in range(2):
                    dve.wait_ge(row0 if b == 0 else row1, 16 * i + 16)
                    dve.tensor_copy(rowf[b][:], row[b][:])
                    dve.drain().then_inc(row_free, 1)
                    for h in range(2):
                        c = 4 * i + (2 * b + h)
                        dve.scalar_tensor_tensor(same[h][:], rowf[b][:, h * CH:(h + 1) * CH], src[:, bass.ds(c, 1)],
                                                 before[:], ALU.is_equal, ALU.mult)
                    dve.drain()
                    for h in range(2):
                        c = 4 * i + (2 * b + h)
                        dve.tensor_reduce(count[:, bass.ds(c, 1)], same[h][:], AX, ALU.max)
            dve.drain()
            dve.tensor_scalar(moved[:], src[:], own[:], -1.0, ALU.subtract, ALU.mult)
            dve.drain()
            dve.tensor_tensor(moved[:], moved[:], count[:], ALU.mult)
            dve.drain()
            dve.tensor_tensor(src[:], src[:], moved[:], ALU.add)
            dve.drain()
            dve.tensor_copy(k["scatter_to"][:], src[:])


def scatter_and_count(nc, d, k):
    with Stage(nc, "edge") as s:
        plan = s.sb("plan", [1, 3, T], I32)
        iota = s.sb("iota", [CH, NODES], I16)
        iota_r = s.sb("iota_r", [CH, R])
        rel, spare = s.sb("rel", [CH, NCH]), s.sb("spare", [CH, NCH])
        key = s.sb("key", [CH, NCH])
        src = s.sb("src", [CH, NCH])
        row_now = [s.sb(f"row_now{b}", [CH, 1], I32) for b in range(2)]
        src_row = s.sb("src_row", [CH, 2 * CH], I32)
        src_rowf = s.sb("src_rowf", [CH, 2 * CH])
        onehot = [s.sb(f"onehot{b}", [CH, NODES], BF16) for b in range(2)]
        place = [s.sb(f"place{b}", [CH, R], BF16) for b in range(2)]
        to_dst = [s.sb(f"to_dst{b}", [CH, R]) for b in range(2)]
        same = [s.sb(f"same{b}", [CH, CH]) for b in range(2)]
        P = [s.sb(f"P{b}", [R, CH]) for b in range(2)]
        S = [s.sb(f"S{b}", [CH, D]) for b in range(2)]
        zeros = s.sb("zeros", [CH, 512], BF16)
        zero_rows = s.sb("zero_rows", [CH, D])
        ones = s.sb("ones", [CH, 1])
        counts = s.sb("counts", [R, NODES])
        ct_ps = s.ps("ct_ps", [R, CTB, 512])
        deg_ps = ct_ps[:, CTB - 1, 500:501]
        ps = s.ps("ps", [CH, 512])
        P_ps = [ps[0:R, b * CH:(b + 1) * CH] for b in range(2)]
        S_ps = ps[:, 256:512]
        loaded, setup, row_in, row_free, onehot_ready, used, P_ready, P_kept, S_ready, S_kept = map(
            s.sem, ("loaded", "setup", "row_in", "row_free", "onehot_ready", "used", "P_ready", "P_kept", "S_ready",
                    "S_kept"))
        started = s.sem("started")
        scattered = [s.sem(f"scattered{b}") for b in range(2)]
        tile_done, evac_dve, evac_act, stored, counts_free, gone = map(
            s.sem, ("tile_done", "evac_dve", "evac_act", "stored", "counts_free", "gone"))
        block = s.block()

        def nothing(t):
            pass

        @block.sync
        def _(sp):
            sp.dma_start(plan[:], k["plan_dram"]).then_inc(loaded, 16)
            sp.dma_start(iota[:], d["iota16"]).then_inc(loaded, 16)
            sp.dma_start(iota_r[:], d["iota_r"]).then_inc(loaded, 16)
            sp.wait_ge(loaded, 48)
            sp.wait_ge(setup, 1)
            sp.sem_inc(counts_free, 1)

            def pair(t, c, n):
                sp.wait_ge(row_free, n + 1)
                sp.dma_start(src_row[:], d["src_row"][:, bass.ds(c * 2 * CH, 2 * CH)].broadcast_to((CH, 2 * CH))
                             ).then_inc(row_in, 16)

            def end(t):
                sp.wait_ge(evac_dve, t + 2)
                sp.wait_ge(evac_act, t + 2)
                sp.dma_start(k["ct_dram"][bass.ds(t, 1)].rearrange("a p n -> (a p) n"), counts[:]).then_inc(stored, 16)
                sp.wait_ge(stored, 16 * t + 16)
                sp.sem_inc(counts_free, 1)

            walk(sp, k, plan, nothing, pair, end)

        @block.gpsimd
        def _(pool):
            pool.wait_ge(loaded, 48)
            pool.wait_ge(setup, 1)
            for b in range(2):
                pool.dma_start(k["support_dram"][b][0:25 * CH].rearrange("(a p) n -> p a n", p=CH),
                               zero_rows[:].unsqueeze(1).broadcast_to((CH, 25, D))).then_inc(gone, 16)
            pool.wait_ge(gone, 32)
            for b in range(2):
                pool.dma_start(k["support_dram"][b][25 * CH:25 * CH + 53], zero_rows[0:53, :]).then_inc(scattered[b], 16)

            def pair(t, c, n):
                for b in range(2):
                    pool.wait_ge(scattered[b], 16 * n + 16)
                    pool.tensor_copy(row_now[b][:], k["scatter_to"][:, bass.ds(2 * c + b, 1)])
                    pool.drain()
                    pool.wait_ge(S_kept, 2 * n + (b + 2))
                    settle(pool, started)
                    pool.indirect_dma_start(k["support_dram"][b], bass.IndirectOffsetOnAxis(ap=row_now[b][:, 0:1], axis=0),
                                            S[b][:], None, compute_op=ALU.add).then_inc(scattered[b], 16)

            walk(pool, k, plan, nothing, pair, nothing)
            last = pool.value_load(plan[0:1, 1, T - 1:T], min_val=1, max_val=PAIRS)
            base = pool.value_load(plan[0:1, 2, T - 1:T], min_val=0, max_val=T * PAIRS)
            for b in range(2):
                pool.wait_ge(scattered[b], 16 * (base + last) + 16)

        @block.scalar
        def _(act):
            act.wait_ge(loaded, 48)

            def pair(t, c, n):
                for b in range(2):
                    act.wait_ge(P_ready, 2 * n + (b + 1))
                    act.activation(P[b][:], P_ps[b], ACT.Copy).then_inc(P_kept, 1)
                    act.wait_ge(S_ready, 2 * n + (b + 1))
                    act.wait_ge(scattered[b], 16 * n + 16)
                    act.activation(S[b][:], S_ps, ACT.Copy).then_inc(S_kept, 1)

            def end(t):
                act.wait_ge(tile_done, t + 1)
                act.wait_ge(counts_free, t + 1)
                for g in range(4, CTB):
                    a, n = CENTRED[g]
                    act.activation(counts[:, a:a + n], ct_ps[:, g, 0:n], ACT.Copy)
                act.activation(k["deg"][:, bass.ds(t, 1)], deg_ps, ACT.Copy)
                act.drain().then_inc(evac_act, 1)

            walk(act, k, plan, nothing, pair, end)

        @block.vector
        def _(dve):
            dve.sem_inc(row_free, 1)
            dve.wait_ge(loaded, 48)
            dve.memset(zeros[:], 0.0)
            dve.memset(zero_rows[:], 0.0)
            dve.memset(ones[:], 1.0)
            dve.tensor_tensor(src[:], k["src_base"][:], k["src_place"][:], ALU.add)
            dve.drain().then_inc(setup, 1)

            def start(t):
                dve.tensor_scalar(rel[:], k["dst"][:], k["tile_start"][:, bass.ds(t, 1)], None, ALU.subtract)
                dve.drain()
                dve.tensor_scalar(spare[:], rel[:], float(R), BIG, ALU.is_ge, ALU.mult)
                dve.drain()
                dve.tensor_tensor(key[:], rel[:], spare[:], ALU.add)
                dve.drain()
                dve.tensor_scalar(spare[:], rel[:], 0.0, -2 * BIG, ALU.is_lt, ALU.mult)
                dve.drain()
                dve.tensor_tensor(rel[:], key[:], spare[:], ALU.add)
                dve.drain()
                dve.tensor_tensor(key[:], rel[:], k["src_base"][:], ALU.add)
                dve.drain()

            def pair(t, c, n):
                dve.wait_ge(row_in, 16 * n + 16)
                dve.tensor_copy(src_rowf[:], src_row[:])
                dve.drain().then_inc(row_free, 1)
                for b in range(2):
                    dve.wait_ge(used, 2 * n + (b + 1))
                    at = bass.ds(2 * c + b, 1)
                    dve.tensor_scalar(to_dst[b][:], iota_r[:], rel[:, at], None, ALU.is_equal)
                    dve.tensor_scalar(same[b][:], src_rowf[:, b * CH:(b + 1) * CH], src[:, at], k["weight"][:, at],
                                      ALU.is_equal, ALU.mult)
                    dve.tensor_scalar(place[b][:], iota_r[:], k["src_place"][:, at], None, ALU.is_equal)
                    dve.tensor_scalar(onehot[b][:], iota[:], key[:, at], None, ALU.is_equal)
                    dve.drain().then_inc(onehot_ready, 1)

            def end(t):
                dve.wait_ge(tile_done, t + 1)
                dve.wait_ge(counts_free, t + 1)
                for g in range(4):
                    a, n = CENTRED[g]
                    dve.tensor_copy(counts[:, a:a + n], ct_ps[:, g, 0:n])
                dve.drain().then_inc(evac_dve, 1)

            walk(dve, k, plan, start, pair, end)

        @block.tensor
        def _(pe):
            pe.wait_ge(loaded, 48)
            pe.wait_ge(setup, 1)
            pe.sem_inc(used, 2)
            pe.sem_inc(evac_dve, 1)
            pe.sem_inc(evac_act, 1)
            pe.sem_inc(S_kept, 1)

            def start(t):
                pe.wait_ge(evac_dve, t + 1)
                pe.wait_ge(evac_act, t + 1)
                for g in range(CTB):
                    pe.matmul(ct_ps[:, g, :], zeros[:, 0:R], zeros[:, 0:512], start=True, stop=False, skip_group_check=True)

            def pair(t, c, n):
                for b in range(2):
                    pe.wait_ge(onehot_ready, 2 * n + (b + 1))
                    for g, (a, m) in enumerate(CENTRED):
                        if g == 3:
                            pe.wait_ge(S_kept, 2 * n + (b + 1))
                            pe.matmul(P_ps[b], to_dst[b][:], same[b][:], start=True, stop=True).then_inc(P_ready, 1)
                        pe.matmul(ct_ps[:, g, 0:m], place[b][:], onehot[b][:, a:a + m], start=False, stop=False,
                                  skip_group_check=True)
                    pe.matmul(deg_ps, to_dst[b][:], ones[:], start=False, stop=False, skip_group_check=True)
                    pe.drain().then_inc(used, 1)
                    pe.wait_ge(P_kept, 2 * n + (b + 1))
                    pe.matmul(S_ps, P[b][:], k["xn"][:, bass.ds(t, 1), :], start=True, stop=True).then_inc(S_ready, 1)

            def end(t):
                pe.drain().then_inc(tile_done, 1)

            walk(pe, k, plan, start, pair, end)


def collect_support(nc, d, k):
    with Stage(nc, "collect") as s:
        loaded = s.sem("loaded")
        block = s.block()

        @block.sync
        def _(sp):
            for b, to in enumerate((k["A"], k["B"])):
                sp.dma_start(to[:], k["support_dram"][b][0:NODES].rearrange("(t p) n -> p t n", p=R)).then_inc(loaded, 16)

        @block.vector
        def _(dve):
            dve.wait_ge(loaded, 32)
            dve.tensor_tensor(k["A"][:], k["A"][:], k["B"][:], ALU.add)


def edge_hidden(nc, d, k):
    with Stage(nc, "hid") as s:
        plan = s.sb("plan", [1, 3, T], I32)
        iota_r = s.sb("iota_r", [CH, R])
        rel = s.sb("rel", [CH, NCH])
        attr = [s.sb(f"attr{b}", [EDIM + 1, CH]) for b in range(2)]
        w1 = s.sb("w1", [EDIM + 1, D])
        to_dst = [s.sb(f"to_dst{b}", [CH, R]) for b in range(2)]
        hidden = [s.sb(f"hidden{b}", [CH, D]) for b in range(2)]
        hid_ps = [s.ps(f"hid_ps{b}", [CH, 512]) for b in range(2)]
        sum_ps = s.ps("sum_ps", [R, 512])
        zeros = s.sb("zeros", [CH, D], BF16)
        loaded, attr0, attr1, attr_free, hid_ready, hid_act, used, onehot_ready, tile_done, evac, setup = map(
            s.sem, ("loaded", "attr0", "attr1", "attr_free", "hid_ready", "hid_act", "used", "onehot_ready",
                    "tile_done", "evac", "setup"))
        block = s.block()

        def nothing(t):
            pass

        @block.sync
        def _(sp):
            sp.dma_start(plan[:], k["plan_dram"]).then_inc(loaded, 16)
            sp.dma_start(iota_r[:], d["iota_r"]).then_inc(loaded, 16)
            sp.dma_start(w1[:], d["ee_w1"]).then_inc(loaded, 16)
            sp.wait_ge(loaded, 48)

            def pair(t, c, n):
                for b in range(2):
                    sp.wait_ge(attr_free, 2 * n + (b + 1))
                    sp.dma_start(attr[b][:], d["attr"][:, bass.ds((2 * c + b) * CH, CH)]).then_inc(
                        attr0 if b == 0 else attr1, 16)

            walk(sp, k, plan, nothing, pair, nothing)

        @block.scalar
        def _(act):
            act.wait_ge(loaded, 48)

            def pair(t, c, n):
                for b in range(2):
                    act.wait_ge(hid_ready, 2 * n + (b + 1))
                    act.wait_ge(used, 2 * n + (b + 1))
                    act.activation(hidden[b][:], hid_ps[b][:, 0:D], ACT.Relu).then_inc(hid_act, 1)

            walk(act, k, plan, nothing, pair, nothing)

        @block.vector
        def _(dve):
            dve.wait_ge(loaded, 48)
            dve.memset(zeros[:], 0.0).then_inc(setup, 1)

            def start(t):
                dve.drain()
                dve.tensor_scalar(rel[:], k["dst"][:], k["tile_start"][:, bass.ds(t, 1)], None, ALU.subtract)
                dve.drain()

            def pair(t, c, n):
                for b in range(2):
                    dve.wait_ge(used, 2 * n + (b + 1))
                    dve.tensor_scalar(to_dst[b][:], iota_r[:], rel[:, bass.ds(2 * c + b, 1)], None,
                                      ALU.is_equal).then_inc(onehot_ready, 1)

            def end(t):
                dve.wait_ge(tile_done, t + 1)
                dve.tensor_copy(k["B"][:, bass.ds(t, 1), :],
                                sum_ps[:, 0:D].rearrange("p (a n) -> p a n", a=1)).then_inc(evac, 1)

            walk(dve, k, plan, start, pair, end)

        @block.tensor
        def _(pe):
            pe.wait_ge(loaded, 48)
            pe.wait_ge(setup, 1)
            pe.sem_inc(used, 2)
            pe.sem_inc(attr_free, 2)
            pe.sem_inc(evac, 1)
            pe.sem_inc(hid_act, 2)

            def start(t):
                pe.wait_ge(evac, t + 1)
                pe.matmul(sum_ps[:, 0:D], zeros[:, 0:R], zeros[:], start=True, stop=False, skip_group_check=True)

            def pair(t, c, n):
                for b in range(2):
                    pe.wait_ge(attr0 if b == 0 else attr1, 16 * n + 16)
                    pe.wait_ge(hid_act, 2 * n + (b + 1))
                    pe.matmul(hid_ps[b][:, 0:D], attr[b][:], w1[:], start=True, stop=True).then_inc(hid_ready, 1)
                    pe.drain().then_inc(attr_free, 1)
                for b in range(2):
                    pe.wait_ge(hid_act, 2 * n + (b + 3))
                    pe.wait_ge(onehot_ready, 2 * n + (b + 1))
                    pe.matmul(sum_ps[:, 0:D], to_dst[b][:], hidden[b][:], start=False, stop=False,
                              skip_group_check=True).then_inc(used, 1)

            def end(t):
                pe.drain().then_inc(tile_done, 1)

            walk(pe, k, plan, start, pair, end)


def aggregate(nc, d, k, name, source, into, finish):
    with Stage(nc, name) as s:
        ct = [s.sb(f"ct{b}", [R, NODES]) for b in range(2)]
        acc = [s.ps(f"acc{b}", [R, 512]) for b in range(2)]
        temp = s.sb("temp", [R, 1, D])
        ct0, ct1, ct_free, acc_ready, acc_free = map(s.sem, ("ct0", "ct1", "ct_free", "acc_ready", "acc_free"))
        block = s.block()

        @block.sync
        def _(sp):
            def load(t, b):
                sp.wait_ge(ct_free, t + 1)
                sp.dma_start(ct[b][:], k["ct_dram"][bass.ds(t, 1)].rearrange("a p n -> (a p) n")).then_inc(
                    ct0 if b == 0 else ct1, 16)

            tiles(sp, load)

        @block.tensor
        def _(pe):
            pe.sem_inc(ct_free, 2)

            def product(t, i, b):
                pe.wait_ge(ct0 if b == 0 else ct1, 16 * i + 16)
                pe.wait_ge(acc_free, t + 1)
                for src in range(T):
                    last = pe.matmul(acc[b][:, 0:D], ct[b][:, src * R:(src + 1) * R], source[:, src, :],
                                     start=(src == 0), stop=(src == T - 1))
                last.then_inc(acc_ready, 1)
                pe.drain().then_inc(ct_free, 1)

            with pe.Fori(0, T // 2) as i:
                for b in range(2):
                    product(2 * i + b, i, b)
            product(T - 1, T // 2, 0)

        @block.vector
        def _(dve):
            dve.sem_inc(acc_free, 2)

            def evacuate(t, b):
                dve.wait_ge(acc_ready, t + 1)
                finish(dve, t, into[:, bass.ds(t, 1), :], acc[b][:, 0:D].rearrange("p (a n) -> p a n", a=1), temp[:])
                dve.drain().then_inc(acc_free, 1)

            tiles(dve, evacuate)



def row_stats(nc, d, k, name, source, kind, width=D):
    with Stage(nc, name) as s:
        stats = s.sb("stats", [R, T, 6])
        mv = s.sb("mv", [R, T, 2])
        rv, root = s.sb("rv", [R, T, 1]), s.sb("root", [R, T, 1])
        squares = [s.sb(f"squares{b}", [R, 1, width]) for b in range(2)]
        var_ready, root_ready = s.sem("var_ready"), s.sem("root_ready")
        block = s.block()

        @block.vector
        def _(dve):
            if kind == "norm":
                def square(t, b):
                    dve.tensor_tensor(squares[b][:], source[:, bass.ds(t, 1), :], source[:, bass.ds(t, 1), :], ALU.mult)
                    dve.drain()
                    dve.tensor_reduce(rv[:, bass.ds(t, 1), :], squares[b][:], AX, ALU.add)

                tiles(dve, square)
                dve.drain().then_inc(var_ready, 1)
            else:
                with dve.Fori(0, T) as t:
                    dve.bn_stats(stats[:, bass.ds(t, 1), :], source[:, bass.ds(t, 1), :])
                dve.drain()
                for t in range(T):
                    dve.bn_aggr(mv[:, t, :], stats[:, t, :])
                dve.drain()
                dve.tensor_scalar(rv[:], mv[:, :, 1:2], LN_EPS, None, ALU.add)
                dve.drain().then_inc(var_ready, 1)
            dve.wait_ge(root_ready, 1)
            if kind == "norm":
                dve.tensor_scalar(rv[:], root[:], 1e-12, None, ALU.max)
                dve.memset(k["shift"][:], 0.0)
                dve.drain()
                dve.reciprocal(k["scale"][:], rv[:])
            else:
                dve.reciprocal(k["scale"][:], root[:])
                dve.drain()
                dve.scalar_tensor_tensor(k["shift"][:], mv[:, :, 0:1], -1.0, k["scale"][:], ALU.mult, ALU.mult)

        @block.scalar
        def _(act):
            act.wait_ge(var_ready, 1)
            act.activation(root[:], rv[:], ACT.Sqrt).then_inc(root_ready, 1)


def normalise(nc, d, k, name, source, rows_to=None, store=False):
    with Stage(nc, name) as s:
        xs = [s.sb(f"xs{b}", [R, D]) for b in range(2)]
        pt = [s.ps(f"pt{b}", [128, 2, 256]) for b in range(2)]
        xs_ready, xs_free, turned, pt_free, rows_ready, stored, started = map(
            s.sem, ("xs_ready", "xs_free", "turned", "pt_free", "rows_ready", "stored", "started"))
        block = s.block()

        @block.vector
        def _(dve):
            dve.sem_inc(pt_free, 2)

            def columns(t, b):
                dve.wait_ge(turned, t + 1)
                dve.tensor_copy(k["xnT"][:, :, rows(t)], pt[b][:, :, 0:R]).then_inc(pt_free, 1)

            tiles(dve, columns)

        @block.scalar
        def _(act):
            def scale(t, b):
                act.wait_ge(xs_free, t + 1)
                if rows_to is not None:
                    act.wait_ge(rows_ready, t + 1)
                settle(act, started)
                act.activation(xs[b][:], source[:, bass.ds(t, 1), :].rearrange("p a n -> p (a n)"), ACT.Identity,
                               bias=k["shift"][:, bass.ds(t, 1), :].rearrange("p a n -> p (a n)"),
                               scale=k["scale"][:, bass.ds(t, 1), :].rearrange("p a n -> p (a n)")).then_inc(xs_ready, 1)

            tiles(act, scale)

        @block.tensor
        def _(pe):
            pe.sem_inc(xs_free, 2)

            def turn(t, b):
                pe.wait_ge(xs_ready, t + 1)
                pe.wait_ge(pt_free, t + 1)
                for c in range(2):
                    last = pe.transpose(pt[b][:, c, 0:R], xs[b][:, c * 128:(c + 1) * 128], k["ident"][0:R, 0:R])
                last.then_inc(turned, 1)
                pe.drain().then_inc(xs_free, 1)

            tiles(pe, turn)

        if rows_to is not None:
            @block.gpsimd
            def _(pool):
                pool.sem_inc(rows_ready, 2)

                def keep(t, b):
                    pool.wait_ge(xs_ready, t + 1)
                    pool.tensor_copy(rows_to[:, bass.ds(t, 1), :],
                                     xs[b][:].rearrange("p (a n) -> p a n", a=1)).then_inc(rows_ready, 1)

                tiles(pool, keep)

        if store:
            @block.sync
            def _(sp):
                sp.wait_ge(rows_ready, T + 2)
                sp.dma_start(k["xn_dram"].rearrange("(t p) n -> p t n", p=R), rows_to[:]).then_inc(stored, 16)
                sp.wait_ge(stored, 16)


def mix_sums(nc, d, k, name, heads, kind, wkv, bkv, gain, shift):
    hd = D // heads
    G = 2 * heads if kind == "ln" else heads
    with Stage(nc, name) as s:
        w = s.sb("w", [128, 2, 2 * D])
        bias = s.sb("bias", [R, 2 * D])
        gn, sh = s.sb("gn", [R, 2 * D]), s.sb("sh", [R, 2 * D])
        mask = s.sb("mask", [128, 128])
        ones = s.sb("ones", [R, 128])
        xt = [s.sb(f"xt{b}", [128, 2, R]) for b in range(2)]
        z = [s.sb(f"z{b}", [R, 2 * D]) for b in range(2)]
        e = s.sb("e", [R, 2 * D])
        sums, sq, var, root = (s.sb(n, [R, G]) for n in ("sums", "sq", "var", "root"))
        kv_ps = [s.ps(f"kv_ps{b}", [R, 512]) for b in range(2)]
        acc = s.ps("acc", [128, 2, 128])
        acc_sum = s.ps("acc_sum", [R, 512])
        zeros = s.sb("zeros", [128, 2 * D], BF16)
        loaded, setup, xt_ready, xt_free, kv_ready, kv_free, z_ready, z_free, part, root_ready, done = map(
            s.sem, ("loaded", "setup", "xt_ready", "xt_free", "kv_ready", "kv_free", "z_ready", "z_free",
                    "part", "root_ready", "done"))
        block = s.block()

        @block.sync
        def _(sp):
            sp.dma_start(w[:], wkv).then_inc(loaded, 16)
            sp.dma_start(bias[:], bkv if bkv is not None else d["zero_row"]).then_inc(loaded, 16)
            sp.dma_start(gn[:], gain if gain is not None else d["zero_row"]).then_inc(loaded, 16)
            sp.dma_start(sh[:], shift if shift is not None else d["zero_row"]).then_inc(loaded, 16)
            sp.dma_start(mask[:], d["mask64"] if hd == 64 else d["mask32"]).then_inc(loaded, 16)
            sp.wait_ge(loaded, 80)

        @block.gpsimd
        def _(pool):
            def fetch(t, b):
                pool.wait_ge(xt_free, t + 1)
                pool.tensor_copy(xt[b][:], k["xnT"][:, :, rows(t)]).then_inc(xt_ready, 1)

            tiles(pool, fetch)

        @block.tensor
        def _(pe):
            pe.wait_ge(loaded, 80)
            pe.wait_ge(setup, 1)
            pe.sem_inc(xt_free, 2)
            pe.sem_inc(z_free, 2)
            pe.matmul(acc[:].rearrange("p a n -> p (a n)"), zeros[:, 0:128], zeros[:, 0:256], start=True, stop=False,
                      skip_group_check=True)
            pe.matmul(acc_sum[:, 0:D], zeros[:, 0:R], zeros[:, 0:D], start=True, stop=False, skip_group_check=True)

            def body(t, b):
                pe.wait_ge(xt_ready, t + 1)
                pe.wait_ge(kv_free, t + 1)
                for c in range(2):
                    last = pe.matmul(kv_ps[b][:], xt[b][:, c, :], w[:, c, :], start=(c == 0), stop=(c == 1))
                last.then_inc(kv_ready, 1)
                pe.drain().then_inc(xt_free, 1)
                pe.wait_ge(z_ready, t + 1)
                for c in range(2):
                    pe.matmul(acc[:, c, :], z[b][:, D + c * 128:D + (c + 1) * 128], z[b][:, c * 128:(c + 1) * 128],
                              start=False, stop=False, skip_group_check=True)
                if kind == "elu":
                    pe.matmul(acc_sum[:, 0:D], ones[:, 0:R], z[b][:, 0:D], start=False, stop=False, skip_group_check=True)
                pe.drain().then_inc(z_free, 1)

            tiles(pe, body)
            pe.drain().then_inc(done, 1)

        @block.scalar
        def _(act):
            def body(t, b):
                if kind == "ln":
                    act.wait_ge(part, 2 * t + 1)
                    act.activation(e[:], z[b][:], ACT.Square).then_inc(root_ready, 1)
                    act.wait_ge(part, 2 * t + 2)
                    act.activation(root[:], var[:], ACT.Sqrt).then_inc(root_ready, 1)
                else:
                    act.wait_ge(part, t + 1)
                    act.activation(e[:, D:2 * D], e[:, 0:D], ACT.Exp).then_inc(root_ready, 1)

            tiles(act, body)

        @block.vector
        def _(dve):
            dve.sem_inc(kv_free, 2)
            dve.wait_ge(loaded, 80)
            dve.memset(zeros[:], 0.0)
            dve.memset(ones[:], 1.0)
            dve.drain().then_inc(setup, 1)

            def body(t, b):
                dve.wait_ge(kv_ready, t + 1)
                dve.wait_ge(z_free, t + 1)
                if kind == "ln":
                    zv = z[b][:].rearrange("p (g n) -> p g n", g=G)
                    dve.tensor_reduce(sums[:], kv_ps[b][:].rearrange("p (g n) -> p g n", g=G), AX, ALU.add)
                    dve.drain()
                    dve.tensor_scalar(sq[:], sums[:], 1.0 / hd, None, ALU.mult)
                    dve.drain()
                    dve.tensor_tensor(zv, kv_ps[b][:].rearrange("p (g n) -> p g n", g=G),
                                      sq[:].unsqueeze(2).broadcast_to((R, G, hd)), ALU.subtract)
                    dve.drain().then_inc(part, 1)
                    dve.drain().then_inc(kv_free, 1)
                    dve.wait_ge(root_ready, 2 * t + 1)
                    dve.tensor_reduce(sums[:], e[:].rearrange("p (g n) -> p g n", g=G), AX, ALU.add)
                    dve.drain()
                    dve.tensor_scalar(var[:], sums[:], 1.0 / hd, LN_EPS, ALU.mult, ALU.add)
                    dve.drain().then_inc(part, 1)
                    dve.wait_ge(root_ready, 2 * t + 2)
                    dve.reciprocal(sq[:], root[:])
                    dve.drain()
                    dve.tensor_tensor(zv, zv, sq[:].unsqueeze(2).broadcast_to((R, G, hd)), ALU.mult)
                    dve.drain()
                    dve.tensor_tensor(z[b][:], z[b][:], gn[:], ALU.mult)
                    dve.drain()
                    dve.tensor_tensor(z[b][:], z[b][:], sh[:], ALU.add)
                    dve.drain().then_inc(z_ready, 1)
                else:
                    dve.tensor_tensor(z[b][:], kv_ps[b][:], bias[:], ALU.add)
                    dve.drain().then_inc(kv_free, 1)
                    dve.tensor_scalar(e[:, 0:D], z[b][:, 0:D], 0.0, None, ALU.min)
                    dve.drain().then_inc(part, 1)
                    dve.wait_ge(root_ready, t + 1)
                    dve.scalar_tensor_tensor(z[b][:, 0:D], z[b][:, 0:D], 0.0, e[:, D:2 * D], ALU.max, ALU.add)
                    dve.drain().then_inc(z_ready, 1)

            tiles(dve, body)
            dve.wait_ge(done, 1)
            for c in range(2):
                dve.scalar_tensor_tensor(k["kvT"][:, c, :], acc[:, c, :], 1.0 / NODES if kind == "ln" else 1.0,
                                         mask[:], ALU.mult, ALU.mult)
            if kind == "elu":
                dve.tensor_copy(k["ksum"][:], acc_sum[:, 0:D])


def fold(nc, d, k, name, wo, wq=None):
    with Stage(nc, name) as s:
        woT = s.sb("woT", [128, 2, D])
        wqs = s.sb("wqs", [128, 2, D])
        m1 = s.sb("m1", [128, 2, D])
        ps1 = [s.ps(f"ps1{c}", [128, 512]) for c in range(2)]
        ps2 = [s.ps(f"ps2{c}", [128, 512]) for c in range(2)]
        loaded, one, two, kept = map(s.sem, ("loaded", "one", "two", "kept"))
        block = s.block()
        dest = m1 if wq is not None else k["fold"]

        @block.sync
        def _(sp):
            sp.dma_start(woT[:], wo).then_inc(loaded, 16)
            sp.dma_start(wqs[:], wq if wq is not None else wo).then_inc(loaded, 16)
            sp.wait_ge(loaded, 32)

        @block.tensor
        def _(pe):
            pe.wait_ge(loaded, 32)
            for c in range(2):
                pe.matmul(ps1[c][:, 0:D], k["kvT"][:, c, :], woT[:, c, :], start=True, stop=True).then_inc(one, 1)
            if wq is not None:
                pe.wait_ge(kept, 1)
                for i in range(2):
                    for c in range(2):
                        last = pe.matmul(ps2[i][:, 0:D], wqs[:, c, i * 128:(i + 1) * 128], m1[:, c, :],
                                         start=(c == 0), stop=(c == 1))
                    last.then_inc(two, 1)

        @block.vector
        def _(dve):
            for c in range(2):
                dve.wait_ge(one, c + 1)
                dve.tensor_copy(dest[:, c, :], ps1[c][:, 0:D])
            dve.drain().then_inc(kept, 1)
            if wq is not None:
                for i in range(2):
                    dve.wait_ge(two, i + 1)
                    dve.tensor_copy(k["fold"][:, i, :], ps2[i][:, 0:D])


def linear_rows(nc, d, k, name, source, weight, nk, prepare, finish, n_out=D, vectors=(), temps=()):
    with Stage(nc, name) as s:
        w = s.sb("w", [128, nk, n_out])
        vec = [s.sb(f"vec{n}", [R, v[1]]) for n, v in enumerate(vectors)]
        tmp = [s.sb(f"tmp{n}", shape) for n, shape in enumerate(temps)]
        xs = [s.sb(f"xs{b}", [R, nk * 128]) for b in range(2)]
        xt = [s.sb(f"xt{b}", [128, nk, R]) for b in range(2)]
        pt = [s.ps(f"pt{b}", [128, 4, 128]) for b in range(2)]
        out = [s.ps(f"out{b}", [R, 512]) for b in range(2)]
        loaded, xs_ready, xs_free, turned, xt_ready, xt_free, out_ready, out_free = map(
            s.sem, ("loaded", "xs_ready", "xs_free", "turned", "xt_ready", "xt_free", "out_ready", "out_free"))
        helper, helped = s.sem("helper"), s.sem("helped")
        block = s.block()
        in_dram = weight is not k["fold"]
        total = 16 * (len(vectors) + in_dram)

        @block.sync
        def _(sp):
            if in_dram:
                sp.dma_start(w[:], weight).then_inc(loaded, 16)
            for v, t in zip(vectors, vec):
                sp.dma_start(t[:], v[0]).then_inc(loaded, 16)
            sp.wait_ge(loaded, total)

        wt = w if in_dram else weight

        @block.scalar
        def _(act):
            act.wait_ge(loaded, total)

            def body(t, b):
                act.wait_ge(turned, t + 1)
                act.wait_ge(xt_free, t + 1)
                act.activation(xt[b][:], pt[b][:, 0:nk, 0:R], ACT.Copy).then_inc(xt_ready, 1)

            tiles(act, body)

        @block.tensor
        def _(pe):
            pe.wait_ge(loaded, total)
            pe.sem_inc(xs_free, 2)
            pe.sem_inc(xt_free, 2)

            def body(t, b):
                pe.wait_ge(xs_ready, t + 1)
                for c in range(nk):
                    last = pe.transpose(pt[b][:, c, 0:R], xs[b][:, c * 128:(c + 1) * 128], k["ident"][0:R, 0:R])
                last.then_inc(turned, 1)
                pe.drain().then_inc(xs_free, 1)
                pe.wait_ge(xt_ready, t + 1)
                pe.wait_ge(out_free, t + 1)
                for c in range(nk):
                    last = pe.matmul(out[b][:, 0:n_out], xt[b][:, c, :], wt[:, c, :], start=(c == 0), stop=(c == nk - 1))
                last.then_inc(out_ready, 1)
                pe.drain().then_inc(xt_free, 1)

            tiles(pe, body)

        @block.vector
        def _(dve):
            dve.wait_ge(loaded, total)
            dve.sem_inc(out_free, 2)

            def body(t, b):
                dve.wait_ge(xs_free, t + 1)
                prepare(dve, t, xs[b], vec, tmp)
                dve.drain().then_inc(xs_ready, 1)
                dve.wait_ge(out_ready, t + 1)
                finish(dve, t, out[b][:, 0:n_out].rearrange("p (a n) -> p a n", a=1), vec, tmp)
                dve.drain().then_inc(out_free, 1)

            tiles(dve, body)


def copy_in(source):
    def prepare(dve, t, xs, vec, tmp):
        dve.tensor_copy(xs[:].rearrange("p (a n) -> p a n", a=1), source[:, bass.ds(t, 1), :])
    return prepare


def elementwise(nc, d, k, name, fn, vectors=(), temps=()):
    with Stage(nc, name) as s:
        vec = [s.sb(f"vec{n}", [R, v[1]]) for n, v in enumerate(vectors)]
        tmp = [[s.sb(f"tmp{n}{b}", shape) for n, shape in enumerate(temps)] for b in range(2)]
        loaded = s.sem("loaded")
        block = s.block()

        @block.sync
        def _(sp):
            for v, t in zip(vectors, vec):
                sp.dma_start(t[:], v[0]).then_inc(loaded, 16)
            if vectors:
                sp.wait_ge(loaded, 16 * len(vectors))

        @block.vector
        def _(dve):
            if vectors:
                dve.wait_ge(loaded, 16 * len(vectors))

            def body(t, b):
                fn(dve, t, vec, tmp[b])
                dve.drain()

            tiles(dve, body)


def project(nc, d, k, name, weight, n_out, into, bias=None):
    with Stage(nc, name) as s:
        w = s.sb("w", [128, 2, n_out])
        bc = s.sb("bc", [R, 1, n_out])
        xt = [s.sb(f"xt{b}", [128, 2, R]) for b in range(2)]
        out = [s.ps(f"out{b}", [R, 512]) for b in range(2)]
        loaded, xt_ready, xt_free, out_ready, out_free = map(
            s.sem, ("loaded", "xt_ready", "xt_free", "out_ready", "out_free"))
        block = s.block()
        total = 16 * (1 + (bias is not None))

        @block.sync
        def _(sp):
            sp.dma_start(w[:], weight).then_inc(loaded, 16)
            if bias is not None:
                sp.dma_start(bc[:].rearrange("p a n -> p (a n)"), bias).then_inc(loaded, 16)
            sp.wait_ge(loaded, total)

        @block.gpsimd
        def _(pool):
            def fetch(t, b):
                pool.wait_ge(xt_free, t + 1)
                pool.tensor_copy(xt[b][:], k["xnT"][:, :, rows(t)]).then_inc(xt_ready, 1)

            tiles(pool, fetch)

        @block.tensor
        def _(pe):
            pe.wait_ge(loaded, total)
            pe.sem_inc(xt_free, 2)

            def body(t, b):
                pe.wait_ge(xt_ready, t + 1)
                pe.wait_ge(out_free, t + 1)
                for c in range(2):
                    last = pe.matmul(out[b][:, 0:n_out], xt[b][:, c, :], w[:, c, :], start=(c == 0), stop=(c == 1))
                last.then_inc(out_ready, 1)
                pe.drain().then_inc(xt_free, 1)

            tiles(pe, body)

        @block.vector
        def _(dve):
            dve.wait_ge(loaded, total)
            dve.sem_inc(out_free, 2)

            def body(t, b):
                dve.wait_ge(out_ready, t + 1)
                row = out[b][:, 0:n_out].rearrange("p (a n) -> p a n", a=1)
                if bias is None:
                    dve.tensor_copy(into[:, bass.ds(t, 1), :], row).then_inc(out_free, 1)
                else:
                    dve.tensor_tensor(into[:, bass.ds(t, 1), :], row, bc[:], ALU.add).then_inc(out_free, 1)

            tiles(dve, body)


def choose(dve, lg, top, hot, spare, down, E):
    dve.tensor_reduce(top, lg, AX, ALU.max)
    dve.drain()
    dve.tensor_tensor(hot, lg, top.broadcast_to((R, T, E)), ALU.is_ge)
    dve.drain()
    dve.tensor_tensor(hot, hot, down.broadcast_to((R, T, E)), ALU.mult)
    dve.drain()
    dve.tensor_reduce(spare, hot, AX, ALU.max)
    dve.drain()
    dve.tensor_tensor(hot, hot, spare.broadcast_to((R, T, E)), ALU.is_equal)
    dve.drain()


def gate(nc, d, k, name, E, kind):
    with Stage(nc, name) as s:
        lg = k["gates"][:, 0:T * E].rearrange("p (t e) -> p t e", e=E)
        one, two = s.sb("one", [R, T, E]), s.sb("two", [R, T, E])
        top1, top2, sp1, sp2 = (s.sb(n, [R, T, 1]) for n in ("top1", "top2", "sp1", "sp2"))
        down = s.sb("down", [R, 1, E])
        loaded, to_exp, exped = s.sem("loaded"), s.sem("to_exp"), s.sem("exped")
        block = s.block()
        soft = kind == "soft_two"

        @block.sync
        def _(sp):
            sp.dma_start(down[:].rearrange("p a n -> p (a n)"), d["down"][:, 32 - E:32]).then_inc(loaded, 16)
            sp.wait_ge(loaded, 16)

        @block.vector
        def _(dve):
            dve.wait_ge(loaded, 16)
            if soft:
                dve.tensor_reduce(top1[:], lg, AX, ALU.max)
                dve.drain()
                dve.tensor_tensor(one[:], lg, top1[:].broadcast_to((R, T, E)), ALU.subtract)
                dve.drain().then_inc(to_exp, 1)
                dve.wait_ge(exped, 1)
                dve.tensor_reduce(sp1[:], two[:], AX, ALU.add)
                dve.drain()
                dve.reciprocal(sp2[:], sp1[:])
                dve.drain()
                dve.tensor_tensor(lg, two[:], sp2[:].broadcast_to((R, T, E)), ALU.mult)
                dve.drain()
            choose(dve, lg, top1[:], one[:], sp1[:], down[:], E)
            if kind == "first":
                dve.tensor_copy(lg, one[:])
                return
            dve.scalar_tensor_tensor(lg, one[:], -1e30, lg, ALU.mult, ALU.add)
            dve.drain()
            choose(dve, lg, top2[:], two[:], sp1[:], down[:], E)
            dve.tensor_tensor(sp1[:], top2[:], top1[:], ALU.subtract)
            dve.drain().then_inc(to_exp, 1)
            dve.wait_ge(exped, 2 if soft else 1)
            dve.tensor_scalar(top1[:], sp2[:], 1.0, None, ALU.add)
            dve.drain()
            dve.reciprocal(top2[:], top1[:])
            dve.drain()
            dve.tensor_tensor(sp1[:], top2[:], sp2[:], ALU.mult)
            dve.tensor_tensor(one[:], one[:], top2[:].broadcast_to((R, T, E)), ALU.mult)
            dve.drain()
            dve.tensor_tensor(two[:], two[:], sp1[:].broadcast_to((R, T, E)), ALU.mult)
            dve.drain()
            dve.tensor_tensor(lg, one[:], two[:], ALU.add)

        @block.scalar
        def _(act):
            if kind == "first":
                return
            n = 0
            if soft:
                act.wait_ge(to_exp, 1)
                act.activation(two[:], one[:], ACT.Exp).then_inc(exped, 1)
                n = 1
            act.wait_ge(to_exp, n + 1)
            act.activation(sp2[:], sp1[:], ACT.Exp).then_inc(exped, 1)


def rank_gate(nc, d, k, name, keep):
    with Stage(nc, name) as s:
        col = s.sb("col", [128, T])
        colT = s.sb("colT", [T, R])
        line = s.sb("line", [128, NODES])
        below = s.sb("below", [R, R])
        c1, c2, c3, c4 = (s.sb(n, [R, T]) for n in ("c1", "c2", "c3", "c4"))
        junk = [s.sb(f"junk{n}", [R, NODES]) for n in range(2)]
        ps = s.ps("ps", [T, 512])
        ready, turned, copied, stored, back, loaded = map(
            s.sem, ("ready", "turned", "copied", "stored", "back", "loaded"))
        w = k["gates"]
        block = s.block()

        @block.sync
        def _(sp):
            sp.dma_start(below[:], d["below"]).then_inc(loaded, 16)
            sp.wait_ge(copied, 1)
            sp.dma_start(k["line_dram"].rearrange("(t p) -> t p", p=R), colT[:]).then_inc(stored, 16)
            sp.wait_ge(stored, 16)
            sp.dma_start(line[0:R, :], k["line_dram"].rearrange("(a n) -> a n", a=1).broadcast_to((R, NODES))).then_inc(back, 16)
            sp.wait_ge(back, 16)
            sp.wait_ge(loaded, 16)

        @block.tensor
        def _(pe):
            pe.wait_ge(ready, 1)
            pe.transpose(ps[:, 0:R], col[0:R, :], k["ident"][0:R, 0:R]).then_inc(turned, 1)

        @block.vector
        def _(dve):
            dve.tensor_copy(col[0:R, :], w[:, 0:T]).then_inc(ready, 1)
            dve.wait_ge(turned, 1)
            dve.tensor_copy(colT[:], ps[:, 0:R]).then_inc(copied, 1)
            dve.wait_ge(back, 16)
            dve.wait_ge(loaded, 16)
            for c in (c1, c2, c3, c4):
                dve.memset(c[:], 0.0)
            dve.drain()
            for t in range(T):
                a, z = t * R, (t + 1) * R
                if t:
                    dve.tensor_scalar(junk[0][:, 0:a], line[0:R, 0:a], w[:, t:t + 1], 0.0, ALU.is_ge, ALU.add,
                                      accum_out=c1[:, t:t + 1])
                dve.tensor_scalar(junk[1][:, a:], line[0:R, a:], w[:, t:t + 1], 0.0, ALU.is_gt, ALU.add,
                                  accum_out=c2[:, t:t + 1])
                dve.drain()
                dve.scalar_tensor_tensor(junk[0][:, 0:R], line[0:R, a:z], w[:, t:t + 1], below[:],
                                         ALU.is_equal, ALU.mult)
                dve.drain()
                dve.tensor_reduce(c3[:, t:t + 1], junk[0][:, 0:R], AX, ALU.add)
                dve.drain()
            dve.tensor_tensor(c4[:], c1[:], c2[:], ALU.add)
            dve.drain()
            dve.tensor_tensor(c1[:], c4[:], c3[:], ALU.add)
            dve.drain()
            dve.scalar_tensor_tensor(c2[:], c1[:], float(keep), w[:, 0:T], ALU.is_lt, ALU.mult)
            dve.drain()
            for e in range(2):
                dve.tensor_copy(w[:, 0:2 * T].rearrange("p (t e) -> p t e", e=2)[:, :, e:e + 1],
                                c2[:].rearrange("p (t e) -> p t e", e=1))


def seed(nc, d, k, name, E, b2, into, base=None, base_row=None):
    with Stage(nc, name) as s:
        w = s.sb("w", [E, D])
        row = s.sb("row", [R, 1, D])
        gs = [s.sb(f"gs{b}", [R, E]) for b in range(2)]
        gt = [s.sb(f"gt{b}", [E, R]) for b in range(2)]
        pt = [s.ps(f"pt{b}", [E, 512]) for b in range(2)]
        out = [s.ps(f"out{b}", [R, 512]) for b in range(2)]
        loaded, gs_ready, gs_free, turned, gt_ready, gt_free, out_ready, out_free = map(
            s.sem, ("loaded", "gs_ready", "gs_free", "turned", "gt_ready", "gt_free", "out_ready", "out_free"))
        block = s.block()
        total = 16 * (1 + (base_row is not None))

        @block.sync
        def _(sp):
            sp.dma_start(w[:], b2).then_inc(loaded, 16)
            if base_row is not None:
                sp.dma_start(row[:].rearrange("p a n -> p (a n)"), base_row).then_inc(loaded, 16)
            sp.wait_ge(loaded, total)

        @block.gpsimd
        def _(pool):
            def body(t, b):
                pool.wait_ge(gs_free, t + 1)
                pool.tensor_copy(gs[b][:], k["gates"][:, bass.ds(t * E, E)]).then_inc(gs_ready, 1)

            tiles(pool, body)

        @block.scalar
        def _(act):

            def body(t, b):
                act.wait_ge(turned, t + 1)
                act.wait_ge(gt_free, t + 1)
                act.activation(gt[b][:], pt[b][:, 0:R], ACT.Copy).then_inc(gt_ready, 1)

            tiles(act, body)

        @block.tensor
        def _(pe):
            pe.wait_ge(loaded, total)
            pe.sem_inc(gs_free, 2)
            pe.sem_inc(gt_free, 2)

            def body(t, b):
                pe.wait_ge(gs_ready, t + 1)
                pe.transpose(pt[b][:, 0:R], gs[b][:], k["ident"][0:R, 0:R]).then_inc(turned, 1)
                pe.drain().then_inc(gs_free, 1)
                pe.wait_ge(gt_ready, t + 1)
                pe.wait_ge(out_free, t + 1)
                pe.matmul(out[b][:, 0:D], gt[b][:], w[:], start=True, stop=True).then_inc(out_ready, 1)
                pe.drain().then_inc(gt_free, 1)

            tiles(pe, body)

        @block.vector
        def _(dve):
            dve.wait_ge(loaded, total)
            dve.sem_inc(out_free, 2)

            def body(t, b):
                dve.wait_ge(out_ready, t + 1)
                to, o = into[:, bass.ds(t, 1), :], out[b][:, 0:D].rearrange("p (a n) -> p a n", a=1)
                if base is not None:
                    dve.tensor_tensor(to, o, base[:, bass.ds(t, 1), :], ALU.add).then_inc(out_free, 1)
                elif base_row is not None:
                    dve.tensor_tensor(to, o, row[:], ALU.add).then_inc(out_free, 1)
                else:
                    dve.tensor_copy(to, o).then_inc(out_free, 1)

            tiles(dve, body)


def experts(nc, d, k, name, E, hp, hc, func, w1, b1, w2, into):
    with Stage(nc, name) as s:
        W1 = [s.sb(f"W1{b}", [128, 2, hc * hp]) for b in range(2)]
        W2 = [s.sb(f"W2{b}", [hp, hc, D]) for b in range(2)]
        bias = s.sb("bias", [hp, E * hc])
        hT = [s.sb(f"hT{b}", [hp, hc, 3 * R]) for b in range(2)]
        h_ps = [s.ps(f"h_ps{c}", [hp, 512]) for c in range(hc)]
        o_ps = s.ps("o_ps", [R, 3, 512])
        loaded, w_in0, w_in1, w_free, h_ready, hT_ready, out_ready, out_free = map(
            s.sem, ("loaded", "w_in0", "w_in1", "w_free", "h_ready", "hT_ready", "out_ready", "out_free"))
        block = s.block()
        started, began = s.sem("started"), s.sem("began")
        per = 10 * hc

        def pairs(eng, body):
            with eng.Fori(0, E // 2) as q:
                for b in range(2):
                    body(2 * q + b, q, b)

        @block.sync
        def _(sp):
            sp.dma_start(bias[:], b1).then_inc(loaded, 16)
            sp.wait_ge(loaded, 16)

            def load(e, q, b):
                sp.wait_ge(w_free, e + 1)
                sp.dma_start(W1[b][:], w1[bass.ds(e, 1)].rearrange("a p c n -> (a p) c n")).then_inc(
                    w_in0 if b == 0 else w_in1, 16)
                sp.dma_start(W2[b][:], w2[bass.ds(e, 1)].rearrange("a p c n -> (a p) c n")).then_inc(
                    w_in0 if b == 0 else w_in1, 16)

            pairs(sp, load)

        @block.tensor
        def _(pe):
            pe.sem_inc(w_free, 2)
            pe.sem_inc(hT_ready, hc)

            def expert(e, q, b):
                pe.wait_ge(w_in0 if b == 0 else w_in1, 32 * q + 32)
                settle(pe, began)

                def group(t, g, n, p):
                    for c in range(hc):
                        pe.wait_ge(hT_ready, e * per + n * hc + (c + 1))
                        for i in range(2):
                            last = pe.matmul(h_ps[c][:, 0:g * R], W1[b][:, i, c * hp:(c + 1) * hp],
                                             k["xnT"][:, i, rows(t, g)], start=(i == 0), stop=(i == 1))
                        last.then_inc(h_ready, 1)
                    pe.wait_ge(hT_ready, e * per + n * hc + 2 * hc)
                    pe.wait_ge(out_free, e * 10 + n + 1)
                    for j in range(g):
                        for c in range(hc):
                            pe.matmul(o_ps[:, 2 * p + j // 2, (j % 2) * D:(j % 2 + 1) * D],
                                      hT[p][:, c, j * R:(j + 1) * R], W2[b][:, c, :], start=(c == 0), stop=(c == hc - 1))
                    pe.drain().then_inc(out_ready, 1)

                groups(pe, group)
                pe.drain().then_inc(w_free, 1)

            pairs(pe, expert)

        @block.scalar
        def _(act):
            act.wait_ge(loaded, 16)
            act.sem_inc(out_ready, 2)

            def expert(e, q, b):
                def group(t, g, n, p):
                    act.wait_ge(out_ready, e * 10 + n + 1)
                    for c in range(hc):
                        act.wait_ge(h_ready, e * per + n * hc + (c + 1))
                        settle(act, started)
                        act.activation(hT[p][:, c, 0:g * R], h_ps[c][:, 0:g * R], func,
                                       bias=bias[:, bass.ds(e * hc + c, 1)]).then_inc(hT_ready, 1)

                groups(act, group)

            pairs(act, expert)

        @block.vector
        def _(dve):
            dve.sem_inc(out_free, 2)

            def expert(e, q, b):
                def group(t, g, n, p):
                    dve.wait_ge(out_ready, e * 10 + n + 3)
                    for j in range(g):
                        to = into[:, bass.ds(t + j, 1), :].rearrange("p a n -> p (a n)")
                        dve.scalar_tensor_tensor(
                            to, o_ps[:, 2 * p + j // 2, (j % 2) * D:(j % 2 + 1) * D],
                            k["gates"][:, bass.ds((t + j) * E + e, 1)], to, ALU.mult, ALU.add)
                    dve.drain().then_inc(out_free, 1)

                groups(dve, group)

            pairs(dve, expert)


def softmax_keys(nc, d, k, name):
    C = 128
    with Stage(nc, name) as s:
        w, g_pre = s.sb("w", [128, 2, 3 * C]), s.sb("g_pre", [128, 2])
        w_out, mask = s.sb("w_out", [C, D]), s.sb("mask", [C, C])
        keys = s.sb("keys", [C, NODES])
        mem_k, mem_v = s.sb("mem_k", [C, 4]), s.sb("mem_v", [4, C])
        most, most4, low = s.sb("most", [C, 1]), s.sb("most4", [C, 1]), s.sb("low", [C, 1])
        ones = s.sb("ones", [R, 1])
        mem_e, mem_t = s.sb("mem_e", [C, 4]), s.sb("mem_t", [4, C])
        xt = [s.sb(f"xt{b}", [128, 2, R]) for b in range(2)]
        ke = [s.sb(f"ke{b}", [C, R]) for b in range(2)]
        ks = [s.sb(f"ks{b}", [R, C]) for b in range(2)]
        vs = [s.sb(f"vs{b}", [R, C]) for b in range(2)]
        ctx = s.sb("ctx", [C, C])
        inv = s.sb("inv", [C, 1])
        k_ps = [s.ps(f"k_ps{b}", [128, 512]) for b in range(2)]
        kv_ps = [s.ps(f"kv_ps{b}", [128, 512]) for b in range(2)]
        acc, acc_sum = s.ps("acc", [C, 512]), s.ps("acc_sum", [C, 512])
        (loaded, w_ready, k_ready, k_kept, low_ready, ke_ready, mem_ready, xt_ready, xt_free, kv_ready, kept,
         used, done, ctx_ready, folded, mem_turned, mem_kept, ke_free) = map(
            s.sem, ("loaded", "w_ready", "k_ready", "k_kept", "low_ready", "ke_ready", "mem_ready", "xt_ready",
                    "xt_free", "kv_ready", "kept", "used", "done", "ctx_ready", "folded", "mem_turned", "mem_kept",
                    "ke_free"))
        started = s.sem("started")
        block = s.block()

        @block.sync
        def _(sp):
            for to, src in ((w, d["w_qkv"]), (g_pre, d["g_pre"]), (w_out, d["w_out"]), (mask, d["mask32"]),
                            (mem_k, d["mem_k"]), (mem_v, d["mem_v"])):
                sp.dma_start(to[:], src).then_inc(loaded, 16)
            sp.wait_ge(loaded, 96)

        @block.gpsimd
        def _(pool):
            def fetch(t, b):
                pool.wait_ge(xt_free, t + 1)
                pool.tensor_copy(xt[b][:], k["xnT"][:, :, rows(t)]).then_inc(xt_ready, 1)

            tiles(pool, fetch)

        @block.vector
        def _(dve):
            dve.wait_ge(loaded, 96)
            dve.memset(ones[:], 1.0)
            for c in range(2):
                dve.tensor_scalar(k["w_qkv"][:, c, :], w[:, c, :], g_pre[:, c:c + 1], None, ALU.mult)
            dve.drain().then_inc(w_ready, 1)
            dve.sem_inc(k_kept, 2)

            def keep(t, g, n, p):
                dve.wait_ge(k_ready, n + 1)
                dve.tensor_copy(keys[:, rows(t, g)], k_ps[p][:, 0:g * R]).then_inc(k_kept, 1)

            groups(dve, keep)
            dve.drain()
            dve.tensor_reduce(most[:], keys[:], AX, ALU.max)
            dve.tensor_reduce(most4[:], mem_k[:], AX, ALU.max)
            dve.drain()
            dve.tensor_tensor(most[:], most[:], most4[:], ALU.max)
            dve.drain()
            dve.tensor_scalar(low[:], most[:], -1.0, None, ALU.mult).then_inc(low_ready, 1)
            dve.wait_ge(mem_turned, 1)
            dve.tensor_copy(mem_t[:], kv_ps[0][0:4, 0:C]).then_inc(mem_kept, 1)

            def body(t, b):
                dve.wait_ge(kv_ready, t + 1)
                dve.wait_ge(used, t + 1)
                dve.tensor_copy(ks[b][:], kv_ps[b][0:R, 0:C])
                dve.tensor_copy(vs[b][:], kv_ps[b][0:R, C:2 * C])
                dve.drain().then_inc(kept, 1)

            tiles(dve, body)
            dve.wait_ge(done, 1)
            dve.tensor_tensor(ctx[:], acc[:, 0:C], mask[:], ALU.mult)
            dve.reciprocal(inv[:], acc_sum[:, 0:1])
            dve.drain().then_inc(ctx_ready, 1)
            dve.wait_ge(folded, 1)
            dve.tensor_scalar(k["fold"][:, 0, :], k_ps[0][:, 0:D], inv[:], 32.0 ** -0.5, ALU.mult, ALU.mult)

        @block.scalar
        def _(act):
            act.wait_ge(low_ready, 1)
            act.activation(mem_e[:], mem_k[:], ACT.Exp, bias=low[:]).then_inc(mem_ready, 1)

            def body(t, b):
                act.wait_ge(ke_free, t + 1)
                settle(act, started)
                act.activation(ke[b][:], keys[:, rows(t)], ACT.Exp, bias=low[:]).then_inc(ke_ready, 1)

            tiles(act, body)

        @block.tensor
        def _(pe):
            pe.wait_ge(w_ready, 1)
            pe.sem_inc(ke_free, 2)
            pe.sem_inc(used, 2)
            pe.sem_inc(xt_free, 2)

            def key(t, g, n, p):
                pe.wait_ge(k_kept, n + 1)
                for c in range(2):
                    last = pe.matmul(k_ps[p][:, 0:g * R], k["w_qkv"][:, c, C:2 * C], k["xnT"][:, c, rows(t, g)],
                                     start=(c == 0), stop=(c == 1))
                last.then_inc(k_ready, 1)

            groups(pe, key)
            pe.wait_ge(mem_ready, 1)
            pe.transpose(kv_ps[0][0:4, 0:C], mem_e[:], k["ident"][:]).then_inc(mem_turned, 1)
            pe.wait_ge(mem_kept, 1)
            pe.matmul(acc[:, 0:C], mem_v[:], mem_t[:], start=True, stop=False, skip_group_check=True)
            pe.matmul(acc_sum[:, 0:1], mem_t[:], ones[0:4, :], start=True, stop=False, skip_group_check=True)

            def body(t, b):
                pe.wait_ge(ke_ready, t + 1)
                pe.wait_ge(xt_ready, t + 1)
                pe.transpose(kv_ps[b][0:R, 0:C], ke[b][:], k["ident"][:])
                for c in range(2):
                    last = pe.matmul(kv_ps[b][0:R, C:2 * C], xt[b][:, c, :], k["w_qkv"][:, c, 2 * C:3 * C],
                                     start=(c == 0), stop=(c == 1))
                last.then_inc(kv_ready, 1)
                pe.drain().then_inc(xt_free, 1)
                pe.drain().then_inc(ke_free, 1)
                pe.wait_ge(kept, t + 1)
                pe.matmul(acc[:, 0:C], vs[b][:], ks[b][:], start=False, stop=False, skip_group_check=True)
                pe.matmul(acc_sum[:, 0:1], ks[b][:], ones[:], start=False, stop=False,
                          skip_group_check=True).then_inc(used, 1)

            tiles(pe, body)
            pe.drain().then_inc(done, 1)
            pe.wait_ge(ctx_ready, 1)
            pe.matmul(k_ps[0][:, 0:D], ctx[:], w_out[:], start=True, stop=True).then_inc(folded, 1)


def batch(nc, name, sb_shapes, dve_steps, act_steps):
    with Stage(nc, name) as s:
        ts = [s.sb(f"t{n}", shape) for n, shape in enumerate(sb_shapes)]
        to_act, to_dve = s.sem("to_act"), s.sem("to_dve")
        block = s.block()

        @block.vector
        def _(dve):
            dve_steps(dve, ts, to_act, to_dve)

        @block.scalar
        def _(act):
            act_steps(act, ts, to_act, to_dve)


def mlp_ln(nc, d, k):
    H = 1024
    with Stage(nc, "mlp") as s:
        w2 = s.sb("w2", [128, 8, H])
        spare = k["xnT"][:].rearrange("p c n -> p (c n)")
        w1 = spare[:, 0:2 * H].rearrange("p (c n) -> p c n", c=2)
        w3 = spare[:, 2 * H:2 * H + 8 * D].rearrange("p (c n) -> p c n", c=8)
        b1, b2, b3 = s.sb("b1", [R, H]), s.sb("b2", [R, H]), s.sb("b3", [R, 1, D])
        g1, be1, g2, be2 = (s.sb(n, [128, 8]) for n in ("g1", "be1", "g2", "be2"))
        xs = s.sb("xs", [R, D])
        xt = s.sb("xt", [128, 2, R])
        z, zn = s.sb("z", [R, H]), s.sb("zn", [R, H])
        hT = s.sb("hT", [128, 8, R])
        stats, mv = s.sb("stats", [R, 2, 6]), s.sb("mv", [R, 2])
        v1, root, inv, shift = (s.sb(n, [R, 1]) for n in ("v1", "root", "inv", "shift"))
        pt = s.ps("pt", [128, 2, 256])
        h_ps = s.ps("h_ps", [R, 2, 512])
        t_ps = s.ps("t_ps", [128, 8, 128])
        y_ps = s.ps("y_ps", [R, 512])
        loaded, xs_ready, turned, xt_ready, h_ready, var_ready, root_ready, inv_ready, zn_ready, zt_ready, hT_ready, \
            y_ready, y_free = map(s.sem, (
                "loaded", "xs_ready", "turned", "xt_ready", "h_ready", "var_ready", "root_ready", "inv_ready",
                "zn_ready", "zt_ready", "hT_ready", "y_ready", "y_free"))
        block = s.block()

        @block.sync
        def _(sp):
            for to, name in ((w1, "m_w1"), (w2, "m_w2"), (w3, "m_w3"), (b1, "m_b1"), (b2, "m_b2"),
                             (g1, "m_g1"), (be1, "m_be1"), (g2, "m_g2"), (be2, "m_be2")):
                sp.dma_start(to[:], d[name]).then_inc(loaded, 16)
            sp.dma_start(b3[:].rearrange("p a n -> p (a n)"), d["m_b3"]).then_inc(loaded, 16)
            sp.wait_ge(loaded, 160)

        @block.tensor
        def _(pe):
            pe.wait_ge(loaded, 160)
            with pe.Fori(0, T) as t:
                pe.wait_ge(xs_ready, t + 1)
                for c in range(2):
                    last = pe.transpose(pt[:, c, 0:R], xs[:, c * 128:(c + 1) * 128], k["ident"][0:R, 0:R])
                last.then_inc(turned, 1)
                pe.wait_ge(xt_ready, t + 1)
                for layer in range(2):
                    lhs, w, nk = ((xt, w1, 2), (hT, w2, 8))[layer]
                    for o in range(2):
                        for c in range(nk):
                            last = pe.matmul(h_ps[:, o, :], lhs[:, c, :], w[:, c, o * 512:(o + 1) * 512],
                                             start=(c == 0), stop=(c == nk - 1))
                        last.then_inc(h_ready, 1)
                    pe.wait_ge(zn_ready, 2 * t + (layer + 1))
                    for c in range(8):
                        last = pe.transpose(t_ps[:, c, 0:R], zn[:, c * 128:(c + 1) * 128], k["ident"][0:R, 0:R])
                    last.then_inc(zt_ready, 1)
                    pe.wait_ge(hT_ready, 2 * t + (layer + 1))
                for c in range(8):
                    last = pe.matmul(y_ps[:, 0:D], hT[:, c, :], w3[:, c, :], start=(c == 0), stop=(c == 7))
                last.then_inc(y_ready, 1)

        @block.scalar
        def _(act):
            act.wait_ge(loaded, 160)
            with act.Fori(0, T) as t:
                act.wait_ge(turned, t + 1)
                act.activation(xt[:], pt[:, :, 0:R], ACT.Copy).then_inc(xt_ready, 1)
                for layer, (g, be) in enumerate(((g1, be1), (g2, be2))):
                    act.wait_ge(var_ready, 2 * t + (layer + 1))
                    act.activation(root[:], v1[:], ACT.Sqrt).then_inc(root_ready, 1)
                    act.wait_ge(inv_ready, 2 * t + (layer + 1))
                    act.activation(zn[:], z[:], ACT.Identity, bias=shift[:], scale=inv[:]).then_inc(zn_ready, 1)
                    act.wait_ge(zt_ready, 2 * t + (layer + 1))
                    for c in range(8):
                        act.activation(hT[:, c, :], t_ps[:, c, 0:R], ACT.Relu, bias=be[:, c:c + 1], scale=g[:, c:c + 1])
                    act.drain().then_inc(hT_ready, 1)

        @block.vector
        def _(dve):
            dve.wait_ge(loaded, 160)
            with dve.Fori(0, T) as t:
                dve.tensor_copy(xs[:].rearrange("p (a n) -> p a n", a=1), k["A"][:, bass.ds(t, 1), :]).then_inc(xs_ready, 1)
                for layer, bias in enumerate((b1, b2)):
                    for o in range(2):
                        dve.wait_ge(h_ready, 4 * t + (2 * layer + o + 1))
                        dve.tensor_tensor(z[:, o * 512:(o + 1) * 512], h_ps[:, o, :], bias[:, o * 512:(o + 1) * 512], ALU.add)
                        dve.drain()
                        dve.bn_stats(stats[:, o, :], z[:, o * 512:(o + 1) * 512])
                    dve.drain()
                    dve.bn_aggr(mv[:], stats[:].rearrange("p a n -> p (a n)"))
                    dve.drain()
                    dve.tensor_scalar(v1[:], mv[:, 1:2], LN_EPS, None, ALU.add).then_inc(var_ready, 1)
                    dve.wait_ge(root_ready, 2 * t + (layer + 1))
                    dve.reciprocal(inv[:], root[:])
                    dve.drain()
                    dve.scalar_tensor_tensor(shift[:], mv[:, 0:1], -1.0, inv[:], ALU.mult, ALU.mult)
                    dve.drain().then_inc(inv_ready, 1)
                dve.wait_ge(y_ready, t + 1)
                row = y_ps[:, 0:D].rearrange("p (a n) -> p a n", a=1)
                dve.tensor_tensor(k["B"][:, bass.ds(t, 1), :], row, b3[:], ALU.add)
                dve.drain()
                dve.tensor_tensor(k["B"][:, bass.ds(t, 1), :], k["B"][:, bass.ds(t, 1), :], k["xn"][:, bass.ds(t, 1), :], ALU.add)


def small_experts(nc, d, k, into):
    with Stage(nc, "ffn2") as s:
        sw1, sw2, sw3 = s.sb("sw1", [128, 2, 256]), s.sb("sw2", [128, 2, 128]), s.sb("sw3", [128, D])
        ew1, ew2, ew3 = s.sb("ew1", [128, 4, 2, 128]), s.sb("ew2", [128, 4, 64]), s.sb("ew3", [64, 4, D])
        sb1, sb2 = s.sb("sb1", [128, 2]), s.sb("sb2", [128, 1])
        eb1, eb2 = s.sb("eb1", [128, 4]), s.sb("eb2", [64, 4])
        h1 = s.sb("h1", [128, 2, 3 * R])
        h2 = s.sb("h2", [128, 3 * R])
        a_ps = [s.ps(f"a_ps{b}", [128, 512]) for b in range(2)]
        b_ps = s.ps("b_ps", [128, 512])
        o_ps = s.ps("o_ps", [R, 3, 512])
        loaded, one_ready, one_kept, two_ready, two_kept, h2_free, out_ready, out_free = map(
            s.sem, ("loaded", "one_ready", "one_kept", "two_ready", "two_kept", "h2_free", "out_ready", "out_free"))
        block = s.block()

        @block.sync
        def _(sp):
            for to, name in ((sw1, "s_w1"), (sw2, "s_w2"), (sw3, "s_w3"), (ew1, "e_w1"), (ew2, "e_w2"), (ew3, "e_w3"),
                             (sb1, "s_b1"), (sb2, "s_b2"), (eb1, "e_b1"), (eb2, "e_b2")):
                sp.dma_start(to[:], d[name]).then_inc(loaded, 16)
            sp.wait_ge(loaded, 160)

        @block.tensor
        def _(pe):
            pe.wait_ge(loaded, 160)

            def group(t, g, n, p):
                for net in range(5):
                    m = 5 * n + net
                    for o in range(2 if net == 0 else 1):
                        for i in range(2):
                            w = sw1[:, i, o * 128:(o + 1) * 128] if net == 0 else ew1[:, net - 1, i, :]
                            last = pe.matmul(a_ps[o][:, 0:g * R], w, k["xnT"][:, i, rows(t, g)], start=(i == 0), stop=(i == 1))
                    last.then_inc(one_ready, 1)
                    pe.wait_ge(one_kept, m + 1)
                    if net == 0:
                        for i in range(2):
                            last = pe.matmul(b_ps[:, 0:g * R], sw2[:, i, :], h1[:, i, 0:g * R], start=(i == 0), stop=(i == 1))
                    else:
                        last = pe.matmul(b_ps[0:64, 0:g * R], ew2[:, net - 1, :], h1[:, 0, 0:g * R], start=True, stop=True)
                    last.then_inc(two_ready, 1)
                    pe.wait_ge(two_kept, m + 1)
                    pe.wait_ge(out_free, m + 1)
                    for j in range(g):
                        if net == 0:
                            last = pe.matmul(o_ps[:, j, 0:D], h2[:, j * R:(j + 1) * R], sw3[:], start=True, stop=True)
                        else:
                            last = pe.matmul(o_ps[:, j, 0:D], h2[0:64, j * R:(j + 1) * R], ew3[:, net - 1, :], start=True, stop=True)
                    last.then_inc(out_ready, 1)
                    pe.drain().then_inc(h2_free, 1)

            groups(pe, group)

        @block.scalar
        def _(act):
            act.wait_ge(loaded, 160)
            act.sem_inc(h2_free, 1)

            def group(t, g, n, p):
                for net in range(5):
                    m = 5 * n + net
                    act.wait_ge(one_ready, m + 1)
                    for o in range(2 if net == 0 else 1):
                        act.activation(h1[:, o, 0:g * R], a_ps[o][:, 0:g * R], ACT.Relu,
                                       bias=sb1[:, o:o + 1] if net == 0 else eb1[:, net - 1:net])
                    act.drain().then_inc(one_kept, 1)
                    act.wait_ge(two_ready, m + 1)
                    act.wait_ge(h2_free, m + 1)
                    if net == 0:
                        act.activation(h2[:, 0:g * R], b_ps[:, 0:g * R], ACT.Relu, bias=sb2[:]).then_inc(two_kept, 1)
                    else:
                        act.activation(h2[0:64, 0:g * R], b_ps[0:64, 0:g * R], ACT.Relu,
                                       bias=eb2[:, net - 1:net]).then_inc(two_kept, 1)

            groups(act, group)

        @block.vector
        def _(dve):
            dve.sem_inc(out_free, 1)

            def group(t, g, n, p):
                for net in range(5):
                    dve.wait_ge(out_ready, 5 * n + net + 1)
                    for j in range(g):
                        to = into[:, bass.ds(t + j, 1), :].rearrange("p a n -> p (a n)")
                        if net == 0:
                            dve.tensor_tensor(to, o_ps[:, j, 0:D], to, ALU.add)
                        else:
                            dve.scalar_tensor_tensor(to, o_ps[:, j, 0:D], k["gates"][:, bass.ds((t + j) * 4 + (net - 1), 1)],
                                                     to, ALU.mult, ALU.add)
                    dve.drain().then_inc(out_free, 1)

            groups(dve, group)


def elu_mix(nc, d, k, name, wq, bq, wkv, bkv, wo, bo, greatest):
    mix_sums(nc, d, k, name + "s", 8, "elu", wkv, bkv, None, None)
    fold(nc, d, k, name + "f", wo)
    project(nc, d, k, name + "q", wq, D, k["A"], bq)
    A, B, x = k["A"], k["B"], k["x"]
    heads_of = [v[:].rearrange("p t (h n) -> p (t h) n", n=32) for v in (A, B)]

    def dve_steps(dve, ts, to_act, to_dve):
        norm, inv = ts
        dve.tensor_scalar(B[:], A[:], 0.0, None, ALU.min)
        dve.drain().then_inc(to_act, 1)
        dve.wait_ge(to_dve, 1)
        dve.scalar_tensor_tensor(A[:], A[:], 0.0, B[:], ALU.max, ALU.add)
        dve.drain()
        dve.tensor_tensor(B[:], A[:], k["ksum"][:].unsqueeze(1).broadcast_to((R, T, D)), ALU.mult)
        dve.drain()
        dve.tensor_reduce(norm[:], heads_of[1], AX, ALU.add)
        dve.drain()
        dve.tensor_scalar(norm[:], norm[:], 1e-6, None, ALU.max if greatest else ALU.add)
        dve.drain()
        dve.reciprocal(inv[:], norm[:])
        dve.drain()
        dve.tensor_tensor(heads_of[0], heads_of[0], inv[:].broadcast_to((R, T * 8, 32)), ALU.mult)

    def act_steps(act, ts, to_act, to_dve):
        act.wait_ge(to_act, 1)
        act.activation(B[:], B[:], ACT.Exp).then_inc(to_dve, 1)

    batch(nc, name + "e", [[R, T * 8, 1]] * 2, dve_steps, act_steps)

    def finish(dve, t, out, vec, tmp):
        dve.tensor_tensor(tmp[0][:], out, vec[0][:].unsqueeze(1), ALU.add)
        dve.drain()
        dve.tensor_tensor(x[:, bass.ds(t, 1), :], x[:, bass.ds(t, 1), :], tmp[0][:], ALU.add)

    linear_rows(nc, d, k, name + "o", A, k["fold"], 2, copy_in(A), finish, vectors=[(bo, D)], temps=[[R, 1, D]])


def add_affine(nc, d, k, name, source, gain, shift, relu):
    row_stats(nc, d, k, name + "s", source, "ln")
    x = k["x"]

    def fn(dve, t, vec, tmp):
        a, b = tmp
        dve.tensor_scalar(a[:], source[:, bass.ds(t, 1), :], col(k["scale"], t), col(k["shift"], t), ALU.mult, ALU.add)
        dve.drain()
        dve.tensor_tensor(b[:], a[:], vec[0][:].unsqueeze(1), ALU.mult)
        dve.drain()
        dve.tensor_tensor(a[:], b[:], vec[1][:].unsqueeze(1), ALU.add)
        dve.drain()
        to = x[:, bass.ds(t, 1), :]
        if relu:
            dve.scalar_tensor_tensor(to, a[:], 0.0, to, ALU.max, ALU.add)
        else:
            dve.tensor_tensor(to, to, a[:], ALU.add)

    elementwise(nc, d, k, name + "a", fn, vectors=[(gain, D), (shift, D)], temps=[[R, 1, D]] * 2)


def col(array, t):
    return array[:, bass.ds(t, 1), :].rearrange("p a n -> p (a n)")


def add_to_x(nc, d, k, name, relu):
    x, A = k["x"], k["A"]

    def dve_steps(dve, ts, to_act, to_dve):
        if relu:
            dve.scalar_tensor_tensor(x[:], A[:], 0.0, x[:], ALU.max, ALU.add)
        else:
            dve.tensor_tensor(x[:], x[:], A[:], ALU.add)

    batch(nc, name, [], dve_steps, lambda act, ts, to_act, to_dve: act.nop())


def layer0(nc, d, k):
    x, xn, A = k["x"], k["xn"], k["A"]
    row_stats(nc, d, k, "l0s", x, "ln")
    normalise(nc, d, k, "l0n", x, xn)
    first_places(nc, d, k)
    scatter_and_count(nc, d, k)
    collect_support(nc, d, k)

    def both(dve, t, xs, vec, tmp):
        dve.tensor_copy(xs[:, 0:D].unsqueeze(1), xn[:, bass.ds(t, 1), :])
        dve.tensor_copy(xs[:, D:2 * D].unsqueeze(1), A[:, bass.ds(t, 1), :])

    def relu_add(dve, t, out, vec, tmp):
        dve.tensor_tensor(tmp[0][:], out, vec[0][:].unsqueeze(1), ALU.add)
        dve.drain()
        to = x[:, bass.ds(t, 1), :]
        dve.scalar_tensor_tensor(to, tmp[0][:], 0.0, to, ALU.max, ALU.add)

    def add(dve, t, out, vec, tmp):
        dve.tensor_tensor(tmp[0][:], out, vec[0][:].unsqueeze(1), ALU.add)
        dve.drain()
        dve.tensor_tensor(x[:, bass.ds(t, 1), :], x[:, bass.ds(t, 1), :], tmp[0][:], ALU.add)

    linear_rows(nc, d, k, "l0g", None, d["g0_w"], 4, both, relu_add, vectors=[(d["g0_b"], D)], temps=[[R, 1, D]])
    mix_sums(nc, d, k, "l0m", 4, "ln", d["m0_wkv"], None, d["m0_gain"], d["m0_shift"])
    fold(nc, d, k, "l0f", d["m0_wo"], d["m0_wq"])
    linear_rows(nc, d, k, "l0o", xn, k["fold"], 2, copy_in(xn), add, vectors=[(d["m0_bo"], D)], temps=[[R, 1, D]])
    row_stats(nc, d, k, "l0t", x, "ln")
    normalise(nc, d, k, "l0u", x)
    gates = k["gates"][:, 0:T * 32].rearrange("p (t e) -> p t e", e=32)
    project(nc, d, k, "l0r", d["r0_w"], 32, gates, d["r0_b"])
    gate(nc, d, k, "l0h", 32, "first")
    seed(nc, d, k, "l0b", 32, d["f0_b2"], A)
    experts(nc, d, k, "l0e", 32, 64, 1, ACT.Relu, d["f0_w1"], d["f0_b1"], d["f0_w2"], A)
    add_to_x(nc, d, k, "l0z", True)


def layer1(nc, d, k):
    x, xn, A, B = k["x"], k["xn"], k["A"], k["B"]
    row_stats(nc, d, k, "l1s", x, "ln")
    normalise(nc, d, k, "l1n", x, xn)

    def dve_steps(dve, ts, to_act, to_dve):
        dve.tensor_scalar(k["deg1"][:], k["deg"][:], 1.0, None, ALU.add)
        dve.tensor_scalar(ts[0][:], k["deg"][:], 1.0, None, ALU.max)
        dve.drain().then_inc(to_act, 1)
        dve.reciprocal(k["rdeg"][:], ts[0][:])
        dve.wait_ge(to_dve, 1)
        dve.reciprocal(k["dinv"][:], ts[1][:])
        dve.drain()
        for t in range(T):
            dve.tensor_scalar(A[:, t, :], xn[:, t, :], k["dinv"][:, t:t + 1], None, ALU.mult)

    def act_steps(act, ts, to_act, to_dve):
        act.wait_ge(to_act, 1)
        act.activation(ts[1][:], k["deg1"][:], ACT.Sqrt).then_inc(to_dve, 1)

    batch(nc, "l1d", [[R, T]] * 2, dve_steps, act_steps)

    def scaled(dve, t, into, acc, temp):
        dve.tensor_tensor(temp, acc, A[:, bass.ds(t, 1), :], ALU.add)
        dve.drain()
        dve.tensor_scalar(into, temp, k["dinv"][:, bass.ds(t, 1)], None, ALU.mult)

    for i in range(3):
        def step(dve, t, out, vec, tmp, last=(i == 2)):
            dve.tensor_tensor(tmp[0][:], out, vec[0][:].unsqueeze(1), ALU.add)
            dve.drain()
            if last:
                dve.tensor_tensor(x[:, bass.ds(t, 1), :], x[:, bass.ds(t, 1), :], tmp[0][:], ALU.add)
            else:
                dve.tensor_scalar(A[:, bass.ds(t, 1), :], tmp[0][:], k["dinv"][:, bass.ds(t, 1)], None, ALU.mult)

        aggregate(nc, d, k, f"l1a{i}", A, B, scaled)
        linear_rows(nc, d, k, f"l1w{i}", B, d[f"g1_w{i}"], 2, copy_in(B), step, vectors=[(d[f"g1_b{i}"], D)],
                    temps=[[R, 1, D]])

    row_stats(nc, d, k, "l1m", xn, "norm")
    batch(nc, "l1c", [], lambda dve, ts, a, b: dve.tensor_scalar(k["scale"][:], k["scale"][:], float(D) ** 0.5, None, ALU.mult),
          lambda act, ts, a, b: act.nop())
    normalise(nc, d, k, "l1r", xn)
    softmax_keys(nc, d, k, "l1k")
    q = A[:].rearrange("p t n -> p (t n)")[:, 0:T * 128].rearrange("p (t n) -> p t n", n=128)
    heads = A[:].rearrange("p t n -> p (t n)")[:, 0:T * 128].rearrange("p (g n) -> p g n", n=32)
    project(nc, d, k, "l1q", k["w_qkv"][:, :, 0:128], 128, q)

    def q_dve(dve, ts, to_act, to_dve):
        most, total = ts
        dve.tensor_reduce(most[:], heads, AX, ALU.max)
        dve.drain()
        dve.tensor_tensor(heads, heads, most[:].broadcast_to((R, T * 4, 32)), ALU.subtract)
        dve.drain().then_inc(to_act, 1)
        dve.wait_ge(to_dve, 1)
        dve.tensor_reduce(most[:], heads, AX, ALU.add)
        dve.drain()
        dve.reciprocal(total[:], most[:])
        dve.drain()
        dve.tensor_tensor(heads, heads, total[:].broadcast_to((R, T * 4, 32)), ALU.mult)

    def q_act(act, ts, to_act, to_dve):
        act.wait_ge(to_act, 1)
        act.activation(q, q, ACT.Exp).then_inc(to_dve, 1)

    batch(nc, "l1x", [[R, T * 4, 1]] * 2, q_dve, q_act)

    def to_b(dve, t, out, vec, tmp):
        dve.tensor_tensor(B[:, bass.ds(t, 1), :], out, vec[0][:].unsqueeze(1), ALU.add)

    linear_rows(nc, d, k, "l1o", q, k["fold"], 1, copy_in(q), to_b, vectors=[(d["m1_b"], D)])
    row_stats(nc, d, k, "l1p", B, "norm")

    def rms_add(dve, t, vec, tmp):
        dve.tensor_scalar(tmp[0][:], B[:, bass.ds(t, 1), :], col(k["scale"], t), float(D) ** 0.5, ALU.mult, ALU.mult)
        dve.drain()
        dve.tensor_tensor(tmp[1][:], tmp[0][:], vec[0][:].unsqueeze(1), ALU.mult)
        dve.drain()
        dve.tensor_tensor(tmp[0][:], tmp[1][:], xn[:, bass.ds(t, 1), :], ALU.add)
        dve.drain()
        dve.tensor_tensor(x[:, bass.ds(t, 1), :], x[:, bass.ds(t, 1), :], tmp[0][:], ALU.add)

    elementwise(nc, d, k, "l1y", rms_add, vectors=[(d["m1_g"], D)], temps=[[R, 1, D]] * 2)

    row_stats(nc, d, k, "l1t", x, "ln")
    normalise(nc, d, k, "l1u", x, xn)
    project(nc, d, k, "l1v", d["f1_wr"], 1, k["gates"][:, 0:T].rearrange("p (t e) -> p t e", e=1), d["f1_br"])
    rank_gate(nc, d, k, "l1i", NODES // 2 - 1)
    seed(nc, d, k, "l1b", 2, d["f1_b2"], A, base=xn)
    experts(nc, d, k, "l1e", 2, 128, 4, ACT.Gelu_apprx_tanh, d["f1_w1"], d["f1_b1"], d["f1_w2"], A)
    add_to_x(nc, d, k, "l1z", False)


def layer2(nc, d, k):
    x, xn, A, B = k["x"], k["xn"], k["A"], k["B"]
    row_stats(nc, d, k, "l2s", x, "ln")
    normalise(nc, d, k, "l2n", x, xn)
    elu_mix(nc, d, k, "l2m", d["m2_wq"], d["m2_bq"], d["m2_wkv"], d["m2_bkv"], d["m2_wo"], d["m2_bo"], False)

    with Stage(nc, "eps") as s:
        raw, ready = s.sb("raw", [R, 1]), s.sem("ready")
        block = s.block()

        @block.sync
        def _(sp):
            sp.dma_start(raw[:], d["eps"]).then_inc(ready, 16)

        @block.vector
        def _(dve):
            dve.wait_ge(ready, 16)
            dve.tensor_scalar(k["eps2"][:], raw[:], 2.0, None, ALU.add)

    def with_self(dve, t, into, acc, temp):
        dve.scalar_tensor_tensor(into, xn[:, bass.ds(t, 1), :], k["eps2"][:], acc, ALU.mult, ALU.add)

    aggregate(nc, d, k, "l2a", xn, A, with_self)
    edge_hidden(nc, d, k)

    def self_hidden(dve, t, xs, vec, tmp):
        dve.scalar_tensor_tensor(xs[:].unsqueeze(1), vec[0][:].unsqueeze(1), 0.0, B[:, bass.ds(t, 1), :], ALU.max, ALU.add)

    def add_messages(dve, t, out, vec, tmp):
        dve.tensor_tensor(tmp[0][:], out, A[:, bass.ds(t, 1), :], ALU.add)
        dve.drain()
        dve.scalar_tensor_tensor(A[:, bass.ds(t, 1), :], vec[1][:].unsqueeze(1), k["deg1"][:, bass.ds(t, 1)], tmp[0][:],
                                 ALU.mult, ALU.add)

    linear_rows(nc, d, k, "l2h", B, d["ee_w2"], 2, self_hidden, add_messages,
                vectors=[(d["ee_b1"], D), (d["ee_b2"], D)], temps=[[R, 1, D]])
    mlp_ln(nc, d, k)
    add_affine(nc, d, k, "l2b", B, d["bn_g"], d["bn_b"], True)

    row_stats(nc, d, k, "l2t", x, "ln")
    normalise(nc, d, k, "l2u", x)
    gates = k["gates"][:, 0:T * 4].rearrange("p (t e) -> p t e", e=4)
    project(nc, d, k, "l2v", d["gW"], 4, gates, d["gb"])
    gate(nc, d, k, "l2i", 4, "soft_two")
    seed(nc, d, k, "l2c", 4, d["eb3"], A, base_row=d["sb3"])
    small_experts(nc, d, k, A)
    add_to_x(nc, d, k, "l2z", False)


def layer3(nc, d, k):
    x, xn, A, B = k["x"], k["xn"], k["A"], k["B"]
    row_stats(nc, d, k, "l3s", x, "ln")
    normalise(nc, d, k, "l3n", x, xn)
    elu_mix(nc, d, k, "l3m", d["m3_wq"], None, d["m3_wkv"], None, d["m3_wo"], d["m3_bo"], True)

    def mean(dve, t, into, acc, temp):
        dve.tensor_scalar(into, acc, k["rdeg"][:, bass.ds(t, 1)], None, ALU.mult)

    aggregate(nc, d, k, "l3a", xn, A, mean)

    def both(dve, t, xs, vec, tmp):
        dve.tensor_copy(xs[:, 0:D].unsqueeze(1), A[:, bass.ds(t, 1), :])
        dve.tensor_copy(xs[:, D:2 * D].unsqueeze(1), xn[:, bass.ds(t, 1), :])

    def to_b(dve, t, out, vec, tmp):
        dve.tensor_tensor(B[:, bass.ds(t, 1), :], out, vec[0][:].unsqueeze(1), ALU.add)

    linear_rows(nc, d, k, "l3g", None, d["g3_w"], 4, both, to_b, vectors=[(d["g3_b"], D)])
    row_stats(nc, d, k, "l3p", B, "norm")

    def unit(dve, t, vec, tmp):
        dve.tensor_scalar(tmp[0][:], B[:, bass.ds(t, 1), :], col(k["scale"], t), 0.0, ALU.mult, ALU.max)
        dve.drain()
        dve.tensor_tensor(B[:, bass.ds(t, 1), :], tmp[0][:], xn[:, bass.ds(t, 1), :], ALU.add)

    elementwise(nc, d, k, "l3u", unit, temps=[[R, 1, D]])
    add_affine(nc, d, k, "l3b", B, d["g3_gamma"], d["g3_beta"], False)

    row_stats(nc, d, k, "l3t", x, "ln")
    normalise(nc, d, k, "l3w", x, xn)
    gates = k["gates"][:, 0:T * 16].rearrange("p (t e) -> p t e", e=16)
    project(nc, d, k, "l3v", d["f3_gw"], 16, gates, d["f3_gb"])
    gate(nc, d, k, "l3i", 16, "two")
    seed(nc, d, k, "l3c", 16, d["f3_b2"], A, base=xn)
    experts(nc, d, k, "l3e", 16, 128, 4, ACT.Relu, d["f3_w1"], d["f3_b1"], d["f3_w2"], A)
    add_affine(nc, d, k, "l3y", A, d["f3_gamma"], d["f3_beta"], False)


def program(nc, d, out, layers=4):
    with Stage(nc, "all") as s:
        k = {n: s.sb(n, [R, T, D]) for n in ("x", "xn", "A", "B")}
        k["nc"] = nc
        k["xnT"] = s.sb("xnT", [128, 2, NODES])
        k["ident"] = s.sb("ident", [128, 128])
        for n in ("dst", "src_base", "src_place", "weight"):
            k[n] = s.sb(n, [CH, NCH])
        for n in ("deg", "deg1", "dinv", "rdeg"):
            k[n] = s.sb(n, [R, T])
        k["scale"], k["shift"] = s.sb("scale", [R, T, 1]), s.sb("shift", [R, T, 1])
        k["tile_start"] = s.sb("tile_start", [128, T])
        k["eps2"] = s.sb("eps2", [R, 1])
        k["kvT"], k["fold"], k["ksum"] = s.sb("kvT", [128, 2, 128]), s.sb("fold", [128, 2, D]), s.sb("ksum", [R, D])
        k["w_qkv"] = s.sb("w_qkv", [128, 2, 384])
        k["gates"] = s.sb("gates", [R, T * 32])
        k["scatter_to"] = s.sb("scatter_to", [CH, NCH], I32)
        k["support_dram"] = [nc.dram_tensor(f"support{b}", (NODES + CH, D), F32, kind="Internal").ap() for b in range(2)]
        k["ct_dram"] = nc.dram_tensor("counts", (T, R, NODES), F32, kind="Internal").ap()
        k["plan_dram"] = nc.dram_tensor("plan", (1, 3, T), I32, kind="Internal").ap()
        k["ends_dram"] = nc.dram_tensor("ends", (2 * T, 1), F32, kind="Internal").ap()
        k["line_dram"] = nc.dram_tensor("line", (NODES,), F32, kind="Internal").ap()

        with Stage(nc, "load") as st:
            loaded = st.sem("loaded")
            block = st.block()

            @block.sync
            def _(sp):
                sp.dma_start(k["x"][:], d["x"].rearrange("(t p) n -> p t n", p=R)).then_inc(loaded, 16)
                sp.dma_start(k["tile_start"][:], d["tile_start"]).then_inc(loaded, 16)
                sp.wait_ge(loaded, 32)

        plan_edges(nc, d, k)
        for layer in (layer0, layer1, layer2, layer3)[:layers]:
            layer(nc, d, k)

        with Stage(nc, "store") as st:
            stored = st.sem("stored")
            block = st.block()

            @block.sync
            def _(sp):
                sp.dma_start(out.rearrange("(t p) n -> p t n", p=R), k["x"][:]).then_inc(stored, 16)
                sp.wait_ge(stored, 16)



def lay_out(i):
    def row(v, n=R):
        return np.repeat(np.asarray(v).reshape(1, -1), n, axis=0)

    def chunks(w):
        w = np.asarray(w)
        return w.reshape(-1, 128, w.shape[1]).transpose(1, 0, 2)

    def columns(v, p=128):
        return np.asarray(v).reshape(-1, p).T

    def edges(v, fill):
        v = np.asarray(v)
        return np.concatenate([v, np.full(NCH * CH - EDGES, fill, v.dtype)]).reshape(NCH, CH).T

    def join(*a, axis=1):
        return np.concatenate([np.asarray(v) for v in a], axis=axis)

    E0, E3 = i["L0_ffn_W1"].shape[0], i["L3_ffn_w1"].shape[0]
    attr = np.concatenate([np.asarray(i["edge_attr_64"]), np.zeros((NCH * CH - EDGES, EDIM), np.float32)])
    kg, kb, vg, vb = (np.tile(np.asarray(i["L0_mix_ln_" + n]), 4) for n in ("k_g", "k_b", "v_g", "v_b"))
    mem = np.asarray(i["L1_mix_mem_kv"])
    w3kv = np.asarray(i["L3_mix_Wkv"])
    blocks = np.arange(128)
    d = {
        "x": i["x"], "src": edges(i["src"], 0), "src_row": np.ascontiguousarray(edges(i["src"], 0).T).reshape(1, -1),
        "own_row": (NODES + np.arange(CH, dtype=np.float32)).reshape(CH, 1),
        "before": (np.arange(CH) < np.arange(CH)[:, None]).astype(np.float32), "dst": edges(i["dst"], -1), "weight": edges(i["edge_weight"], 0),
        "attr": np.concatenate([attr.T, np.ones((1, NCH * CH), np.float32)]),
        "pair_up": row(np.arange(NCH) // 2 + 1, CH).astype(np.float32),
        "pair_down": row(PAIRS - np.arange(NCH) // 2, CH).astype(np.float32),
        "ident": np.eye(128, dtype=np.float32),
        "iota16": row(np.arange(NODES), CH).astype(np.int16), "iota_r": row(np.arange(R), CH).astype(np.float32),
        "tile_start": row(np.arange(T) * R, 128).astype(np.float32),
        "mask64": (blocks[:, None] // 64 == blocks // 64).astype(np.float32),
        "mask32": (blocks[:, None] // 32 == blocks // 32).astype(np.float32),
        "below": (np.arange(R) < np.arange(R)[:, None]).astype(np.float32),
        "down": row(32 - np.arange(32)).astype(np.float32),
        "zero_row": np.zeros((R, 2 * D), np.float32),
        "g0_w": chunks(i["L0_gnn_W"]), "g0_b": row(i["L0_gnn_b"]),
        "m0_wkv": chunks(join(np.asarray(i["L0_mix_wk"]).T, np.asarray(i["L0_mix_wv"]).T)),
        "m0_gain": row(np.concatenate([kg, vg])), "m0_shift": row(np.concatenate([kb, vb])),
        "m0_wo": chunks(np.asarray(i["L0_mix_wo"]).T), "m0_wq": chunks(i["L0_mix_wq"]), "m0_bo": row(i["L0_mix_bo"]),
        "r0_w": chunks(np.asarray(i["L0_ffn_router_w"]).T), "r0_b": row(i["L0_ffn_router_b"]),
        "f0_w1": np.asarray(i["L0_ffn_W1"]).reshape(E0, 2, 128, 64).transpose(0, 2, 1, 3),
        "f0_b1": np.asarray(i["L0_ffn_b1"]).T, "f0_w2": np.asarray(i["L0_ffn_W2"]).reshape(E0, 64, 1, D),
        "f0_b2": i["L0_ffn_b2"],
        "w_qkv": chunks(i["L1_mix_w_qkv"]), "g_pre": columns(i["L1_mix_g_pre"]), "w_out": i["L1_mix_w_out"],
        "mem_k": mem[0].reshape(128, 4), "mem_v": mem[1].reshape(128, 4).T,
        "m1_b": row(i["L1_mix_b_out"]), "m1_g": row(i["L1_mix_g_out"]),
        "f1_wr": chunks(i["L1_ffn_wr"]), "f1_br": row(i["L1_ffn_br"]),
        "f1_w1": np.asarray(i["L1_ffn_w1"]).reshape(2, 128, 2, 512).transpose(2, 1, 0, 3),
        "f1_b1": columns(i["L1_ffn_b1"]),
        "f1_w2": np.asarray(i["L1_ffn_w2"]).reshape(2, 4, 128, D).transpose(0, 2, 1, 3),
        "f1_b2": np.stack([np.asarray(i["L1_ffn_b2"]), np.zeros(D, np.float32)]),
        "m2_wq": chunks(i["L2_mix_wq"]), "m2_bq": row(i["L2_mix_bq"]),
        "m2_wkv": chunks(join(i["L2_mix_wk"], i["L2_mix_wv"])),
        "m2_bkv": row(join(i["L2_mix_bk"], i["L2_mix_bv"], axis=0)),
        "m2_wo": chunks(i["L2_mix_wo"]), "m2_bo": row(i["L2_mix_bo"]),
        "eps": row(i["L2_gnn_eps"]),
        "ee_w1": join(i["L2_gnn_ee_w1"], np.asarray(i["L2_gnn_ee_b1"]).reshape(1, -1), axis=0),
        "ee_b1": row(i["L2_gnn_ee_b1"]), "ee_w2": chunks(i["L2_gnn_ee_w2"]), "ee_b2": row(i["L2_gnn_ee_b2"]),
        "m_w1": chunks(i["L2_gnn_w1"]), "m_w2": chunks(i["L2_gnn_w2"]), "m_w3": chunks(i["L2_gnn_w3"]),
        "m_b1": row(i["L2_gnn_b1"]), "m_b2": row(i["L2_gnn_b2"]), "m_b3": row(i["L2_gnn_b3"]),
        "m_g1": columns(i["L2_gnn_g1"]), "m_be1": columns(i["L2_gnn_be1"]),
        "m_g2": columns(i["L2_gnn_g2"]), "m_be2": columns(i["L2_gnn_be2"]),
        "bn_g": row(i["L2_gnn_bn_g"]), "bn_b": row(i["L2_gnn_bn_b"]),
        "gW": chunks(i["L2_ffn_gW"]), "gb": row(i["L2_ffn_gb"]), "eb3": i["L2_ffn_eb3"], "sb3": row(i["L2_ffn_sb3"]),
        "s_w1": chunks(i["L2_ffn_sW1"]), "s_w2": chunks(i["L2_ffn_sW2"]), "s_w3": i["L2_ffn_sW3"],
        "e_w1": np.asarray(i["L2_ffn_eW1"]).reshape(4, 2, 128, 128).transpose(2, 0, 1, 3),
        "e_w2": np.asarray(i["L2_ffn_eW2"]).transpose(1, 0, 2), "e_w3": np.asarray(i["L2_ffn_eW3"]).transpose(1, 0, 2),
        "s_b1": columns(i["L2_ffn_sb1"]), "s_b2": columns(i["L2_ffn_sb2"]),
        "e_b1": np.asarray(i["L2_ffn_eb1"]).T, "e_b2": np.asarray(i["L2_ffn_eb2"]).T,
        "m3_wq": chunks(np.asarray(i["L3_mix_Wq"]).T), "m3_wkv": chunks(w3kv.T),
        "m3_wo": chunks(np.asarray(i["L3_mix_Wproj"]).T), "m3_bo": row(i["L3_mix_bproj"]),
        "g3_w": chunks(join(np.asarray(i["L3_gnn_W_l"]).T, np.asarray(i["L3_gnn_W_r"]).T, axis=0)),
        "g3_b": row(i["L3_gnn_b_l"]), "g3_gamma": row(i["L3_gnn_gamma"]), "g3_beta": row(i["L3_gnn_beta"]),
        "f3_gw": chunks(i["L3_ffn_gate_w"]), "f3_gb": row(i["L3_ffn_gate_b"]),
        "f3_w1": np.asarray(i["L3_ffn_w1"]).reshape(E3, 2, 128, 512).transpose(0, 2, 1, 3),
        "f3_b1": columns(np.asarray(i["L3_ffn_b1"]).reshape(-1)),
        "f3_w2": np.asarray(i["L3_ffn_w2"]).reshape(E3, 4, 128, D).transpose(0, 2, 1, 3),
        "f3_b2": i["L3_ffn_b2"], "f3_gamma": row(i["L3_ffn_gamma"]), "f3_beta": row(i["L3_ffn_beta"]),
    }
    for n in range(3):
        d[f"g1_w{n}"], d[f"g1_b{n}"] = chunks(i[f"L1_gnn_W{n + 1}"]), row(i[f"L1_gnn_b{n + 1}"])
    return {n: np.ascontiguousarray(v) for n, v in d.items()}


def kernel(**inputs):
    import concourse.bacc as bacc
    from concourse.bass_utils import run_bass_kernel_spmd as run

    nc = bacc.Bacc("TRN2", target_bir_lowering=False, num_devices=1)
    arrays, d = {}, {}
    for name, a in lay_out(inputs).items():
        arrays[f"in_{name}"] = a
        d[name] = nc.dram_tensor(f"in_{name}", a.shape, mybir.dt.from_np(a.dtype), kind="ExternalInput").ap()
    out = nc.dram_tensor("out_rows", (NODES, D), F32, kind="ExternalOutput").ap()
    program(nc, d, out, LAYERS)
    return run(nc, [arrays], core_ids=[0]).results[0]["out_rows"]


LAYERS = 4
```

```python
from contextlib import ExitStack

import numpy as np

import concourse.bass as bass
from concourse import mybir

F32, BF16, I32, I16 = mybir.dt.float32, mybir.dt.bfloat16, mybir.dt.int32, mybir.dt.int16
ALU = mybir.AluOpType
ACT = mybir.ActivationFunctionType
AX = mybir.AxisListType.X

NODES, D = 3125, 256
T, R = 25, 125
EDGES, CH = 50000, 128
PAIRS = -(-EDGES // (2 * CH))
NCH = 2 * PAIRS
WIDE = -(-NODES // 8) * 8
EDIM = 64
LN_EPS = 1e-5
BLOCKS = max(NODES // 128 + 32, 2 * NODES // 128 + 16) + 1
CTB = 7
CENTRED = [(g * 500, min(500, NODES - g * 500)) for g in range(CTB)]


class Stage:

    def __init__(self, nc, name):
        self.nc, self.name, self.stack, self.sems = nc, name, ExitStack(), []

    def __enter__(self):
        self.stack.__enter__()
        return self

    def __exit__(self, *e):
        self.stack.__exit__(*e)
        if self.sems and e[0] is None:
            self.nc.clear_and_free_semaphores(self.sems)
            self.nc.all_engine_barrier(sem_only=True)

    def sb(self, name, shape, dt=F32):
        return self.stack.enter_context(self.nc.sbuf_tensor(f"{self.name}_{name}", shape, dt))

    def ps(self, name, shape, dt=F32):
        return self.stack.enter_context(self.nc.psum_tensor(f"{self.name}_{name}", shape, dt))

    def sem(self, name):
        self.sems.append(self.nc.alloc_semaphore(f"{self.name}_{name}"))
        return self.sems[-1]

    def block(self):
        return self.stack.enter_context(self.nc.Block())


def tiles(eng, body):
    with eng.Fori(0, T // 2) as i:
        body(2 * i, 0)
        body(2 * i + 1, 1)
    body(T - 1, 0)


def pipelined(first, second):
    def emit(eng):
        first(0, 0)
        with eng.Fori(0, T // 2) as i:
            first(2 * i + 1, 1)
            second(2 * i, 0)
            first(2 * i + 2, 0)
            second(2 * i + 1, 1)
        second(T - 1, 0)
    return emit


def ahead(first, second, first_leads):
    def emit(eng):
        def both(t, b):
            for step, tile in ((first, t + 2), (second, t)) if first_leads else ((second, t), (first, t + 2)):
                step(tile, b)

        first(0, 0)
        first(1, 1)
        with eng.Fori(0, (T - 3) // 2) as i:
            both(2 * i, 0)
            both(2 * i + 1, 1)
        both(T - 3, 0)
        second(T - 2, 1)
        second(T - 1, 0)
    return emit


def groups(eng, body):
    with eng.Fori(0, 5) as i:
        body(5 * i, 3, 2 * i, 0)
        body(5 * i + 3, 2, 2 * i + 1, 1)


def settle(eng, started):
    eng.sem_inc(started, 1)


def rows(t, n=1):
    return bass.ds(t * R, n * R)



def plan_edges(nc, d, k):
    with Stage(nc, "plan") as s:
        dst_i, src_i = s.sb("dst_i", [CH, NCH], I32), s.sb("src_i", [CH, NCH], I32)
        pair_up, pair_down = s.sb("pair_up", [CH, NCH]), s.sb("pair_down", [CH, NCH])
        rel, over, inside = (s.sb(n, [CH, NCH]) for n in ("rel", "over", "inside"))
        ends = s.sb("ends", [CH, 2 * T])
        most, spare = s.sb("most", [2 * T, 1]), s.sb("spare", [2 * T, 1])
        line = s.sb("line", [1, 2, T])
        plan = s.sb("plan", [1, 3, T])
        ones = s.sb("ones", [1, T])
        cum = s.sb("cum", [1, T])
        plan_i = s.sb("plan_i", [1, 3, T], I32)
        ends_t = s.ps("ends_t", [CH, CH])
        zero_rows, zeroed, cleared = s.sb("zero_rows", [CH, D]), s.sem("zeroed"), s.sem("cleared")
        loaded, ends_ready, turned, most_ready, stored, back = map(
            s.sem, ("loaded", "ends_ready", "turned", "most_ready", "stored", "back"))
        planned = s.sem("planned")
        block = s.block()

        @block.sync
        def _(sp):
            sp.dma_start(dst_i[:], d["dst"]).then_inc(loaded, 16)
            sp.dma_start(src_i[:], d["src"]).then_inc(loaded, 16)
            sp.dma_start(pair_up[:], d["pair_up"]).then_inc(loaded, 16)
            sp.dma_start(pair_down[:], d["pair_down"]).then_inc(loaded, 16)
            sp.dma_start(k["weight"][:], d["weight"]).then_inc(loaded, 16)
            sp.dma_start(k["ident"][:], d["ident"]).then_inc(loaded, 16)
            sp.wait_ge(most_ready, 1)
            sp.dma_start(k["ends_dram"], most[:]).then_inc(stored, 16)
            sp.wait_ge(stored, 16)
            sp.dma_start(line[:], k["ends_dram"].rearrange("(a b t) o -> a b (t o)", a=1, b=2)).then_inc(back, 16)
            sp.wait_ge(planned, 1)
            sp.dma_start(k["plan_dram"], plan_i[:]).then_inc(stored, 16)
            sp.wait_ge(stored, 32)

        @block.scalar
        def _(act):
            act.wait_ge(cleared, 1)
            act.dma_start(k["sorted_dram"].rearrange("(a p) n -> p a n", p=128),
                          zero_rows[:].unsqueeze(1).broadcast_to((128, BLOCKS + 1, D))).then_inc(zeroed, 16)
            act.dma_start(k["result_dram"].rearrange("(a p) n -> p a n", p=128),
                          zero_rows[:].unsqueeze(1).broadcast_to((128, BLOCKS, D))).then_inc(zeroed, 16)
            act.wait_ge(zeroed, 32)

        @block.vector
        def _(dve):
            dve.memset(zero_rows[:], 0.0).then_inc(cleared, 1)
            dve.wait_ge(loaded, 96)
            dve.tensor_copy(k["dst"][:], dst_i[:])
            dve.tensor_copy(over[:], src_i[:])
            dve.memset(ones[:], 1.0)
            dve.drain()
            dve.tensor_scalar(k["src_base"][:], over[:], float(R), float(R), ALU.is_ge, ALU.mult)
            dve.drain()
            for t in range(2, T):
                dve.tensor_scalar(inside[:], over[:], float(t * R), float(R), ALU.is_ge, ALU.mult)
                dve.drain()
                dve.tensor_tensor(k["src_base"][:], k["src_base"][:], inside[:], ALU.add)
                dve.drain()
            dve.tensor_tensor(k["src_place"][:], over[:], k["src_base"][:], ALU.subtract)
            dve.drain()
            for t in range(T):
                dve.tensor_scalar(over[:], k["dst"][:], float(t * R), None, ALU.is_ge)
                dve.tensor_scalar(rel[:], k["dst"][:], float((t + 1) * R), None, ALU.is_lt)
                dve.drain()
                dve.tensor_tensor(inside[:], over[:], rel[:], ALU.mult)
                dve.drain()
                dve.tensor_tensor(over[:], inside[:], pair_up[:], ALU.mult)
                dve.tensor_tensor(rel[:], inside[:], pair_down[:], ALU.mult)
                dve.drain()
                dve.tensor_reduce(ends[:, t:t + 1], over[:], AX, ALU.max)
                dve.tensor_reduce(ends[:, T + t:T + t + 1], rel[:], AX, ALU.max)
                dve.drain()
            dve.drain().then_inc(ends_ready, 1)
            dve.wait_ge(turned, 1)
            dve.tensor_reduce(most[:], ends_t[0:2 * T, :], AX, ALU.max).then_inc(most_ready, 1)
            dve.wait_ge(back, 16)
            dve.tensor_scalar(plan[:, 0, :], line[:, 1, :], -1.0, float(PAIRS), ALU.mult, ALU.add)
            dve.drain()
            dve.tensor_tensor(plan[:, 1, :], line[:, 0, :], plan[:, 0, :], ALU.subtract)
            dve.tensor_scalar(plan[:, 0, :], plan[:, 0, :], float(PAIRS - 1), None, ALU.min)
            dve.drain()
            dve.tensor_scalar(plan[:, 1, :], plan[:, 1, :], 1.0, None, ALU.max)
            dve.drain()
            dve.tensor_tensor_scan(cum[:], ones[:], plan[:, 1, :], 0.0, ALU.mult, ALU.add)
            dve.drain()
            dve.tensor_tensor(plan[:, 2, :], cum[:], plan[:, 1, :], ALU.subtract)
            dve.drain()
            dve.tensor_copy(plan_i[:], plan[:]).then_inc(planned, 1)

        @block.tensor
        def _(pe):
            pe.wait_ge(ends_ready, 1)
            pe.transpose(ends_t[0:2 * T, :], ends[:], k["ident"][:]).then_inc(turned, 1)


def walk(eng, k, plan, body_tile_start, body_pair, body_tile_end):
    with eng.Fori(0, T) as t:
        first = eng.value_load(plan[0:1, 0, bass.ds(t, 1)], min_val=0, max_val=PAIRS - 1)
        count = eng.value_load(plan[0:1, 1, bass.ds(t, 1)], min_val=1, max_val=PAIRS)
        before = eng.value_load(plan[0:1, 2, bass.ds(t, 1)], min_val=0, max_val=T * PAIRS)
        body_tile_start(t)
        with eng.Fori(0, count) as j:
            pair = k["nc"].s_assert_within(first + j, 0, PAIRS - 1, skip_runtime_bounds_check_because="the plan keeps first + count at most PAIRS")
            body_pair(t, pair, before + j)
        body_tile_end(t)


def first_places(nc, d, k):
    with Stage(nc, "first") as s:
        LOT = 14
        row = [s.sb(f"row{b}", [CH, LOT * CH], I32) for b in range(2)]
        rowf = s.sb("rowf", [CH, LOT * CH])
        src_i = s.sb("src_i", [CH, NCH], I32)
        src, moved = s.sb("src", [CH, NCH]), s.sb("moved", [CH, NCH])
        own, before = s.sb("own", [CH, 1]), s.sb("before", [CH, CH])
        same = s.sb("same", [CH, LOT, CH])
        count = s.sb("count", [CH, NCH])
        loaded, row0, row1, row_free = map(s.sem, ("loaded", "row0", "row1", "row_free"))
        block = s.block()

        @block.sync
        def _(sp):
            sp.dma_start(src_i[:], d["src"]).then_inc(loaded, 16)
            sp.dma_start(own[:], d["own_row"]).then_inc(loaded, 16)
            sp.dma_start(before[:], d["before"]).then_inc(loaded, 16)
            with sp.Fori(0, NCH // (2 * LOT)) as i:
                for b in range(2):
                    sp.wait_ge(row_free, 2 * i + (b + 1))
                    sp.dma_start(row[b][:], d["src_row"][:, bass.ds((2 * i + b) * LOT * CH, LOT * CH)].broadcast_to((CH, LOT * CH))
                                 ).then_inc(row0 if b == 0 else row1, 16)
            sp.wait_ge(loaded, 48)

        @block.vector
        def _(dve):
            dve.sem_inc(row_free, 2)
            dve.wait_ge(loaded, 48)
            dve.tensor_copy(src[:], src_i[:])
            dve.drain()
            with dve.Fori(0, NCH // (2 * LOT)) as i:
                for b in range(2):
                    dve.wait_ge(row0 if b == 0 else row1, 16 * i + 16)
                    dve.tensor_copy(rowf[:], row[b][:])
                    dve.drain().then_inc(row_free, 1)
                    for h in range(LOT):
                        dve.scalar_tensor_tensor(same[:, h, :], rowf[:, h * CH:(h + 1) * CH],
                                                 src[:, bass.ds(2 * LOT * i + (b * LOT + h), 1)], before[:],
                                                 ALU.is_equal, ALU.mult)
                    dve.drain()
                    dve.tensor_reduce(count[:, bass.ds(2 * LOT * i + b * LOT, LOT)], same[:], AX, ALU.max)
                    dve.drain()
            dve.drain()
            dve.tensor_scalar(moved[:], src[:], own[:], -1.0, ALU.subtract, ALU.mult)
            dve.drain()
            dve.tensor_tensor(moved[:], moved[:], count[:], ALU.mult)
            dve.drain()
            dve.tensor_tensor(src[:], src[:], moved[:], ALU.add)
            dve.drain()
            dve.tensor_copy(k["scatter_to"][:], src[:])


def scatter_and_count(nc, d, k):
    with Stage(nc, "edge") as s:
        plan = s.sb("plan", [1, 3, T], I32)
        iota = s.sb("iota", [CH, WIDE], I16)
        iota_r = s.sb("iota_r", [CH, R])
        rel, spare = s.sb("rel", [CH, NCH]), s.sb("spare", [CH, NCH])
        key, valid = s.sb("key", [CH, NCH]), s.sb("valid", [CH, NCH])
        src = s.sb("src", [CH, NCH])
        row_now = [s.sb(f"row_now{b}", [CH, 1], I32) for b in range(2)]
        src_row = s.sb("src_row", [CH, 2 * CH], I32)
        src_rowf = s.sb("src_rowf", [CH, 2 * CH])
        onehot = [s.sb(f"onehot{b}", [CH, WIDE], BF16) for b in range(2)]
        place = [s.sb(f"place{b}", [CH, R], BF16) for b in range(2)]
        to_dst = [s.sb(f"to_dst{b}", [CH, R]) for b in range(2)]
        same = [s.sb(f"same{b}", [CH, CH]) for b in range(2)]
        P = [s.sb(f"P{b}", [R, CH]) for b in range(2)]
        S = [s.sb(f"S{b}", [CH, D]) for b in range(2)]
        zeros = s.sb("zeros", [CH, 512], BF16)
        zero_rows = s.sb("zero_rows", [CH, D])
        ones = s.sb("ones", [CH, 1])
        counts = s.sb("counts", [R, NODES])
        ct_ps = s.ps("ct_ps", [R, CTB, 512])
        deg_ps = ct_ps[:, CTB - 1, 500:501]
        ps = s.ps("ps", [CH, 512])
        P_ps = [ps[0:R, b * CH:(b + 1) * CH] for b in range(2)]
        S_ps = ps[:, 256:512]
        loaded, setup, row_in, row_free, onehot_ready, used, P_ready, P_kept, S_ready, S_kept = map(
            s.sem, ("loaded", "setup", "row_in", "row_free", "onehot_ready", "used", "P_ready", "P_kept", "S_ready",
                    "S_kept"))
        started, row_copied = s.sem("started"), s.sem("row_copied")
        scattered = [s.sem(f"scattered{b}") for b in range(2)]
        tile_done, evac_dve, evac_act, stored, gone = map(
            s.sem, ("tile_done", "evac_dve", "evac_act", "stored", "gone"))
        block = s.block()

        def nothing(t):
            pass

        @block.sync
        def _(sp):
            sp.dma_start(plan[:], k["plan_dram"]).then_inc(loaded, 16)
            sp.dma_start(iota[:], d["iota16"]).then_inc(loaded, 16)
            sp.dma_start(iota_r[:], d["iota_r"]).then_inc(loaded, 16)
            sp.wait_ge(loaded, 48)
            sp.wait_ge(setup, 1)

            def pair(t, c, n):
                sp.wait_ge(row_free, n + 1)
                sp.dma_start(src_row[:], d["src_row"][:, bass.ds(c * 2 * CH, 2 * CH)].broadcast_to((CH, 2 * CH))
                             ).then_inc(row_in, 16)

            walk(sp, k, plan, nothing, pair, nothing)

        @block.gpsimd
        def _(pool):
            pool.wait_ge(loaded, 48)
            pool.wait_ge(setup, 1)
            for b in range(2):
                pool.dma_start(k["support_dram"][b][0:25 * CH].rearrange("(a p) n -> p a n", p=CH),
                               zero_rows[:].unsqueeze(1).broadcast_to((CH, 25, D))).then_inc(gone, 16)
            pool.wait_ge(gone, 32)
            for b in range(2):
                pool.dma_start(k["support_dram"][b][25 * CH:25 * CH + 53], zero_rows[0:53, :]).then_inc(scattered[b], 16)

            def pair(t, c, n):
                for b in range(2):
                    pool.wait_ge(scattered[b], 16 * n + 16)
                    pool.tensor_copy(row_now[b][:], k["scatter_to"][:, bass.ds(2 * c + b, 1)]).then_inc(row_copied, 1)
                    pool.wait_ge(row_copied, 2 * n + (b + 1))
                    pool.wait_ge(S_kept, 2 * n + (b + 2))
                    settle(pool, started)
                    pool.indirect_dma_start(k["support_dram"][b], bass.IndirectOffsetOnAxis(ap=row_now[b][:, 0:1], axis=0),
                                            S[b][:], None, compute_op=ALU.add).then_inc(scattered[b], 16)

            walk(pool, k, plan, nothing, pair, nothing)
            last = pool.value_load(plan[0:1, 1, T - 1:T], min_val=1, max_val=PAIRS)
            base = pool.value_load(plan[0:1, 2, T - 1:T], min_val=0, max_val=T * PAIRS)
            for b in range(2):
                pool.wait_ge(scattered[b], 16 * (base + last) + 16)

        @block.scalar
        def _(act):
            act.wait_ge(loaded, 48)

            def pair(t, c, n):
                for b in range(2):
                    act.wait_ge(P_ready, 2 * n + (b + 1))
                    act.activation(P[b][:], P_ps[b], ACT.Copy).then_inc(P_kept, 1)
                    act.wait_ge(S_ready, 2 * n + (b + 1))
                    act.wait_ge(scattered[b], 16 * n + 16)
                    act.activation(S[b][:], S_ps, ACT.Copy).then_inc(S_kept, 1)

            def end(t):
                act.wait_ge(tile_done, t + 1)
                act.wait_ge(stored, 16 * t + 16)
                for g in range(4, CTB):
                    a, n = CENTRED[g]
                    act.activation(counts[:, a:a + n], ct_ps[:, g, 0:n], ACT.Copy)
                act.activation(k["deg"][:, bass.ds(t, 1)], deg_ps, ACT.Copy)
                act.drain().then_inc(evac_act, 1)
                act.wait_ge(evac_act, t + 2)
                act.wait_ge(evac_dve, t + 2)
                settle(act, started)
                act.dma_start(k["ct_dram"][bass.ds(t, 1)].rearrange("a p n -> (a p) n"), counts[:]).then_inc(stored, 16)

            act.sem_inc(stored, 16)
            walk(act, k, plan, nothing, pair, end)
            act.wait_ge(stored, 16 * T + 16)

        @block.vector
        def _(dve):
            dve.sem_inc(row_free, 1)
            dve.wait_ge(loaded, 48)
            dve.memset(zeros[:], 0.0)
            dve.memset(zero_rows[:], 0.0)
            dve.memset(ones[:], 1.0)
            dve.tensor_tensor(src[:], k["src_base"][:], k["src_place"][:], ALU.add)
            dve.drain().then_inc(setup, 1)

            def start(t):
                dve.tensor_scalar(rel[:], k["dst"][:], k["tile_start"][:, bass.ds(t, 1)], None, ALU.subtract)
                dve.drain()
                dve.tensor_tensor(key[:], rel[:], k["src_base"][:], ALU.add)
                dve.tensor_scalar(spare[:], rel[:], float(R), None, ALU.is_lt)
                dve.drain()
                dve.scalar_tensor_tensor(valid[:], rel[:], 0.0, spare[:], ALU.is_ge, ALU.mult)
                dve.drain()

            start(0)

            def pair(t, c, n):
                dve.wait_ge(row_in, 16 * n + 16)
                dve.tensor_copy(src_rowf[:], src_row[:])
                dve.drain().then_inc(row_free, 1)
                for b in range(2):
                    dve.wait_ge(used, 2 * n + (b + 1))
                    at = bass.ds(2 * c + b, 1)
                    dve.tensor_scalar(to_dst[b][:], iota_r[:], rel[:, at], None, ALU.is_equal)
                    dve.tensor_scalar(same[b][:], src_rowf[:, b * CH:(b + 1) * CH], src[:, at], k["weight"][:, at],
                                      ALU.is_equal, ALU.mult)
                    dve.tensor_scalar(place[b][:], iota[:, 0:R], k["src_place"][:, at], valid[:, at], ALU.is_equal, ALU.mult)
                    dve.tensor_scalar(onehot[b][:], iota[:], key[:, at], None, ALU.is_equal)
                    dve.drain().then_inc(onehot_ready, 1)

            def end(t):
                start(t + 1)
                dve.wait_ge(tile_done, t + 1)
                dve.wait_ge(stored, 16 * t + 16)
                for g in range(4):
                    a, n = CENTRED[g]
                    dve.tensor_copy(counts[:, a:a + n], ct_ps[:, g, 0:n])
                dve.drain().then_inc(evac_dve, 1)

            walk(dve, k, plan, nothing, pair, end)

        @block.tensor
        def _(pe):
            pe.wait_ge(loaded, 48)
            pe.wait_ge(setup, 1)
            pe.sem_inc(used, 2)
            pe.sem_inc(evac_dve, 1)
            pe.sem_inc(evac_act, 1)
            pe.sem_inc(S_kept, 1)

            def start(t):
                pe.wait_ge(evac_dve, t + 1)
                pe.wait_ge(evac_act, t + 1)
                for g in range(CTB):
                    pe.matmul(ct_ps[:, g, :], zeros[:, 0:R], zeros[:, 0:512], start=True, stop=False, skip_group_check=True)

            def pair(t, c, n):
                for b in range(2):
                    pe.wait_ge(onehot_ready, 2 * n + (b + 1))
                    for g, (a, m) in enumerate(CENTRED):
                        if g == 4:
                            pe.wait_ge(S_kept, 2 * n + (b + 1))
                            pe.matmul(P_ps[b], to_dst[b][:], same[b][:], start=True, stop=True).then_inc(P_ready, 1)
                        pe.matmul(ct_ps[:, g, 0:m], place[b][:], onehot[b][:, a:a + m], start=False, stop=False,
                                  skip_group_check=True)
                    pe.matmul(deg_ps, to_dst[b][:], ones[:], start=False, stop=False,
                              skip_group_check=True).then_inc(used, 1)
                    pe.wait_ge(P_kept, 2 * n + (b + 1))
                    pe.matmul(S_ps, P[b][:], k["xn"][:, bass.ds(t, 1), :], start=True, stop=True).then_inc(S_ready, 1)

            def end(t):
                pe.drain().then_inc(tile_done, 1)

            walk(pe, k, plan, start, pair, end)


def collect_support(nc, d, k):
    with Stage(nc, "collect") as s:
        loaded = s.sem("loaded")
        block = s.block()

        @block.sync
        def _(sp):
            for b, to in enumerate((k["A"], k["B"])):
                sp.dma_start(to[:], k["support_dram"][b][0:NODES].rearrange("(t p) n -> p t n", p=R)).then_inc(loaded, 16)

        @block.vector
        def _(dve):
            dve.wait_ge(loaded, 32)
            dve.tensor_tensor(k["A"][:], k["A"][:], k["B"][:], ALU.add)


def edge_hidden(nc, d, k):
    with Stage(nc, "hid") as s:
        plan = s.sb("plan", [1, 3, T], I32)
        iota_r = s.sb("iota_r", [CH, R])
        rel = s.sb("rel", [CH, NCH])
        attr = [s.sb(f"attr{b}", [EDIM + 1, CH]) for b in range(2)]
        landed = [s.sb(f"landed{b}", [EDIM + 1, CH]) for b in range(2)]
        w1 = s.sb("w1", [EDIM + 1, D])
        to_dst = [s.sb(f"to_dst{b}", [CH, R]) for b in range(2)]
        hidden = [s.sb(f"hidden{b}", [CH, D]) for b in range(2)]
        hid_ps = [s.ps(f"hid_ps{b}", [CH, 512]) for b in range(2)]
        sum_ps = s.ps("sum_ps", [R, 512])
        zeros = s.sb("zeros", [CH, D], BF16)
        land0, land1, attr_ready, started = map(s.sem, ("land0", "land1", "attr_ready", "started"))
        loaded, hid_ready, hid_act, used, onehot_ready, tile_done, evac, setup = map(
            s.sem, ("loaded", "hid_ready", "hid_act", "used", "onehot_ready",
                    "tile_done", "evac", "setup"))
        block = s.block()

        def nothing(t):
            pass

        @block.sync
        def _(sp):
            sp.dma_start(plan[:], k["plan_dram"]).then_inc(loaded, 16)
            sp.dma_start(iota_r[:], d["iota_r"]).then_inc(loaded, 16)
            sp.dma_start(w1[:], d["ee_w1"]).then_inc(loaded, 16)
            sp.wait_ge(loaded, 48)

            def pair(t, c, n):
                for b in range(2):
                    sp.wait_ge(attr_ready, 2 * n + (b + 1))
                    sp.dma_start(landed[b][:], d["attr"][:, bass.ds((2 * c + b) * CH, CH)]).then_inc(
                        land0 if b == 0 else land1, 16)

            walk(sp, k, plan, nothing, pair, nothing)

        @block.gpsimd
        def _(pool):
            pool.wait_ge(loaded, 48)
            pool.sem_inc(attr_ready, 2)

            def pair(t, c, n):
                for b in range(2):
                    pool.wait_ge(land0 if b == 0 else land1, 16 * n + 16)
                    pool.wait_ge(hid_ready, 2 * n + (b + 1))
                    settle(pool, started)
                    pool.tensor_copy(attr[b][:], landed[b][:]).then_inc(attr_ready, 1)

            walk(pool, k, plan, nothing, pair, nothing)

        @block.scalar
        def _(act):
            act.wait_ge(loaded, 48)

            def pair(t, c, n):
                for b in range(2):
                    act.wait_ge(hid_ready, 2 * n + (b + 3))
                    act.wait_ge(used, 2 * n + (b + 1))
                    act.activation(hidden[b][:], hid_ps[b][:, 0:D], ACT.Relu).then_inc(hid_act, 1)

            walk(act, k, plan, nothing, pair, nothing)

        @block.vector
        def _(dve):
            dve.wait_ge(loaded, 48)
            dve.memset(zeros[:], 0.0).then_inc(setup, 1)

            def start(t):
                dve.drain()
                dve.tensor_scalar(rel[:], k["dst"][:], k["tile_start"][:, bass.ds(t, 1)], None, ALU.subtract)
                dve.drain()

            def pair(t, c, n):
                for b in range(2):
                    dve.wait_ge(used, 2 * n + (b + 1))
                    dve.tensor_scalar(to_dst[b][:], iota_r[:], rel[:, bass.ds(2 * c + b, 1)], None,
                                      ALU.is_equal).then_inc(onehot_ready, 1)

            def end(t):
                dve.wait_ge(tile_done, t + 1)
                dve.tensor_copy(k["B"][:, bass.ds(t, 1), :],
                                sum_ps[:, 0:D].rearrange("p (a n) -> p a n", a=1)).then_inc(evac, 1)

            walk(dve, k, plan, start, pair, end)

        @block.tensor
        def _(pe):
            pe.wait_ge(loaded, 48)
            pe.wait_ge(setup, 1)
            pe.sem_inc(used, 2)
            pe.sem_inc(hid_ready, 2)
            pe.sem_inc(evac, 1)
            pe.sem_inc(hid_act, 2)

            def start(t):
                pe.wait_ge(evac, t + 1)
                pe.matmul(sum_ps[:, 0:D], zeros[:, 0:R], zeros[:], start=True, stop=False, skip_group_check=True)

            def pair(t, c, n):
                for b in range(2):
                    pe.wait_ge(attr_ready, 2 * n + (b + 3))
                    pe.wait_ge(hid_act, 2 * n + (b + 1))
                    pe.matmul(hid_ps[b][:, 0:D], attr[b][:], w1[:], start=True, stop=True).then_inc(hid_ready, 1)
                for b in range(2):
                    pe.wait_ge(hid_act, 2 * n + (b + 3))
                    pe.wait_ge(onehot_ready, 2 * n + (b + 1))
                    pe.matmul(sum_ps[:, 0:D], to_dst[b][:], hidden[b][:], start=False, stop=False,
                              skip_group_check=True).then_inc(used, 1)

            def end(t):
                pe.drain().then_inc(tile_done, 1)

            walk(pe, k, plan, start, pair, end)


def aggregate(nc, d, k, name, source, into, finish):
    with Stage(nc, name) as s:
        ct = [s.sb(f"ct{b}", [R, NODES]) for b in range(2)]
        acc = [s.ps(f"acc{b}", [R, 512]) for b in range(2)]
        temp = s.sb("temp", [R, 1, D])
        ct0, ct1, ct_free, acc_ready, acc_free = map(s.sem, ("ct0", "ct1", "ct_free", "acc_ready", "acc_free"))
        block = s.block()

        @block.sync
        def _(sp):
            def load(t, b):
                sp.wait_ge(ct_free, t + 1)
                sp.dma_start(ct[b][:], k["ct_dram"][bass.ds(t, 1)].rearrange("a p n -> (a p) n")).then_inc(
                    ct0 if b == 0 else ct1, 16)

            tiles(sp, load)

        @block.tensor
        def _(pe):
            pe.sem_inc(ct_free, 2)

            def product(t, i, b):
                pe.wait_ge(ct0 if b == 0 else ct1, 16 * i + 16)
                pe.wait_ge(acc_free, t + 1)
                for src in range(T):
                    last = pe.matmul(acc[b][:, 0:D], ct[b][:, src * R:(src + 1) * R], source[:, src, :],
                                     start=(src == 0), stop=(src == T - 1))
                last.then_inc(acc_ready, 1)
                pe.drain().then_inc(ct_free, 1)

            with pe.Fori(0, T // 2) as i:
                for b in range(2):
                    product(2 * i + b, i, b)
            product(T - 1, T // 2, 0)

        @block.vector
        def _(dve):
            dve.sem_inc(acc_free, 2)

            def evacuate(t, b):
                dve.wait_ge(acc_ready, t + 1)
                finish(dve, t, into[:, bass.ds(t, 1), :], acc[b][:, 0:D].rearrange("p (a n) -> p a n", a=1), temp[:])
                dve.drain().then_inc(acc_free, 1)

            tiles(dve, evacuate)



def row_stats(nc, d, k, name, source, kind, width=D):
    with Stage(nc, name) as s:
        stats = s.sb("stats", [R, T, 6])
        mv = s.sb("mv", [R, T, 2])
        rv, root = s.sb("rv", [R, T, 1]), s.sb("root", [R, T, 1])
        squares = [s.sb(f"squares{b}", [R, 1, width]) for b in range(2)]
        var_ready, root_ready = s.sem("var_ready"), s.sem("root_ready")
        block = s.block()

        @block.vector
        def _(dve):
            if kind == "norm":
                def square(t, b):
                    dve.tensor_tensor(squares[b][:], source[:, bass.ds(t, 1), :], source[:, bass.ds(t, 1), :], ALU.mult)
                    dve.drain()
                    dve.tensor_reduce(rv[:, bass.ds(t, 1), :], squares[b][:], AX, ALU.add)

                tiles(dve, square)
                dve.drain().then_inc(var_ready, 1)
            else:
                with dve.Fori(0, T) as t:
                    dve.bn_stats(stats[:, bass.ds(t, 1), :], source[:, bass.ds(t, 1), :])
                dve.drain()
                for t in range(T):
                    dve.bn_aggr(mv[:, t, :], stats[:, t, :])
                dve.drain()
                dve.tensor_scalar(rv[:], mv[:, :, 1:2], LN_EPS, None, ALU.add)
                dve.drain().then_inc(var_ready, 1)
            dve.wait_ge(root_ready, 1)
            if kind == "norm":
                dve.tensor_scalar(rv[:], root[:], 1e-12, None, ALU.max)
                dve.memset(k["shift"][:], 0.0)
                dve.drain()
                dve.reciprocal(k["scale"][:], rv[:])
            else:
                dve.reciprocal(k["scale"][:], root[:])
                dve.drain()
                dve.scalar_tensor_tensor(k["shift"][:], mv[:, :, 0:1], -1.0, k["scale"][:], ALU.mult, ALU.mult)

        @block.scalar
        def _(act):
            act.wait_ge(var_ready, 1)
            act.activation(root[:], rv[:], ACT.Sqrt).then_inc(root_ready, 1)


def normalise(nc, d, k, name, source, rows_to=None, store=False):
    with Stage(nc, name) as s:
        xs = [s.sb(f"xs{b}", [R, D]) for b in range(2)]
        pt = [s.ps(f"pt{b}", [128, 2, 256]) for b in range(2)]
        xs_ready, xs_free, turned, pt_free, rows_ready, stored, started = map(
            s.sem, ("xs_ready", "xs_free", "turned", "pt_free", "rows_ready", "stored", "started"))
        block = s.block()

        @block.vector
        def _(dve):
            dve.sem_inc(pt_free, 2)

            def columns(t, b):
                dve.wait_ge(turned, t + 1)
                dve.tensor_copy(k["xnT"][:, :, rows(t)], pt[b][:, :, 0:R]).then_inc(pt_free, 1)

            tiles(dve, columns)

        @block.scalar
        def _(act):
            def scale(t, b):
                act.wait_ge(xs_free, t + 1)
                if rows_to is not None:
                    act.wait_ge(rows_ready, t + 1)
                settle(act, started)
                act.activation(xs[b][:], source[:, bass.ds(t, 1), :].rearrange("p a n -> p (a n)"), ACT.Identity,
                               bias=k["shift"][:, bass.ds(t, 1), :].rearrange("p a n -> p (a n)"),
                               scale=k["scale"][:, bass.ds(t, 1), :].rearrange("p a n -> p (a n)")).then_inc(xs_ready, 1)

            tiles(act, scale)

        @block.tensor
        def _(pe):
            pe.sem_inc(xs_free, 2)

            def turn(t, b):
                pe.wait_ge(xs_ready, t + 1)
                pe.wait_ge(pt_free, t + 1)
                for c in range(2):
                    last = pe.transpose(pt[b][:, c, 0:R], xs[b][:, c * 128:(c + 1) * 128], k["ident"][0:R, 0:R])
                last.then_inc(turned, 1)
                pe.drain().then_inc(xs_free, 1)

            tiles(pe, turn)

        if rows_to is not None:
            @block.gpsimd
            def _(pool):
                pool.sem_inc(rows_ready, 2)

                def keep(t, b):
                    pool.wait_ge(xs_ready, t + 1)
                    pool.tensor_copy(rows_to[:, bass.ds(t, 1), :],
                                     xs[b][:].rearrange("p (a n) -> p a n", a=1)).then_inc(rows_ready, 1)

                tiles(pool, keep)

        if store:
            @block.sync
            def _(sp):
                sp.wait_ge(rows_ready, T + 2)
                sp.dma_start(k["xn_dram"].rearrange("(t p) n -> p t n", p=R), rows_to[:]).then_inc(stored, 16)
                sp.wait_ge(stored, 16)


def mix_sums(nc, d, k, name, heads, kind, wkv, bkv, gain, shift):
    hd = D // heads
    G = 2 * heads if kind == "ln" else heads
    with Stage(nc, name) as s:
        w = s.sb("w", [128, 2, 2 * D])
        bias = s.sb("bias", [R, 2 * D])
        gn, sh = s.sb("gn", [R, 2 * D]), s.sb("sh", [R, 2 * D])
        mask = s.sb("mask", [128, 128])
        ones = s.sb("ones", [R, 128])
        xt = [s.sb(f"xt{b}", [128, 2, R]) for b in range(2)]
        z = [s.sb(f"z{b}", [R, 2 * D]) for b in range(2)]
        e = s.sb("e", [R, 2 * D])
        sums, sq, var, root = (s.sb(n, [R, G]) for n in ("sums", "sq", "var", "root"))
        kv_ps = [s.ps(f"kv_ps{b}", [R, 512]) for b in range(2)]
        acc = s.ps("acc", [128, 2, 128])
        acc_sum = s.ps("acc_sum", [R, 512])
        zeros = s.sb("zeros", [128, 2 * D], BF16)
        loaded, setup, xt_ready, xt_free, kv_ready, kv_free, z_ready, z_free, part, root_ready, done = map(
            s.sem, ("loaded", "setup", "xt_ready", "xt_free", "kv_ready", "kv_free", "z_ready", "z_free",
                    "part", "root_ready", "done"))
        block = s.block()

        @block.sync
        def _(sp):
            sp.dma_start(w[:], wkv).then_inc(loaded, 16)
            sp.dma_start(bias[:], bkv if bkv is not None else d["zero_row"]).then_inc(loaded, 16)
            sp.dma_start(gn[:], gain if gain is not None else d["zero_row"]).then_inc(loaded, 16)
            sp.dma_start(sh[:], shift if shift is not None else d["zero_row"]).then_inc(loaded, 16)
            sp.dma_start(mask[:], d["mask64"] if hd == 64 else d["mask32"]).then_inc(loaded, 16)
            sp.wait_ge(loaded, 80)

        @block.gpsimd
        def _(pool):
            def fetch(t, b):
                pool.wait_ge(xt_free, t + 1)
                pool.tensor_copy(xt[b][:], k["xnT"][:, :, rows(t)]).then_inc(xt_ready, 1)

            tiles(pool, fetch)

        @block.tensor
        def _(pe):
            pe.wait_ge(loaded, 80)
            pe.wait_ge(setup, 1)
            pe.sem_inc(xt_free, 2)
            pe.sem_inc(z_free, 2)
            pe.matmul(acc[:].rearrange("p a n -> p (a n)"), zeros[:, 0:128], zeros[:, 0:256], start=True, stop=False,
                      skip_group_check=True)
            pe.matmul(acc_sum[:, 0:D], zeros[:, 0:R], zeros[:, 0:D], start=True, stop=False, skip_group_check=True)

            def make(t, b):
                pe.wait_ge(xt_ready, t + 1)
                pe.wait_ge(kv_free, t + 1)
                for c in range(2):
                    last = pe.matmul(kv_ps[b][:], xt[b][:, c, :], w[:, c, :], start=(c == 0), stop=(c == 1))
                last.then_inc(kv_ready, 1)
                pe.drain().then_inc(xt_free, 1)

            def body(t, b):
                pe.wait_ge(z_ready, t + 1)
                for c in range(2):
                    pe.matmul(acc[:, c, :], z[b][:, D + c * 128:D + (c + 1) * 128], z[b][:, c * 128:(c + 1) * 128],
                              start=False, stop=False, skip_group_check=True)
                if kind == "elu":
                    pe.matmul(acc_sum[:, 0:D], ones[:, 0:R], z[b][:, 0:D], start=False, stop=False, skip_group_check=True)
                pe.drain().then_inc(z_free, 1)

            pipelined(make, body)(pe)
            pe.drain().then_inc(done, 1)

        @block.scalar
        def _(act):
            def body(t, b):
                if kind == "ln":
                    act.wait_ge(part, 2 * t + 1)
                    act.activation(e[:], z[b][:], ACT.Square).then_inc(root_ready, 1)
                    act.wait_ge(part, 2 * t + 2)
                    act.activation(root[:], var[:], ACT.Sqrt).then_inc(root_ready, 1)
                else:
                    act.wait_ge(part, t + 1)
                    act.activation(e[:, D:2 * D], e[:, 0:D], ACT.Exp).then_inc(root_ready, 1)

            tiles(act, body)

        @block.vector
        def _(dve):
            dve.sem_inc(kv_free, 2)
            dve.wait_ge(loaded, 80)
            dve.memset(zeros[:], 0.0)
            dve.memset(ones[:], 1.0)
            dve.drain().then_inc(setup, 1)

            def body(t, b):
                dve.wait_ge(kv_ready, t + 1)
                dve.wait_ge(z_free, t + 1)
                if kind == "ln":
                    zv = z[b][:].rearrange("p (g n) -> p g n", g=G)
                    dve.tensor_reduce(sums[:], kv_ps[b][:].rearrange("p (g n) -> p g n", g=G), AX, ALU.add)
                    dve.drain()
                    dve.tensor_scalar(sq[:], sums[:], 1.0 / hd, None, ALU.mult)
                    dve.drain()
                    dve.tensor_tensor(zv, kv_ps[b][:].rearrange("p (g n) -> p g n", g=G),
                                      sq[:].unsqueeze(2).broadcast_to((R, G, hd)), ALU.subtract)
                    dve.drain().then_inc(part, 1)
                    dve.drain().then_inc(kv_free, 1)
                    dve.wait_ge(root_ready, 2 * t + 1)
                    dve.tensor_reduce(sums[:], e[:].rearrange("p (g n) -> p g n", g=G), AX, ALU.add)
                    dve.drain()
                    dve.tensor_scalar(var[:], sums[:], 1.0 / hd, LN_EPS, ALU.mult, ALU.add)
                    dve.drain().then_inc(part, 1)
                    dve.wait_ge(root_ready, 2 * t + 2)
                    dve.reciprocal(sq[:], root[:])
                    dve.drain()
                    dve.tensor_tensor(zv, zv, sq[:].unsqueeze(2).broadcast_to((R, G, hd)), ALU.mult)
                    dve.drain()
                    dve.tensor_tensor(z[b][:], z[b][:], gn[:], ALU.mult)
                    dve.drain()
                    dve.tensor_tensor(z[b][:], z[b][:], sh[:], ALU.add)
                    dve.drain().then_inc(z_ready, 1)
                else:
                    dve.tensor_tensor(z[b][:], kv_ps[b][:], bias[:], ALU.add)
                    dve.drain().then_inc(kv_free, 1)
                    dve.tensor_scalar(e[:, 0:D], z[b][:, 0:D], 0.0, None, ALU.min)
                    dve.drain().then_inc(part, 1)
                    dve.wait_ge(root_ready, t + 1)
                    dve.scalar_tensor_tensor(z[b][:, 0:D], z[b][:, 0:D], 0.0, e[:, D:2 * D], ALU.max, ALU.add)
                    dve.drain().then_inc(z_ready, 1)

            tiles(dve, body)
            dve.wait_ge(done, 1)
            for c in range(2):
                dve.scalar_tensor_tensor(k["kvT"][:, c, :], acc[:, c, :], 1.0 / NODES if kind == "ln" else 1.0,
                                         mask[:], ALU.mult, ALU.mult)
            if kind == "elu":
                dve.tensor_copy(k["ksum"][:], acc_sum[:, 0:D])


def fold(nc, d, k, name, wo, wq=None):
    with Stage(nc, name) as s:
        woT = s.sb("woT", [128, 2, D])
        wqs = s.sb("wqs", [128, 2, D])
        m1 = s.sb("m1", [128, 2, D])
        ps1 = [s.ps(f"ps1{c}", [128, 512]) for c in range(2)]
        ps2 = [s.ps(f"ps2{c}", [128, 512]) for c in range(2)]
        loaded, one, two, kept = map(s.sem, ("loaded", "one", "two", "kept"))
        block = s.block()
        dest = m1 if wq is not None else k["fold"]

        @block.sync
        def _(sp):
            sp.dma_start(woT[:], wo).then_inc(loaded, 16)
            sp.dma_start(wqs[:], wq if wq is not None else wo).then_inc(loaded, 16)
            sp.wait_ge(loaded, 32)

        @block.tensor
        def _(pe):
            pe.wait_ge(loaded, 32)
            for c in range(2):
                pe.matmul(ps1[c][:, 0:D], k["kvT"][:, c, :], woT[:, c, :], start=True, stop=True).then_inc(one, 1)
            if wq is not None:
                pe.wait_ge(kept, 1)
                for i in range(2):
                    for c in range(2):
                        last = pe.matmul(ps2[i][:, 0:D], wqs[:, c, i * 128:(i + 1) * 128], m1[:, c, :],
                                         start=(c == 0), stop=(c == 1))
                    last.then_inc(two, 1)

        @block.vector
        def _(dve):
            for c in range(2):
                dve.wait_ge(one, c + 1)
                dve.tensor_copy(dest[:, c, :], ps1[c][:, 0:D])
            dve.drain().then_inc(kept, 1)
            if wq is not None:
                for i in range(2):
                    dve.wait_ge(two, i + 1)
                    dve.tensor_copy(k["fold"][:, i, :], ps2[i][:, 0:D])


def linear_rows(nc, d, k, name, source, weight, nk, prepare, finish, n_out=D, vectors=(), temps=()):
    with Stage(nc, name) as s:
        w = s.sb("w", [128, nk, n_out])
        vec = [s.sb(f"vec{n}", [R, v[1]]) for n, v in enumerate(vectors)]
        tmp = [s.sb(f"tmp{n}", shape) for n, shape in enumerate(temps)]
        xs = [s.sb(f"xs{b}", [R, nk * 128]) for b in range(2)]
        xt = [s.sb(f"xt{b}", [128, nk, R]) for b in range(2)]
        pt = [s.ps(f"pt{b}", [128, 4, 128]) for b in range(2)]
        out = [s.ps(f"out{b}", [R, 512]) for b in range(2)]
        loaded, xs_ready, xs_free, turned, xt_ready, xt_free, out_ready, out_free = map(
            s.sem, ("loaded", "xs_ready", "xs_free", "turned", "xt_ready", "xt_free", "out_ready", "out_free"))
        helper, helped = s.sem("helper"), s.sem("helped")
        block = s.block()
        in_dram = weight is not k["fold"]
        total = 16 * (len(vectors) + in_dram)

        @block.sync
        def _(sp):
            if in_dram:
                sp.dma_start(w[:], weight).then_inc(loaded, 16)
            for v, t in zip(vectors, vec):
                sp.dma_start(t[:], v[0]).then_inc(loaded, 16)
            sp.wait_ge(loaded, total)

        wt = w if in_dram else weight

        @block.scalar
        def _(act):
            act.wait_ge(loaded, total)

            def body(t, b):
                act.wait_ge(turned, t + 1)
                act.wait_ge(xt_free, t + 1)
                act.activation(xt[b][:], pt[b][:, 0:nk, 0:R], ACT.Copy).then_inc(xt_ready, 1)

            tiles(act, body)

        @block.tensor
        def _(pe):
            pe.wait_ge(loaded, total)
            pe.sem_inc(xs_free, 2)
            pe.sem_inc(xt_free, 2)

            def turn(t, b):
                pe.wait_ge(xs_ready, t + 1)
                pe.wait_ge(xt_ready, t + 1)
                for c in range(nk):
                    last = pe.transpose(pt[b][:, c, 0:R], xs[b][:, c * 128:(c + 1) * 128], k["ident"][0:R, 0:R])
                last.then_inc(turned, 1)
                pe.drain().then_inc(xs_free, 1)

            def body(t, b):
                pe.wait_ge(xt_ready, t + 3)
                pe.wait_ge(out_free, t + 1)
                for c in range(nk):
                    last = pe.matmul(out[b][:, 0:n_out], xt[b][:, c, :], wt[:, c, :], start=(c == 0), stop=(c == nk - 1))
                last.then_inc(out_ready, 1)
                pe.drain().then_inc(xt_free, 1)

            pe.sem_inc(xt_ready, 2)
            ahead(turn, body, False)(pe)

        @block.vector
        def _(dve):
            dve.wait_ge(loaded, total)
            dve.sem_inc(out_free, 2)

            def before(t, b):
                dve.wait_ge(xs_free, t + 1)
                prepare(dve, t, xs[b], vec, tmp)
                dve.drain().then_inc(xs_ready, 1)

            def body(t, b):
                dve.wait_ge(out_ready, t + 1)
                finish(dve, t, out[b][:, 0:n_out].rearrange("p (a n) -> p a n", a=1), vec, tmp)
                dve.drain().then_inc(out_free, 1)

            ahead(before, body, True)(dve)


def copy_in(source):
    def prepare(dve, t, xs, vec, tmp):
        dve.tensor_copy(xs[:].rearrange("p (a n) -> p a n", a=1), source[:, bass.ds(t, 1), :])
    return prepare


def elementwise(nc, d, k, name, fn, vectors=(), temps=()):
    with Stage(nc, name) as s:
        vec = [s.sb(f"vec{n}", [R, v[1]]) for n, v in enumerate(vectors)]
        tmp = [[s.sb(f"tmp{n}{b}", shape) for n, shape in enumerate(temps)] for b in range(2)]
        loaded = s.sem("loaded")
        block = s.block()

        @block.sync
        def _(sp):
            for v, t in zip(vectors, vec):
                sp.dma_start(t[:], v[0]).then_inc(loaded, 16)
            if vectors:
                sp.wait_ge(loaded, 16 * len(vectors))

        @block.vector
        def _(dve):
            if vectors:
                dve.wait_ge(loaded, 16 * len(vectors))

            def body(t, b):
                fn(dve, t, vec, tmp[b])
                dve.drain()

            tiles(dve, body)


def project(nc, d, k, name, weight, n_out, into, bias=None, add=False):
    with Stage(nc, name) as s:
        w = s.sb("w", [128, 2, n_out])
        bc = s.sb("bc", [R, 1, n_out])
        xt = [s.sb(f"xt{b}", [128, 2, R]) for b in range(2)]
        out = [s.ps(f"out{b}", [R, 512]) for b in range(2)]
        loaded, xt_ready, xt_free, out_ready, out_free = map(
            s.sem, ("loaded", "xt_ready", "xt_free", "out_ready", "out_free"))
        block = s.block()
        total = 16 * (1 + (bias is not None))

        @block.sync
        def _(sp):
            sp.dma_start(w[:], weight).then_inc(loaded, 16)
            if bias is not None:
                sp.dma_start(bc[:].rearrange("p a n -> p (a n)"), bias).then_inc(loaded, 16)
            sp.wait_ge(loaded, total)

        @block.gpsimd
        def _(pool):
            def fetch(t, b):
                pool.wait_ge(xt_free, t + 1)
                pool.tensor_copy(xt[b][:], k["xnT"][:, :, rows(t)]).then_inc(xt_ready, 1)

            tiles(pool, fetch)

        @block.tensor
        def _(pe):
            pe.wait_ge(loaded, total)
            pe.sem_inc(xt_free, 2)

            def body(t, b):
                pe.wait_ge(xt_ready, t + 1)
                pe.wait_ge(out_free, t + 1)
                for c in range(2):
                    last = pe.matmul(out[b][:, 0:n_out], xt[b][:, c, :], w[:, c, :], start=(c == 0), stop=(c == 1))
                last.then_inc(out_ready, 1)
                pe.drain().then_inc(xt_free, 1)

            tiles(pe, body)

        @block.vector
        def _(dve):
            dve.wait_ge(loaded, total)
            dve.sem_inc(out_free, 2)

            def body(t, b):
                dve.wait_ge(out_ready, t + 1)
                row = out[b][:, 0:n_out].rearrange("p (a n) -> p a n", a=1)
                to = into[:, bass.ds(t, 1), :]
                if bias is None:
                    dve.tensor_copy(to, row).then_inc(out_free, 1)
                elif add:
                    dve.tensor_tensor(to, to, row, ALU.add)
                    dve.drain().then_inc(out_free, 1)
                    dve.tensor_tensor(to, to, bc[:], ALU.add)
                else:
                    dve.tensor_tensor(to, row, bc[:], ALU.add).then_inc(out_free, 1)

            tiles(dve, body)


def choose(dve, lg, top, hot, spare, down, E):
    dve.tensor_reduce(top, lg, AX, ALU.max)
    dve.drain()
    dve.tensor_tensor(hot, lg, top.broadcast_to((R, T, E)), ALU.is_ge)
    dve.drain()
    dve.tensor_tensor(hot, hot, down.broadcast_to((R, T, E)), ALU.mult)
    dve.drain()
    dve.tensor_reduce(spare, hot, AX, ALU.max)
    dve.drain()
    dve.tensor_tensor(hot, hot, spare.broadcast_to((R, T, E)), ALU.is_equal)
    dve.drain()


def gate(nc, d, k, name, E, kind):
    with Stage(nc, name) as s:
        lg = k["gates"][:, 0:T * E].rearrange("p (t e) -> p t e", e=E)
        one, two = s.sb("one", [R, T, E]), s.sb("two", [R, T, E])
        top1, top2, sp1, sp2 = (s.sb(n, [R, T, 1]) for n in ("top1", "top2", "sp1", "sp2"))
        down = s.sb("down", [R, 1, E])
        loaded, to_exp, exped = s.sem("loaded"), s.sem("to_exp"), s.sem("exped")
        block = s.block()
        soft = kind == "soft_two"

        @block.sync
        def _(sp):
            sp.dma_start(down[:].rearrange("p a n -> p (a n)"), d["down"][:, 32 - E:32]).then_inc(loaded, 16)
            sp.wait_ge(loaded, 16)

        @block.vector
        def _(dve):
            dve.wait_ge(loaded, 16)
            if soft:
                dve.tensor_reduce(top1[:], lg, AX, ALU.max)
                dve.drain()
                dve.tensor_tensor(one[:], lg, top1[:].broadcast_to((R, T, E)), ALU.subtract)
                dve.drain().then_inc(to_exp, 1)
                dve.wait_ge(exped, 1)
                dve.tensor_reduce(sp1[:], two[:], AX, ALU.add)
                dve.drain()
                dve.reciprocal(sp2[:], sp1[:])
                dve.drain()
                dve.tensor_tensor(lg, two[:], sp2[:].broadcast_to((R, T, E)), ALU.mult)
                dve.drain()
            choose(dve, lg, top1[:], one[:], sp1[:], down[:], E)
            dve.tensor_copy(k["hots"][0][:, 0:T * E].rearrange("p (t e) -> p t e", e=E), one[:])
            if kind == "first":
                return
            dve.scalar_tensor_tensor(lg, one[:], -1e30, lg, ALU.mult, ALU.add)
            dve.drain()
            choose(dve, lg, top2[:], two[:], sp1[:], down[:], E)
            dve.tensor_copy(k["hots"][1][:, 0:T * E].rearrange("p (t e) -> p t e", e=E), two[:])
            dve.tensor_tensor(sp1[:], top2[:], top1[:], ALU.subtract)
            dve.drain().then_inc(to_exp, 1)
            dve.wait_ge(exped, 2 if soft else 1)
            dve.tensor_scalar(top1[:], sp2[:], 1.0, None, ALU.add)
            dve.drain()
            dve.reciprocal(top2[:], top1[:])
            dve.drain()
            dve.tensor_tensor(sp1[:], top2[:], sp2[:], ALU.mult)
            dve.drain()
            dve.tensor_copy(k["slot_gate"][0][:].unsqueeze(2), top2[:])
            dve.tensor_copy(k["slot_gate"][1][:].unsqueeze(2), sp1[:])
            dve.tensor_tensor(one[:], one[:], top2[:].broadcast_to((R, T, E)), ALU.mult)
            dve.drain()
            dve.tensor_tensor(two[:], two[:], sp1[:].broadcast_to((R, T, E)), ALU.mult)
            dve.drain()
            dve.tensor_tensor(lg, one[:], two[:], ALU.add)

        @block.scalar
        def _(act):
            if kind == "first":
                return
            n = 0
            if soft:
                act.wait_ge(to_exp, 1)
                act.activation(two[:], one[:], ACT.Exp).then_inc(exped, 1)
                n = 1
            act.wait_ge(to_exp, n + 1)
            act.activation(sp2[:], sp1[:], ACT.Exp).then_inc(exped, 1)


def rank_gate(nc, d, k, name, keep):
    with Stage(nc, name) as s:
        col = s.sb("col", [128, T])
        colT = s.sb("colT", [T, R])
        line = s.sb("line", [128, NODES])
        below = s.sb("below", [R, R])
        c1, c2, c3, c4 = (s.sb(n, [R, T]) for n in ("c1", "c2", "c3", "c4"))
        junk = [s.sb(f"junk{n}", [R, NODES]) for n in range(2)]
        ps = s.ps("ps", [T, 512])
        ready, turned, copied, stored, back, loaded = map(
            s.sem, ("ready", "turned", "copied", "stored", "back", "loaded"))
        w = k["gates"]
        block = s.block()

        @block.sync
        def _(sp):
            sp.dma_start(below[:], d["below"]).then_inc(loaded, 16)
            sp.wait_ge(copied, 1)
            sp.dma_start(k["line_dram"].rearrange("(t p) -> t p", p=R), colT[:]).then_inc(stored, 16)
            sp.wait_ge(stored, 16)
            sp.dma_start(line[0:R, :], k["line_dram"].rearrange("(a n) -> a n", a=1).broadcast_to((R, NODES))).then_inc(back, 16)
            sp.wait_ge(back, 16)
            sp.wait_ge(loaded, 16)

        @block.tensor
        def _(pe):
            pe.wait_ge(ready, 1)
            pe.transpose(ps[:, 0:R], col[0:R, :], k["ident"][0:R, 0:R]).then_inc(turned, 1)

        @block.vector
        def _(dve):
            dve.tensor_copy(col[0:R, :], w[:, 0:T]).then_inc(ready, 1)
            dve.wait_ge(turned, 1)
            dve.tensor_copy(colT[:], ps[:, 0:R]).then_inc(copied, 1)
            dve.wait_ge(back, 16)
            dve.wait_ge(loaded, 16)
            for c in (c1, c2, c3, c4):
                dve.memset(c[:], 0.0)
            dve.drain()
            for t in range(T):
                a, z = t * R, (t + 1) * R
                if t:
                    dve.tensor_scalar(junk[0][:, 0:a], line[0:R, 0:a], w[:, t:t + 1], 0.0, ALU.is_ge, ALU.add,
                                      accum_out=c1[:, t:t + 1])
                dve.tensor_scalar(junk[1][:, a:], line[0:R, a:], w[:, t:t + 1], 0.0, ALU.is_gt, ALU.add,
                                  accum_out=c2[:, t:t + 1])
                dve.drain()
                dve.scalar_tensor_tensor(junk[0][:, 0:R], line[0:R, a:z], w[:, t:t + 1], below[:],
                                         ALU.is_equal, ALU.mult)
                dve.drain()
                dve.tensor_reduce(c3[:, t:t + 1], junk[0][:, 0:R], AX, ALU.add)
                dve.drain()
            dve.tensor_tensor(c4[:], c1[:], c2[:], ALU.add)
            dve.drain()
            dve.tensor_tensor(c1[:], c4[:], c3[:], ALU.add)
            dve.drain()
            dve.scalar_tensor_tensor(c2[:], c1[:], float(keep), w[:, 0:T], ALU.is_lt, ALU.mult)
            dve.drain()
            for e in range(2):
                dve.tensor_copy(w[:, 0:2 * T].rearrange("p (t e) -> p t e", e=2)[:, :, e:e + 1],
                                c2[:].rearrange("p (t e) -> p t e", e=1))


def seed(nc, d, k, name, E, b2, into, base=None, base_row=None):
    with Stage(nc, name) as s:
        w = s.sb("w", [E, D])
        row = s.sb("row", [R, 1, D])
        gs = [s.sb(f"gs{b}", [R, E]) for b in range(2)]
        gt = [s.sb(f"gt{b}", [E, R]) for b in range(2)]
        pt = [s.ps(f"pt{b}", [E, 512]) for b in range(2)]
        out = [s.ps(f"out{b}", [R, 512]) for b in range(2)]
        loaded, gs_ready, gs_free, turned, gt_ready, gt_free, out_ready, out_free = map(
            s.sem, ("loaded", "gs_ready", "gs_free", "turned", "gt_ready", "gt_free", "out_ready", "out_free"))
        block = s.block()
        total = 16 * (1 + (base_row is not None))

        @block.sync
        def _(sp):
            sp.dma_start(w[:], b2).then_inc(loaded, 16)
            if base_row is not None:
                sp.dma_start(row[:].rearrange("p a n -> p (a n)"), base_row).then_inc(loaded, 16)
            sp.wait_ge(loaded, total)

        @block.gpsimd
        def _(pool):
            def body(t, b):
                pool.wait_ge(gs_free, t + 1)
                pool.tensor_copy(gs[b][:], k["gates"][:, bass.ds(t * E, E)]).then_inc(gs_ready, 1)

            tiles(pool, body)

        @block.scalar
        def _(act):

            def body(t, b):
                act.wait_ge(turned, t + 1)
                act.wait_ge(gt_free, t + 1)
                act.activation(gt[b][:], pt[b][:, 0:R], ACT.Copy).then_inc(gt_ready, 1)

            tiles(act, body)

        @block.tensor
        def _(pe):
            pe.wait_ge(loaded, total)
            pe.sem_inc(gs_free, 2)
            pe.sem_inc(gt_free, 2)

            def body(t, b):
                pe.wait_ge(gs_ready, t + 1)
                pe.transpose(pt[b][:, 0:R], gs[b][:], k["ident"][0:R, 0:R]).then_inc(turned, 1)
                pe.drain().then_inc(gs_free, 1)
                pe.wait_ge(gt_ready, t + 1)
                pe.wait_ge(out_free, t + 1)
                pe.matmul(out[b][:, 0:D], gt[b][:], w[:], start=True, stop=True).then_inc(out_ready, 1)
                pe.drain().then_inc(gt_free, 1)

            tiles(pe, body)

        @block.vector
        def _(dve):
            dve.wait_ge(loaded, total)
            dve.sem_inc(out_free, 2)

            def body(t, b):
                dve.wait_ge(out_ready, t + 1)
                to, o = into[:, bass.ds(t, 1), :], out[b][:, 0:D].rearrange("p (a n) -> p a n", a=1)
                if base is not None:
                    dve.tensor_tensor(to, o, base[:, bass.ds(t, 1), :], ALU.add).then_inc(out_free, 1)
                elif base_row is not None:
                    dve.tensor_tensor(to, o, row[:], ALU.add).then_inc(out_free, 1)
                else:
                    dve.tensor_copy(to, o).then_inc(out_free, 1)

            tiles(dve, body)


def experts(nc, d, k, name, E, hp, hc, func, w1, b1, w2, into):
    with Stage(nc, name) as s:
        W1 = [s.sb(f"W1{b}", [128, 2, hc * hp]) for b in range(2)]
        W2 = [s.sb(f"W2{b}", [hp, hc, D]) for b in range(2)]
        bias = s.sb("bias", [hp, E * hc])
        hT = [s.sb(f"hT{b}", [hp, hc, 3 * R]) for b in range(2)]
        h_ps = [s.ps(f"h_ps{c}", [hp, 512]) for c in range(hc)]
        o_ps = s.ps("o_ps", [R, 3, 512])
        loaded, w_in0, w_in1, w_free, h_ready, hT_ready, out_ready, out_free = map(
            s.sem, ("loaded", "w_in0", "w_in1", "w_free", "h_ready", "hT_ready", "out_ready", "out_free"))
        block = s.block()
        started, began = s.sem("started"), s.sem("began")
        per = 10 * hc

        def pairs(eng, body):
            with eng.Fori(0, E // 2) as q:
                for b in range(2):
                    body(2 * q + b, q, b)

        @block.sync
        def _(sp):
            sp.dma_start(bias[:], b1).then_inc(loaded, 16)
            sp.wait_ge(loaded, 16)

            def load(e, q, b):
                sp.wait_ge(w_free, e + 1)
                sp.dma_start(W1[b][:], w1[bass.ds(e, 1)].rearrange("a p c n -> (a p) c n")).then_inc(
                    w_in0 if b == 0 else w_in1, 16)
                sp.dma_start(W2[b][:], w2[bass.ds(e, 1)].rearrange("a p c n -> (a p) c n")).then_inc(
                    w_in0 if b == 0 else w_in1, 16)

            pairs(sp, load)

        @block.tensor
        def _(pe):
            pe.sem_inc(w_free, 2)
            pe.sem_inc(hT_ready, hc)

            def expert(e, q, b):
                pe.wait_ge(w_in0 if b == 0 else w_in1, 32 * q + 32)
                settle(pe, began)

                def group(t, g, n, p):
                    for c in range(hc):
                        pe.wait_ge(hT_ready, e * per + n * hc + (c + 1))
                        for i in range(2):
                            last = pe.matmul(h_ps[c][:, 0:g * R], W1[b][:, i, c * hp:(c + 1) * hp],
                                             k["xnT"][:, i, rows(t, g)], start=(i == 0), stop=(i == 1))
                        last.then_inc(h_ready, 1)
                    pe.wait_ge(hT_ready, e * per + n * hc + 2 * hc)
                    pe.wait_ge(out_free, e * 10 + n + 1)
                    for j in range(g):
                        for c in range(hc):
                            pe.matmul(o_ps[:, 2 * p + j // 2, (j % 2) * D:(j % 2 + 1) * D],
                                      hT[p][:, c, j * R:(j + 1) * R], W2[b][:, c, :], start=(c == 0), stop=(c == hc - 1))
                    pe.drain().then_inc(out_ready, 1)

                groups(pe, group)
                pe.drain().then_inc(w_free, 1)

            pairs(pe, expert)

        @block.scalar
        def _(act):
            act.wait_ge(loaded, 16)
            act.sem_inc(out_ready, 2)

            def expert(e, q, b):
                def group(t, g, n, p):
                    act.wait_ge(out_ready, e * 10 + n + 1)
                    for c in range(hc):
                        act.wait_ge(h_ready, e * per + n * hc + (c + 1))
                        settle(act, started)
                        act.activation(hT[p][:, c, 0:g * R], h_ps[c][:, 0:g * R], func,
                                       bias=bias[:, bass.ds(e * hc + c, 1)]).then_inc(hT_ready, 1)

                groups(act, group)

            pairs(act, expert)

        @block.vector
        def _(dve):
            dve.sem_inc(out_free, 2)

            def expert(e, q, b):
                def group(t, g, n, p):
                    dve.wait_ge(out_ready, e * 10 + n + 3)
                    for j in range(g):
                        to = into[:, bass.ds(t + j, 1), :].rearrange("p a n -> p (a n)")
                        dve.scalar_tensor_tensor(
                            to, o_ps[:, 2 * p + j // 2, (j % 2) * D:(j % 2 + 1) * D],
                            k["gates"][:, bass.ds((t + j) * E + e, 1)], to, ALU.mult, ALU.add)
                    dve.drain().then_inc(out_free, 1)

                groups(dve, group)

            pairs(dve, expert)


def expert_places(nc, d, k, name, E, hots):
    with Stage(nc, name) as s:
        per = min(T, 512 // E)
        lots = [(a, min(per, T - a)) for a in range(0, T, per)]
        above, ones = s.sb("above", [R, R]), s.sb("ones", [R, R])
        chosen, rank, prod = (s.sb(n, [R, T, E]) for n in ("chosen", "rank", "prod"))
        before = s.sb("before", [R, T + 1, E])
        blocks, cum, base, start = (s.sb(n, [R, E]) for n in ("blocks", "cum", "base", "start"))
        pos = s.sb("pos", [R, T, len(hots)])
        rank_ps, total_ps = s.ps("rank_ps", [R, len(lots), 512]), s.ps("total_ps", [R, len(lots), 512])
        loaded, ready, counted = s.sem("loaded"), s.sem("ready"), s.sem("counted")
        block = s.block()

        @block.sync
        def _(sp):
            sp.dma_start(above[:], d["above"]).then_inc(loaded, 16)

        @block.tensor
        def _(pe):
            pe.wait_ge(loaded, 16)
            pe.wait_ge(ready, 1)
            for g, (a, n) in enumerate(lots):
                rhs = chosen[:, a:a + n, :].rearrange("p t e -> p (t e)")
                pe.matmul(rank_ps[:, g, 0:n * E], above[:], rhs, start=True, stop=True)
                pe.matmul(total_ps[:, g, 0:n * E], ones[:], rhs, start=True, stop=True)
            pe.drain().then_inc(counted, 1)

        @block.vector
        def _(dve):
            dve.memset(ones[:], 1.0)
            dve.memset(before[:, 0, :], 0.0)
            dve.memset(blocks[:], 1.0)
            if len(hots) == 2:
                dve.tensor_tensor(chosen[:], hots[0], hots[1], ALU.add)
            else:
                dve.tensor_copy(chosen[:], hots[0])
            dve.drain().then_inc(ready, 1)
            dve.wait_ge(counted, 1)
            for g, (a, n) in enumerate(lots):
                for t in range(a, a + n):
                    dve.tensor_tensor(before[:, t + 1, :], before[:, t, :], total_ps[:, g, (t - a) * E:(t - a + 1) * E], ALU.add)
                    dve.drain()
                dve.tensor_tensor(rank[:, a:a + n, :], rank_ps[:, g, 0:n * E].rearrange("p (t e) -> p t e", e=E),
                                  before[:, a:a + n, :], ALU.add)
            for m in range(1, -(-NODES // 128)):
                dve.scalar_tensor_tensor(blocks[:], before[:, T, :], float(128 * m), blocks[:], ALU.is_gt, ALU.add)
                dve.drain()
            dve.tensor_tensor_scan(cum[:], ones[:, 0:E], blocks[:], 0.0, ALU.mult, ALU.add)
            dve.drain()
            dve.tensor_tensor(base[:], cum[:], blocks[:], ALU.subtract)
            dve.drain()
            dve.tensor_scalar(start[:], base[:], 128.0, None, ALU.mult)
            dve.tensor_copy(k["blocks"][:, 0, 0:E], blocks[0:1, :])
            dve.tensor_copy(k["blocks"][:, 1, 0:E], base[0:1, :])
            dve.drain()
            dve.tensor_tensor(rank[:], rank[:], start[:].unsqueeze(1).broadcast_to((R, T, E)), ALU.add)
            dve.drain()
            for slot, hot in enumerate(hots):
                dve.tensor_tensor(prod[:], rank[:], hot, ALU.mult)
                dve.drain()
                dve.tensor_reduce(pos[:, :, slot:slot + 1], prod[:], AX, ALU.add)
                dve.drain()
            dve.tensor_copy(k["pos"][:, :, 0:len(hots)], pos[:])


def parities(eng, body):
    body(0, 0, 0, first=True)
    body(1, 0, 1, first=True)
    with eng.Fori(1, T // 2) as i:
        body(2 * i, i, 0)
        body(2 * i + 1, i, 1)
    body(T - 1, T // 2, 0)


def sort_rows(nc, d, k, name, source, slots):
    with Stage(nc, name) as s:
        buf = [s.sb(f"buf{b}", [R, D]) for b in range(2)]
        to = [s.sb(f"to{b}", [R, slots], I32) for b in range(2)]
        rows_ready, to_ready, started = s.sem("rows_ready"), s.sem("to_ready"), s.sem("started")
        sent = [s.sem(f"sent{b}") for b in range(2)]
        block = s.block()

        @block.scalar
        def _(act):
            def fill(t, i, b, first=False):
                if not first:
                    act.wait_ge(sent[b], 16 * slots * i)
                settle(act, started)
                act.activation(buf[b][:].unsqueeze(1), source[:, bass.ds(t, 1), :], ACT.Copy).then_inc(rows_ready, 1)

            parities(act, fill)

        @block.gpsimd
        def _(pool):
            def send(t, i, b, first=False):
                if not first:
                    pool.wait_ge(sent[b], 16 * slots * i)
                pool.tensor_copy(to[b][:].unsqueeze(1), k["pos"][:, bass.ds(t, 1), 0:slots]).then_inc(to_ready, 1)
                pool.wait_ge(to_ready, t + 1)
                pool.wait_ge(rows_ready, t + 1)
                settle(pool, started)
                for slot in range(slots):
                    pool.indirect_dma_start(k["sorted_dram"], bass.IndirectOffsetOnAxis(ap=to[b][:, slot:slot + 1], axis=0),
                                            buf[b][:], None).then_inc(sent[b], 16)

            parities(pool, send)
            pool.wait_ge(sent[0], 16 * slots * (T // 2 + 1))
            pool.wait_ge(sent[1], 16 * slots * (T // 2))


def unsort_rows(nc, d, k, name, slots, combine):
    with Stage(nc, name) as s:
        buf = [[s.sb(f"buf{b}{n}", [R, D]) for n in range(slots)] for b in range(2)]
        to = [s.sb(f"to{b}", [R, slots], I32) for b in range(2)]
        buf_free, to_ready, started = s.sem("buf_free"), s.sem("to_ready"), s.sem("started")
        got = [s.sem(f"got{b}") for b in range(2)]
        block = s.block()

        @block.gpsimd
        def _(pool):
            pool.sem_inc(buf_free, 2)

            def fetch(t, i, b, first=False):
                pool.wait_ge(buf_free, t + 1)
                pool.tensor_copy(to[b][:].unsqueeze(1), k["pos"][:, bass.ds(t, 1), 0:slots]).then_inc(to_ready, 1)
                pool.wait_ge(to_ready, t + 1)
                settle(pool, started)
                for slot in range(slots):
                    pool.indirect_dma_start(buf[b][slot][:], None, k["result_dram"],
                                            bass.IndirectOffsetOnAxis(ap=to[b][:, slot:slot + 1], axis=0)).then_inc(got[b], 16)

            parities(pool, fetch)

        @block.vector
        def _(dve):
            def add(t, i, b, first=False):
                dve.wait_ge(got[b], 16 * slots * i + 16 * slots)
                combine(dve, t, [a[:].unsqueeze(1) for a in buf[b]])
                dve.drain().then_inc(buf_free, 1)

            parities(dve, add)


def sorted_experts(nc, d, k, name, E, hp, hc, w1, b1, w2, b2):
    with Stage(nc, name) as s:
        W1 = [s.sb(f"W1{b}", [128, 2, hc * hp]) for b in range(2)]
        W2 = [s.sb(f"W2{b}", [hp, hc, D]) for b in range(2)]
        B2 = [s.sb(f"B2{b}", [128, D]) for b in range(2)]
        bias = s.sb("bias", [hp, E * hc])
        xr, xT, y = s.sb("xr", [128, D]), s.sb("xT", [128, 2, 128]), s.sb("y", [128, D])
        hT = s.sb("hT", [hp, hc, 128])
        h_ps = [s.ps(f"h_ps{c}", [hp, 512]) for c in range(hc)]
        pt, o_ps = s.ps("pt", [128, 2, 256]), s.ps("o_ps", [128, 512])
        loaded, w_free, b2_free, x_in, turned, xT_ready, h_ready, hT_ready, out_ready, y_ready, y_stored, started = map(
            s.sem, ("loaded", "w_free", "b2_free", "x_in", "turned", "xT_ready", "h_ready", "hT_ready", "out_ready",
                    "y_ready", "y_stored", "started"))
        w_in = [s.sem(f"w_in{b}") for b in range(2)]
        block = s.block()
        most = -(-NODES // 128)

        def every(eng, begin, each, end):
            with eng.Fori(0, E // 2) as q:
                for b in range(2):
                    e = 2 * q + b
                    begin(e, q, b)
                    count = eng.value_load(k["blocks"][0:1, 0, bass.ds(e, 1)], min_val=1, max_val=most)
                    base = eng.value_load(k["blocks"][0:1, 1, bass.ds(e, 1)], min_val=0, max_val=E * most)
                    with eng.Fori(0, count) as j:
                        g = k["nc"].s_assert_within(base + j, 0, BLOCKS - 1,
                                                    skip_runtime_bounds_check_because="all blocks are at most BLOCKS")
                        each(e, b, g)
                    end(e, b)

        def nothing(*a):
            pass

        @block.gpsimd
        def _(pool):
            pool.dma_start(bias[:], b1).then_inc(loaded, 16)
            with pool.Fori(0, E // 2) as q:
                for b in range(2):
                    e = 2 * q + b
                    pool.wait_ge(w_free, e + 1)
                    pool.wait_ge(b2_free, e + 1)
                    settle(pool, started)
                    pool.dma_start(W1[b][:], w1[bass.ds(e, 1)].rearrange("a p c n -> (a p) c n")).then_inc(w_in[b], 16)
                    pool.dma_start(W2[b][:], w2[bass.ds(e, 1)].rearrange("a p c n -> (a p) c n")).then_inc(w_in[b], 16)
                    pool.dma_start(B2[b][:], b2[bass.ds(e, 1), :].broadcast_to((128, D))).then_inc(w_in[b], 16)

        @block.sync
        def _(sp):
            sp.sem_inc(y_stored, 16)
            sp.dma_start(xr[:], k["sorted_dram"][0:128]).then_inc(x_in, 16)

            def each(e, b, g):
                sp.wait_ge(turned, g + 1)
                settle(sp, started)
                sp.dma_start(xr[:], k["sorted_dram"][bass.ds((g + 1) * 128, 128)]).then_inc(x_in, 16)
                sp.wait_ge(y_ready, g + 2)
                settle(sp, started)
                sp.dma_start(k["result_dram"][bass.ds(g * 128, 128)], y[:]).then_inc(y_stored, 16)

            every(sp, nothing, each, nothing)
            count = sp.value_load(k["blocks"][0:1, 0, E - 1:E], min_val=1, max_val=most)
            base = sp.value_load(k["blocks"][0:1, 1, E - 1:E], min_val=0, max_val=E * most)
            sp.wait_ge(y_stored, 16 * (count + base) + 16)
            sp.wait_ge(x_in, 16 * (count + base) + 16)
            settle(sp, started)

        @block.tensor
        def _(pe):
            pe.sem_inc(w_free, 2)

            def turn(g):
                pe.wait_ge(x_in, 16 * g + 16)
                for c in range(2):
                    pe.transpose(pt[:, c, 0:128], xr[:, c * 128:(c + 1) * 128], k["ident"][:])
                pe.drain().then_inc(turned, 1)

            turn(0)

            def begin(e, q, b):
                pe.wait_ge(w_in[b], 48 * q + 48)
                settle(pe, started)

            def each(e, b, g):
                pe.wait_ge(xT_ready, g + 1)
                for c in range(hc):
                    for i in range(2):
                        last = pe.matmul(h_ps[c][:, 0:128], W1[b][:, i, c * hp:(c + 1) * hp], xT[:, i, :],
                                         start=(i == 0), stop=(i == 1))
                    last.then_inc(h_ready, 1)
                turn(g + 1)
                pe.wait_ge(y_ready, g + 1)
                for c in range(hc):
                    pe.wait_ge(hT_ready, hc * g + (c + 1))
                    pe.matmul(o_ps[:, 0:D], hT[:, c, :], W2[b][:, c, :], start=(c == 0), stop=(c == hc - 1))
                pe.drain().then_inc(out_ready, 1)

            def end(e, b):
                pe.drain().then_inc(w_free, 1)

            every(pe, begin, each, end)

        @block.scalar
        def _(act):
            act.wait_ge(loaded, 16)

            def each(e, b, g):
                for c in range(hc):
                    act.wait_ge(h_ready, hc * g + (c + 1))
                    settle(act, started)
                    act.activation(hT[:, c, :], h_ps[c][:, 0:128], ACT.Relu,
                                   bias=bias[:, bass.ds(e * hc + c, 1)]).then_inc(hT_ready, 1)

            every(act, nothing, each, nothing)

        @block.vector
        def _(dve):
            dve.sem_inc(y_ready, 1)
            dve.sem_inc(b2_free, 2)

            def to_columns(g):
                dve.wait_ge(turned, g + 1)
                dve.tensor_copy(xT[:], pt[:, :, 0:128]).then_inc(xT_ready, 1)

            to_columns(0)

            def begin(e, q, b):
                dve.wait_ge(w_in[b], 48 * q + 48)
                settle(dve, started)

            def each(e, b, g):
                to_columns(g + 1)
                dve.wait_ge(out_ready, g + 1)
                dve.wait_ge(y_stored, 16 * g + 16)
                dve.tensor_tensor(y[:], o_ps[:, 0:D], B2[b][:], ALU.add)
                dve.drain().then_inc(y_ready, 1)

            def end(e, b):
                dve.drain().then_inc(b2_free, 1)

            every(dve, begin, each, end)


def softmax_keys(nc, d, k, name):
    C = 128
    with Stage(nc, name) as s:
        w, g_pre = s.sb("w", [128, 2, 3 * C]), s.sb("g_pre", [128, 2])
        w_out, mask = s.sb("w_out", [C, D]), s.sb("mask", [C, C])
        keys = s.sb("keys", [C, NODES])
        mem_k, mem_v = s.sb("mem_k", [C, 4]), s.sb("mem_v", [4, C])
        most, most4, low = s.sb("most", [C, 1]), s.sb("most4", [C, 1]), s.sb("low", [C, 1])
        ones = s.sb("ones", [R, 1])
        mem_e, mem_t = s.sb("mem_e", [C, 4]), s.sb("mem_t", [4, C])
        xt = [s.sb(f"xt{b}", [128, 2, R]) for b in range(2)]
        ke = [s.sb(f"ke{b}", [C, R]) for b in range(2)]
        ks = [s.sb(f"ks{b}", [R, C]) for b in range(2)]
        vs = [s.sb(f"vs{b}", [R, C]) for b in range(2)]
        ctx = s.sb("ctx", [C, C])
        inv = s.sb("inv", [C, 1])
        k_ps = [s.ps(f"k_ps{b}", [128, 512]) for b in range(2)]
        kv_ps = [s.ps(f"kv_ps{b}", [128, 512]) for b in range(2)]
        acc, acc_sum = s.ps("acc", [C, 512]), s.ps("acc_sum", [C, 512])
        (loaded, w_ready, k_ready, k_kept, low_ready, ke_ready, mem_ready, xt_ready, xt_free, kv_ready, kept,
         used, done, ctx_ready, folded, mem_turned, mem_kept, ke_free) = map(
            s.sem, ("loaded", "w_ready", "k_ready", "k_kept", "low_ready", "ke_ready", "mem_ready", "xt_ready",
                    "xt_free", "kv_ready", "kept", "used", "done", "ctx_ready", "folded", "mem_turned", "mem_kept",
                    "ke_free"))
        started = s.sem("started")
        block = s.block()

        @block.sync
        def _(sp):
            for to, src in ((w, d["w_qkv"]), (g_pre, d["g_pre"]), (w_out, d["w_out"]), (mask, d["mask32"]),
                            (mem_k, d["mem_k"]), (mem_v, d["mem_v"])):
                sp.dma_start(to[:], src).then_inc(loaded, 16)
            sp.wait_ge(loaded, 96)

        @block.gpsimd
        def _(pool):
            def fetch(t, b):
                pool.wait_ge(xt_free, t + 1)
                pool.tensor_copy(xt[b][:], k["xnT"][:, :, rows(t)]).then_inc(xt_ready, 1)

            tiles(pool, fetch)

        @block.vector
        def _(dve):
            dve.wait_ge(loaded, 96)
            dve.memset(ones[:], 1.0)
            for c in range(2):
                dve.tensor_scalar(k["w_qkv"][:, c, :], w[:, c, :], g_pre[:, c:c + 1], None, ALU.mult)
            dve.drain().then_inc(w_ready, 1)
            dve.sem_inc(k_kept, 2)

            def keep(t, g, n, p):
                dve.wait_ge(k_ready, n + 1)
                dve.tensor_copy(keys[:, rows(t, g)], k_ps[p][:, 0:g * R]).then_inc(k_kept, 1)

            groups(dve, keep)
            dve.drain()
            dve.tensor_reduce(most[:], keys[:], AX, ALU.max)
            dve.tensor_reduce(most4[:], mem_k[:], AX, ALU.max)
            dve.drain()
            dve.tensor_tensor(most[:], most[:], most4[:], ALU.max)
            dve.drain()
            dve.tensor_scalar(low[:], most[:], -1.0, None, ALU.mult).then_inc(low_ready, 1)
            dve.wait_ge(mem_turned, 1)
            dve.tensor_copy(mem_t[:], kv_ps[0][0:4, 0:C]).then_inc(mem_kept, 1)

            def body(t, b):
                dve.wait_ge(kv_ready, t + 1)
                dve.wait_ge(used, t + 1)
                dve.tensor_copy(ks[b][:], kv_ps[b][0:R, 0:C])
                dve.tensor_copy(vs[b][:], kv_ps[b][0:R, C:2 * C])
                dve.drain().then_inc(kept, 1)

            tiles(dve, body)
            dve.wait_ge(done, 1)
            dve.tensor_tensor(ctx[:], acc[:, 0:C], mask[:], ALU.mult)
            dve.reciprocal(inv[:], acc_sum[:, 0:1])
            dve.drain().then_inc(ctx_ready, 1)
            dve.wait_ge(folded, 1)
            dve.tensor_scalar(k["fold"][:, 0, :], k_ps[0][:, 0:D], inv[:], 32.0 ** -0.5, ALU.mult, ALU.mult)

        @block.scalar
        def _(act):
            act.wait_ge(low_ready, 1)
            act.activation(mem_e[:], mem_k[:], ACT.Exp, bias=low[:]).then_inc(mem_ready, 1)

            def body(t, b):
                act.wait_ge(ke_free, t + 1)
                settle(act, started)
                act.activation(ke[b][:], keys[:, rows(t)], ACT.Exp, bias=low[:]).then_inc(ke_ready, 1)

            tiles(act, body)

        @block.tensor
        def _(pe):
            pe.wait_ge(w_ready, 1)
            pe.sem_inc(ke_free, 2)
            pe.sem_inc(used, 2)
            pe.sem_inc(xt_free, 2)

            def key(t, g, n, p):
                pe.wait_ge(k_kept, n + 1)
                for c in range(2):
                    last = pe.matmul(k_ps[p][:, 0:g * R], k["w_qkv"][:, c, C:2 * C], k["xnT"][:, c, rows(t, g)],
                                     start=(c == 0), stop=(c == 1))
                last.then_inc(k_ready, 1)

            groups(pe, key)
            pe.wait_ge(mem_ready, 1)
            pe.transpose(kv_ps[0][0:4, 0:C], mem_e[:], k["ident"][:]).then_inc(mem_turned, 1)
            pe.wait_ge(mem_kept, 1)
            pe.matmul(acc[:, 0:C], mem_v[:], mem_t[:], start=True, stop=False, skip_group_check=True)
            pe.matmul(acc_sum[:, 0:1], mem_t[:], ones[0:4, :], start=True, stop=False, skip_group_check=True)

            def body(t, b):
                pe.wait_ge(ke_ready, t + 1)
                pe.wait_ge(xt_ready, t + 1)
                pe.transpose(kv_ps[b][0:R, 0:C], ke[b][:], k["ident"][:])
                for c in range(2):
                    last = pe.matmul(kv_ps[b][0:R, C:2 * C], xt[b][:, c, :], k["w_qkv"][:, c, 2 * C:3 * C],
                                     start=(c == 0), stop=(c == 1))
                last.then_inc(kv_ready, 1)
                pe.drain().then_inc(xt_free, 1)
                pe.drain().then_inc(ke_free, 1)
                pe.wait_ge(kept, t + 1)
                pe.matmul(acc[:, 0:C], vs[b][:], ks[b][:], start=False, stop=False, skip_group_check=True)
                pe.matmul(acc_sum[:, 0:1], ks[b][:], ones[:], start=False, stop=False,
                          skip_group_check=True).then_inc(used, 1)

            tiles(pe, body)
            pe.drain().then_inc(done, 1)
            pe.wait_ge(ctx_ready, 1)
            pe.matmul(k_ps[0][:, 0:D], ctx[:], w_out[:], start=True, stop=True).then_inc(folded, 1)


def batch(nc, name, sb_shapes, dve_steps, act_steps):
    with Stage(nc, name) as s:
        ts = [s.sb(f"t{n}", shape) for n, shape in enumerate(sb_shapes)]
        to_act, to_dve = s.sem("to_act"), s.sem("to_dve")
        block = s.block()

        @block.vector
        def _(dve):
            dve_steps(dve, ts, to_act, to_dve)

        @block.scalar
        def _(act):
            act_steps(act, ts, to_act, to_dve)


def mlp_ln(nc, d, k):
    H = 1024
    with Stage(nc, "mlp") as s:
        w2 = s.sb("w2", [128, 8, H])
        spare = k["xnT"][:].rearrange("p c n -> p (c n)")
        w1 = spare[:, 0:2 * H].rearrange("p (c n) -> p c n", c=2)
        w3 = spare[:, 2 * H:2 * H + 8 * D].rearrange("p (c n) -> p c n", c=8)
        b1, b2, b3 = s.sb("b1", [R, H]), s.sb("b2", [R, H]), s.sb("b3", [R, 1, D])
        g1, be1, g2, be2 = (s.sb(n, [128, 8]) for n in ("g1", "be1", "g2", "be2"))
        xs = k["hots"][0][:, 0:D]
        xt = s.sb("xt", [128, 2, R])
        z = [spare[0:R, 2 * H + 8 * D + n * H:2 * H + 8 * D + (n + 1) * H] for n in range(2)]
        zn = [s.sb(f"zn{n}", [R, H]) for n in range(2)]
        hT = [s.sb(f"hT{n}", [128, 8, R]) for n in range(2)]
        stats, mv = s.sb("stats", [R, 2, 6]), s.sb("mv", [R, 2])
        v1, root, inv, shift = ([s.sb(f"{a}{n}", [R, 1]) for n in range(2)] for a in ("v1", "root", "inv", "shift"))
        h_ps = [s.ps(f"h_ps{n}", [R, 2, 512]) for n in range(2)]
        t_ps = s.ps("t_ps", [128, 8, 128])
        pt = s.ps("pt", [128, 2, 256])
        y_ps = s.ps("y_ps", [R, 512])
        loaded, xs_ready, turned, xt_ready, y_ready = map(s.sem, ("loaded", "xs_ready", "turned", "xt_ready", "y_ready"))
        h_ready, var_ready, root_ready, inv_ready, zn_ready, zt_ready, hT_ready = (
            [s.sem(f"{a}{n}") for n in range(2)]
            for a in ("h_ready", "var_ready", "root_ready", "inv_ready", "zn_ready", "zt_ready", "hT_ready"))
        block = s.block()

        @block.sync
        def _(sp):
            for to, name in ((w1, "m_w1"), (w2, "m_w2"), (w3, "m_w3"), (b1, "m_b1"), (b2, "m_b2"),
                             (g1, "m_g1"), (be1, "m_be1"), (g2, "m_g2"), (be2, "m_be2")):
                sp.dma_start(to[:], d[name]).then_inc(loaded, 16)
            sp.dma_start(b3[:].rearrange("p a n -> p (a n)"), d["m_b3"]).then_inc(loaded, 16)
            sp.wait_ge(loaded, 160)

        @block.tensor
        def _(pe):
            pe.wait_ge(loaded, 160)

            def first_layer(t):
                pe.wait_ge(xs_ready, t + 1)
                for c in range(2):
                    last = pe.transpose(pt[:, c, 0:R], xs[:, c * 128:(c + 1) * 128], k["ident"][0:R, 0:R])
                last.then_inc(turned, 1)
                pe.wait_ge(xt_ready, t + 1)
                for o in range(2):
                    for c in range(2):
                        last = pe.matmul(h_ps[0][:, o, :], xt[:, c, :], w1[:, c, o * 512:(o + 1) * 512],
                                         start=(c == 0), stop=(c == 1))
                    last.then_inc(h_ready[0], 1)

            def turn(t, layer):
                pe.wait_ge(zn_ready[layer], t + 1)
                for c in range(8):
                    last = pe.transpose(t_ps[:, c, 0:R], zn[layer][:, c * 128:(c + 1) * 128], k["ident"][0:R, 0:R])
                    if c % 4 == 3:
                        last.then_inc(zt_ready[layer], 1)

            def second_layer(t):
                turn(t, 0)
                for o in range(2):
                    for c in range(8):
                        if o == 0:
                            pe.wait_ge(hT_ready[0], 8 * t + (c + 1))
                        last = pe.matmul(h_ps[1][:, o, :], hT[0][:, c, :], w2[:, c, o * 512:(o + 1) * 512],
                                         start=(c == 0), stop=(c == 7))
                    last.then_inc(h_ready[1], 1)

            def last_layer(t):
                turn(t, 1)
                for c in range(8):
                    pe.wait_ge(hT_ready[1], 8 * t + (c + 1))
                    last = pe.matmul(y_ps[:, 0:D], hT[1][:, c, :], w3[:, c, :], start=(c == 0), stop=(c == 7))
                last.then_inc(y_ready, 1)

            first_layer(0)
            with pe.Fori(0, T - 1) as t:
                second_layer(t)
                first_layer(t + 1)
                last_layer(t)
            second_layer(T - 1)
            last_layer(T - 1)

        @block.scalar
        def _(act):
            act.wait_ge(loaded, 160)

            def columns(t):
                act.wait_ge(turned, t + 1)
                act.activation(xt[:], pt[:, :, 0:R], ACT.Copy).then_inc(xt_ready, 1)

            def normed(t, layer):
                act.wait_ge(var_ready[layer], t + 1)
                act.activation(root[layer][:], v1[layer][:], ACT.Sqrt).then_inc(root_ready[layer], 1)
                act.wait_ge(inv_ready[layer], t + 1)
                act.activation(zn[layer][:], z[layer], ACT.Identity, bias=shift[layer][:],
                               scale=inv[layer][:]).then_inc(zn_ready[layer], 1)

            def relu(t, layer):
                g, be = ((g1, be1), (g2, be2))[layer]
                for c in range(8):
                    if c % 4 == 0:
                        act.wait_ge(zt_ready[layer], 2 * t + (c // 4 + 1))
                    act.activation(hT[layer][:, c, :], t_ps[:, c, 0:R], ACT.Relu, bias=be[:, c:c + 1],
                                   scale=g[:, c:c + 1]).then_inc(hT_ready[layer], 1)

            columns(0)
            normed(0, 0)
            with act.Fori(0, T - 1) as t:
                relu(t, 0)
                columns(t + 1)
                normed(t, 1)
                relu(t, 1)
                normed(t + 1, 0)
            relu(T - 1, 0)
            normed(T - 1, 1)
            relu(T - 1, 1)

        @block.vector
        def _(dve):
            dve.wait_ge(loaded, 160)

            def fetch(t):
                dve.tensor_copy(xs.rearrange("p (a n) -> p a n", a=1), k["A"][:, bass.ds(t, 1), :]).then_inc(xs_ready, 1)

            def norm(t, layer):
                bias = (b1, b2)[layer]
                for o in range(2):
                    dve.wait_ge(h_ready[layer], 2 * t + (o + 1))
                    dve.tensor_tensor(z[layer][:, o * 512:(o + 1) * 512], h_ps[layer][:, o, :],
                                      bias[:, o * 512:(o + 1) * 512], ALU.add)
                    dve.drain()
                    dve.bn_stats(stats[:, o, :], z[layer][:, o * 512:(o + 1) * 512])
                dve.drain()
                dve.bn_aggr(mv[:], stats[:].rearrange("p a n -> p (a n)"))
                dve.drain()
                dve.tensor_scalar(v1[layer][:], mv[:, 1:2], LN_EPS, None, ALU.add).then_inc(var_ready[layer], 1)
                dve.wait_ge(root_ready[layer], t + 1)
                dve.reciprocal(inv[layer][:], root[layer][:])
                dve.drain()
                dve.scalar_tensor_tensor(shift[layer][:], mv[:, 0:1], -1.0, inv[layer][:], ALU.mult, ALU.mult)
                dve.drain().then_inc(inv_ready[layer], 1)

            def result(t):
                dve.wait_ge(y_ready, t + 1)
                row = y_ps[:, 0:D].rearrange("p (a n) -> p a n", a=1)
                dve.tensor_tensor(k["B"][:, bass.ds(t, 1), :], row, b3[:], ALU.add)
                dve.drain()
                dve.tensor_tensor(k["B"][:, bass.ds(t, 1), :], k["B"][:, bass.ds(t, 1), :], k["xn"][:, bass.ds(t, 1), :], ALU.add)

            fetch(0)
            norm(0, 0)
            with dve.Fori(0, T - 1) as t:
                fetch(t + 1)
                norm(t, 1)
                norm(t + 1, 0)
                result(t)
            norm(T - 1, 1)
            result(T - 1)


def small_experts(nc, d, k, into):
    with Stage(nc, "ffn2") as s:
        sw1, sw2, sw3 = s.sb("sw1", [128, 2, 256]), s.sb("sw2", [128, 2, 128]), s.sb("sw3", [128, D])
        ew1, ew2, ew3 = s.sb("ew1", [128, 4, 2, 128]), s.sb("ew2", [128, 4, 64]), s.sb("ew3", [64, 4, D])
        sb1, sb2 = s.sb("sb1", [128, 2]), s.sb("sb2", [128, 1])
        eb1, eb2 = s.sb("eb1", [128, 4]), s.sb("eb2", [64, 4])
        h1 = s.sb("h1", [128, 2, 3 * R])
        h2 = s.sb("h2", [128, 3 * R])
        a_ps = [s.ps(f"a_ps{b}", [128, 512]) for b in range(2)]
        b_ps = s.ps("b_ps", [128, 512])
        o_ps = s.ps("o_ps", [R, 3, 512])
        loaded, one_ready, one_kept, two_ready, two_kept, h2_free, out_ready, out_free = map(
            s.sem, ("loaded", "one_ready", "one_kept", "two_ready", "two_kept", "h2_free", "out_ready", "out_free"))
        block = s.block()

        @block.sync
        def _(sp):
            for to, name in ((sw1, "s_w1"), (sw2, "s_w2"), (sw3, "s_w3"), (ew1, "e_w1"), (ew2, "e_w2"), (ew3, "e_w3"),
                             (sb1, "s_b1"), (sb2, "s_b2"), (eb1, "e_b1"), (eb2, "e_b2")):
                sp.dma_start(to[:], d[name]).then_inc(loaded, 16)
            sp.wait_ge(loaded, 160)

        @block.tensor
        def _(pe):
            pe.wait_ge(loaded, 160)

            def group(t, g, n, p):
                for net in range(5):
                    m = 5 * n + net
                    for o in range(2 if net == 0 else 1):
                        for i in range(2):
                            w = sw1[:, i, o * 128:(o + 1) * 128] if net == 0 else ew1[:, net - 1, i, :]
                            last = pe.matmul(a_ps[o][:, 0:g * R], w, k["xnT"][:, i, rows(t, g)], start=(i == 0), stop=(i == 1))
                    last.then_inc(one_ready, 1)
                    pe.wait_ge(one_kept, m + 1)
                    if net == 0:
                        for i in range(2):
                            last = pe.matmul(b_ps[:, 0:g * R], sw2[:, i, :], h1[:, i, 0:g * R], start=(i == 0), stop=(i == 1))
                    else:
                        last = pe.matmul(b_ps[0:64, 0:g * R], ew2[:, net - 1, :], h1[:, 0, 0:g * R], start=True, stop=True)
                    last.then_inc(two_ready, 1)
                    pe.wait_ge(two_kept, m + 1)
                    pe.wait_ge(out_free, m + 1)
                    for j in range(g):
                        if net == 0:
                            last = pe.matmul(o_ps[:, j, 0:D], h2[:, j * R:(j + 1) * R], sw3[:], start=True, stop=True)
                        else:
                            last = pe.matmul(o_ps[:, j, 0:D], h2[0:64, j * R:(j + 1) * R], ew3[:, net - 1, :], start=True, stop=True)
                    last.then_inc(out_ready, 1)
                    pe.drain().then_inc(h2_free, 1)

            groups(pe, group)

        @block.scalar
        def _(act):
            act.wait_ge(loaded, 160)
            act.sem_inc(h2_free, 1)

            def group(t, g, n, p):
                for net in range(5):
                    m = 5 * n + net
                    act.wait_ge(one_ready, m + 1)
                    for o in range(2 if net == 0 else 1):
                        act.activation(h1[:, o, 0:g * R], a_ps[o][:, 0:g * R], ACT.Relu,
                                       bias=sb1[:, o:o + 1] if net == 0 else eb1[:, net - 1:net])
                    act.drain().then_inc(one_kept, 1)
                    act.wait_ge(two_ready, m + 1)
                    act.wait_ge(h2_free, m + 1)
                    if net == 0:
                        act.activation(h2[:, 0:g * R], b_ps[:, 0:g * R], ACT.Relu, bias=sb2[:]).then_inc(two_kept, 1)
                    else:
                        act.activation(h2[0:64, 0:g * R], b_ps[0:64, 0:g * R], ACT.Relu,
                                       bias=eb2[:, net - 1:net]).then_inc(two_kept, 1)

            groups(act, group)

        @block.vector
        def _(dve):
            dve.sem_inc(out_free, 1)

            def group(t, g, n, p):
                for net in range(5):
                    dve.wait_ge(out_ready, 5 * n + net + 1)
                    for j in range(g):
                        to = into[:, bass.ds(t + j, 1), :].rearrange("p a n -> p (a n)")
                        if net == 0:
                            dve.tensor_tensor(to, o_ps[:, j, 0:D], to, ALU.add)
                        else:
                            dve.scalar_tensor_tensor(to, o_ps[:, j, 0:D], k["gates"][:, bass.ds((t + j) * 4 + (net - 1), 1)],
                                                     to, ALU.mult, ALU.add)
                    dve.drain().then_inc(out_free, 1)

            groups(dve, group)


def elu_mix(nc, d, k, name, wq, bq, wkv, bkv, wo, bo, greatest):
    mix_sums(nc, d, k, name + "s", 8, "elu", wkv, bkv, None, None)
    fold(nc, d, k, name + "f", wo)
    project(nc, d, k, name + "q", wq, D, k["A"], bq)
    A, B, x = k["A"], k["B"], k["x"]
    heads_of = [v[:].rearrange("p t (h n) -> p (t h) n", n=32) for v in (A, B)]

    def dve_steps(dve, ts, to_act, to_dve):
        norm, inv = ts
        dve.tensor_scalar(B[:], A[:], 0.0, None, ALU.min)
        dve.drain().then_inc(to_act, 1)
        dve.wait_ge(to_dve, 1)
        dve.scalar_tensor_tensor(A[:], A[:], 0.0, B[:], ALU.max, ALU.add)
        dve.drain()
        dve.tensor_tensor(B[:], A[:], k["ksum"][:].unsqueeze(1).broadcast_to((R, T, D)), ALU.mult)
        dve.drain()
        dve.tensor_reduce(norm[:], heads_of[1], AX, ALU.add)
        dve.drain()
        dve.tensor_scalar(norm[:], norm[:], 1e-6, None, ALU.max if greatest else ALU.add)
        dve.drain()
        dve.reciprocal(inv[:], norm[:])
        dve.drain()
        dve.tensor_tensor(heads_of[0], heads_of[0], inv[:].broadcast_to((R, T * 8, 32)), ALU.mult)

    def act_steps(act, ts, to_act, to_dve):
        act.wait_ge(to_act, 1)
        act.activation(B[:], B[:], ACT.Exp).then_inc(to_dve, 1)

    batch(nc, name + "e", [[R, T * 8, 1]] * 2, dve_steps, act_steps)

    def finish(dve, t, out, vec, tmp):
        dve.tensor_tensor(tmp[0][:], out, vec[0][:].unsqueeze(1), ALU.add)
        dve.drain()
        dve.tensor_tensor(x[:, bass.ds(t, 1), :], x[:, bass.ds(t, 1), :], tmp[0][:], ALU.add)

    linear_rows(nc, d, k, name + "o", A, k["fold"], 2, copy_in(A), finish, vectors=[(bo, D)], temps=[[R, 1, D]])


def add_affine(nc, d, k, name, source, gain, shift, relu):
    row_stats(nc, d, k, name + "s", source, "ln")
    x = k["x"]

    def fn(dve, t, vec, tmp):
        a, b = tmp
        dve.tensor_scalar(a[:], source[:, bass.ds(t, 1), :], col(k["scale"], t), col(k["shift"], t), ALU.mult, ALU.add)
        dve.drain()
        dve.tensor_tensor(b[:], a[:], vec[0][:].unsqueeze(1), ALU.mult)
        dve.drain()
        dve.tensor_tensor(a[:], b[:], vec[1][:].unsqueeze(1), ALU.add)
        dve.drain()
        to = x[:, bass.ds(t, 1), :]
        if relu:
            dve.scalar_tensor_tensor(to, a[:], 0.0, to, ALU.max, ALU.add)
        else:
            dve.tensor_tensor(to, to, a[:], ALU.add)

    elementwise(nc, d, k, name + "a", fn, vectors=[(gain, D), (shift, D)], temps=[[R, 1, D]] * 2)


def col(array, t):
    return array[:, bass.ds(t, 1), :].rearrange("p a n -> p (a n)")


def add_to_x(nc, d, k, name, relu):
    x, A = k["x"], k["A"]

    def dve_steps(dve, ts, to_act, to_dve):
        if relu:
            dve.scalar_tensor_tensor(x[:], A[:], 0.0, x[:], ALU.max, ALU.add)
        else:
            dve.tensor_tensor(x[:], x[:], A[:], ALU.add)

    batch(nc, name, [], dve_steps, lambda act, ts, to_act, to_dve: act.nop())


def layer0(nc, d, k):
    x, xn, A = k["x"], k["xn"], k["A"]
    row_stats(nc, d, k, "l0s", x, "ln")
    normalise(nc, d, k, "l0n", x, xn)
    first_places(nc, d, k)
    scatter_and_count(nc, d, k)
    collect_support(nc, d, k)

    def both(dve, t, xs, vec, tmp):
        dve.tensor_copy(xs[:, 0:D].unsqueeze(1), xn[:, bass.ds(t, 1), :])
        dve.tensor_copy(xs[:, D:2 * D].unsqueeze(1), A[:, bass.ds(t, 1), :])

    def relu_add(dve, t, out, vec, tmp):
        dve.tensor_tensor(tmp[0][:], out, vec[0][:].unsqueeze(1), ALU.add)
        dve.drain()
        to = x[:, bass.ds(t, 1), :]
        dve.scalar_tensor_tensor(to, tmp[0][:], 0.0, to, ALU.max, ALU.add)

    linear_rows(nc, d, k, "l0g", None, d["g0_w"], 4, both, relu_add, vectors=[(d["g0_b"], D)], temps=[[R, 1, D]])
    mix_sums(nc, d, k, "l0m", 4, "ln", d["m0_wkv"], None, d["m0_gain"], d["m0_shift"])
    fold(nc, d, k, "l0f", d["m0_wo"], d["m0_wq"])
    project(nc, d, k, "l0o", k["fold"][:], D, x, d["m0_bo"], add=True)
    row_stats(nc, d, k, "l0t", x, "ln")
    normalise(nc, d, k, "l0u", x, xn)
    gates = k["gates"][:, 0:T * 32].rearrange("p (t e) -> p t e", e=32)
    project(nc, d, k, "l0r", d["r0_w"], 32, gates, d["r0_b"])
    gate(nc, d, k, "l0h", 32, "first")
    expert_places(nc, d, k, "l0p", 32, [k["hots"][0][:].rearrange("p (t e) -> p t e", e=32)])
    sort_rows(nc, d, k, "l0v", xn, 1)
    sorted_experts(nc, d, k, "l0e", 32, 64, 1, d["f0_w1"], d["f0_b1"], d["f0_w2"], d["f0_b2"])

    def relu_to_x(dve, t, got):
        to = x[:, bass.ds(t, 1), :]
        dve.scalar_tensor_tensor(to, got[0], 0.0, to, ALU.max, ALU.add)

    unsort_rows(nc, d, k, "l0w", 1, relu_to_x)


def layer1(nc, d, k):
    x, xn, A, B = k["x"], k["xn"], k["A"], k["B"]
    row_stats(nc, d, k, "l1s", x, "ln")
    normalise(nc, d, k, "l1n", x, xn)

    def dve_steps(dve, ts, to_act, to_dve):
        dve.tensor_scalar(k["deg1"][:], k["deg"][:], 1.0, None, ALU.add)
        dve.tensor_scalar(ts[0][:], k["deg"][:], 1.0, None, ALU.max)
        dve.drain().then_inc(to_act, 1)
        dve.reciprocal(k["rdeg"][:], ts[0][:])
        dve.wait_ge(to_dve, 1)
        dve.reciprocal(k["dinv"][:], ts[1][:])
        dve.drain()
        for t in range(T):
            dve.tensor_scalar(A[:, t, :], xn[:, t, :], k["dinv"][:, t:t + 1], None, ALU.mult)

    def act_steps(act, ts, to_act, to_dve):
        act.wait_ge(to_act, 1)
        act.activation(ts[1][:], k["deg1"][:], ACT.Sqrt).then_inc(to_dve, 1)

    batch(nc, "l1d", [[R, T]] * 2, dve_steps, act_steps)

    def scaled(dve, t, into, acc, temp):
        dve.tensor_tensor(temp, acc, A[:, bass.ds(t, 1), :], ALU.add)
        dve.drain()
        dve.tensor_scalar(into, temp, k["dinv"][:, bass.ds(t, 1)], None, ALU.mult)

    for i in range(3):
        def step(dve, t, out, vec, tmp, last=(i == 2)):
            dve.tensor_tensor(tmp[0][:], out, vec[0][:].unsqueeze(1), ALU.add)
            dve.drain()
            if last:
                dve.tensor_tensor(x[:, bass.ds(t, 1), :], x[:, bass.ds(t, 1), :], tmp[0][:], ALU.add)
            else:
                dve.tensor_scalar(A[:, bass.ds(t, 1), :], tmp[0][:], k["dinv"][:, bass.ds(t, 1)], None, ALU.mult)

        aggregate(nc, d, k, f"l1a{i}", A, B, scaled)
        linear_rows(nc, d, k, f"l1w{i}", B, d[f"g1_w{i}"], 2, copy_in(B), step, vectors=[(d[f"g1_b{i}"], D)],
                    temps=[[R, 1, D]])

    row_stats(nc, d, k, "l1m", xn, "norm")
    batch(nc, "l1c", [], lambda dve, ts, a, b: dve.tensor_scalar(k["scale"][:], k["scale"][:], float(D) ** 0.5, None, ALU.mult),
          lambda act, ts, a, b: act.nop())
    normalise(nc, d, k, "l1r", xn)
    softmax_keys(nc, d, k, "l1k")
    q = A[:].rearrange("p t n -> p (t n)")[:, 0:T * 128].rearrange("p (t n) -> p t n", n=128)
    heads = A[:].rearrange("p t n -> p (t n)")[:, 0:T * 128].rearrange("p (g n) -> p g n", n=32)
    project(nc, d, k, "l1q", k["w_qkv"][:, :, 0:128], 128, q)

    def q_dve(dve, ts, to_act, to_dve):
        most, total = ts
        dve.tensor_reduce(most[:], heads, AX, ALU.max)
        dve.drain()
        dve.tensor_tensor(heads, heads, most[:].broadcast_to((R, T * 4, 32)), ALU.subtract)
        dve.drain().then_inc(to_act, 1)
        dve.wait_ge(to_dve, 1)
        dve.tensor_reduce(most[:], heads, AX, ALU.add)
        dve.drain()
        dve.reciprocal(total[:], most[:])
        dve.drain()
        dve.tensor_tensor(heads, heads, total[:].broadcast_to((R, T * 4, 32)), ALU.mult)

    def q_act(act, ts, to_act, to_dve):
        act.wait_ge(to_act, 1)
        act.activation(q, q, ACT.Exp).then_inc(to_dve, 1)

    batch(nc, "l1x", [[R, T * 4, 1]] * 2, q_dve, q_act)

    def to_b(dve, t, out, vec, tmp):
        dve.tensor_tensor(B[:, bass.ds(t, 1), :], out, vec[0][:].unsqueeze(1), ALU.add)

    linear_rows(nc, d, k, "l1o", q, k["fold"], 1, copy_in(q), to_b, vectors=[(d["m1_b"], D)])
    row_stats(nc, d, k, "l1p", B, "norm")

    def rms_add(dve, t, vec, tmp):
        dve.tensor_scalar(tmp[0][:], B[:, bass.ds(t, 1), :], col(k["scale"], t), float(D) ** 0.5, ALU.mult, ALU.mult)
        dve.drain()
        dve.tensor_tensor(tmp[1][:], tmp[0][:], vec[0][:].unsqueeze(1), ALU.mult)
        dve.drain()
        dve.tensor_tensor(tmp[0][:], tmp[1][:], xn[:, bass.ds(t, 1), :], ALU.add)
        dve.drain()
        dve.tensor_tensor(x[:, bass.ds(t, 1), :], x[:, bass.ds(t, 1), :], tmp[0][:], ALU.add)

    elementwise(nc, d, k, "l1y", rms_add, vectors=[(d["m1_g"], D)], temps=[[R, 1, D]] * 2)

    row_stats(nc, d, k, "l1t", x, "ln")
    normalise(nc, d, k, "l1u", x, xn)
    project(nc, d, k, "l1v", d["f1_wr"], 1, k["gates"][:, 0:T].rearrange("p (t e) -> p t e", e=1), d["f1_br"])
    rank_gate(nc, d, k, "l1i", NODES // 2 - 1)
    seed(nc, d, k, "l1b", 2, d["f1_b2"], A, base=xn)
    experts(nc, d, k, "l1e", 2, 128, 4, ACT.Gelu_apprx_tanh, d["f1_w1"], d["f1_b1"], d["f1_w2"], A)
    add_to_x(nc, d, k, "l1z", False)


def layer2(nc, d, k):
    x, xn, A, B = k["x"], k["xn"], k["A"], k["B"]
    row_stats(nc, d, k, "l2s", x, "ln")
    normalise(nc, d, k, "l2n", x, xn)
    elu_mix(nc, d, k, "l2m", d["m2_wq"], d["m2_bq"], d["m2_wkv"], d["m2_bkv"], d["m2_wo"], d["m2_bo"], False)

    with Stage(nc, "eps") as s:
        raw, ready = s.sb("raw", [R, 1]), s.sem("ready")
        block = s.block()

        @block.sync
        def _(sp):
            sp.dma_start(raw[:], d["eps"]).then_inc(ready, 16)

        @block.vector
        def _(dve):
            dve.wait_ge(ready, 16)
            dve.tensor_scalar(k["eps2"][:], raw[:], 2.0, None, ALU.add)

    def with_self(dve, t, into, acc, temp):
        dve.scalar_tensor_tensor(into, xn[:, bass.ds(t, 1), :], k["eps2"][:], acc, ALU.mult, ALU.add)

    aggregate(nc, d, k, "l2a", xn, A, with_self)
    edge_hidden(nc, d, k)

    def self_hidden(dve, t, xs, vec, tmp):
        dve.scalar_tensor_tensor(xs[:].unsqueeze(1), vec[0][:].unsqueeze(1), 0.0, B[:, bass.ds(t, 1), :], ALU.max, ALU.add)

    def add_messages(dve, t, out, vec, tmp):
        dve.tensor_tensor(tmp[0][:], out, A[:, bass.ds(t, 1), :], ALU.add)
        dve.drain()
        dve.scalar_tensor_tensor(A[:, bass.ds(t, 1), :], vec[1][:].unsqueeze(1), k["deg1"][:, bass.ds(t, 1)], tmp[0][:],
                                 ALU.mult, ALU.add)

    linear_rows(nc, d, k, "l2h", B, d["ee_w2"], 2, self_hidden, add_messages,
                vectors=[(d["ee_b1"], D), (d["ee_b2"], D)], temps=[[R, 1, D]])
    mlp_ln(nc, d, k)
    add_affine(nc, d, k, "l2b", B, d["bn_g"], d["bn_b"], True)

    row_stats(nc, d, k, "l2t", x, "ln")
    normalise(nc, d, k, "l2u", x)
    gates = k["gates"][:, 0:T * 4].rearrange("p (t e) -> p t e", e=4)
    project(nc, d, k, "l2v", d["gW"], 4, gates, d["gb"])
    gate(nc, d, k, "l2i", 4, "soft_two")
    seed(nc, d, k, "l2c", 4, d["eb3"], A, base_row=d["sb3"])
    small_experts(nc, d, k, A)
    add_to_x(nc, d, k, "l2z", False)


def layer3(nc, d, k):
    x, xn, A, B = k["x"], k["xn"], k["A"], k["B"]
    row_stats(nc, d, k, "l3s", x, "ln")
    normalise(nc, d, k, "l3n", x, xn)
    elu_mix(nc, d, k, "l3m", d["m3_wq"], None, d["m3_wkv"], None, d["m3_wo"], d["m3_bo"], True)

    def mean(dve, t, into, acc, temp):
        dve.tensor_scalar(into, acc, k["rdeg"][:, bass.ds(t, 1)], None, ALU.mult)

    aggregate(nc, d, k, "l3a", xn, A, mean)

    def both(dve, t, xs, vec, tmp):
        dve.tensor_copy(xs[:, 0:D].unsqueeze(1), A[:, bass.ds(t, 1), :])
        dve.tensor_copy(xs[:, D:2 * D].unsqueeze(1), xn[:, bass.ds(t, 1), :])

    def to_b(dve, t, out, vec, tmp):
        dve.tensor_tensor(B[:, bass.ds(t, 1), :], out, vec[0][:].unsqueeze(1), ALU.add)

    linear_rows(nc, d, k, "l3g", None, d["g3_w"], 4, both, to_b, vectors=[(d["g3_b"], D)])
    row_stats(nc, d, k, "l3p", B, "norm")

    def unit(dve, t, vec, tmp):
        dve.tensor_scalar(tmp[0][:], B[:, bass.ds(t, 1), :], col(k["scale"], t), 0.0, ALU.mult, ALU.max)
        dve.drain()
        dve.tensor_tensor(B[:, bass.ds(t, 1), :], tmp[0][:], xn[:, bass.ds(t, 1), :], ALU.add)

    elementwise(nc, d, k, "l3u", unit, temps=[[R, 1, D]])
    add_affine(nc, d, k, "l3b", B, d["g3_gamma"], d["g3_beta"], False)

    row_stats(nc, d, k, "l3t", x, "ln")
    normalise(nc, d, k, "l3w", x, xn)
    gates = k["gates"][:, 0:T * 16].rearrange("p (t e) -> p t e", e=16)
    project(nc, d, k, "l3v", d["f3_gw"], 16, gates, d["f3_gb"])
    gate(nc, d, k, "l3i", 16, "two")
    expert_places(nc, d, k, "l3q", 16, [hot[:, 0:T * 16].rearrange("p (t e) -> p t e", e=16) for hot in k["hots"]])
    sort_rows(nc, d, k, "l3r", xn, 2)
    sorted_experts(nc, d, k, "l3e", 16, 128, 4, d["f3_w1"], d["f3_b1"], d["f3_w2"], d["f3_b2"])

    def gated_sum(dve, t, got):
        to = A[:, bass.ds(t, 1), :]
        dve.scalar_tensor_tensor(to, got[0], k["slot_gate"][0][:, bass.ds(t, 1)], xn[:, bass.ds(t, 1), :], ALU.mult, ALU.add)
        dve.drain()
        dve.scalar_tensor_tensor(to, got[1], k["slot_gate"][1][:, bass.ds(t, 1)], to, ALU.mult, ALU.add)

    unsort_rows(nc, d, k, "l3x", 2, gated_sum)
    add_affine(nc, d, k, "l3y", A, d["f3_gamma"], d["f3_beta"], False)


def program(nc, d, out, layers=4):
    with Stage(nc, "all") as s:
        k = {n: s.sb(n, [R, T, D]) for n in ("x", "xn", "A", "B")}
        k["nc"] = nc
        k["xnT"] = s.sb("xnT", [128, 2, NODES])
        k["ident"] = s.sb("ident", [128, 128])
        for n in ("dst", "src_base", "src_place", "weight"):
            k[n] = s.sb(n, [CH, NCH])
        for n in ("deg", "deg1", "dinv", "rdeg"):
            k[n] = s.sb(n, [R, T])
        k["scale"], k["shift"] = s.sb("scale", [R, T, 1]), s.sb("shift", [R, T, 1])
        k["tile_start"] = s.sb("tile_start", [128, T + 1])
        k["eps2"] = s.sb("eps2", [R, 1])
        k["kvT"], k["fold"], k["ksum"] = s.sb("kvT", [128, 2, 128]), s.sb("fold", [128, 2, D]), s.sb("ksum", [R, D])
        k["w_qkv"] = s.sb("w_qkv", [128, 2, 384])
        k["gates"] = s.sb("gates", [R, T * 32])
        k["hots"] = [s.sb("hots0", [R, T * 32]), s.sb("hots1", [R, T * 16])]
        k["slot_gate"] = [s.sb(f"slot_gate{n}", [R, T]) for n in range(2)]
        k["pos"], k["blocks"] = s.sb("pos", [R, T, 2], I32), s.sb("blocks", [1, 2, 32], I32)
        k["sorted_dram"] = nc.dram_tensor("sorted", ((BLOCKS + 1) * 128, D), F32, kind="Internal").ap()
        k["result_dram"] = nc.dram_tensor("result", (BLOCKS * 128, D), F32, kind="Internal").ap()
        k["scatter_to"] = s.sb("scatter_to", [CH, NCH], I32)
        k["support_dram"] = [nc.dram_tensor(f"support{b}", (NODES + CH, D), F32, kind="Internal").ap() for b in range(2)]
        k["ct_dram"] = nc.dram_tensor("counts", (T, R, NODES), F32, kind="Internal").ap()
        k["plan_dram"] = nc.dram_tensor("plan", (1, 3, T), I32, kind="Internal").ap()
        k["ends_dram"] = nc.dram_tensor("ends", (2 * T, 1), F32, kind="Internal").ap()
        k["line_dram"] = nc.dram_tensor("line", (NODES,), F32, kind="Internal").ap()

        with Stage(nc, "load") as st:
            loaded = st.sem("loaded")
            block = st.block()

            @block.sync
            def _(sp):
                sp.dma_start(k["x"][:], d["x"].rearrange("(t p) n -> p t n", p=R)).then_inc(loaded, 16)
                sp.dma_start(k["tile_start"][:], d["tile_start"]).then_inc(loaded, 16)
                sp.wait_ge(loaded, 32)

        plan_edges(nc, d, k)
        for layer in (layer0, layer1, layer2, layer3)[:layers]:
            layer(nc, d, k)

        with Stage(nc, "store") as st:
            stored = st.sem("stored")
            block = st.block()

            @block.sync
            def _(sp):
                sp.dma_start(out.rearrange("(t p) n -> p t n", p=R), k["x"][:]).then_inc(stored, 16)
                sp.wait_ge(stored, 16)



def lay_out(i):
    def row(v, n=R):
        return np.repeat(np.asarray(v).reshape(1, -1), n, axis=0)

    def chunks(w):
        w = np.asarray(w)
        return w.reshape(-1, 128, w.shape[1]).transpose(1, 0, 2)

    def columns(v, p=128):
        return np.asarray(v).reshape(-1, p).T

    def edges(v, fill):
        v = np.asarray(v)
        return np.concatenate([v, np.full(NCH * CH - EDGES, fill, v.dtype)]).reshape(NCH, CH).T

    def join(*a, axis=1):
        return np.concatenate([np.asarray(v) for v in a], axis=axis)

    E0, E3 = i["L0_ffn_W1"].shape[0], i["L3_ffn_w1"].shape[0]
    attr = np.concatenate([np.asarray(i["edge_attr_64"]), np.zeros((NCH * CH - EDGES, EDIM), np.float32)])
    kg, kb, vg, vb = (np.tile(np.asarray(i["L0_mix_ln_" + n]), 4) for n in ("k_g", "k_b", "v_g", "v_b"))
    mem = np.asarray(i["L1_mix_mem_kv"])
    w3kv = np.asarray(i["L3_mix_Wkv"])
    blocks = np.arange(128)
    d = {
        "x": i["x"], "src": edges(i["src"], 0), "src_row": np.ascontiguousarray(edges(i["src"], 0).T).reshape(1, -1),
        "own_row": (NODES + np.arange(CH, dtype=np.float32)).reshape(CH, 1),
        "before": (np.arange(CH) < np.arange(CH)[:, None]).astype(np.float32), "dst": edges(i["dst"], -1), "weight": edges(i["edge_weight"], 0),
        "attr": np.concatenate([attr.T, np.ones((1, NCH * CH), np.float32)]),
        "pair_up": row(np.arange(NCH) // 2 + 1, CH).astype(np.float32),
        "pair_down": row(PAIRS - np.arange(NCH) // 2, CH).astype(np.float32),
        "ident": np.eye(128, dtype=np.float32),
        "iota16": row(np.arange(WIDE), CH).astype(np.int16), "iota_r": row(np.arange(R), CH).astype(np.float32),
        "tile_start": row(np.arange(T + 1) * R, 128).astype(np.float32),
        "mask64": (blocks[:, None] // 64 == blocks // 64).astype(np.float32),
        "mask32": (blocks[:, None] // 32 == blocks // 32).astype(np.float32),
        "above": (np.arange(R)[:, None] < np.arange(R)).astype(np.float32),
        "below": (np.arange(R) < np.arange(R)[:, None]).astype(np.float32),
        "down": row(32 - np.arange(32)).astype(np.float32),
        "zero_row": np.zeros((R, 2 * D), np.float32),
        "g0_w": chunks(i["L0_gnn_W"]), "g0_b": row(i["L0_gnn_b"]),
        "m0_wkv": chunks(join(np.asarray(i["L0_mix_wk"]).T, np.asarray(i["L0_mix_wv"]).T)),
        "m0_gain": row(np.concatenate([kg, vg])), "m0_shift": row(np.concatenate([kb, vb])),
        "m0_wo": chunks(np.asarray(i["L0_mix_wo"]).T), "m0_wq": chunks(i["L0_mix_wq"]), "m0_bo": row(i["L0_mix_bo"]),
        "r0_w": chunks(np.asarray(i["L0_ffn_router_w"]).T), "r0_b": row(i["L0_ffn_router_b"]),
        "f0_w1": np.asarray(i["L0_ffn_W1"]).reshape(E0, 2, 128, 64).transpose(0, 2, 1, 3),
        "f0_b1": np.asarray(i["L0_ffn_b1"]).T, "f0_w2": np.asarray(i["L0_ffn_W2"]).reshape(E0, 64, 1, D),
        "f0_b2": i["L0_ffn_b2"],
        "w_qkv": chunks(i["L1_mix_w_qkv"]), "g_pre": columns(i["L1_mix_g_pre"]), "w_out": i["L1_mix_w_out"],
        "mem_k": mem[0].reshape(128, 4), "mem_v": mem[1].reshape(128, 4).T,
        "m1_b": row(i["L1_mix_b_out"]), "m1_g": row(i["L1_mix_g_out"]),
        "f1_wr": chunks(i["L1_ffn_wr"]), "f1_br": row(i["L1_ffn_br"]),
        "f1_w1": np.asarray(i["L1_ffn_w1"]).reshape(2, 128, 2, 512).transpose(2, 1, 0, 3),
        "f1_b1": columns(i["L1_ffn_b1"]),
        "f1_w2": np.asarray(i["L1_ffn_w2"]).reshape(2, 4, 128, D).transpose(0, 2, 1, 3),
        "f1_b2": np.stack([np.asarray(i["L1_ffn_b2"]), np.zeros(D, np.float32)]),
        "m2_wq": chunks(i["L2_mix_wq"]), "m2_bq": row(i["L2_mix_bq"]),
        "m2_wkv": chunks(join(i["L2_mix_wk"], i["L2_mix_wv"])),
        "m2_bkv": row(join(i["L2_mix_bk"], i["L2_mix_bv"], axis=0)),
        "m2_wo": chunks(i["L2_mix_wo"]), "m2_bo": row(i["L2_mix_bo"]),
        "eps": row(i["L2_gnn_eps"]),
        "ee_w1": join(i["L2_gnn_ee_w1"], np.asarray(i["L2_gnn_ee_b1"]).reshape(1, -1), axis=0),
        "ee_b1": row(i["L2_gnn_ee_b1"]), "ee_w2": chunks(i["L2_gnn_ee_w2"]), "ee_b2": row(i["L2_gnn_ee_b2"]),
        "m_w1": chunks(i["L2_gnn_w1"]), "m_w2": chunks(i["L2_gnn_w2"]), "m_w3": chunks(i["L2_gnn_w3"]),
        "m_b1": row(i["L2_gnn_b1"]), "m_b2": row(i["L2_gnn_b2"]), "m_b3": row(i["L2_gnn_b3"]),
        "m_g1": columns(i["L2_gnn_g1"]), "m_be1": columns(i["L2_gnn_be1"]),
        "m_g2": columns(i["L2_gnn_g2"]), "m_be2": columns(i["L2_gnn_be2"]),
        "bn_g": row(i["L2_gnn_bn_g"]), "bn_b": row(i["L2_gnn_bn_b"]),
        "gW": chunks(i["L2_ffn_gW"]), "gb": row(i["L2_ffn_gb"]), "eb3": i["L2_ffn_eb3"], "sb3": row(i["L2_ffn_sb3"]),
        "s_w1": chunks(i["L2_ffn_sW1"]), "s_w2": chunks(i["L2_ffn_sW2"]), "s_w3": i["L2_ffn_sW3"],
        "e_w1": np.asarray(i["L2_ffn_eW1"]).reshape(4, 2, 128, 128).transpose(2, 0, 1, 3),
        "e_w2": np.asarray(i["L2_ffn_eW2"]).transpose(1, 0, 2), "e_w3": np.asarray(i["L2_ffn_eW3"]).transpose(1, 0, 2),
        "s_b1": columns(i["L2_ffn_sb1"]), "s_b2": columns(i["L2_ffn_sb2"]),
        "e_b1": np.asarray(i["L2_ffn_eb1"]).T, "e_b2": np.asarray(i["L2_ffn_eb2"]).T,
        "m3_wq": chunks(np.asarray(i["L3_mix_Wq"]).T), "m3_wkv": chunks(w3kv.T),
        "m3_wo": chunks(np.asarray(i["L3_mix_Wproj"]).T), "m3_bo": row(i["L3_mix_bproj"]),
        "g3_w": chunks(join(np.asarray(i["L3_gnn_W_l"]).T, np.asarray(i["L3_gnn_W_r"]).T, axis=0)),
        "g3_b": row(i["L3_gnn_b_l"]), "g3_gamma": row(i["L3_gnn_gamma"]), "g3_beta": row(i["L3_gnn_beta"]),
        "f3_gw": chunks(i["L3_ffn_gate_w"]), "f3_gb": row(i["L3_ffn_gate_b"]),
        "f3_w1": np.asarray(i["L3_ffn_w1"]).reshape(E3, 2, 128, 512).transpose(0, 2, 1, 3),
        "f3_b1": columns(np.asarray(i["L3_ffn_b1"]).reshape(-1)),
        "f3_w2": np.asarray(i["L3_ffn_w2"]).reshape(E3, 4, 128, D).transpose(0, 2, 1, 3),
        "f3_b2": i["L3_ffn_b2"], "f3_gamma": row(i["L3_ffn_gamma"]), "f3_beta": row(i["L3_ffn_beta"]),
    }
    for n in range(3):
        d[f"g1_w{n}"], d[f"g1_b{n}"] = chunks(i[f"L1_gnn_W{n + 1}"]), row(i[f"L1_gnn_b{n + 1}"])
    return {n: np.ascontiguousarray(v) for n, v in d.items()}


def kernel(**inputs):
    import concourse.bacc as bacc
    from concourse.bass_utils import run_bass_kernel_spmd as run

    nc = bacc.Bacc("TRN2", target_bir_lowering=False, num_devices=1)
    arrays, d = {}, {}
    for name, a in lay_out(inputs).items():
        arrays[f"in_{name}"] = a
        d[name] = nc.dram_tensor(f"in_{name}", a.shape, mybir.dt.from_np(a.dtype), kind="ExternalInput").ap()
    out = nc.dram_tensor("out_rows", (NODES, D), F32, kind="ExternalOutput").ap()
    program(nc, d, out, LAYERS)
    return run(nc, [arrays], core_ids=[0]).results[0]["out_rows"]


LAYERS = 4
```

```python
from contextlib import ExitStack

import numpy as np

import concourse.bass as bass
from concourse import mybir

F32, BF16, I32, I16 = mybir.dt.float32, mybir.dt.bfloat16, mybir.dt.int32, mybir.dt.int16
ALU = mybir.AluOpType
ACT = mybir.ActivationFunctionType
AX = mybir.AxisListType.X

NODES, D = 3125, 256
T, R = 25, 125
EDGES, CH = 50000, 128
PAIRS = -(-EDGES // (2 * CH))
NCH = 2 * PAIRS
WIDE = -(-NODES // 8) * 8
EDIM = 64
LN_EPS = 1e-5
BLOCKS = max(NODES // 128 + 32, 2 * NODES // 128 + 16) + 1
CTB = 7
CENTRED = [(g * 500, min(500, NODES - g * 500)) for g in range(CTB)]


class Stage:

    def __init__(self, nc, name):
        self.nc, self.name, self.stack, self.sems = nc, name, ExitStack(), []

    def __enter__(self):
        self.stack.__enter__()
        return self

    def __exit__(self, *e):
        self.stack.__exit__(*e)
        if self.sems and e[0] is None:
            self.nc.clear_and_free_semaphores(self.sems)
            self.nc.all_engine_barrier(sem_only=True)

    def sb(self, name, shape, dt=F32):
        return self.stack.enter_context(self.nc.sbuf_tensor(f"{self.name}_{name}", shape, dt))

    def ps(self, name, shape, dt=F32):
        return self.stack.enter_context(self.nc.psum_tensor(f"{self.name}_{name}", shape, dt))

    def sem(self, name):
        self.sems.append(self.nc.alloc_semaphore(f"{self.name}_{name}"))
        return self.sems[-1]

    def block(self):
        return self.stack.enter_context(self.nc.Block())


def tiles(eng, body):
    with eng.Fori(0, T // 2) as i:
        body(2 * i, 0)
        body(2 * i + 1, 1)
    body(T - 1, 0)


def pipelined(first, second):
    def emit(eng):
        first(0, 0)
        with eng.Fori(0, T // 2) as i:
            first(2 * i + 1, 1)
            second(2 * i, 0)
            first(2 * i + 2, 0)
            second(2 * i + 1, 1)
        second(T - 1, 0)
    return emit


def ahead(first, second, first_leads):
    def emit(eng):
        def both(t, b):
            for step, tile in ((first, t + 2), (second, t)) if first_leads else ((second, t), (first, t + 2)):
                step(tile, b)

        first(0, 0)
        first(1, 1)
        with eng.Fori(0, (T - 3) // 2) as i:
            both(2 * i, 0)
            both(2 * i + 1, 1)
        both(T - 3, 0)
        second(T - 2, 1)
        second(T - 1, 0)
    return emit


def groups(eng, body):
    with eng.Fori(0, 5) as i:
        body(5 * i, 3, 2 * i, 0)
        body(5 * i + 3, 2, 2 * i + 1, 1)


def settle(eng, started):
    eng.sem_inc(started, 1)


def rows(t, n=1):
    return bass.ds(t * R, n * R)



def plan_edges(nc, d, k):
    with Stage(nc, "plan") as s:
        dst_i, src_i = s.sb("dst_i", [CH, NCH], I32), s.sb("src_i", [CH, NCH], I32)
        pair_up, pair_down = s.sb("pair_up", [CH, NCH]), s.sb("pair_down", [CH, NCH])
        rel, over, inside = (s.sb(n, [CH, NCH]) for n in ("rel", "over", "inside"))
        ends = s.sb("ends", [CH, 2 * T])
        most, spare = s.sb("most", [2 * T, 1]), s.sb("spare", [2 * T, 1])
        line = s.sb("line", [1, 2, T])
        plan = s.sb("plan", [1, 3, T])
        ones = s.sb("ones", [1, T])
        cum = s.sb("cum", [1, T])
        plan_i = s.sb("plan_i", [1, 3, T], I32)
        ends_t = s.ps("ends_t", [CH, CH])
        zero_rows, zeroed, cleared = s.sb("zero_rows", [CH, D]), s.sem("zeroed"), s.sem("cleared")
        loaded, ends_ready, turned, most_ready, stored, back = map(
            s.sem, ("loaded", "ends_ready", "turned", "most_ready", "stored", "back"))
        planned = s.sem("planned")
        block = s.block()

        @block.sync
        def _(sp):
            sp.dma_start(dst_i[:], d["dst"]).then_inc(loaded, 16)
            sp.dma_start(src_i[:], d["src"]).then_inc(loaded, 16)
            sp.dma_start(pair_up[:], d["pair_up"]).then_inc(loaded, 16)
            sp.dma_start(pair_down[:], d["pair_down"]).then_inc(loaded, 16)
            sp.dma_start(k["weight"][:], d["weight"]).then_inc(loaded, 16)
            sp.dma_start(k["ident"][:], d["ident"]).then_inc(loaded, 16)
            sp.wait_ge(most_ready, 1)
            sp.dma_start(k["ends_dram"], most[:]).then_inc(stored, 16)
            sp.wait_ge(stored, 16)
            sp.dma_start(line[:], k["ends_dram"].rearrange("(a b t) o -> a b (t o)", a=1, b=2)).then_inc(back, 16)
            sp.wait_ge(planned, 1)
            sp.dma_start(k["plan_dram"], plan_i[:]).then_inc(stored, 16)
            sp.wait_ge(stored, 32)

        @block.scalar
        def _(act):
            act.wait_ge(cleared, 1)
            act.wait_ge(loaded, 96)
            act.dma_start(k["sorted_dram"].rearrange("(a p) n -> p a n", p=128),
                          zero_rows[:].unsqueeze(1).broadcast_to((128, BLOCKS + 1, D))).then_inc(zeroed, 16)
            act.dma_start(k["result_dram"].rearrange("(a p) n -> p a n", p=128),
                          zero_rows[:].unsqueeze(1).broadcast_to((128, BLOCKS, D))).then_inc(zeroed, 16)
            act.wait_ge(zeroed, 32)

        @block.vector
        def _(dve):
            dve.memset(zero_rows[:], 0.0).then_inc(cleared, 1)
            dve.wait_ge(loaded, 96)
            dve.tensor_copy(k["dst"][:], dst_i[:])
            dve.tensor_copy(over[:], src_i[:])
            dve.memset(ones[:], 1.0)
            dve.drain()
            dve.tensor_scalar(k["src_base"][:], over[:], float(R), float(R), ALU.is_ge, ALU.mult)
            dve.drain()
            for t in range(2, T):
                dve.tensor_scalar(inside[:], over[:], float(t * R), float(R), ALU.is_ge, ALU.mult)
                dve.drain()
                dve.tensor_tensor(k["src_base"][:], k["src_base"][:], inside[:], ALU.add)
                dve.drain()
            dve.tensor_tensor(k["src_place"][:], over[:], k["src_base"][:], ALU.subtract)
            dve.drain()
            for t in range(T):
                dve.tensor_scalar(over[:], k["dst"][:], float(t * R), None, ALU.is_ge)
                dve.tensor_scalar(rel[:], k["dst"][:], float((t + 1) * R), None, ALU.is_lt)
                dve.drain()
                dve.tensor_tensor(inside[:], over[:], rel[:], ALU.mult)
                dve.drain()
                dve.tensor_tensor(over[:], inside[:], pair_up[:], ALU.mult)
                dve.tensor_tensor(rel[:], inside[:], pair_down[:], ALU.mult)
                dve.drain()
                dve.tensor_reduce(ends[:, t:t + 1], over[:], AX, ALU.max)
                dve.tensor_reduce(ends[:, T + t:T + t + 1], rel[:], AX, ALU.max)
                dve.drain()
            dve.drain().then_inc(ends_ready, 1)
            dve.wait_ge(turned, 1)
            dve.tensor_reduce(most[:], ends_t[0:2 * T, :], AX, ALU.max).then_inc(most_ready, 1)
            dve.wait_ge(back, 16)
            dve.tensor_scalar(plan[:, 0, :], line[:, 1, :], -1.0, float(PAIRS), ALU.mult, ALU.add)
            dve.drain()
            dve.tensor_tensor(plan[:, 1, :], line[:, 0, :], plan[:, 0, :], ALU.subtract)
            dve.tensor_scalar(plan[:, 0, :], plan[:, 0, :], float(PAIRS - 1), None, ALU.min)
            dve.drain()
            dve.tensor_scalar(plan[:, 1, :], plan[:, 1, :], 1.0, None, ALU.max)
            dve.drain()
            dve.tensor_tensor_scan(cum[:], ones[:], plan[:, 1, :], 0.0, ALU.mult, ALU.add)
            dve.drain()
            dve.tensor_tensor(plan[:, 2, :], cum[:], plan[:, 1, :], ALU.subtract)
            dve.drain()
            dve.tensor_copy(plan_i[:], plan[:]).then_inc(planned, 1)

        @block.tensor
        def _(pe):
            pe.wait_ge(ends_ready, 1)
            pe.transpose(ends_t[0:2 * T, :], ends[:], k["ident"][:]).then_inc(turned, 1)


def walk(eng, k, plan, body_tile_start, body_pair, body_tile_end, most=PAIRS):
    with eng.Fori(0, T) as t:
        first = eng.value_load(plan[0:1, 0, bass.ds(t, 1)], min_val=0, max_val=most - 1)
        count = eng.value_load(plan[0:1, 1, bass.ds(t, 1)], min_val=1, max_val=most)
        before = eng.value_load(plan[0:1, 2, bass.ds(t, 1)], min_val=0, max_val=T * most)
        body_tile_start(t)
        with eng.Fori(0, count) as j:
            pair = k["nc"].s_assert_within(first + j, 0, most - 1, skip_runtime_bounds_check_because="the plan keeps first + count inside the edges")
            body_pair(t, pair, before + j)
        body_tile_end(t)


def first_places(nc, d, k):
    with Stage(nc, "first") as s:
        LOT = 14
        row = [s.sb(f"row{b}", [CH, LOT * CH], I32) for b in range(2)]
        src_i = s.sb("src_i", [CH, NCH], I32)
        src, moved = s.sb("src", [CH, NCH]), s.sb("moved", [CH, NCH])
        own, before = s.sb("own", [CH, 1]), s.sb("before", [CH, CH])
        same = s.sb("same", [CH, LOT, CH])
        count = s.sb("count", [CH, NCH])
        loaded, row0, row1, row_free = map(s.sem, ("loaded", "row0", "row1", "row_free"))
        block = s.block()

        @block.sync
        def _(sp):
            sp.dma_start(src_i[:], d["src"]).then_inc(loaded, 16)
            sp.dma_start(own[:], d["own_row"]).then_inc(loaded, 16)
            sp.dma_start(before[:], d["before"]).then_inc(loaded, 16)
            with sp.Fori(0, NCH // (2 * LOT)) as i:
                for b in range(2):
                    sp.wait_ge(row_free, 2 * i + (b + 1))
                    sp.dma_start(row[b][:], d["src_row"][:, bass.ds((2 * i + b) * LOT * CH, LOT * CH)].broadcast_to((CH, LOT * CH))
                                 ).then_inc(row0 if b == 0 else row1, 16)
            sp.wait_ge(loaded, 48)

        @block.vector
        def _(dve):
            dve.sem_inc(row_free, 2)
            dve.wait_ge(loaded, 48)
            dve.tensor_copy(src[:], src_i[:])
            dve.memset(count[:], 0.0)
            dve.drain()
            with dve.Fori(0, NCH // (2 * LOT)) as i:
                for b in range(2):
                    dve.wait_ge(row0 if b == 0 else row1, 16 * i + 16)
                    for h in range(LOT):
                        dve.scalar_tensor_tensor(same[:, h, :], row[b][:, h * CH:(h + 1) * CH],
                                                 src[:, bass.ds(2 * LOT * i + (b * LOT + h), 1)], before[:],
                                                 ALU.is_equal, ALU.mult,
                                                 accum_out=count[:, bass.ds(2 * LOT * i + (b * LOT + h), 1)])
                    dve.drain().then_inc(row_free, 1)
            dve.drain()
            dve.tensor_scalar(moved[:], src[:], own[:], -1.0, ALU.subtract, ALU.mult)
            dve.tensor_scalar(count[:], count[:], 1.0, None, ALU.min)
            dve.drain()
            dve.tensor_tensor(moved[:], moved[:], count[:], ALU.mult)
            dve.drain()
            dve.tensor_tensor(src[:], src[:], moved[:], ALU.add)
            dve.drain()
            dve.tensor_copy(k["scatter_to"][:], src[:])


def scatter_and_count(nc, d, k):
    with Stage(nc, "edge") as s:
        plan = s.sb("plan", [1, 3, T], I32)
        iota = s.sb("iota", [CH, WIDE], I16)
        iota_r = s.sb("iota_r", [CH, R])
        rel, spare = s.sb("rel", [CH, NCH]), s.sb("spare", [CH, NCH])
        key, valid = s.sb("key", [CH, NCH]), s.sb("valid", [CH, NCH])
        src = s.sb("src", [CH, NCH])
        row_now = [s.sb(f"row_now{b}", [CH, 1], I32) for b in range(2)]
        src_row = [s.sb(f"src_row{b}", [CH, CH], I32) for b in range(2)]
        row_in = [s.sem(f"row_in{b}") for b in range(2)]
        onehot = [s.sb(f"onehot{b}", [CH, WIDE], BF16) for b in range(2)]
        place = [s.sb(f"place{b}", [CH, R], BF16) for b in range(2)]
        to_dst = [s.sb(f"to_dst{b}", [CH, R]) for b in range(2)]
        same = [s.sb(f"same{b}", [CH, CH]) for b in range(2)]
        P = [s.sb(f"P{b}", [R, CH]) for b in range(2)]
        S = [s.sb(f"S{b}", [CH, D]) for b in range(2)]
        zeros = s.sb("zeros", [CH, 512], BF16)
        zero_rows = s.sb("zero_rows", [CH, D])
        ones = s.sb("ones", [CH, 1])
        counts = s.sb("counts", [R, NODES])
        ct_ps = s.ps("ct_ps", [R, CTB, 512])
        deg_ps = ct_ps[:, CTB - 1, 500:501]
        ps = s.ps("ps", [CH, 512])
        P_ps = [ps[0:R, b * CH:(b + 1) * CH] for b in range(2)]
        S_ps = ps[:, 256:512]
        loaded, setup, row_free, onehot_ready, used, P_ready, P_kept, S_ready, S_kept = map(
            s.sem, ("loaded", "setup", "row_free", "onehot_ready", "used", "P_ready", "P_kept", "S_ready",
                    "S_kept"))
        started, row_copied = s.sem("started"), s.sem("row_copied")
        scattered = [s.sem(f"scattered{b}") for b in range(2)]
        tile_done, evac_dve, evac_act, stored, gone = map(
            s.sem, ("tile_done", "evac_dve", "evac_act", "stored", "gone"))
        block = s.block()

        def nothing(t):
            pass

        @block.sync
        def _(sp):
            sp.dma_start(plan[:], k["plan_dram"]).then_inc(loaded, 16)
            sp.dma_start(iota[:], d["iota16"]).then_inc(loaded, 16)
            sp.dma_start(iota_r[:], d["iota_r"]).then_inc(loaded, 16)
            sp.wait_ge(loaded, 48)
            sp.wait_ge(setup, 1)

            def pair(t, c, n):
                for b in range(2):
                    sp.wait_ge(row_free, 2 * n + (b + 1))
                    sp.dma_start(src_row[b][:], d["src_row"][:, bass.ds((c * 2 + b) * CH, CH)].broadcast_to((CH, CH))
                                 ).then_inc(row_in[b], 16)

            walk(sp, k, plan, nothing, pair, nothing)

        @block.gpsimd
        def _(pool):
            pool.wait_ge(loaded, 48)
            pool.wait_ge(setup, 1)
            for b in range(2):
                pool.dma_start(k["support_dram"][b][0:25 * CH].rearrange("(a p) n -> p a n", p=CH),
                               zero_rows[:].unsqueeze(1).broadcast_to((CH, 25, D))).then_inc(gone, 16)
            pool.wait_ge(gone, 32)
            for b in range(2):
                pool.dma_start(k["support_dram"][b][25 * CH:25 * CH + 53], zero_rows[0:53, :]).then_inc(scattered[b], 16)

            def pair(t, c, n):
                for b in range(2):
                    pool.wait_ge(scattered[b], 16 * n + 16)
                    pool.tensor_copy(row_now[b][:], k["scatter_to"][:, bass.ds(2 * c + b, 1)]).then_inc(row_copied, 1)
                    pool.wait_ge(row_copied, 2 * n + (b + 1))
                    pool.wait_ge(S_kept, 2 * n + (b + 2))
                    settle(pool, started)
                    pool.indirect_dma_start(k["support_dram"][b], bass.IndirectOffsetOnAxis(ap=row_now[b][:, 0:1], axis=0),
                                            S[b][:], None, compute_op=ALU.add).then_inc(scattered[b], 16)

            walk(pool, k, plan, nothing, pair, nothing)
            last = pool.value_load(plan[0:1, 1, T - 1:T], min_val=1, max_val=PAIRS)
            base = pool.value_load(plan[0:1, 2, T - 1:T], min_val=0, max_val=T * PAIRS)
            for b in range(2):
                pool.wait_ge(scattered[b], 16 * (base + last) + 16)

        @block.scalar
        def _(act):
            act.wait_ge(loaded, 48)

            def pair(t, c, n):
                for b in range(2):
                    act.wait_ge(P_ready, 2 * n + (b + 1))
                    act.activation(P[b][:], P_ps[b], ACT.Copy).then_inc(P_kept, 1)
                    act.wait_ge(S_ready, 2 * n + (b + 1))
                    act.wait_ge(scattered[b], 16 * n + 16)
                    act.activation(S[b][:], S_ps, ACT.Copy).then_inc(S_kept, 1)

            def end(t):
                act.wait_ge(tile_done, t + 1)
                act.wait_ge(stored, 16 * t + 16)
                for g in range(4, CTB):
                    a, n = CENTRED[g]
                    act.activation(counts[:, a:a + n], ct_ps[:, g, 0:n], ACT.Copy)
                act.activation(k["deg"][:, bass.ds(t, 1)], deg_ps, ACT.Copy)
                act.drain().then_inc(evac_act, 1)
                act.wait_ge(evac_act, t + 2)
                act.wait_ge(evac_dve, t + 2)
                settle(act, started)
                act.dma_start(k["ct_dram"][bass.ds(t, 1)].rearrange("a p n -> (a p) n"), counts[:]).then_inc(stored, 16)

            act.sem_inc(stored, 16)
            walk(act, k, plan, nothing, pair, end)
            act.wait_ge(stored, 16 * T + 16)

        @block.vector
        def _(dve):
            dve.sem_inc(row_free, 2)
            dve.wait_ge(loaded, 48)
            dve.memset(zeros[:], 0.0)
            dve.memset(zero_rows[:], 0.0)
            dve.memset(ones[:], 1.0)
            dve.tensor_tensor(src[:], k["src_base"][:], k["src_place"][:], ALU.add)
            dve.drain().then_inc(setup, 1)

            def start(t):
                dve.tensor_scalar(rel[:], k["dst"][:], k["tile_start"][:, bass.ds(t, 1)], None, ALU.subtract)
                dve.drain()
                dve.tensor_tensor(key[:], rel[:], k["src_base"][:], ALU.add)
                dve.tensor_scalar(spare[:], rel[:], float(R), None, ALU.is_lt)
                dve.drain()
                dve.scalar_tensor_tensor(valid[:], rel[:], 0.0, spare[:], ALU.is_ge, ALU.mult)
                dve.drain()

            start(0)

            def pair(t, c, n):
                for b in range(2):
                    dve.wait_ge(used, 2 * n + (b + 1))
                    at = bass.ds(2 * c + b, 1)
                    dve.tensor_scalar(to_dst[b][:], iota_r[:], rel[:, at], None, ALU.is_equal)
                    dve.wait_ge(row_in[b], 16 * n + 16)
                    settle(dve, started)
                    dve.tensor_scalar(same[b][:], src_row[b][:], src[:, at], k["weight"][:, at],
                                      ALU.is_equal, ALU.mult).then_inc(row_free, 1)
                    dve.tensor_scalar(place[b][:], iota[:, 0:R], k["src_place"][:, at], valid[:, at], ALU.is_equal, ALU.mult)
                    dve.tensor_scalar(onehot[b][:], iota[:], key[:, at], None, ALU.is_equal)
                    dve.drain().then_inc(onehot_ready, 1)

            def end(t):
                start(t + 1)
                dve.wait_ge(tile_done, t + 1)
                dve.wait_ge(stored, 16 * t + 16)
                for g in range(4):
                    a, n = CENTRED[g]
                    dve.tensor_copy(counts[:, a:a + n], ct_ps[:, g, 0:n])
                dve.drain().then_inc(evac_dve, 1)

            walk(dve, k, plan, nothing, pair, end)

        @block.tensor
        def _(pe):
            pe.wait_ge(loaded, 48)
            pe.wait_ge(setup, 1)
            pe.sem_inc(used, 2)
            pe.sem_inc(evac_dve, 1)
            pe.sem_inc(evac_act, 1)
            pe.sem_inc(S_kept, 1)

            def start(t):
                pe.wait_ge(evac_dve, t + 1)
                pe.wait_ge(evac_act, t + 1)
                for g in range(CTB):
                    pe.matmul(ct_ps[:, g, :], zeros[:, 0:R], zeros[:, 0:512], start=True, stop=False, skip_group_check=True)

            def pair(t, c, n):
                for b in range(2):
                    pe.wait_ge(onehot_ready, 2 * n + (b + 1))
                    for g, (a, m) in enumerate(CENTRED):
                        if g == 4:
                            pe.wait_ge(S_kept, 2 * n + (b + 1))
                            pe.matmul(P_ps[b], to_dst[b][:], same[b][:], start=True, stop=True).then_inc(P_ready, 1)
                        pe.matmul(ct_ps[:, g, 0:m], place[b][:], onehot[b][:, a:a + m], start=False, stop=False,
                                  skip_group_check=True)
                    pe.matmul(deg_ps, to_dst[b][:], ones[:], start=False, stop=False,
                              skip_group_check=True).then_inc(used, 1)
                    pe.wait_ge(P_kept, 2 * n + (b + 1))
                    pe.matmul(S_ps, P[b][:], k["xn"][:, bass.ds(t, 1), :], start=True, stop=True).then_inc(S_ready, 1)

            def end(t):
                pe.drain().then_inc(tile_done, 1)

            walk(pe, k, plan, start, pair, end)


def collect_support(nc, d, k):
    with Stage(nc, "collect") as s:
        loaded = s.sem("loaded")
        block = s.block()

        @block.sync
        def _(sp):
            for b, to in enumerate((k["A"], k["B"])):
                sp.dma_start(to[:], k["support_dram"][b][0:NODES].rearrange("(t p) n -> p t n", p=R)).then_inc(loaded, 16)

        @block.vector
        def _(dve):
            dve.wait_ge(loaded, 32)
            dve.tensor_tensor(k["A"][:], k["A"][:], k["B"][:], ALU.add)


def edge_hidden(nc, d, k):
    Q, QUADS = 4, NCH // 4
    with Stage(nc, "hid") as s:
        pairs_of = s.sb("pairs_of", [1, 3, T], I32)
        ends = s.sb("ends", [1, T], I32)
        plan, plan_f = s.sb("plan", [1, 3, T], I32), s.sb("plan_f", [1, 3, T])
        ones, cum = s.sb("ones", [1, T]), s.sb("cum", [1, T])
        iota_r = s.sb("iota_r", [CH, R])
        rel = s.sb("rel", [CH, NCH])
        attr = [s.sb(f"attr{b}", [EDIM + 1, CH]) for b in range(Q)]
        w1 = s.sb("w1", [EDIM + 1, D])
        to_dst = [s.sb(f"to_dst{b}", [CH, R]) for b in range(Q)]
        hidden = [s.sb(f"hidden{b}", [CH, D]) for b in range(Q)]
        hid_ps = [s.ps(f"hid_ps{b}", [CH, 512]) for b in range(Q)]
        sum_ps = s.ps("sum_ps", [R, 512])
        zeros = s.sb("zeros", [CH, D], BF16)
        loaded, hid_ready, hid_act, used, onehot_ready, tile_done, evac, setup, planned = map(
            s.sem, ("loaded", "hid_ready", "hid_act", "used", "onehot_ready", "tile_done", "evac", "setup", "planned"))
        attr_in = [s.sem(f"attr_in{b}") for b in range(Q)]
        block = s.block()

        def nothing(t):
            pass

        def quads(eng, start, body, end):
            eng.wait_ge(planned, 1)
            walk(eng, k, plan, start, body, end, QUADS)

        @block.sync
        def _(sp):
            sp.dma_start(pairs_of[:], k["plan_dram"]).then_inc(loaded, 16)
            sp.dma_start(iota_r[:], d["iota_r"]).then_inc(loaded, 16)
            sp.dma_start(w1[:], d["ee_w1"]).then_inc(loaded, 16)
            sp.wait_ge(loaded, 48)

            def quad(t, c, n):
                for b in range(Q):
                    sp.wait_ge(hid_ready, Q * n + (b + 1))
                    sp.dma_start(attr[b][:], d["attr"][:, bass.ds((Q * c + b) * CH, CH)]).then_inc(attr_in[b], 16)

            quads(sp, nothing, quad, nothing)

        @block.scalar
        def _(act):
            act.wait_ge(loaded, 48)

            def quad(t, c, n):
                for b in range(Q):
                    act.wait_ge(hid_ready, Q * n + (b + 1 + Q))
                    act.wait_ge(used, Q * n + (b + 1))
                    act.activation(hidden[b][:], hid_ps[b][:, 0:D], ACT.Relu).then_inc(hid_act, 1)

            quads(act, nothing, quad, nothing)

        @block.vector
        def _(dve):
            dve.wait_ge(loaded, 48)
            dve.memset(zeros[:], 0.0).then_inc(setup, 1)
            dve.memset(ones[:], 1.0)
            dve.tensor_tensor(ends[:], pairs_of[:, 0, :], pairs_of[:, 1, :], ALU.add)
            dve.drain()
            dve.tensor_scalar(ends[:], ends[:], 1.0, None, ALU.subtract)
            dve.drain()
            dve.tensor_scalar(plan[:, 0, :], pairs_of[:, 0, :], 1, None, ALU.arith_shift_right)
            dve.tensor_scalar(plan[:, 1, :], ends[:], 1, None, ALU.arith_shift_right)
            dve.drain()
            dve.tensor_copy(plan_f[:, 0:2, :], plan[:, 0:2, :])
            dve.drain()
            dve.tensor_tensor(plan_f[:, 1, :], plan_f[:, 1, :], plan_f[:, 0, :], ALU.subtract)
            dve.drain()
            dve.tensor_scalar(plan_f[:, 1, :], plan_f[:, 1, :], 1.0, None, ALU.add)
            dve.drain()
            dve.tensor_tensor_scan(cum[:], ones[:], plan_f[:, 1, :], 0.0, ALU.mult, ALU.add)
            dve.drain()
            dve.tensor_tensor(plan_f[:, 2, :], cum[:], plan_f[:, 1, :], ALU.subtract)
            dve.drain()
            dve.tensor_copy(plan[:], plan_f[:])
            dve.drain().then_inc(planned, 1)

            def start(t):
                dve.drain()
                dve.tensor_scalar(rel[:], k["dst"][:], k["tile_start"][:, bass.ds(t, 1)], None, ALU.subtract)
                dve.drain()

            def quad(t, c, n):
                for b in range(Q):
                    dve.wait_ge(used, Q * n + (b + 1))
                    dve.tensor_scalar(to_dst[b][:], iota_r[:], rel[:, bass.ds(Q * c + b, 1)], None,
                                      ALU.is_equal).then_inc(onehot_ready, 1)

            def end(t):
                dve.wait_ge(tile_done, t + 1)
                dve.tensor_copy(k["B"][:, bass.ds(t, 1), :],
                                sum_ps[:, 0:D].rearrange("p (a n) -> p a n", a=1)).then_inc(evac, 1)

            quads(dve, start, quad, end)

        @block.tensor
        def _(pe):
            pe.wait_ge(loaded, 48)
            pe.wait_ge(setup, 1)
            pe.sem_inc(used, Q)
            pe.sem_inc(evac, 1)
            pe.sem_inc(hid_act, Q)
            pe.sem_inc(hid_ready, Q)

            def start(t):
                pe.wait_ge(evac, t + 1)
                pe.matmul(sum_ps[:, 0:D], zeros[:, 0:R], zeros[:], start=True, stop=False, skip_group_check=True)

            def quad(t, c, n):
                def make(b):
                    pe.wait_ge(attr_in[b], 16 * n + 16)
                    pe.wait_ge(hid_act, Q * n + (b + 1))
                    pe.matmul(hid_ps[b][:, 0:D], attr[b][:], w1[:], start=True, stop=True).then_inc(hid_ready, 1)

                def add(b):
                    pe.wait_ge(hid_act, Q * n + (b + 1 + Q))
                    pe.wait_ge(onehot_ready, Q * n + (b + 1))
                    pe.matmul(sum_ps[:, 0:D], to_dst[b][:], hidden[b][:], start=False, stop=False,
                              skip_group_check=True).then_inc(used, 1)

                make(0)
                make(1)
                for b in range(2, Q):
                    add(b - 2)
                    make(b)
                add(Q - 2)
                add(Q - 1)

            def end(t):
                pe.drain().then_inc(tile_done, 1)

            quads(pe, start, quad, end)


def aggregate(nc, d, k, name, source, into, finish):
    with Stage(nc, name) as s:
        ct = [s.sb(f"ct{b}", [R, NODES]) for b in range(2)]
        acc = [s.ps(f"acc{b}", [R, 512]) for b in range(2)]
        temp = s.sb("temp", [R, 1, D])
        ct0, ct1, acc_ready, acc_free = map(s.sem, ("ct0", "ct1", "acc_ready", "acc_free"))
        block = s.block()

        @block.sync
        def _(sp):
            def load(t, b):
                sp.wait_ge(acc_ready, t + 1)
                sp.dma_start(ct[b][:], k["ct_dram"][bass.ds(t, 1)].rearrange("a p n -> (a p) n")).then_inc(
                    ct0 if b == 0 else ct1, 16)

            tiles(sp, load)

        @block.tensor
        def _(pe):
            pe.sem_inc(acc_ready, 2)

            def product(t, i, b):
                pe.wait_ge(ct0 if b == 0 else ct1, 16 * i + 16)
                pe.wait_ge(acc_free, t + 1)
                for src in range(T):
                    last = pe.matmul(acc[b][:, 0:D], ct[b][:, src * R:(src + 1) * R], source[:, src, :],
                                     start=(src == 0), stop=(src == T - 1))
                last.then_inc(acc_ready, 1)

            with pe.Fori(0, T // 2) as i:
                for b in range(2):
                    product(2 * i + b, i, b)
            product(T - 1, T // 2, 0)

        @block.vector
        def _(dve):
            dve.sem_inc(acc_free, 2)

            def evacuate(t, b):
                dve.wait_ge(acc_ready, t + 3)
                finish(dve, t, into[:, bass.ds(t, 1), :], acc[b][:, 0:D].rearrange("p (a n) -> p a n", a=1), temp[:])
                dve.drain().then_inc(acc_free, 1)

            tiles(dve, evacuate)



def row_stats(nc, d, k, name, source, kind, width=D):
    with Stage(nc, name) as s:
        stats = s.sb("stats", [R, T, 6])
        mv = s.sb("mv", [R, T, 2])
        rv, root = s.sb("rv", [R, T, 1]), s.sb("root", [R, T, 1])
        squares = [s.sb(f"squares{b}", [R, 1, width]) for b in range(2)]
        var_ready, root_ready = s.sem("var_ready"), s.sem("root_ready")
        block = s.block()

        @block.vector
        def _(dve):
            if kind == "norm":
                def square(t, b):
                    dve.tensor_tensor(squares[b][:], source[:, bass.ds(t, 1), :], source[:, bass.ds(t, 1), :], ALU.mult)
                    dve.drain()
                    dve.tensor_reduce(rv[:, bass.ds(t, 1), :], squares[b][:], AX, ALU.add)

                tiles(dve, square)
                dve.drain().then_inc(var_ready, 1)
            else:
                with dve.Fori(0, T) as t:
                    dve.bn_stats(stats[:, bass.ds(t, 1), :], source[:, bass.ds(t, 1), :])
                dve.drain()
                for t in range(T):
                    dve.bn_aggr(mv[:, t, :], stats[:, t, :])
                dve.drain()
                dve.tensor_scalar(rv[:], mv[:, :, 1:2], LN_EPS, None, ALU.add)
                dve.drain().then_inc(var_ready, 1)
            dve.wait_ge(root_ready, 1)
            if kind == "norm":
                dve.tensor_scalar(rv[:], root[:], 1e-12, None, ALU.max)
                dve.memset(k["shift"][:], 0.0)
                dve.drain()
                dve.reciprocal(k["scale"][:], rv[:])
            else:
                dve.reciprocal(k["scale"][:], root[:])
                dve.drain()
                dve.scalar_tensor_tensor(k["shift"][:], mv[:, :, 0:1], -1.0, k["scale"][:], ALU.mult, ALU.mult)

        @block.scalar
        def _(act):
            act.wait_ge(var_ready, 1)
            act.activation(root[:], rv[:], ACT.Sqrt).then_inc(root_ready, 1)


def normalise(nc, d, k, name, source, rows_to=None, store=False):
    with Stage(nc, name) as s:
        xs = [s.sb(f"xs{b}", [R, D]) for b in range(2)]
        pt = [s.ps(f"pt{b}", [128, 2, 256]) for b in range(2)]
        xs_ready, turned, pt_free, rows_ready, stored, started = map(
            s.sem, ("xs_ready", "turned", "pt_free", "rows_ready", "stored", "started"))
        block = s.block()

        @block.vector
        def _(dve):
            dve.sem_inc(pt_free, 2)

            def columns(t, b):
                dve.wait_ge(turned, t + 3)
                dve.tensor_copy(k["xnT"][:, :, rows(t)], pt[b][:, :, 0:R]).then_inc(pt_free, 1)

            tiles(dve, columns)

        @block.scalar
        def _(act):
            def scale(t, b):
                act.wait_ge(turned, t + 1)
                if rows_to is not None:
                    act.wait_ge(rows_ready, t + 1)
                settle(act, started)
                act.activation(xs[b][:], source[:, bass.ds(t, 1), :].rearrange("p a n -> p (a n)"), ACT.Identity,
                               bias=k["shift"][:, bass.ds(t, 1), :].rearrange("p a n -> p (a n)"),
                               scale=k["scale"][:, bass.ds(t, 1), :].rearrange("p a n -> p (a n)")).then_inc(xs_ready, 1)

            tiles(act, scale)

        @block.tensor
        def _(pe):
            pe.sem_inc(turned, 2)

            def turn(t, b):
                pe.wait_ge(xs_ready, t + 1)
                pe.wait_ge(pt_free, t + 1)
                for c in range(2):
                    last = pe.transpose(pt[b][:, c, 0:R], xs[b][:, c * 128:(c + 1) * 128], k["ident"][0:R, 0:R])
                last.then_inc(turned, 1)

            tiles(pe, turn)

        if rows_to is not None:
            @block.gpsimd
            def _(pool):
                pool.sem_inc(rows_ready, 2)

                def keep(t, b):
                    pool.wait_ge(xs_ready, t + 1)
                    pool.tensor_copy(rows_to[:, bass.ds(t, 1), :],
                                     xs[b][:].rearrange("p (a n) -> p a n", a=1)).then_inc(rows_ready, 1)

                tiles(pool, keep)

        if store:
            @block.sync
            def _(sp):
                sp.wait_ge(rows_ready, T + 2)
                sp.dma_start(k["xn_dram"].rearrange("(t p) n -> p t n", p=R), rows_to[:]).then_inc(stored, 16)
                sp.wait_ge(stored, 16)


def mix_sums(nc, d, k, name, heads, kind, wkv, bkv, gain, shift):
    hd = D // heads
    G = 2 * heads if kind == "ln" else heads
    with Stage(nc, name) as s:
        w = s.sb("w", [128, 2, 2 * D])
        bias = s.sb("bias", [R, 2 * D])
        gn, sh = s.sb("gn", [R, 2 * D]), s.sb("sh", [R, 2 * D])
        mask = s.sb("mask", [128, 128])
        ones = s.sb("ones", [R, 128])
        xt = [s.sb(f"xt{b}", [128, 2, R]) for b in range(2)]
        z = [s.sb(f"z{b}", [R, 2 * D]) for b in range(2)]
        e = s.sb("e", [R, 2 * D])
        sums, sq, var, root = (s.sb(n, [R, G]) for n in ("sums", "sq", "var", "root"))
        kv_ps = [s.ps(f"kv_ps{b}", [R, 512]) for b in range(2)]
        acc = s.ps("acc", [128, 2, 128])
        acc_sum = s.ps("acc_sum", [R, 512])
        zeros = s.sb("zeros", [128, 2 * D], BF16)
        loaded, setup, xt_ready, kv_ready, kv_free, z_ready, z_free, part, root_ready, done = map(
            s.sem, ("loaded", "setup", "xt_ready", "kv_ready", "kv_free", "z_ready", "z_free",
                    "part", "root_ready", "done"))
        block = s.block()

        @block.sync
        def _(sp):
            sp.dma_start(w[:], wkv).then_inc(loaded, 16)
            sp.dma_start(bias[:], bkv if bkv is not None else d["zero_row"]).then_inc(loaded, 16)
            sp.dma_start(gn[:], gain if gain is not None else d["zero_row"]).then_inc(loaded, 16)
            sp.dma_start(sh[:], shift if shift is not None else d["zero_row"]).then_inc(loaded, 16)
            sp.dma_start(mask[:], d["mask64"] if hd == 64 else d["mask32"]).then_inc(loaded, 16)
            sp.wait_ge(loaded, 80)

        @block.gpsimd
        def _(pool):
            def fetch(t, b):
                pool.wait_ge(kv_ready, t + 1)
                pool.tensor_copy(xt[b][:], k["xnT"][:, :, rows(t)]).then_inc(xt_ready, 1)

            tiles(pool, fetch)

        @block.tensor
        def _(pe):
            pe.wait_ge(loaded, 80)
            pe.wait_ge(setup, 1)
            pe.sem_inc(kv_ready, 2)
            pe.sem_inc(z_free, 2)
            pe.matmul(acc[:].rearrange("p a n -> p (a n)"), zeros[:, 0:128], zeros[:, 0:256], start=True, stop=False,
                      skip_group_check=True)
            pe.matmul(acc_sum[:, 0:D], zeros[:, 0:R], zeros[:, 0:D], start=True, stop=False, skip_group_check=True)

            def make(t, b):
                pe.wait_ge(xt_ready, t + 1)
                pe.wait_ge(kv_free, t + 1)
                for c in range(2):
                    last = pe.matmul(kv_ps[b][:], xt[b][:, c, :], w[:, c, :], start=(c == 0), stop=(c == 1))
                last.then_inc(kv_ready, 1)

            def body(t, b):
                pe.wait_ge(z_ready, t + 1)
                for c in range(2):
                    last = pe.matmul(acc[:, c, :], z[b][:, D + c * 128:D + (c + 1) * 128], z[b][:, c * 128:(c + 1) * 128],
                                     start=False, stop=False, skip_group_check=True)
                if kind == "elu":
                    last = pe.matmul(acc_sum[:, 0:D], ones[:, 0:R], z[b][:, 0:D], start=False, stop=False, skip_group_check=True)
                last.then_inc(z_free, 1)

            pipelined(make, body)(pe)
            pe.drain().then_inc(done, 1)

        @block.scalar
        def _(act):
            def body(t, b):
                if kind == "ln":
                    act.wait_ge(part, 2 * t + 1)
                    act.activation(e[:], z[b][:], ACT.Square).then_inc(root_ready, 1)
                    act.wait_ge(part, 2 * t + 2)
                    act.activation(root[:], var[:], ACT.Sqrt).then_inc(root_ready, 1)
                else:
                    act.wait_ge(part, t + 1)
                    act.activation(e[:, D:2 * D], e[:, 0:D], ACT.Exp).then_inc(root_ready, 1)

            tiles(act, body)

        @block.vector
        def _(dve):
            dve.sem_inc(kv_free, 2)
            dve.wait_ge(loaded, 80)
            dve.memset(zeros[:], 0.0)
            dve.memset(ones[:], 1.0)
            dve.drain().then_inc(setup, 1)

            def body(t, b):
                dve.wait_ge(kv_ready, t + 3)
                dve.wait_ge(z_free, t + 1)
                if kind == "ln":
                    zv = z[b][:].rearrange("p (g n) -> p g n", g=G)
                    dve.tensor_reduce(sums[:], kv_ps[b][:].rearrange("p (g n) -> p g n", g=G), AX, ALU.add)
                    dve.drain()
                    dve.tensor_scalar(sq[:], sums[:], 1.0 / hd, None, ALU.mult)
                    dve.drain()
                    dve.tensor_tensor(zv, kv_ps[b][:].rearrange("p (g n) -> p g n", g=G),
                                      sq[:].unsqueeze(2).broadcast_to((R, G, hd)), ALU.subtract)
                    dve.drain().then_inc(part, 1)
                    dve.drain().then_inc(kv_free, 1)
                    dve.wait_ge(root_ready, 2 * t + 1)
                    dve.tensor_reduce(sums[:], e[:].rearrange("p (g n) -> p g n", g=G), AX, ALU.add)
                    dve.drain()
                    dve.tensor_scalar(var[:], sums[:], 1.0 / hd, LN_EPS, ALU.mult, ALU.add)
                    dve.drain().then_inc(part, 1)
                    dve.wait_ge(root_ready, 2 * t + 2)
                    dve.reciprocal(sq[:], root[:])
                    dve.drain()
                    dve.tensor_tensor(zv, zv, sq[:].unsqueeze(2).broadcast_to((R, G, hd)), ALU.mult)
                    dve.drain()
                    dve.tensor_tensor(z[b][:], z[b][:], gn[:], ALU.mult)
                    dve.drain()
                    dve.tensor_tensor(z[b][:], z[b][:], sh[:], ALU.add)
                    dve.drain().then_inc(z_ready, 1)
                else:
                    dve.tensor_tensor(z[b][:], kv_ps[b][:], bias[:], ALU.add)
                    dve.drain().then_inc(kv_free, 1)
                    dve.tensor_scalar(e[:, 0:D], z[b][:, 0:D], 0.0, None, ALU.min)
                    dve.drain().then_inc(part, 1)
                    dve.wait_ge(root_ready, t + 1)
                    dve.scalar_tensor_tensor(z[b][:, 0:D], z[b][:, 0:D], 0.0, e[:, D:2 * D], ALU.max, ALU.add)
                    dve.drain().then_inc(z_ready, 1)

            tiles(dve, body)
            dve.wait_ge(done, 1)
            for c in range(2):
                dve.scalar_tensor_tensor(k["kvT"][:, c, :], acc[:, c, :], 1.0 / NODES if kind == "ln" else 1.0,
                                         mask[:], ALU.mult, ALU.mult)
            if kind == "elu":
                dve.tensor_copy(k["ksum"][:], acc_sum[:, 0:D])


def fold(nc, d, k, name, wo, wq=None):
    with Stage(nc, name) as s:
        woT = s.sb("woT", [128, 2, D])
        wqs = s.sb("wqs", [128, 2, D])
        m1 = s.sb("m1", [128, 2, D])
        ps1 = [s.ps(f"ps1{c}", [128, 512]) for c in range(2)]
        ps2 = [s.ps(f"ps2{c}", [128, 512]) for c in range(2)]
        loaded, one, two, kept = map(s.sem, ("loaded", "one", "two", "kept"))
        block = s.block()
        dest = m1 if wq is not None else k["fold"]

        @block.sync
        def _(sp):
            sp.dma_start(woT[:], wo).then_inc(loaded, 16)
            sp.dma_start(wqs[:], wq if wq is not None else wo).then_inc(loaded, 16)
            sp.wait_ge(loaded, 32)

        @block.tensor
        def _(pe):
            pe.wait_ge(loaded, 32)
            for c in range(2):
                pe.matmul(ps1[c][:, 0:D], k["kvT"][:, c, :], woT[:, c, :], start=True, stop=True).then_inc(one, 1)
            if wq is not None:
                pe.wait_ge(kept, 1)
                for i in range(2):
                    for c in range(2):
                        last = pe.matmul(ps2[i][:, 0:D], wqs[:, c, i * 128:(i + 1) * 128], m1[:, c, :],
                                         start=(c == 0), stop=(c == 1))
                    last.then_inc(two, 1)

        @block.vector
        def _(dve):
            for c in range(2):
                dve.wait_ge(one, c + 1)
                dve.tensor_copy(dest[:, c, :], ps1[c][:, 0:D])
            dve.drain().then_inc(kept, 1)
            if wq is not None:
                for i in range(2):
                    dve.wait_ge(two, i + 1)
                    dve.tensor_copy(k["fold"][:, i, :], ps2[i][:, 0:D])


def linear_rows(nc, d, k, name, source, weight, nk, prepare, finish, n_out=D, vectors=(), temps=()):
    with Stage(nc, name) as s:
        w = s.sb("w", [128, nk, n_out])
        vec = [s.sb(f"vec{n}", [R, v[1]]) for n, v in enumerate(vectors)]
        tmp = [s.sb(f"tmp{n}", shape) for n, shape in enumerate(temps)]
        xs = [s.sb(f"xs{b}", [R, nk * 128]) for b in range(2)]
        xt = [s.sb(f"xt{b}", [128, nk, R]) for b in range(2)]
        pt = [s.ps(f"pt{b}", [128, 4, 128]) for b in range(2)]
        out = [s.ps(f"out{b}", [R, 512]) for b in range(2)]
        loaded, xs_ready, turned, xt_ready, out_ready, out_free = map(
            s.sem, ("loaded", "xs_ready", "turned", "xt_ready", "out_ready", "out_free"))
        block = s.block()
        in_dram = weight is not k["fold"]
        total = 16 * (len(vectors) + in_dram)

        @block.sync
        def _(sp):
            if in_dram:
                sp.dma_start(w[:], weight).then_inc(loaded, 16)
            for v, t in zip(vectors, vec):
                sp.dma_start(t[:], v[0]).then_inc(loaded, 16)
            sp.wait_ge(loaded, total)

        wt = w if in_dram else weight

        @block.scalar
        def _(act):
            act.wait_ge(loaded, total)

            def body(t, b):
                act.wait_ge(turned, t + 3)
                act.wait_ge(out_ready, t + 1)
                act.activation(xt[b][:], pt[b][:, 0:nk, 0:R], ACT.Copy).then_inc(xt_ready, 1)

            tiles(act, body)

        @block.tensor
        def _(pe):
            pe.wait_ge(loaded, total)
            pe.sem_inc(turned, 2)
            pe.sem_inc(out_ready, 2)

            def turn(t, b):
                pe.wait_ge(xs_ready, t + 1)
                pe.wait_ge(xt_ready, t + 1)
                for c in range(nk):
                    last = pe.transpose(pt[b][:, c, 0:R], xs[b][:, c * 128:(c + 1) * 128], k["ident"][0:R, 0:R])
                last.then_inc(turned, 1)

            def body(t, b):
                pe.wait_ge(xt_ready, t + 3)
                pe.wait_ge(out_free, t + 1)
                for c in range(nk):
                    last = pe.matmul(out[b][:, 0:n_out], xt[b][:, c, :], wt[:, c, :], start=(c == 0), stop=(c == nk - 1))
                last.then_inc(out_ready, 1)

            pe.sem_inc(xt_ready, 2)
            ahead(turn, body, False)(pe)

        @block.vector
        def _(dve):
            dve.wait_ge(loaded, total)
            dve.sem_inc(out_free, 2)

            def before(t, b):
                dve.wait_ge(turned, t + 1)
                prepare(dve, t, xs[b], vec, tmp)
                dve.drain().then_inc(xs_ready, 1)

            def body(t, b):
                dve.wait_ge(out_ready, t + 3)
                finish(dve, t, out[b][:, 0:n_out].rearrange("p (a n) -> p a n", a=1), vec, tmp)
                dve.drain().then_inc(out_free, 1)

            ahead(before, body, True)(dve)


def copy_in(source):
    def prepare(dve, t, xs, vec, tmp):
        dve.tensor_copy(xs[:].rearrange("p (a n) -> p a n", a=1), source[:, bass.ds(t, 1), :])
    return prepare


def elementwise(nc, d, k, name, fn, vectors=(), temps=()):
    with Stage(nc, name) as s:
        vec = [s.sb(f"vec{n}", [R, v[1]]) for n, v in enumerate(vectors)]
        tmp = [[s.sb(f"tmp{n}{b}", shape) for n, shape in enumerate(temps)] for b in range(2)]
        loaded = s.sem("loaded")
        block = s.block()

        @block.sync
        def _(sp):
            for v, t in zip(vectors, vec):
                sp.dma_start(t[:], v[0]).then_inc(loaded, 16)
            if vectors:
                sp.wait_ge(loaded, 16 * len(vectors))

        @block.vector
        def _(dve):
            if vectors:
                dve.wait_ge(loaded, 16 * len(vectors))

            def body(t, b):
                fn(dve, t, vec, tmp[b])
                dve.drain()

            tiles(dve, body)


def project(nc, d, k, name, weight, n_out, into, bias=None, add=False):
    with Stage(nc, name) as s:
        w = s.sb("w", [128, 2, n_out])
        bc = s.sb("bc", [R, 1, n_out])
        xt = [s.sb(f"xt{b}", [128, 2, R]) for b in range(2)]
        out = [s.ps(f"out{b}", [R, 512]) for b in range(2)]
        loaded, xt_ready, out_ready, out_free, started = map(
            s.sem, ("loaded", "xt_ready", "out_ready", "out_free", "started"))
        block = s.block()
        total = 16 * (1 + (bias is not None))

        @block.sync
        def _(sp):
            sp.dma_start(w[:], weight).then_inc(loaded, 16)
            if bias is not None:
                sp.dma_start(bc[:].rearrange("p a n -> p (a n)"), bias).then_inc(loaded, 16)
            sp.wait_ge(loaded, total)

        @block.scalar
        def _(act):
            def fetch(t, b):
                act.wait_ge(out_ready, t + 1)
                settle(act, started)
                act.activation(xt[b][:], k["xnT"][:, :, rows(t)], ACT.Copy).then_inc(xt_ready, 1)

            tiles(act, fetch)

        @block.tensor
        def _(pe):
            pe.wait_ge(loaded, total)
            pe.sem_inc(out_ready, 2)

            def body(t, b):
                pe.wait_ge(xt_ready, t + 1)
                pe.wait_ge(out_free, t + 1)
                for c in range(2):
                    last = pe.matmul(out[b][:, 0:n_out], xt[b][:, c, :], w[:, c, :], start=(c == 0), stop=(c == 1))
                last.then_inc(out_ready, 1)

            tiles(pe, body)

        @block.vector
        def _(dve):
            dve.wait_ge(loaded, total)
            dve.sem_inc(out_free, 2)

            def body(t, b):
                dve.wait_ge(out_ready, t + 3)
                row = out[b][:, 0:n_out].rearrange("p (a n) -> p a n", a=1)
                to = into[:, bass.ds(t, 1), :]
                if bias is None:
                    dve.tensor_copy(to, row).then_inc(out_free, 1)
                elif add:
                    dve.tensor_tensor(to, to, row, ALU.add)
                    dve.drain().then_inc(out_free, 1)
                    dve.tensor_tensor(to, to, bc[:], ALU.add)
                else:
                    dve.tensor_tensor(to, row, bc[:], ALU.add).then_inc(out_free, 1)

            tiles(dve, body)


def choose(dve, lg, top, hot, spare, down, E):
    dve.tensor_reduce(top, lg, AX, ALU.max)
    dve.drain()
    dve.tensor_tensor(hot, lg, top.broadcast_to((R, T, E)), ALU.is_ge)
    dve.drain()
    dve.tensor_tensor(hot, hot, down.broadcast_to((R, T, E)), ALU.mult)
    dve.drain()
    dve.tensor_reduce(spare, hot, AX, ALU.max)
    dve.drain()
    dve.tensor_tensor(hot, hot, spare.broadcast_to((R, T, E)), ALU.is_equal)
    dve.drain()


def gate(nc, d, k, name, E, kind):
    with Stage(nc, name) as s:
        lg = k["gates"][:, 0:T * E].rearrange("p (t e) -> p t e", e=E)
        one, two = s.sb("one", [R, T, E]), s.sb("two", [R, T, E])
        top1, top2, sp1, sp2 = (s.sb(n, [R, T, 1]) for n in ("top1", "top2", "sp1", "sp2"))
        down = s.sb("down", [R, 1, E])
        loaded, to_exp, exped = s.sem("loaded"), s.sem("to_exp"), s.sem("exped")
        block = s.block()
        soft = kind == "soft_two"

        @block.sync
        def _(sp):
            sp.dma_start(down[:].rearrange("p a n -> p (a n)"), d["down"][:, 32 - E:32]).then_inc(loaded, 16)
            sp.wait_ge(loaded, 16)

        @block.vector
        def _(dve):
            dve.wait_ge(loaded, 16)
            if soft:
                dve.tensor_reduce(top1[:], lg, AX, ALU.max)
                dve.drain()
                dve.tensor_tensor(one[:], lg, top1[:].broadcast_to((R, T, E)), ALU.subtract)
                dve.drain().then_inc(to_exp, 1)
                dve.wait_ge(exped, 1)
                dve.tensor_reduce(sp1[:], two[:], AX, ALU.add)
                dve.drain()
                dve.reciprocal(sp2[:], sp1[:])
                dve.drain()
                dve.tensor_tensor(lg, two[:], sp2[:].broadcast_to((R, T, E)), ALU.mult)
                dve.drain()
            choose(dve, lg, top1[:], one[:], sp1[:], down[:], E)
            dve.tensor_copy(k["hots"][0][:, 0:T * E].rearrange("p (t e) -> p t e", e=E), one[:])
            if kind == "first":
                return
            dve.scalar_tensor_tensor(lg, one[:], -1e30, lg, ALU.mult, ALU.add)
            dve.drain()
            choose(dve, lg, top2[:], two[:], sp1[:], down[:], E)
            dve.tensor_copy(k["hots"][1][:, 0:T * E].rearrange("p (t e) -> p t e", e=E), two[:])
            dve.tensor_tensor(sp1[:], top2[:], top1[:], ALU.subtract)
            dve.drain().then_inc(to_exp, 1)
            dve.wait_ge(exped, 2 if soft else 1)
            dve.tensor_scalar(top1[:], sp2[:], 1.0, None, ALU.add)
            dve.drain()
            dve.reciprocal(top2[:], top1[:])
            dve.drain()
            dve.tensor_tensor(sp1[:], top2[:], sp2[:], ALU.mult)
            dve.drain()
            dve.tensor_copy(k["slot_gate"][0][:].unsqueeze(2), top2[:])
            dve.tensor_copy(k["slot_gate"][1][:].unsqueeze(2), sp1[:])
            dve.tensor_tensor(one[:], one[:], top2[:].broadcast_to((R, T, E)), ALU.mult)
            dve.drain()
            dve.tensor_tensor(two[:], two[:], sp1[:].broadcast_to((R, T, E)), ALU.mult)
            dve.drain()
            dve.tensor_tensor(lg, one[:], two[:], ALU.add)

        @block.scalar
        def _(act):
            if kind == "first":
                return
            n = 0
            if soft:
                act.wait_ge(to_exp, 1)
                act.activation(two[:], one[:], ACT.Exp).then_inc(exped, 1)
                n = 1
            act.wait_ge(to_exp, n + 1)
            act.activation(sp2[:], sp1[:], ACT.Exp).then_inc(exped, 1)


def rank_gate(nc, d, k, name, keep):
    with Stage(nc, name) as s:
        col = s.sb("col", [128, T])
        colT = s.sb("colT", [T, R])
        line = s.sb("line", [128, NODES])
        below = s.sb("below", [R, R])
        c1, c2, c3, c4 = (s.sb(n, [R, T]) for n in ("c1", "c2", "c3", "c4"))
        junk = [s.sb(f"junk{n}", [R, NODES]) for n in range(2)]
        ps = s.ps("ps", [T, 512])
        ready, turned, copied, stored, back, loaded = map(
            s.sem, ("ready", "turned", "copied", "stored", "back", "loaded"))
        w = k["gates"]
        block = s.block()

        @block.sync
        def _(sp):
            sp.dma_start(below[:], d["below"]).then_inc(loaded, 16)
            sp.wait_ge(copied, 1)
            sp.dma_start(k["line_dram"].rearrange("(t p) -> t p", p=R), colT[:]).then_inc(stored, 16)
            sp.wait_ge(stored, 16)
            sp.dma_start(line[0:R, :], k["line_dram"].rearrange("(a n) -> a n", a=1).broadcast_to((R, NODES))).then_inc(back, 16)
            sp.wait_ge(back, 16)
            sp.wait_ge(loaded, 16)

        @block.tensor
        def _(pe):
            pe.wait_ge(ready, 1)
            pe.transpose(ps[:, 0:R], col[0:R, :], k["ident"][0:R, 0:R]).then_inc(turned, 1)

        @block.vector
        def _(dve):
            dve.tensor_copy(col[0:R, :], w[:, 0:T]).then_inc(ready, 1)
            dve.wait_ge(turned, 1)
            dve.tensor_copy(colT[:], ps[:, 0:R]).then_inc(copied, 1)
            dve.wait_ge(back, 16)
            dve.wait_ge(loaded, 16)
            for c in (c1, c2, c3, c4):
                dve.memset(c[:], 0.0)
            dve.drain()
            for t in range(T):
                a, z = t * R, (t + 1) * R
                if t:
                    dve.tensor_scalar(junk[0][:, 0:a], line[0:R, 0:a], w[:, t:t + 1], 0.0, ALU.is_ge, ALU.add,
                                      accum_out=c1[:, t:t + 1])
                dve.tensor_scalar(junk[1][:, a:], line[0:R, a:], w[:, t:t + 1], 0.0, ALU.is_gt, ALU.add,
                                  accum_out=c2[:, t:t + 1])
                dve.drain()
                dve.scalar_tensor_tensor(junk[0][:, 0:R], line[0:R, a:z], w[:, t:t + 1], below[:],
                                         ALU.is_equal, ALU.mult, accum_out=c3[:, t:t + 1])
                dve.drain()
            dve.tensor_tensor(c4[:], c1[:], c2[:], ALU.add)
            dve.drain()
            dve.tensor_tensor(c1[:], c4[:], c3[:], ALU.add)
            dve.drain()
            dve.scalar_tensor_tensor(c2[:], c1[:], float(keep), w[:, 0:T], ALU.is_lt, ALU.mult)
            dve.drain()
            for e in range(2):
                dve.tensor_copy(w[:, 0:2 * T].rearrange("p (t e) -> p t e", e=2)[:, :, e:e + 1],
                                c2[:].rearrange("p (t e) -> p t e", e=1))


def experts(nc, d, k, name, E, hp, hc, func, w1, b1, w2, into):
    with Stage(nc, name) as s:
        W1 = [s.sb(f"W1{b}", [128, 2, hc * hp]) for b in range(2)]
        W2 = [s.sb(f"W2{b}", [hp, hc, D]) for b in range(2)]
        bias = s.sb("bias", [hp, E * hc])
        hT = [s.sb(f"hT{b}", [hp, hc, 3 * R]) for b in range(2)]
        h_ps = [s.ps(f"h_ps{c}", [hp, 512]) for c in range(hc)]
        o_ps = s.ps("o_ps", [R, 3, 512])
        loaded, w_in0, w_in1, w_free, h_ready, hT_ready, out_ready, out_free = map(
            s.sem, ("loaded", "w_in0", "w_in1", "w_free", "h_ready", "hT_ready", "out_ready", "out_free"))
        block = s.block()
        started, began = s.sem("started"), s.sem("began")
        per = 10 * hc

        def pairs(eng, body):
            with eng.Fori(0, E // 2) as q:
                for b in range(2):
                    body(2 * q + b, q, b)

        @block.sync
        def _(sp):
            sp.dma_start(bias[:], b1).then_inc(loaded, 16)
            sp.wait_ge(loaded, 16)

            def load(e, q, b):
                sp.wait_ge(w_free, e + 1)
                sp.dma_start(W1[b][:], w1[bass.ds(e, 1)].rearrange("a p c n -> (a p) c n")).then_inc(
                    w_in0 if b == 0 else w_in1, 16)
                sp.dma_start(W2[b][:], w2[bass.ds(e, 1)].rearrange("a p c n -> (a p) c n")).then_inc(
                    w_in0 if b == 0 else w_in1, 16)

            pairs(sp, load)

        @block.tensor
        def _(pe):
            pe.sem_inc(w_free, 2)
            pe.sem_inc(hT_ready, hc)

            def expert(e, q, b):
                pe.wait_ge(w_in0 if b == 0 else w_in1, 32 * q + 32)
                settle(pe, began)

                def group(t, g, n, p):
                    for c in range(hc):
                        pe.wait_ge(hT_ready, e * per + n * hc + (c + 1))
                        for i in range(2):
                            last = pe.matmul(h_ps[c][:, 0:g * R], W1[b][:, i, c * hp:(c + 1) * hp],
                                             k["xnT"][:, i, rows(t, g)], start=(i == 0), stop=(i == 1))
                        last.then_inc(h_ready, 1)
                    pe.wait_ge(hT_ready, e * per + n * hc + 2 * hc)
                    pe.wait_ge(out_free, e * 10 + n + 1)
                    for j in range(g):
                        for c in range(hc):
                            last = pe.matmul(o_ps[:, 2 * p + j // 2, (j % 2) * D:(j % 2 + 1) * D],
                                      hT[p][:, c, j * R:(j + 1) * R], W2[b][:, c, :], start=(c == 0), stop=(c == hc - 1))
                    last.then_inc(out_ready, 1)

                groups(pe, group)
                pe.drain().then_inc(w_free, 1)

            pairs(pe, expert)

        @block.scalar
        def _(act):
            act.wait_ge(loaded, 16)
            act.sem_inc(out_ready, 2)

            def expert(e, q, b):
                def group(t, g, n, p):
                    act.wait_ge(out_ready, e * 10 + n + 1)
                    for c in range(hc):
                        act.wait_ge(h_ready, e * per + n * hc + (c + 1))
                        settle(act, started)
                        act.activation(hT[p][:, c, 0:g * R], h_ps[c][:, 0:g * R], func,
                                       bias=bias[:, bass.ds(e * hc + c, 1)]).then_inc(hT_ready, 1)

                groups(act, group)

            pairs(act, expert)

        @block.vector
        def _(dve):
            dve.sem_inc(out_free, 2)

            def expert(e, q, b):
                def group(t, g, n, p):
                    dve.wait_ge(out_ready, e * 10 + n + 3)
                    for j in range(g):
                        to = into[:, bass.ds(t + j, 1), :].rearrange("p a n -> p (a n)")
                        dve.scalar_tensor_tensor(
                            to, o_ps[:, 2 * p + j // 2, (j % 2) * D:(j % 2 + 1) * D],
                            k["gates"][:, bass.ds((t + j) * E + e, 1)], to, ALU.mult, ALU.add)
                    dve.drain().then_inc(out_free, 1)

                groups(dve, group)

            pairs(dve, expert)


def expert_places(nc, d, k, name, E, hots):
    with Stage(nc, name) as s:
        per = min(T, 512 // E)
        lots = [(a, min(per, T - a)) for a in range(0, T, per)]
        above, ones = s.sb("above", [R, R]), s.sb("ones", [R, R])
        chosen, rank, prod = (s.sb(n, [R, T, E]) for n in ("chosen", "rank", "prod"))
        before = s.sb("before", [R, T + 1, E])
        blocks, cum, base, start = (s.sb(n, [R, E]) for n in ("blocks", "cum", "base", "start"))
        pos = s.sb("pos", [R, T, len(hots)])
        rank_ps, total_ps = s.ps("rank_ps", [R, len(lots), 512]), s.ps("total_ps", [R, len(lots), 512])
        loaded, ready, counted = s.sem("loaded"), s.sem("ready"), s.sem("counted")
        block = s.block()

        @block.sync
        def _(sp):
            sp.dma_start(above[:], d["above"]).then_inc(loaded, 16)

        @block.tensor
        def _(pe):
            pe.wait_ge(loaded, 16)
            pe.wait_ge(ready, 1)
            for g, (a, n) in enumerate(lots):
                rhs = chosen[:, a:a + n, :].rearrange("p t e -> p (t e)")
                pe.matmul(rank_ps[:, g, 0:n * E], above[:], rhs, start=True, stop=True)
                pe.matmul(total_ps[:, g, 0:n * E], ones[:], rhs, start=True, stop=True)
            pe.drain().then_inc(counted, 1)

        @block.vector
        def _(dve):
            dve.memset(ones[:], 1.0)
            dve.memset(before[:, 0, :], 0.0)
            dve.memset(blocks[:], 1.0)
            if len(hots) == 2:
                dve.tensor_tensor(chosen[:], hots[0], hots[1], ALU.add)
            else:
                dve.tensor_copy(chosen[:], hots[0])
            dve.drain().then_inc(ready, 1)
            dve.wait_ge(counted, 1)
            for g, (a, n) in enumerate(lots):
                for t in range(a, a + n):
                    dve.tensor_tensor(before[:, t + 1, :], before[:, t, :], total_ps[:, g, (t - a) * E:(t - a + 1) * E], ALU.add)
                    dve.drain()
                dve.tensor_tensor(rank[:, a:a + n, :], rank_ps[:, g, 0:n * E].rearrange("p (t e) -> p t e", e=E),
                                  before[:, a:a + n, :], ALU.add)
            for m in range(1, -(-NODES // 128)):
                dve.scalar_tensor_tensor(blocks[:], before[:, T, :], float(128 * m), blocks[:], ALU.is_gt, ALU.add)
                dve.drain()
            dve.tensor_tensor_scan(cum[:], ones[:, 0:E], blocks[:], 0.0, ALU.mult, ALU.add)
            dve.drain()
            dve.tensor_tensor(base[:], cum[:], blocks[:], ALU.subtract)
            dve.drain()
            dve.tensor_scalar(start[:], base[:], 128.0, None, ALU.mult)
            dve.tensor_copy(k["blocks"][:, 0, 0:E], blocks[0:1, :])
            dve.tensor_copy(k["blocks"][:, 1, 0:E], base[0:1, :])
            dve.drain()
            dve.tensor_tensor(rank[:], rank[:], start[:].unsqueeze(1).broadcast_to((R, T, E)), ALU.add)
            dve.drain()
            for slot, hot in enumerate(hots):
                dve.tensor_tensor(prod[:], rank[:], hot, ALU.mult)
                dve.drain()
                dve.tensor_reduce(pos[:, :, slot:slot + 1], prod[:], AX, ALU.add)
                dve.drain()
            dve.tensor_copy(k["pos"][:, :, 0:len(hots)], pos[:])


def parities(eng, body):
    body(0, 0, 0, first=True)
    body(1, 0, 1, first=True)
    with eng.Fori(1, T // 2) as i:
        body(2 * i, i, 0)
        body(2 * i + 1, i, 1)
    body(T - 1, T // 2, 0)


def sort_rows(nc, d, k, name, source, slots):
    with Stage(nc, name) as s:
        buf = [s.sb(f"buf{b}", [R, D]) for b in range(2)]
        to = [s.sb(f"to{b}", [R, slots], I32) for b in range(2)]
        rows_ready, to_ready, started = s.sem("rows_ready"), s.sem("to_ready"), s.sem("started")
        sent = [s.sem(f"sent{b}") for b in range(2)]
        block = s.block()

        @block.scalar
        def _(act):
            def fill(t, i, b, first=False):
                if not first:
                    act.wait_ge(sent[b], 16 * slots * i)
                settle(act, started)
                act.activation(buf[b][:].unsqueeze(1), source[:, bass.ds(t, 1), :], ACT.Copy).then_inc(rows_ready, 1)

            parities(act, fill)

        @block.gpsimd
        def _(pool):
            def send(t, i, b, first=False):
                if not first:
                    pool.wait_ge(sent[b], 16 * slots * i)
                pool.tensor_copy(to[b][:].unsqueeze(1), k["pos"][:, bass.ds(t, 1), 0:slots]).then_inc(to_ready, 1)
                pool.wait_ge(to_ready, t + 1)
                pool.wait_ge(rows_ready, t + 1)
                settle(pool, started)
                for slot in range(slots):
                    pool.indirect_dma_start(k["sorted_dram"], bass.IndirectOffsetOnAxis(ap=to[b][:, slot:slot + 1], axis=0),
                                            buf[b][:], None).then_inc(sent[b], 16)

            parities(pool, send)
            pool.wait_ge(sent[0], 16 * slots * (T // 2 + 1))
            pool.wait_ge(sent[1], 16 * slots * (T // 2))


def unsort_rows(nc, d, k, name, slots, combine):
    with Stage(nc, name) as s:
        buf = [[s.sb(f"buf{b}{n}", [R, D]) for n in range(slots)] for b in range(2)]
        to = [s.sb(f"to{b}", [R, slots], I32) for b in range(2)]
        buf_free, to_ready, started = s.sem("buf_free"), s.sem("to_ready"), s.sem("started")
        got = [s.sem(f"got{b}") for b in range(2)]
        block = s.block()

        @block.gpsimd
        def _(pool):
            pool.sem_inc(buf_free, 2)

            def fetch(t, i, b, first=False):
                pool.wait_ge(buf_free, t + 1)
                pool.tensor_copy(to[b][:].unsqueeze(1), k["pos"][:, bass.ds(t, 1), 0:slots]).then_inc(to_ready, 1)
                pool.wait_ge(to_ready, t + 1)
                settle(pool, started)
                for slot in range(slots):
                    pool.indirect_dma_start(buf[b][slot][:], None, k["result_dram"],
                                            bass.IndirectOffsetOnAxis(ap=to[b][:, slot:slot + 1], axis=0)).then_inc(got[b], 16)

            parities(pool, fetch)

        @block.vector
        def _(dve):
            def add(t, i, b, first=False):
                dve.wait_ge(got[b], 16 * slots * i + 16 * slots)
                combine(dve, t, [a[:].unsqueeze(1) for a in buf[b]])
                dve.drain().then_inc(buf_free, 1)

            parities(dve, add)


def sorted_experts(nc, d, k, name, E, hp, hc, w1, b1, w2, b2):
    with Stage(nc, name) as s:
        W1 = [s.sb(f"W1{b}", [128, 2, hc * hp]) for b in range(2)]
        W2 = [s.sb(f"W2{b}", [hp, hc, D]) for b in range(2)]
        B2 = [s.sb(f"B2{b}", [128, D]) for b in range(2)]
        bias = s.sb("bias", [hp, E * hc])
        xr, xT, y = s.sb("xr", [128, D]), s.sb("xT", [128, 2, 128]), s.sb("y", [128, D])
        hT = s.sb("hT", [hp, hc, 128])
        h_ps = [s.ps(f"h_ps{c}", [hp, 512]) for c in range(hc)]
        pt, o_ps = s.ps("pt", [128, 2, 256]), s.ps("o_ps", [128, 512])
        loaded, w_free, b2_free, x_in, turned, xT_ready, h_ready, hT_ready, out_ready, y_ready, y_stored, started = map(
            s.sem, ("loaded", "w_free", "b2_free", "x_in", "turned", "xT_ready", "h_ready", "hT_ready", "out_ready",
                    "y_ready", "y_stored", "started"))
        w_in = [s.sem(f"w_in{b}") for b in range(2)]
        block = s.block()
        most = -(-NODES // 128)

        def every(eng, begin, each, end):
            with eng.Fori(0, E // 2) as q:
                for b in range(2):
                    e = 2 * q + b
                    begin(e, q, b)
                    count = eng.value_load(k["blocks"][0:1, 0, bass.ds(e, 1)], min_val=1, max_val=most)
                    base = eng.value_load(k["blocks"][0:1, 1, bass.ds(e, 1)], min_val=0, max_val=E * most)
                    with eng.Fori(0, count) as j:
                        g = k["nc"].s_assert_within(base + j, 0, BLOCKS - 1,
                                                    skip_runtime_bounds_check_because="all blocks are at most BLOCKS")
                        each(e, b, g)
                    end(e, b)

        def nothing(*a):
            pass

        @block.gpsimd
        def _(pool):
            pool.dma_start(bias[:], b1).then_inc(loaded, 16)
            with pool.Fori(0, E // 2) as q:
                for b in range(2):
                    e = 2 * q + b
                    pool.wait_ge(w_free, e + 1)
                    pool.wait_ge(b2_free, e + 1)
                    settle(pool, started)
                    pool.dma_start(W1[b][:], w1[bass.ds(e, 1)].rearrange("a p c n -> (a p) c n")).then_inc(w_in[b], 16)
                    pool.dma_start(W2[b][:], w2[bass.ds(e, 1)].rearrange("a p c n -> (a p) c n")).then_inc(w_in[b], 16)
                    pool.dma_start(B2[b][:], b2[bass.ds(e, 1), :].broadcast_to((128, D))).then_inc(w_in[b], 16)

        @block.sync
        def _(sp):
            sp.dma_start(xr[:], k["sorted_dram"][0:128]).then_inc(x_in, 16)

            def each(e, b, g):
                sp.wait_ge(turned, g + 1)
                settle(sp, started)
                sp.dma_start(xr[:], k["sorted_dram"][bass.ds((g + 1) * 128, 128)]).then_inc(x_in, 16)

            every(sp, nothing, each, nothing)
            count = sp.value_load(k["blocks"][0:1, 0, E - 1:E], min_val=1, max_val=most)
            base = sp.value_load(k["blocks"][0:1, 1, E - 1:E], min_val=0, max_val=E * most)
            sp.wait_ge(x_in, 16 * (count + base) + 16)
            settle(sp, started)

        @block.tensor
        def _(pe):
            pe.sem_inc(w_free, 2)

            def turn(g):
                pe.wait_ge(x_in, 16 * g + 16)
                for c in range(2):
                    last = pe.transpose(pt[:, c, 0:128], xr[:, c * 128:(c + 1) * 128], k["ident"][:])
                last.then_inc(turned, 1)

            turn(0)

            def begin(e, q, b):
                pe.wait_ge(w_in[b], 48 * q + 48)
                settle(pe, started)

            def each(e, b, g):
                pe.wait_ge(xT_ready, g + 1)
                for c in range(hc):
                    for i in range(2):
                        last = pe.matmul(h_ps[c][:, 0:128], W1[b][:, i, c * hp:(c + 1) * hp], xT[:, i, :],
                                         start=(i == 0), stop=(i == 1))
                    last.then_inc(h_ready, 1)
                turn(g + 1)
                pe.wait_ge(y_ready, g + 1)
                for c in range(hc):
                    pe.wait_ge(hT_ready, hc * g + (c + 1))
                    last = pe.matmul(o_ps[:, 0:D], hT[:, c, :], W2[b][:, c, :], start=(c == 0), stop=(c == hc - 1))
                last.then_inc(out_ready, 1)

            def end(e, b):
                pe.drain().then_inc(w_free, 1)

            every(pe, begin, each, end)

        @block.scalar
        def _(act):
            act.wait_ge(loaded, 16)

            def each(e, b, g):
                for c in range(hc):
                    act.wait_ge(h_ready, hc * g + (c + 1))
                    settle(act, started)
                    act.activation(hT[:, c, :], h_ps[c][:, 0:128], ACT.Relu,
                                   bias=bias[:, bass.ds(e * hc + c, 1)]).then_inc(hT_ready, 1)
                act.wait_ge(y_ready, g + 2)
                settle(act, started)
                act.dma_start(k["result_dram"][bass.ds(g * 128, 128)], y[:]).then_inc(y_stored, 16)

            act.sem_inc(y_stored, 16)
            every(act, nothing, each, nothing)
            count = act.value_load(k["blocks"][0:1, 0, E - 1:E], min_val=1, max_val=most)
            base = act.value_load(k["blocks"][0:1, 1, E - 1:E], min_val=0, max_val=E * most)
            act.wait_ge(y_stored, 16 * (count + base) + 16)
            settle(act, started)

        @block.vector
        def _(dve):
            dve.sem_inc(y_ready, 1)
            dve.sem_inc(b2_free, 2)

            def to_columns(g):
                dve.wait_ge(turned, g + 1)
                dve.tensor_copy(xT[:], pt[:, :, 0:128]).then_inc(xT_ready, 1)

            to_columns(0)

            def begin(e, q, b):
                dve.wait_ge(w_in[b], 48 * q + 48)
                settle(dve, started)

            def each(e, b, g):
                to_columns(g + 1)
                dve.wait_ge(out_ready, g + 1)
                dve.wait_ge(y_stored, 16 * g + 16)
                dve.tensor_tensor(y[:], o_ps[:, 0:D], B2[b][:], ALU.add)
                dve.drain().then_inc(y_ready, 1)

            def end(e, b):
                dve.drain().then_inc(b2_free, 1)

            every(dve, begin, each, end)


def softmax_keys(nc, d, k, name):
    C = 128
    with Stage(nc, name) as s:
        w, g_pre = s.sb("w", [128, 2, 3 * C]), s.sb("g_pre", [128, 2])
        w_out, mask = s.sb("w_out", [C, D]), s.sb("mask", [C, C])
        keys = s.sb("keys", [C, NODES])
        mem_k, mem_v = s.sb("mem_k", [C, 4]), s.sb("mem_v", [4, C])
        most, most4, low = s.sb("most", [C, 1]), s.sb("most4", [C, 1]), s.sb("low", [C, 1])
        ones = s.sb("ones", [R, 1])
        mem_e, mem_t = s.sb("mem_e", [C, 4]), s.sb("mem_t", [4, C])
        xt = [s.sb(f"xt{b}", [128, 2, R]) for b in range(2)]
        ke = [s.sb(f"ke{b}", [C, R]) for b in range(2)]
        ks = [s.sb(f"ks{b}", [R, C]) for b in range(2)]
        vs = [s.sb(f"vs{b}", [R, C]) for b in range(2)]
        ctx = s.sb("ctx", [C, C])
        inv = s.sb("inv", [C, 1])
        k_ps = [s.ps(f"k_ps{b}", [128, 512]) for b in range(2)]
        kv_ps = [s.ps(f"kv_ps{b}", [128, 512]) for b in range(2)]
        acc, acc_sum = s.ps("acc", [C, 512]), s.ps("acc_sum", [C, 512])
        (loaded, w_ready, k_ready, k_kept, low_ready, ke_ready, mem_ready, xt_ready, kv_ready, kept,
         used, done, ctx_ready, folded, mem_turned, mem_kept) = map(
            s.sem, ("loaded", "w_ready", "k_ready", "k_kept", "low_ready", "ke_ready", "mem_ready", "xt_ready",
                    "kv_ready", "kept", "used", "done", "ctx_ready", "folded", "mem_turned", "mem_kept"))
        started = s.sem("started")
        block = s.block()

        @block.sync
        def _(sp):
            for to, src in ((w, d["w_qkv"]), (g_pre, d["g_pre"]), (w_out, d["w_out"]), (mask, d["mask32"]),
                            (mem_k, d["mem_k"]), (mem_v, d["mem_v"])):
                sp.dma_start(to[:], src).then_inc(loaded, 16)
            sp.wait_ge(loaded, 96)

        @block.gpsimd
        def _(pool):
            def fetch(t, b):
                pool.wait_ge(kv_ready, t + 1)
                pool.tensor_copy(xt[b][:], k["xnT"][:, :, rows(t)]).then_inc(xt_ready, 1)

            tiles(pool, fetch)

        @block.vector
        def _(dve):
            dve.wait_ge(loaded, 96)
            dve.memset(ones[:], 1.0)
            for c in range(2):
                dve.tensor_scalar(k["w_qkv"][:, c, :], w[:, c, :], g_pre[:, c:c + 1], None, ALU.mult)
            dve.drain().then_inc(w_ready, 1)
            dve.sem_inc(k_kept, 2)

            def keep(t, g, n, p):
                dve.wait_ge(k_ready, n + 1)
                dve.tensor_copy(keys[:, rows(t, g)], k_ps[p][:, 0:g * R]).then_inc(k_kept, 1)

            groups(dve, keep)
            dve.drain()
            dve.tensor_reduce(most[:], keys[:], AX, ALU.max)
            dve.tensor_reduce(most4[:], mem_k[:], AX, ALU.max)
            dve.drain()
            dve.tensor_tensor(most[:], most[:], most4[:], ALU.max)
            dve.drain()
            dve.tensor_scalar(low[:], most[:], -1.0, None, ALU.mult).then_inc(low_ready, 1)
            dve.wait_ge(mem_turned, 1)
            dve.tensor_copy(mem_t[:], kv_ps[0][0:4, 0:C]).then_inc(mem_kept, 1)

            def body(t, b):
                dve.wait_ge(kv_ready, t + 3)
                dve.wait_ge(used, t + 1)
                dve.tensor_copy(ks[b][:], kv_ps[b][0:R, 0:C])
                dve.tensor_copy(vs[b][:], kv_ps[b][0:R, C:2 * C])
                dve.drain().then_inc(kept, 1)

            tiles(dve, body)
            dve.wait_ge(done, 1)
            dve.tensor_tensor(ctx[:], acc[:, 0:C], mask[:], ALU.mult)
            dve.reciprocal(inv[:], acc_sum[:, 0:1])
            dve.drain().then_inc(ctx_ready, 1)
            dve.wait_ge(folded, 1)
            dve.tensor_scalar(k["fold"][:, 0, :], k_ps[0][:, 0:D], inv[:], 32.0 ** -0.5, ALU.mult, ALU.mult)

        @block.scalar
        def _(act):
            act.wait_ge(low_ready, 1)
            act.activation(mem_e[:], mem_k[:], ACT.Exp, bias=low[:]).then_inc(mem_ready, 1)

            def body(t, b):
                act.wait_ge(kv_ready, t + 1)
                settle(act, started)
                act.activation(ke[b][:], keys[:, rows(t)], ACT.Exp, bias=low[:]).then_inc(ke_ready, 1)

            tiles(act, body)

        @block.tensor
        def _(pe):
            pe.wait_ge(w_ready, 1)
            pe.sem_inc(kv_ready, 2)
            pe.sem_inc(used, 2)

            def key(t, g, n, p):
                pe.wait_ge(k_kept, n + 1)
                for c in range(2):
                    last = pe.matmul(k_ps[p][:, 0:g * R], k["w_qkv"][:, c, C:2 * C], k["xnT"][:, c, rows(t, g)],
                                     start=(c == 0), stop=(c == 1))
                last.then_inc(k_ready, 1)

            groups(pe, key)
            pe.wait_ge(mem_ready, 1)
            pe.transpose(kv_ps[0][0:4, 0:C], mem_e[:], k["ident"][:]).then_inc(mem_turned, 1)
            pe.wait_ge(mem_kept, 1)
            pe.matmul(acc[:, 0:C], mem_v[:], mem_t[:], start=True, stop=False, skip_group_check=True)
            pe.matmul(acc_sum[:, 0:1], mem_t[:], ones[0:4, :], start=True, stop=False, skip_group_check=True)

            def make(t, b):
                pe.wait_ge(ke_ready, t + 1)
                pe.wait_ge(xt_ready, t + 1)
                pe.transpose(kv_ps[b][0:R, 0:C], ke[b][:], k["ident"][:])
                for c in range(2):
                    last = pe.matmul(kv_ps[b][0:R, C:2 * C], xt[b][:, c, :], k["w_qkv"][:, c, 2 * C:3 * C],
                                     start=(c == 0), stop=(c == 1))
                last.then_inc(kv_ready, 1)

            def add(t, b):
                pe.wait_ge(kept, t + 1)
                pe.matmul(acc[:, 0:C], vs[b][:], ks[b][:], start=False, stop=False, skip_group_check=True)
                pe.matmul(acc_sum[:, 0:1], ks[b][:], ones[:], start=False, stop=False,
                          skip_group_check=True).then_inc(used, 1)

            ahead(make, add, False)(pe)
            pe.drain().then_inc(done, 1)
            pe.wait_ge(ctx_ready, 1)
            pe.matmul(k_ps[0][:, 0:D], ctx[:], w_out[:], start=True, stop=True).then_inc(folded, 1)


def batch(nc, name, sb_shapes, dve_steps, act_steps):
    with Stage(nc, name) as s:
        ts = [s.sb(f"t{n}", shape) for n, shape in enumerate(sb_shapes)]
        to_act, to_dve = s.sem("to_act"), s.sem("to_dve")
        block = s.block()

        @block.vector
        def _(dve):
            dve_steps(dve, ts, to_act, to_dve)

        @block.scalar
        def _(act):
            act_steps(act, ts, to_act, to_dve)


def mlp_ln(nc, d, k):
    H = 1024
    with Stage(nc, "mlp") as s:
        w2 = s.sb("w2", [128, 8, H])
        spare = k["xnT"][:].rearrange("p c n -> p (c n)")
        w1 = spare[:, 0:2 * H].rearrange("p (c n) -> p c n", c=2)
        w3 = spare[:, 2 * H:2 * H + 8 * D].rearrange("p (c n) -> p c n", c=8)
        b1, b2, b3 = s.sb("b1", [R, H]), s.sb("b2", [R, H]), s.sb("b3", [R, 1, D])
        g1, be1, g2, be2 = (s.sb(n, [128, 8]) for n in ("g1", "be1", "g2", "be2"))
        xs = k["hots"][0][:, 0:D]
        xt = s.sb("xt", [128, 2, R])
        z = [spare[0:R, 2 * H + 8 * D + n * H:2 * H + 8 * D + (n + 1) * H] for n in range(2)]
        zn = [s.sb(f"zn{n}", [R, H]) for n in range(2)]
        hT = [s.sb(f"hT{n}", [128, 8, R]) for n in range(2)]
        stats, mv = s.sb("stats", [R, 2, 6]), s.sb("mv", [R, 2])
        v1, root, inv, shift = ([s.sb(f"{a}{n}", [R, 1]) for n in range(2)] for a in ("v1", "root", "inv", "shift"))
        h_ps = [s.ps(f"h_ps{n}", [R, 2, 512]) for n in range(2)]
        t_ps = s.ps("t_ps", [128, 8, 128])
        pt = s.ps("pt", [128, 2, 256])
        y_ps = s.ps("y_ps", [R, 512])
        loaded, xs_ready, turned, xt_ready, y_ready = map(s.sem, ("loaded", "xs_ready", "turned", "xt_ready", "y_ready"))
        h_ready, var_ready, root_ready, inv_ready, zn_ready, zt_ready, hT_ready = (
            [s.sem(f"{a}{n}") for n in range(2)]
            for a in ("h_ready", "var_ready", "root_ready", "inv_ready", "zn_ready", "zt_ready", "hT_ready"))
        block = s.block()

        @block.sync
        def _(sp):
            for to, name in ((w1, "m_w1"), (w2, "m_w2"), (w3, "m_w3"), (b1, "m_b1"), (b2, "m_b2"),
                             (g1, "m_g1"), (be1, "m_be1"), (g2, "m_g2"), (be2, "m_be2")):
                sp.dma_start(to[:], d[name]).then_inc(loaded, 16)
            sp.dma_start(b3[:].rearrange("p a n -> p (a n)"), d["m_b3"]).then_inc(loaded, 16)
            sp.wait_ge(loaded, 160)

        @block.tensor
        def _(pe):
            pe.wait_ge(loaded, 160)

            def first_layer(t):
                pe.wait_ge(xs_ready, t + 1)
                for c in range(2):
                    last = pe.transpose(pt[:, c, 0:R], xs[:, c * 128:(c + 1) * 128], k["ident"][0:R, 0:R])
                last.then_inc(turned, 1)
                pe.wait_ge(xt_ready, t + 1)
                for o in range(2):
                    for c in range(2):
                        last = pe.matmul(h_ps[0][:, o, :], xt[:, c, :], w1[:, c, o * 512:(o + 1) * 512],
                                         start=(c == 0), stop=(c == 1))
                    last.then_inc(h_ready[0], 1)

            def turn(t, layer):
                pe.wait_ge(zn_ready[layer], t + 1)
                for c in range(8):
                    last = pe.transpose(t_ps[:, c, 0:R], zn[layer][:, c * 128:(c + 1) * 128], k["ident"][0:R, 0:R])
                    if c % 4 == 3:
                        last.then_inc(zt_ready[layer], 1)

            def second_layer(t):
                turn(t, 0)
                for o in range(2):
                    for c in range(8):
                        if o == 0:
                            pe.wait_ge(hT_ready[0], 8 * t + (c + 1))
                        last = pe.matmul(h_ps[1][:, o, :], hT[0][:, c, :], w2[:, c, o * 512:(o + 1) * 512],
                                         start=(c == 0), stop=(c == 7))
                    last.then_inc(h_ready[1], 1)

            def last_layer(t):
                turn(t, 1)
                for c in range(8):
                    pe.wait_ge(hT_ready[1], 8 * t + (c + 1))
                    last = pe.matmul(y_ps[:, 0:D], hT[1][:, c, :], w3[:, c, :], start=(c == 0), stop=(c == 7))
                last.then_inc(y_ready, 1)

            first_layer(0)
            with pe.Fori(0, T - 1) as t:
                second_layer(t)
                first_layer(t + 1)
                last_layer(t)
            second_layer(T - 1)
            last_layer(T - 1)

        @block.scalar
        def _(act):
            act.wait_ge(loaded, 160)

            def columns(t):
                act.wait_ge(turned, t + 1)
                act.activation(xt[:], pt[:, :, 0:R], ACT.Copy).then_inc(xt_ready, 1)

            def normed(t, layer):
                act.wait_ge(var_ready[layer], t + 1)
                act.activation(root[layer][:], v1[layer][:], ACT.Sqrt).then_inc(root_ready[layer], 1)
                act.wait_ge(inv_ready[layer], t + 1)
                act.activation(zn[layer][:], z[layer], ACT.Identity, bias=shift[layer][:],
                               scale=inv[layer][:]).then_inc(zn_ready[layer], 1)

            def relu(t, layer):
                g, be = ((g1, be1), (g2, be2))[layer]
                for c in range(8):
                    if c % 4 == 0:
                        act.wait_ge(zt_ready[layer], 2 * t + (c // 4 + 1))
                    act.activation(hT[layer][:, c, :], t_ps[:, c, 0:R], ACT.Relu, bias=be[:, c:c + 1],
                                   scale=g[:, c:c + 1]).then_inc(hT_ready[layer], 1)

            columns(0)
            normed(0, 0)
            with act.Fori(0, T - 1) as t:
                relu(t, 0)
                columns(t + 1)
                normed(t, 1)
                relu(t, 1)
                normed(t + 1, 0)
            relu(T - 1, 0)
            normed(T - 1, 1)
            relu(T - 1, 1)

        @block.vector
        def _(dve):
            dve.wait_ge(loaded, 160)

            def fetch(t):
                dve.tensor_copy(xs.rearrange("p (a n) -> p a n", a=1), k["A"][:, bass.ds(t, 1), :]).then_inc(xs_ready, 1)

            def norm(t, layer):
                bias = (b1, b2)[layer]
                for o in range(2):
                    dve.wait_ge(h_ready[layer], 2 * t + (o + 1))
                    dve.tensor_tensor(z[layer][:, o * 512:(o + 1) * 512], h_ps[layer][:, o, :],
                                      bias[:, o * 512:(o + 1) * 512], ALU.add)
                    dve.drain()
                    dve.bn_stats(stats[:, o, :], z[layer][:, o * 512:(o + 1) * 512])
                dve.drain()
                dve.bn_aggr(mv[:], stats[:].rearrange("p a n -> p (a n)"))
                dve.drain()
                dve.tensor_scalar(v1[layer][:], mv[:, 1:2], LN_EPS, None, ALU.add).then_inc(var_ready[layer], 1)
                dve.wait_ge(root_ready[layer], t + 1)
                dve.reciprocal(inv[layer][:], root[layer][:])
                dve.drain()
                dve.scalar_tensor_tensor(shift[layer][:], mv[:, 0:1], -1.0, inv[layer][:], ALU.mult, ALU.mult)
                dve.drain().then_inc(inv_ready[layer], 1)

            def result(t):
                dve.wait_ge(y_ready, t + 1)
                row = y_ps[:, 0:D].rearrange("p (a n) -> p a n", a=1)
                dve.tensor_tensor(k["B"][:, bass.ds(t, 1), :], row, b3[:], ALU.add)
                dve.drain()
                dve.tensor_tensor(k["B"][:, bass.ds(t, 1), :], k["B"][:, bass.ds(t, 1), :], k["xn"][:, bass.ds(t, 1), :], ALU.add)

            fetch(0)
            norm(0, 0)
            with dve.Fori(0, T - 1) as t:
                fetch(t + 1)
                norm(t, 1)
                norm(t + 1, 0)
                result(t)
            norm(T - 1, 1)
            result(T - 1)


def small_experts(nc, d, k, into):
    with Stage(nc, "ffn2") as s:
        sw1, sw2, sw3 = s.sb("sw1", [128, 2, 256]), s.sb("sw2", [128, 2, 128]), s.sb("sw3", [128, D])
        ew1, ew2, ew3 = s.sb("ew1", [128, 4, 2, 128]), s.sb("ew2", [128, 4, 64]), s.sb("ew3", [65, 4, D])
        sb1, sb2 = s.sb("sb1", [128, 2]), s.sb("sb2", [128, 1])
        eb1, eb2 = s.sb("eb1", [128, 4]), s.sb("eb2", [64, 4])
        h1 = s.sb("h1", [128, 2, 3 * R])
        h2 = s.sb("h2", [128, 3 * R])
        h2e = s.sb("h2e", [65, 3 * R])
        sb3 = s.sb("sb3", [R, D])
        a_ps = [s.ps(f"a_ps{b}", [128, 512]) for b in range(2)]
        b_ps = s.ps("b_ps", [128, 512])
        o_ps = s.ps("o_ps", [R, 3, 512])
        loaded, one_ready, one_kept, two_ready, two_kept, out_ready, out_free = map(
            s.sem, ("loaded", "one_ready", "one_kept", "two_ready", "two_kept", "out_ready", "out_free"))
        block = s.block()

        @block.sync
        def _(sp):
            for to, name in ((sw1, "s_w1"), (sw2, "s_w2"), (sw3, "s_w3"), (ew1, "e_w1"), (ew2, "e_w2"), (ew3, "e_w3"),
                             (sb1, "s_b1"), (sb2, "s_b2"), (eb1, "e_b1"), (eb2, "e_b2"), (sb3, "sb3")):
                sp.dma_start(to[:], d[name]).then_inc(loaded, 16)
            sp.wait_ge(loaded, 176)

        @block.tensor
        def _(pe):
            pe.wait_ge(loaded, 176)

            def group(t, g, n, p):
                def first(net):
                    for o in range(2 if net == 0 else 1):
                        for i in range(2):
                            w = sw1[:, i, o * 128:(o + 1) * 128] if net == 0 else ew1[:, net - 1, i, :]
                            last = pe.matmul(a_ps[o][:, 0:g * R], w, k["xnT"][:, i, rows(t, g)], start=(i == 0), stop=(i == 1))
                    last.then_inc(one_ready, 1)

                def second(net):
                    pe.wait_ge(one_kept, 5 * n + net + 1)
                    if net == 0:
                        for i in range(2):
                            last = pe.matmul(b_ps[:, 0:g * R], sw2[:, i, :], h1[:, i, 0:g * R], start=(i == 0), stop=(i == 1))
                    else:
                        last = pe.matmul(b_ps[0:64, 0:g * R], ew2[:, net - 1, :], h1[:, 0, 0:g * R], start=True, stop=True)
                    last.then_inc(two_ready, 1)

                def third(net):
                    pe.wait_ge(two_kept, 5 * n + net + 1)
                    pe.wait_ge(out_free, 5 * n + net + 1)
                    for j in range(g):
                        if net == 0:
                            last = pe.matmul(o_ps[:, j, 0:D], h2[:, j * R:(j + 1) * R], sw3[:], start=True, stop=True)
                        else:
                            last = pe.matmul(o_ps[:, j, 0:D], h2e[:, j * R:(j + 1) * R], ew3[:, net - 1, :], start=True, stop=True)
                    last.then_inc(out_ready, 1)

                first(0)
                second(0)
                for net in range(1, 5):
                    first(net)
                    third(net - 1)
                    second(net)
                third(4)

            groups(pe, group)

        @block.scalar
        def _(act):
            act.wait_ge(loaded, 176)

            def group(t, g, n, p):
                for net in range(5):
                    m = 5 * n + net
                    act.wait_ge(one_ready, m + 1)
                    for o in range(2 if net == 0 else 1):
                        act.activation(h1[:, o, 0:g * R], a_ps[o][:, 0:g * R], ACT.Relu,
                                       bias=sb1[:, o:o + 1] if net == 0 else eb1[:, net - 1:net])
                    act.drain().then_inc(one_kept, 1)
                    act.wait_ge(two_ready, m + 1)
                    if net == 0:
                        act.activation(h2[:, 0:g * R], b_ps[:, 0:g * R], ACT.Relu, bias=sb2[:]).then_inc(two_kept, 1)
                    else:
                        act.activation(h2e[0:64, 0:g * R], b_ps[0:64, 0:g * R], ACT.Relu,
                                       bias=eb2[:, net - 1:net]).then_inc(two_kept, 1)

            groups(act, group)

        @block.vector
        def _(dve):
            dve.memset(h2e[64:65, :], 1.0).then_inc(out_free, 1)
            dve.wait_ge(loaded, 176)

            def group(t, g, n, p):
                for net in range(5):
                    dve.wait_ge(out_ready, 5 * n + net + 1)
                    for j in range(g):
                        to = into[:, bass.ds(t + j, 1), :].rearrange("p a n -> p (a n)")
                        if net == 0:
                            dve.tensor_tensor(to, o_ps[:, j, 0:D], sb3[:], ALU.add)
                        else:
                            dve.scalar_tensor_tensor(to, o_ps[:, j, 0:D], k["gates"][:, bass.ds((t + j) * 4 + (net - 1), 1)],
                                                     to, ALU.mult, ALU.add)
                    dve.drain().then_inc(out_free, 1)

            groups(dve, group)


def elu_mix(nc, d, k, name, wq, bq, wkv, bkv, wo, bo, greatest):
    mix_sums(nc, d, k, name + "s", 8, "elu", wkv, bkv, None, None)
    fold(nc, d, k, name + "f", wo)
    project(nc, d, k, name + "q", wq, D, k["A"], bq)
    A, B, x = k["A"], k["B"], k["x"]
    heads_of = [v[:].rearrange("p t (h n) -> p (t h) n", n=32) for v in (A, B)]

    def dve_steps(dve, ts, to_act, to_dve):
        norm, inv = ts
        dve.tensor_scalar(B[:], A[:], 0.0, None, ALU.min)
        dve.drain().then_inc(to_act, 1)
        dve.wait_ge(to_dve, 1)
        dve.scalar_tensor_tensor(A[:], A[:], 0.0, B[:], ALU.max, ALU.add)
        dve.drain()
        dve.tensor_tensor(B[:], A[:], k["ksum"][:].unsqueeze(1).broadcast_to((R, T, D)), ALU.mult)
        dve.drain()
        dve.tensor_reduce(norm[:], heads_of[1], AX, ALU.add)
        dve.drain()
        dve.tensor_scalar(norm[:], norm[:], 1e-6, None, ALU.max if greatest else ALU.add)
        dve.drain()
        dve.reciprocal(inv[:], norm[:])
        dve.drain()
        dve.tensor_tensor(heads_of[0], heads_of[0], inv[:].broadcast_to((R, T * 8, 32)), ALU.mult)

    def act_steps(act, ts, to_act, to_dve):
        act.wait_ge(to_act, 1)
        act.activation(B[:], B[:], ACT.Exp).then_inc(to_dve, 1)

    batch(nc, name + "e", [[R, T * 8, 1]] * 2, dve_steps, act_steps)

    def finish(dve, t, out, vec, tmp):
        dve.tensor_tensor(tmp[0][:], out, vec[0][:].unsqueeze(1), ALU.add)
        dve.drain()
        dve.tensor_tensor(x[:, bass.ds(t, 1), :], x[:, bass.ds(t, 1), :], tmp[0][:], ALU.add)

    linear_rows(nc, d, k, name + "o", A, k["fold"], 2, copy_in(A), finish, vectors=[(bo, D)], temps=[[R, 1, D]])


def add_affine(nc, d, k, name, source, gain, shift, relu):
    row_stats(nc, d, k, name + "s", source, "ln")
    x = k["x"]

    def steps(dve, part, to, vec):
        dve.tensor_tensor(part, part, vec[0][:].unsqueeze(1).broadcast_to((R, 5, D)), ALU.mult)
        dve.drain()
        dve.tensor_tensor(part, part, vec[1][:].unsqueeze(1).broadcast_to((R, 5, D)), ALU.add)
        dve.drain()
        if relu:
            dve.scalar_tensor_tensor(to(x), part, 0.0, to(x), ALU.max, ALU.add)
        else:
            dve.tensor_tensor(to(x), to(x), part, ALU.add)

    scaled_steps(nc, d, k, name + "a", source, ACT.Identity, steps, vectors=[(gain, D), (shift, D)])


def scaled_steps(nc, d, k, name, source, func, steps, vectors=()):
    with Stage(nc, name) as s:
        vec = [s.sb(f"vec{n}", [R, v[1]]) for n, v in enumerate(vectors)]
        loaded, scaled, started = s.sem("loaded"), s.sem("scaled"), s.sem("started")
        block = s.block()

        @block.sync
        def _(sp):
            for v, t in zip(vectors, vec):
                sp.dma_start(t[:], v[0]).then_inc(loaded, 16)
            if vectors:
                sp.wait_ge(loaded, 16 * len(vectors))

        @block.scalar
        def _(act):
            with act.Fori(0, T) as t:
                act.activation(source[:, bass.ds(t, 1), :].rearrange("p a n -> p (a n)"),
                               source[:, bass.ds(t, 1), :].rearrange("p a n -> p (a n)"), func,
                               bias=col(k["shift"], t), scale=col(k["scale"], t)).then_inc(scaled, 1)

        @block.vector
        def _(dve):
            if vectors:
                dve.wait_ge(loaded, 16 * len(vectors))
            with dve.Fori(0, T // 5) as i:
                dve.wait_ge(scaled, 5 * i + 5)
                to = lambda array: array[:, bass.ds(5 * i, 5), :]
                steps(dve, to(source), to, vec)
                dve.drain()


def col(array, t):
    return array[:, bass.ds(t, 1), :].rearrange("p a n -> p (a n)")


def add_to_x(nc, d, k, name, relu):
    x, A = k["x"], k["A"]

    def dve_steps(dve, ts, to_act, to_dve):
        if relu:
            dve.scalar_tensor_tensor(x[:], A[:], 0.0, x[:], ALU.max, ALU.add)
        else:
            dve.tensor_tensor(x[:], x[:], A[:], ALU.add)

    batch(nc, name, [], dve_steps, lambda act, ts, to_act, to_dve: act.nop())


def layer0(nc, d, k):
    x, xn, A = k["x"], k["xn"], k["A"]
    row_stats(nc, d, k, "l0s", x, "ln")
    normalise(nc, d, k, "l0n", x, xn)
    first_places(nc, d, k)
    scatter_and_count(nc, d, k)
    collect_support(nc, d, k)

    def both(dve, t, xs, vec, tmp):
        dve.tensor_copy(xs[:, 0:D].unsqueeze(1), xn[:, bass.ds(t, 1), :])
        dve.tensor_copy(xs[:, D:2 * D].unsqueeze(1), A[:, bass.ds(t, 1), :])

    def relu_add(dve, t, out, vec, tmp):
        dve.tensor_tensor(tmp[0][:], out, vec[0][:].unsqueeze(1), ALU.add)
        dve.drain()
        to = x[:, bass.ds(t, 1), :]
        dve.scalar_tensor_tensor(to, tmp[0][:], 0.0, to, ALU.max, ALU.add)

    linear_rows(nc, d, k, "l0g", None, d["g0_w"], 4, both, relu_add, vectors=[(d["g0_b"], D)], temps=[[R, 1, D]])
    mix_sums(nc, d, k, "l0m", 4, "ln", d["m0_wkv"], None, d["m0_gain"], d["m0_shift"])
    fold(nc, d, k, "l0f", d["m0_wo"], d["m0_wq"])
    project(nc, d, k, "l0o", k["fold"][:], D, x, d["m0_bo"], add=True)
    row_stats(nc, d, k, "l0t", x, "ln")
    normalise(nc, d, k, "l0u", x, xn)
    gates = k["gates"][:, 0:T * 32].rearrange("p (t e) -> p t e", e=32)
    project(nc, d, k, "l0r", d["r0_w"], 32, gates, d["r0_b"])
    gate(nc, d, k, "l0h", 32, "first")
    expert_places(nc, d, k, "l0p", 32, [k["hots"][0][:].rearrange("p (t e) -> p t e", e=32)])
    sort_rows(nc, d, k, "l0v", xn, 1)
    sorted_experts(nc, d, k, "l0e", 32, 64, 1, d["f0_w1"], d["f0_b1"], d["f0_w2"], d["f0_b2"])

    def relu_to_x(dve, t, got):
        to = x[:, bass.ds(t, 1), :]
        dve.scalar_tensor_tensor(to, got[0], 0.0, to, ALU.max, ALU.add)

    unsort_rows(nc, d, k, "l0w", 1, relu_to_x)


def layer1(nc, d, k):
    x, xn, A, B = k["x"], k["xn"], k["A"], k["B"]
    row_stats(nc, d, k, "l1s", x, "ln")
    normalise(nc, d, k, "l1n", x, xn)

    def dve_steps(dve, ts, to_act, to_dve):
        dve.tensor_scalar(k["deg1"][:], k["deg"][:], 1.0, None, ALU.add)
        dve.tensor_scalar(ts[0][:], k["deg"][:], 1.0, None, ALU.max)
        dve.drain().then_inc(to_act, 1)
        dve.reciprocal(k["rdeg"][:], ts[0][:])
        dve.wait_ge(to_dve, 1)
        dve.reciprocal(k["dinv"][:], ts[1][:])
        dve.drain()
        for t in range(T):
            dve.tensor_scalar(A[:, t, :], xn[:, t, :], k["dinv"][:, t:t + 1], None, ALU.mult)

    def act_steps(act, ts, to_act, to_dve):
        act.wait_ge(to_act, 1)
        act.activation(ts[1][:], k["deg1"][:], ACT.Sqrt).then_inc(to_dve, 1)

    batch(nc, "l1d", [[R, T]] * 2, dve_steps, act_steps)

    def scaled(dve, t, into, acc, temp):
        dve.tensor_tensor(temp, acc, A[:, bass.ds(t, 1), :], ALU.add)
        dve.drain()
        dve.tensor_scalar(into, temp, k["dinv"][:, bass.ds(t, 1)], None, ALU.mult)

    for i in range(3):
        def step(dve, t, out, vec, tmp, last=(i == 2)):
            dve.tensor_tensor(tmp[0][:], out, vec[0][:].unsqueeze(1), ALU.add)
            dve.drain()
            if last:
                dve.tensor_tensor(x[:, bass.ds(t, 1), :], x[:, bass.ds(t, 1), :], tmp[0][:], ALU.add)
            else:
                dve.tensor_scalar(A[:, bass.ds(t, 1), :], tmp[0][:], k["dinv"][:, bass.ds(t, 1)], None, ALU.mult)

        aggregate(nc, d, k, f"l1a{i}", A, B, scaled)
        linear_rows(nc, d, k, f"l1w{i}", B, d[f"g1_w{i}"], 2, copy_in(B), step, vectors=[(d[f"g1_b{i}"], D)],
                    temps=[[R, 1, D]])

    row_stats(nc, d, k, "l1m", xn, "norm")
    batch(nc, "l1c", [], lambda dve, ts, a, b: dve.tensor_scalar(k["scale"][:], k["scale"][:], float(D) ** 0.5, None, ALU.mult),
          lambda act, ts, a, b: act.nop())
    normalise(nc, d, k, "l1r", xn)
    softmax_keys(nc, d, k, "l1k")
    q = A[:].rearrange("p t n -> p (t n)")[:, 0:T * 128].rearrange("p (t n) -> p t n", n=128)
    heads = A[:].rearrange("p t n -> p (t n)")[:, 0:T * 128].rearrange("p (g n) -> p g n", n=32)
    project(nc, d, k, "l1q", k["w_qkv"][:, :, 0:128], 128, q)

    def q_dve(dve, ts, to_act, to_dve):
        most, total = ts
        dve.tensor_reduce(most[:], heads, AX, ALU.max)
        dve.drain()
        dve.tensor_tensor(heads, heads, most[:].broadcast_to((R, T * 4, 32)), ALU.subtract)
        dve.drain().then_inc(to_act, 1)
        dve.wait_ge(to_dve, 1)
        dve.tensor_reduce(most[:], heads, AX, ALU.add)
        dve.drain()
        dve.reciprocal(total[:], most[:])
        dve.drain()
        dve.tensor_tensor(heads, heads, total[:].broadcast_to((R, T * 4, 32)), ALU.mult)

    def q_act(act, ts, to_act, to_dve):
        act.wait_ge(to_act, 1)
        act.activation(q, q, ACT.Exp).then_inc(to_dve, 1)

    batch(nc, "l1x", [[R, T * 4, 1]] * 2, q_dve, q_act)

    def to_b(dve, t, out, vec, tmp):
        dve.tensor_tensor(B[:, bass.ds(t, 1), :], out, vec[0][:].unsqueeze(1), ALU.add)

    linear_rows(nc, d, k, "l1o", q, k["fold"], 1, copy_in(q), to_b, vectors=[(d["m1_b"], D)])
    row_stats(nc, d, k, "l1p", B, "norm")

    def rms_add(dve, part, to, vec):
        dve.scalar_tensor_tensor(part, part, float(D) ** 0.5, vec[0][:].unsqueeze(1).broadcast_to((R, 5, D)),
                                 ALU.mult, ALU.mult)
        dve.drain()
        dve.tensor_tensor(part, part, to(xn), ALU.add)
        dve.drain()
        dve.tensor_tensor(to(x), to(x), part, ALU.add)

    scaled_steps(nc, d, k, "l1y", B, ACT.Identity, rms_add, vectors=[(d["m1_g"], D)])

    row_stats(nc, d, k, "l1t", x, "ln")
    normalise(nc, d, k, "l1u", x, xn)
    project(nc, d, k, "l1v", d["f1_wr"], 1, k["gates"][:, 0:T].rearrange("p (t e) -> p t e", e=1), d["f1_br"])
    rank_gate(nc, d, k, "l1i", NODES // 2 - 1)

    def gated_bias(dve, t, vec, tmp):
        dve.scalar_tensor_tensor(A[:, bass.ds(t, 1), :], vec[0][:].unsqueeze(1), k["gates"][:, bass.ds(2 * t, 1)],
                                 xn[:, bass.ds(t, 1), :], ALU.mult, ALU.add)

    elementwise(nc, d, k, "l1b", gated_bias, vectors=[(d["f1_b2"], D)])
    experts(nc, d, k, "l1e", 2, 128, 4, ACT.Gelu_apprx_tanh, d["f1_w1"], d["f1_b1"], d["f1_w2"], A)
    add_to_x(nc, d, k, "l1z", False)


def layer2(nc, d, k):
    x, xn, A, B = k["x"], k["xn"], k["A"], k["B"]
    row_stats(nc, d, k, "l2s", x, "ln")
    normalise(nc, d, k, "l2n", x, xn)
    elu_mix(nc, d, k, "l2m", d["m2_wq"], d["m2_bq"], d["m2_wkv"], d["m2_bkv"], d["m2_wo"], d["m2_bo"], False)

    with Stage(nc, "eps") as s:
        raw, ready = s.sb("raw", [R, 1]), s.sem("ready")
        block = s.block()

        @block.sync
        def _(sp):
            sp.dma_start(raw[:], d["eps"]).then_inc(ready, 16)

        @block.vector
        def _(dve):
            dve.wait_ge(ready, 16)
            dve.tensor_scalar(k["eps2"][:], raw[:], 2.0, None, ALU.add)

    def with_self(dve, t, into, acc, temp):
        dve.scalar_tensor_tensor(into, xn[:, bass.ds(t, 1), :], k["eps2"][:], acc, ALU.mult, ALU.add)

    aggregate(nc, d, k, "l2a", xn, A, with_self)
    edge_hidden(nc, d, k)

    def self_hidden(dve, t, xs, vec, tmp):
        dve.scalar_tensor_tensor(xs[:].unsqueeze(1), vec[0][:].unsqueeze(1), 0.0, B[:, bass.ds(t, 1), :], ALU.max, ALU.add)

    def add_messages(dve, t, out, vec, tmp):
        dve.tensor_tensor(tmp[0][:], out, A[:, bass.ds(t, 1), :], ALU.add)
        dve.drain()
        dve.scalar_tensor_tensor(A[:, bass.ds(t, 1), :], vec[1][:].unsqueeze(1), k["deg1"][:, bass.ds(t, 1)], tmp[0][:],
                                 ALU.mult, ALU.add)

    linear_rows(nc, d, k, "l2h", B, d["ee_w2"], 2, self_hidden, add_messages,
                vectors=[(d["ee_b1"], D), (d["ee_b2"], D)], temps=[[R, 1, D]])
    mlp_ln(nc, d, k)
    add_affine(nc, d, k, "l2b", B, d["bn_g"], d["bn_b"], True)

    row_stats(nc, d, k, "l2t", x, "ln")
    normalise(nc, d, k, "l2u", x)
    gates = k["gates"][:, 0:T * 4].rearrange("p (t e) -> p t e", e=4)
    project(nc, d, k, "l2v", d["gW"], 4, gates, d["gb"])
    gate(nc, d, k, "l2i", 4, "soft_two")
    small_experts(nc, d, k, A)
    add_to_x(nc, d, k, "l2z", False)


def layer3(nc, d, k):
    x, xn, A, B = k["x"], k["xn"], k["A"], k["B"]
    row_stats(nc, d, k, "l3s", x, "ln")
    normalise(nc, d, k, "l3n", x, xn)
    elu_mix(nc, d, k, "l3m", d["m3_wq"], None, d["m3_wkv"], None, d["m3_wo"], d["m3_bo"], True)

    def mean(dve, t, into, acc, temp):
        dve.tensor_scalar(into, acc, k["rdeg"][:, bass.ds(t, 1)], None, ALU.mult)

    aggregate(nc, d, k, "l3a", xn, A, mean)

    def both(dve, t, xs, vec, tmp):
        dve.tensor_copy(xs[:, 0:D].unsqueeze(1), A[:, bass.ds(t, 1), :])
        dve.tensor_copy(xs[:, D:2 * D].unsqueeze(1), xn[:, bass.ds(t, 1), :])

    def to_b(dve, t, out, vec, tmp):
        dve.tensor_tensor(B[:, bass.ds(t, 1), :], out, vec[0][:].unsqueeze(1), ALU.add)

    linear_rows(nc, d, k, "l3g", None, d["g3_w"], 4, both, to_b, vectors=[(d["g3_b"], D)])
    row_stats(nc, d, k, "l3p", B, "norm")

    def unit(dve, part, to, vec):
        dve.tensor_tensor(part, part, to(xn), ALU.add)

    scaled_steps(nc, d, k, "l3u", B, ACT.Relu, unit)
    add_affine(nc, d, k, "l3b", B, d["g3_gamma"], d["g3_beta"], False)

    row_stats(nc, d, k, "l3t", x, "ln")
    normalise(nc, d, k, "l3w", x, xn)
    gates = k["gates"][:, 0:T * 16].rearrange("p (t e) -> p t e", e=16)
    project(nc, d, k, "l3v", d["f3_gw"], 16, gates, d["f3_gb"])
    gate(nc, d, k, "l3i", 16, "two")
    expert_places(nc, d, k, "l3q", 16, [hot[:, 0:T * 16].rearrange("p (t e) -> p t e", e=16) for hot in k["hots"]])
    sort_rows(nc, d, k, "l3r", xn, 2)
    sorted_experts(nc, d, k, "l3e", 16, 128, 4, d["f3_w1"], d["f3_b1"], d["f3_w2"], d["f3_b2"])

    def gated_sum(dve, t, got):
        to = A[:, bass.ds(t, 1), :]
        dve.scalar_tensor_tensor(to, got[0], k["slot_gate"][0][:, bass.ds(t, 1)], xn[:, bass.ds(t, 1), :], ALU.mult, ALU.add)
        dve.drain()
        dve.scalar_tensor_tensor(to, got[1], k["slot_gate"][1][:, bass.ds(t, 1)], to, ALU.mult, ALU.add)

    unsort_rows(nc, d, k, "l3x", 2, gated_sum)
    add_affine(nc, d, k, "l3y", A, d["f3_gamma"], d["f3_beta"], False)


def program(nc, d, out, layers=4):
    with Stage(nc, "all") as s:
        k = {n: s.sb(n, [R, T, D]) for n in ("x", "xn", "A", "B")}
        k["nc"] = nc
        k["xnT"] = s.sb("xnT", [128, 2, NODES])
        k["ident"] = s.sb("ident", [128, 128])
        for n in ("dst", "src_base", "src_place", "weight"):
            k[n] = s.sb(n, [CH, NCH])
        for n in ("deg", "deg1", "dinv", "rdeg"):
            k[n] = s.sb(n, [R, T])
        k["scale"], k["shift"] = s.sb("scale", [R, T, 1]), s.sb("shift", [R, T, 1])
        k["tile_start"] = s.sb("tile_start", [128, T + 1])
        k["eps2"] = s.sb("eps2", [R, 1])
        k["kvT"], k["fold"], k["ksum"] = s.sb("kvT", [128, 2, 128]), s.sb("fold", [128, 2, D]), s.sb("ksum", [R, D])
        k["w_qkv"] = s.sb("w_qkv", [128, 2, 384])
        k["gates"] = s.sb("gates", [R, T * 32])
        k["hots"] = [s.sb("hots0", [R, T * 32]), s.sb("hots1", [R, T * 16])]
        k["slot_gate"] = [s.sb(f"slot_gate{n}", [R, T]) for n in range(2)]
        k["pos"], k["blocks"] = s.sb("pos", [R, T, 2], I32), s.sb("blocks", [1, 2, 32], I32)
        k["sorted_dram"] = nc.dram_tensor("sorted", ((BLOCKS + 1) * 128, D), F32, kind="Internal").ap()
        k["result_dram"] = nc.dram_tensor("result", (BLOCKS * 128, D), F32, kind="Internal").ap()
        k["scatter_to"] = s.sb("scatter_to", [CH, NCH], I32)
        k["support_dram"] = [nc.dram_tensor(f"support{b}", (NODES + CH, D), F32, kind="Internal").ap() for b in range(2)]
        k["ct_dram"] = nc.dram_tensor("counts", (T, R, NODES), F32, kind="Internal").ap()
        k["plan_dram"] = nc.dram_tensor("plan", (1, 3, T), I32, kind="Internal").ap()
        k["ends_dram"] = nc.dram_tensor("ends", (2 * T, 1), F32, kind="Internal").ap()
        k["line_dram"] = nc.dram_tensor("line", (NODES,), F32, kind="Internal").ap()

        with Stage(nc, "load") as st:
            loaded = st.sem("loaded")
            block = st.block()

            @block.sync
            def _(sp):
                sp.dma_start(k["x"][:], d["x"].rearrange("(t p) n -> p t n", p=R)).then_inc(loaded, 16)
                sp.dma_start(k["tile_start"][:], d["tile_start"]).then_inc(loaded, 16)
                sp.wait_ge(loaded, 32)

        plan_edges(nc, d, k)
        for layer in (layer0, layer1, layer2, layer3)[:layers]:
            layer(nc, d, k)

        with Stage(nc, "store") as st:
            stored = st.sem("stored")
            block = st.block()

            @block.sync
            def _(sp):
                sp.dma_start(out.rearrange("(t p) n -> p t n", p=R), k["x"][:]).then_inc(stored, 16)
                sp.wait_ge(stored, 16)



def lay_out(i):
    def row(v, n=R):
        return np.repeat(np.asarray(v).reshape(1, -1), n, axis=0)

    def chunks(w):
        w = np.asarray(w)
        return w.reshape(-1, 128, w.shape[1]).transpose(1, 0, 2)

    def columns(v, p=128):
        return np.asarray(v).reshape(-1, p).T

    def edges(v, fill):
        v = np.asarray(v)
        return np.concatenate([v, np.full(NCH * CH - EDGES, fill, v.dtype)]).reshape(NCH, CH).T

    def join(*a, axis=1):
        return np.concatenate([np.asarray(v) for v in a], axis=axis)

    E0, E3 = i["L0_ffn_W1"].shape[0], i["L3_ffn_w1"].shape[0]
    attr = np.concatenate([np.asarray(i["edge_attr_64"]), np.zeros((NCH * CH - EDGES, EDIM), np.float32)])
    kg, kb, vg, vb = (np.tile(np.asarray(i["L0_mix_ln_" + n]), 4) for n in ("k_g", "k_b", "v_g", "v_b"))
    mem = np.asarray(i["L1_mix_mem_kv"])
    w3kv = np.asarray(i["L3_mix_Wkv"])
    blocks = np.arange(128)
    d = {
        "x": i["x"], "src": edges(i["src"], 0), "src_row": np.ascontiguousarray(edges(i["src"], 0).T).reshape(1, -1),
        "own_row": (NODES + np.arange(CH, dtype=np.float32)).reshape(CH, 1),
        "before": (np.arange(CH) < np.arange(CH)[:, None]).astype(np.float32), "dst": edges(i["dst"], -1), "weight": edges(i["edge_weight"], 0),
        "attr": np.concatenate([attr.T, np.ones((1, NCH * CH), np.float32)]),
        "pair_up": row(np.arange(NCH) // 2 + 1, CH).astype(np.float32),
        "pair_down": row(PAIRS - np.arange(NCH) // 2, CH).astype(np.float32),
        "ident": np.eye(128, dtype=np.float32),
        "iota16": row(np.arange(WIDE), CH).astype(np.int16), "iota_r": row(np.arange(R), CH).astype(np.float32),
        "tile_start": row(np.arange(T + 1) * R, 128).astype(np.float32),
        "mask64": (blocks[:, None] // 64 == blocks // 64).astype(np.float32),
        "mask32": (blocks[:, None] // 32 == blocks // 32).astype(np.float32),
        "above": (np.arange(R)[:, None] < np.arange(R)).astype(np.float32),
        "below": (np.arange(R) < np.arange(R)[:, None]).astype(np.float32),
        "down": row(32 - np.arange(32)).astype(np.float32),
        "zero_row": np.zeros((R, 2 * D), np.float32),
        "g0_w": chunks(i["L0_gnn_W"]), "g0_b": row(i["L0_gnn_b"]),
        "m0_wkv": chunks(join(np.asarray(i["L0_mix_wk"]).T, np.asarray(i["L0_mix_wv"]).T)),
        "m0_gain": row(np.concatenate([kg, vg])), "m0_shift": row(np.concatenate([kb, vb])),
        "m0_wo": chunks(np.asarray(i["L0_mix_wo"]).T), "m0_wq": chunks(i["L0_mix_wq"]), "m0_bo": row(i["L0_mix_bo"]),
        "r0_w": chunks(np.asarray(i["L0_ffn_router_w"]).T), "r0_b": row(i["L0_ffn_router_b"]),
        "f0_w1": np.asarray(i["L0_ffn_W1"]).reshape(E0, 2, 128, 64).transpose(0, 2, 1, 3),
        "f0_b1": np.asarray(i["L0_ffn_b1"]).T, "f0_w2": np.asarray(i["L0_ffn_W2"]).reshape(E0, 64, 1, D),
        "f0_b2": i["L0_ffn_b2"],
        "w_qkv": chunks(i["L1_mix_w_qkv"]), "g_pre": columns(i["L1_mix_g_pre"]), "w_out": i["L1_mix_w_out"],
        "mem_k": mem[0].reshape(128, 4), "mem_v": mem[1].reshape(128, 4).T,
        "m1_b": row(i["L1_mix_b_out"]), "m1_g": row(i["L1_mix_g_out"]),
        "f1_wr": chunks(i["L1_ffn_wr"]), "f1_br": row(i["L1_ffn_br"]),
        "f1_w1": np.asarray(i["L1_ffn_w1"]).reshape(2, 128, 2, 512).transpose(2, 1, 0, 3),
        "f1_b1": columns(i["L1_ffn_b1"]),
        "f1_w2": np.asarray(i["L1_ffn_w2"]).reshape(2, 4, 128, D).transpose(0, 2, 1, 3),
        "f1_b2": row(i["L1_ffn_b2"]),
        "m2_wq": chunks(i["L2_mix_wq"]), "m2_bq": row(i["L2_mix_bq"]),
        "m2_wkv": chunks(join(i["L2_mix_wk"], i["L2_mix_wv"])),
        "m2_bkv": row(join(i["L2_mix_bk"], i["L2_mix_bv"], axis=0)),
        "m2_wo": chunks(i["L2_mix_wo"]), "m2_bo": row(i["L2_mix_bo"]),
        "eps": row(i["L2_gnn_eps"]),
        "ee_w1": join(i["L2_gnn_ee_w1"], np.asarray(i["L2_gnn_ee_b1"]).reshape(1, -1), axis=0),
        "ee_b1": row(i["L2_gnn_ee_b1"]), "ee_w2": chunks(i["L2_gnn_ee_w2"]), "ee_b2": row(i["L2_gnn_ee_b2"]),
        "m_w1": chunks(i["L2_gnn_w1"]), "m_w2": chunks(i["L2_gnn_w2"]), "m_w3": chunks(i["L2_gnn_w3"]),
        "m_b1": row(i["L2_gnn_b1"]), "m_b2": row(i["L2_gnn_b2"]), "m_b3": row(i["L2_gnn_b3"]),
        "m_g1": columns(i["L2_gnn_g1"]), "m_be1": columns(i["L2_gnn_be1"]),
        "m_g2": columns(i["L2_gnn_g2"]), "m_be2": columns(i["L2_gnn_be2"]),
        "bn_g": row(i["L2_gnn_bn_g"]), "bn_b": row(i["L2_gnn_bn_b"]),
        "gW": chunks(i["L2_ffn_gW"]), "gb": row(i["L2_ffn_gb"]), "sb3": row(i["L2_ffn_sb3"]),
        "s_w1": chunks(i["L2_ffn_sW1"]), "s_w2": chunks(i["L2_ffn_sW2"]), "s_w3": i["L2_ffn_sW3"],
        "e_w1": np.asarray(i["L2_ffn_eW1"]).reshape(4, 2, 128, 128).transpose(2, 0, 1, 3),
        "e_w2": np.asarray(i["L2_ffn_eW2"]).transpose(1, 0, 2), "e_w3": join(np.asarray(i["L2_ffn_eW3"]).transpose(1, 0, 2), np.asarray(i["L2_ffn_eb3"])[None], axis=0),
        "s_b1": columns(i["L2_ffn_sb1"]), "s_b2": columns(i["L2_ffn_sb2"]),
        "e_b1": np.asarray(i["L2_ffn_eb1"]).T, "e_b2": np.asarray(i["L2_ffn_eb2"]).T,
        "m3_wq": chunks(np.asarray(i["L3_mix_Wq"]).T), "m3_wkv": chunks(w3kv.T),
        "m3_wo": chunks(np.asarray(i["L3_mix_Wproj"]).T), "m3_bo": row(i["L3_mix_bproj"]),
        "g3_w": chunks(join(np.asarray(i["L3_gnn_W_l"]).T, np.asarray(i["L3_gnn_W_r"]).T, axis=0)),
        "g3_b": row(i["L3_gnn_b_l"]), "g3_gamma": row(i["L3_gnn_gamma"]), "g3_beta": row(i["L3_gnn_beta"]),
        "f3_gw": chunks(i["L3_ffn_gate_w"]), "f3_gb": row(i["L3_ffn_gate_b"]),
        "f3_w1": np.asarray(i["L3_ffn_w1"]).reshape(E3, 2, 128, 512).transpose(0, 2, 1, 3),
        "f3_b1": columns(np.asarray(i["L3_ffn_b1"]).reshape(-1)),
        "f3_w2": np.asarray(i["L3_ffn_w2"]).reshape(E3, 4, 128, D).transpose(0, 2, 1, 3),
        "f3_b2": i["L3_ffn_b2"], "f3_gamma": row(i["L3_ffn_gamma"]), "f3_beta": row(i["L3_ffn_beta"]),
    }
    for n in range(3):
        d[f"g1_w{n}"], d[f"g1_b{n}"] = chunks(i[f"L1_gnn_W{n + 1}"]), row(i[f"L1_gnn_b{n + 1}"])
    return {n: np.ascontiguousarray(v) for n, v in d.items()}


def kernel(**inputs):
    import concourse.bacc as bacc
    from concourse.bass_utils import run_bass_kernel_spmd as run

    nc = bacc.Bacc("TRN2", target_bir_lowering=False, num_devices=1)
    arrays, d = {}, {}
    for name, a in lay_out(inputs).items():
        arrays[f"in_{name}"] = a
        d[name] = nc.dram_tensor(f"in_{name}", a.shape, mybir.dt.from_np(a.dtype), kind="ExternalInput").ap()
    out = nc.dram_tensor("out_rows", (NODES, D), F32, kind="ExternalOutput").ap()
    program(nc, d, out, LAYERS)
    return run(nc, [arrays], core_ids=[0]).results[0]["out_rows"]


LAYERS = 4
```
